# Optimizing a Trainium2 kernel written in Bass

```python
import numpy as np
import jax
import jax.numpy as jnp

def _softmax(x, axis=-1):
    return jax.nn.softmax(x, axis=axis)

def _gelu(x):
    return jax.nn.gelu(x, approximate=True)

def _silu(x):
    return jax.nn.silu(x)

def _sigmoid(x):
    return jax.nn.sigmoid(x)

def _layernorm(x, axis=-1, eps=1e-05):
    m = jnp.mean(x, axis=axis, keepdims=True)
    v = jnp.var(x, axis=axis, keepdims=True)
    return (x - m) / jnp.sqrt(v + eps)

def _scatter_add(tgt, idx, src, axis=0):
    return tgt.at[idx].add(src)

def _segment_sum(src, seg, n):
    return jax.ops.segment_sum(src, seg, n)
kernel_name = 'mk_gps_d2_gnn_r8_c2e217'

def setup_inputs(seed: int=0):
    np.random.seed(seed)
    _w = jnp.asarray

    def _rec_inputs():
        import jax
        import jax.numpy as jnp
        _gk = jax.random.key(seed)
        x = -0.0006008 + 1.001 * jax.random.normal(jax.random.fold_in(_gk, 1), (6250, 256), jnp.float32)
        src = jax.random.randint(jax.random.fold_in(_gk, 2), (100000,), 0, 6250, jnp.int32)
        dst = jnp.minimum((6250 * jax.random.uniform(jax.random.fold_in(_gk, 3), (100000,)) ** 2.0).astype(jnp.int32), 49999)
        _o = jnp.argsort(dst, stable=True)
        src = src[_o]
        dst = dst[_o]
        edge_attr_3 = 0.000669165 + 0.999965 * jax.random.normal(jax.random.fold_in(_gk, 11), (100000, 3), jnp.float32)
        return (x, src, dst, edge_attr_3)
    x, src, dst, edge_attr_3 = _rec_inputs()

    def _L0_gnn_setup():
        import jax, jax.numpy as jnp
        import numpy as np
        EPS = 1e-05

        def _gcn_conv(x, W, row, col, n_nodes):
            xl = x @ W.T
            ones = jnp.ones(row.shape[0], dtype=x.dtype)
            deg = jax.ops.segment_sum(ones, col, num_segments=n_nodes)
            dis = jnp.where(deg > 0, deg ** (-0.5), 0.0).astype(x.dtype)
            norm = dis[row] * dis[col]
            msg = xl[row] * norm[:, None]
            return jax.ops.segment_sum(msg, col, num_segments=n_nodes)

        def _batchnorm(x, gamma, beta):
            m = jnp.mean(x, axis=0)
            v = jnp.mean((x - m) ** 2, axis=0)
            return (x - m) * jax.lax.rsqrt(v + EPS) * gamma + beta
        key = jax.random.key(seed)
        k1, k2, k3, k4 = jax.random.split(key, 4)
        N, C, IC, E = (1250, 256, 512, 20000)
        x = jax.random.normal(k1, (N, C), dtype=jnp.float32)
        es = jax.random.randint(k2, (2, E), 0, N, dtype=jnp.int64)
        W1 = jax.random.normal(k3, (IC, C), dtype=jnp.float32) * (1.0 / np.sqrt(C))
        W2 = jax.random.normal(k4, (C, IC), dtype=jnp.float32) * (1.0 / np.sqrt(IC))
        g1 = jnp.ones((IC,), jnp.float32)
        b1 = jnp.zeros((IC,), jnp.float32)
        g2 = jnp.ones((C,), jnp.float32)
        b2 = jnp.zeros((C,), jnp.float32)
        return {'x': x, 'es': es, 'W1': W1, 'g1': g1, 'b1': b1, 'W2': W2, 'g2': g2, 'b2': b2}
    _L0_gnn_all = _L0_gnn_setup()
    _L0_gnn_in = {k: v for k, v in _L0_gnn_all.items() if k in ('W1', 'g1', 'b1', 'W2', 'g2', 'b2')}
    del _L0_gnn_all

    def _L0_mix_setup():
        import jax, jax.numpy as jnp
        import numpy as np
        HEADS = 8
        DIM_HEAD = 64
        EPS = 1e-05

        def _inst_norm_lastdim(t):
            mu = jnp.mean(t, axis=-1, keepdims=True)
            var = jnp.mean(jnp.square(t - mu), axis=-1, keepdims=True)
            return (t - mu) * jax.lax.rsqrt(var + EPS)
        key = jax.random.key(seed)
        k1, k2, k3, k4 = jax.random.split(key, 4)
        b, n, dim = (4, 1024, 256)
        inner = HEADS * DIM_HEAD
        x = jax.random.normal(k1, (b, n, dim), dtype=jnp.float32)
        Wqkv = jax.random.normal(k2, (3 * inner, dim), dtype=jnp.float32) * (1.0 / np.sqrt(dim))
        Wout = jax.random.normal(k3, (dim, inner), dtype=jnp.float32) * (1.0 / np.sqrt(inner))
        bout = jax.random.normal(k4, (dim,), dtype=jnp.float32) * 0.01
        return {'x': x, 'Wqkv': Wqkv, 'Wout': Wout, 'bout': bout}
    _L0_mix_all = _L0_mix_setup()
    _L0_mix_in = {k: v for k, v in _L0_mix_all.items() if k in ('Wqkv', 'Wout', 'bout')}
    del _L0_mix_all

    def _L0_ffn_setup():
        import jax, jax.numpy as jnp
        import numpy as np
        B, S, D, E, H, K = (4, 512, 256, 8, 512, 2)
        key = jax.random.key(seed)
        ks = jax.random.split(key, 6)
        x = jax.random.normal(ks[0], (B, S, D), jnp.float32)
        Wg = jax.random.normal(ks[1], (D, E), jnp.float32) * 0.02
        bg = jnp.zeros((E,), jnp.float32)
        W1 = jax.random.normal(ks[2], (E, D, H), jnp.float32) * 0.02
        b1 = jnp.zeros((E, H), jnp.float32)
        W2 = jax.random.normal(ks[3], (E, H, D), jnp.float32) * 0.02
        b2 = jnp.zeros((E, D), jnp.float32)
        return {'x': x, 'Wg': Wg, 'bg': bg, 'W1': W1, 'b1': b1, 'W2': W2, 'b2': b2}
    _L0_ffn_all = _L0_ffn_setup()
    _L0_ffn_in = {k: v for k, v in _L0_ffn_all.items() if k in ('Wg', 'bg', 'W1', 'b1', 'W2', 'b2')}
    del _L0_ffn_all

    def _L1_gnn_setup():
        import jax, jax.numpy as jnp
        import numpy as np
        N = 6250
        H = 256
        E = 100000
        F = 3
        DIST_SCALE = 4.0
        LN_EPS = 1e-05
        key = jax.random.key(seed)
        ks = jax.random.split(key, 8)
        x = jax.random.normal(ks[0], (N, H), dtype=jnp.float32)
        edge_index = jax.random.randint(ks[1], (2, E), 0, N, dtype=jnp.int64)
        edge_attr = jax.random.normal(ks[2], (E, F), dtype=jnp.float32)
        W1 = jax.random.normal(ks[3], (H, H), dtype=jnp.float32) * 0.02
        b1 = jnp.zeros((H,), dtype=jnp.float32)
        W2 = jax.random.normal(ks[4], (H, H), dtype=jnp.float32) * 0.02
        b2 = jnp.zeros((H,), dtype=jnp.float32)
        gamma = jnp.ones((H,), dtype=jnp.float32)
        beta = jnp.zeros((H,), dtype=jnp.float32)
        return {'x': x, 'edge_index': edge_index, 'edge_attr': edge_attr, 'W1': W1, 'b1': b1, 'W2': W2, 'b2': b2, 'gamma': gamma, 'beta': beta}
    _L1_gnn_all = _L1_gnn_setup()
    _L1_gnn_in = {k: v for k, v in _L1_gnn_all.items() if k in ('W1', 'b1', 'W2', 'b2', 'gamma', 'beta')}
    del _L1_gnn_all

    def _L1_mix_setup():
        import jax, jax.numpy as jnp
        import numpy as np
        NUM_HEADS = 8
        key = jax.random.key(seed)
        ks = jax.random.split(key, 5)
        B, N, C = (8, 2048, 256)
        x = jax.random.normal(ks[0], (B, N, C), dtype=jnp.float32)
        Wq = jax.random.normal(ks[1], (C, C), dtype=jnp.float32) * 0.02
        Wkv = jax.random.normal(ks[2], (2 * C, C), dtype=jnp.float32) * 0.02
        Wproj = jax.random.normal(ks[3], (C, C), dtype=jnp.float32) * 0.02
        bproj = jnp.zeros((C,), dtype=jnp.float32)
        return {'x': x, 'Wq': Wq, 'Wkv': Wkv, 'Wproj': Wproj, 'bproj': bproj}
    _L1_mix_all = _L1_mix_setup()
    _L1_mix_in = {k: v for k, v in _L1_mix_all.items() if k in ('Wq', 'Wkv', 'Wproj', 'bproj')}
    del _L1_mix_all

    def _L1_ffn_setup():
        import jax, jax.numpy as jnp
        import numpy as np
        B, A = (512, 8)
        IN, OUT = (256, 256)
        SH1, SH2 = (256, 128)
        EH1, EH2 = (128, 64)
        E, TOPK = (4, 2)

        def _shared_mlp(x, W1, b1, W2, b2, W3, b3):
            h = jax.nn.relu(x @ W1 + b1)
            h = jax.nn.relu(h @ W2 + b2)
            return h @ W3 + b3

        def _experts_mlp(x, eW1, eb1, eW2, eb2, eW3, eb3):
            h = jax.nn.relu(jnp.einsum('baf,efh->ebah', x, eW1) + eb1[:, None, None, :])
            h = jax.nn.relu(jnp.einsum('ebah,ehg->ebag', h, eW2) + eb2[:, None, None, :])
            o = jnp.einsum('ebag,ego->ebao', h, eW3) + eb3[:, None, None, :]
            return jnp.moveaxis(o, 0, -1)
        key = jax.random.key(seed)
        ks = jax.random.split(key, 16)
        s = 0.05
        return {'x': jax.random.normal(ks[0], (B, A, IN), jnp.float32), 'sW1': jax.random.normal(ks[1], (IN, SH1), jnp.float32) * s, 'sb1': jnp.zeros((SH1,), jnp.float32), 'sW2': jax.random.normal(ks[2], (SH1, SH2), jnp.float32) * s, 'sb2': jnp.zeros((SH2,), jnp.float32), 'sW3': jax.random.normal(ks[3], (SH2, OUT), jnp.float32) * s, 'sb3': jnp.zeros((OUT,), jnp.float32), 'eW1': jax.random.normal(ks[4], (E, IN, EH1), jnp.float32) * s, 'eb1': jnp.zeros((E, EH1), jnp.float32), 'eW2': jax.random.normal(ks[5], (E, EH1, EH2), jnp.float32) * s, 'eb2': jnp.zeros((E, EH2), jnp.float32), 'eW3': jax.random.normal(ks[6], (E, EH2, OUT), jnp.float32) * s, 'eb3': jnp.zeros((E, OUT), jnp.float32), 'gW': jax.random.normal(ks[7], (IN, E), jnp.float32) * s, 'gb': jnp.zeros((E,), jnp.float32)}
    _L1_ffn_all = _L1_ffn_setup()
    _L1_ffn_in = {k: v for k, v in _L1_ffn_all.items() if k in ('sW1', 'sb1', 'sW2', 'sb2', 'sW3', 'sb3', 'eW1', 'eb1', 'eW2', 'eb2', 'eW3', 'eb3', 'gW', 'gb')}
    del _L1_ffn_all
    return {'x': x, 'src': src, 'dst': dst, 'edge_attr_3': edge_attr_3, 'L0_gnn_W1': _L0_gnn_in['W1'], 'L0_gnn_g1': _L0_gnn_in['g1'], 'L0_gnn_b1': _L0_gnn_in['b1'], 'L0_gnn_W2': _L0_gnn_in['W2'], 'L0_gnn_g2': _L0_gnn_in['g2'], 'L0_gnn_b2': _L0_gnn_in['b2'], 'L0_mix_Wqkv': _L0_mix_in['Wqkv'], 'L0_mix_Wout': _L0_mix_in['Wout'], 'L0_mix_bout': _L0_mix_in['bout'], 'L0_ffn_Wg': _L0_ffn_in['Wg'], 'L0_ffn_bg': _L0_ffn_in['bg'], 'L0_ffn_W1': _L0_ffn_in['W1'], 'L0_ffn_b1': _L0_ffn_in['b1'], 'L0_ffn_W2': _L0_ffn_in['W2'], 'L0_ffn_b2': _L0_ffn_in['b2'], 'L1_gnn_W1': _L1_gnn_in['W1'], 'L1_gnn_b1': _L1_gnn_in['b1'], 'L1_gnn_W2': _L1_gnn_in['W2'], 'L1_gnn_b2': _L1_gnn_in['b2'], 'L1_gnn_gamma': _L1_gnn_in['gamma'], 'L1_gnn_beta': _L1_gnn_in['beta'], 'L1_mix_Wq': _L1_mix_in['Wq'], 'L1_mix_Wkv': _L1_mix_in['Wkv'], 'L1_mix_Wproj': _L1_mix_in['Wproj'], 'L1_mix_bproj': _L1_mix_in['bproj'], 'L1_ffn_sW1': _L1_ffn_in['sW1'], 'L1_ffn_sb1': _L1_ffn_in['sb1'], 'L1_ffn_sW2': _L1_ffn_in['sW2'], 'L1_ffn_sb2': _L1_ffn_in['sb2'], 'L1_ffn_sW3': _L1_ffn_in['sW3'], 'L1_ffn_sb3': _L1_ffn_in['sb3'], 'L1_ffn_eW1': _L1_ffn_in['eW1'], 'L1_ffn_eb1': _L1_ffn_in['eb1'], 'L1_ffn_eW2': _L1_ffn_in['eW2'], 'L1_ffn_eb2': _L1_ffn_in['eb2'], 'L1_ffn_eW3': _L1_ffn_in['eW3'], 'L1_ffn_eb3': _L1_ffn_in['eb3'], 'L1_ffn_gW': _L1_ffn_in['gW'], 'L1_ffn_gb': _L1_ffn_in['gb']}

def reference(x, src, dst, edge_attr_3, L0_gnn_W1, L0_gnn_g1, L0_gnn_b1, L0_gnn_W2, L0_gnn_g2, L0_gnn_b2, L0_mix_Wqkv, L0_mix_Wout, L0_mix_bout, L0_ffn_Wg, L0_ffn_bg, L0_ffn_W1, L0_ffn_b1, L0_ffn_W2, L0_ffn_b2, L1_gnn_W1, L1_gnn_b1, L1_gnn_W2, L1_gnn_b2, L1_gnn_gamma, L1_gnn_beta, L1_mix_Wq, L1_mix_Wkv, L1_mix_Wproj, L1_mix_bproj, L1_ffn_sW1, L1_ffn_sb1, L1_ffn_sW2, L1_ffn_sb2, L1_ffn_sW3, L1_ffn_sb3, L1_ffn_eW1, L1_ffn_eb1, L1_ffn_eW2, L1_ffn_eb2, L1_ffn_eW3, L1_ffn_eb3, L1_ffn_gW, L1_ffn_gb):
    import jax
    import jax.numpy as jnp

    def _L0_gnn_ref(x, es, W1, g1, b1, W2, g2, b2):
        import jax, jax.numpy as jnp
        import numpy as np
        EPS = 1e-05

        def _gcn_conv(x, W, row, col, n_nodes):
            xl = x @ W.T
            ones = jnp.ones(row.shape[0], dtype=x.dtype)
            deg = jax.ops.segment_sum(ones, col, num_segments=n_nodes)
            dis = jnp.where(deg > 0, deg ** (-0.5), 0.0).astype(x.dtype)
            norm = dis[row] * dis[col]
            msg = xl[row] * norm[:, None]
            return jax.ops.segment_sum(msg, col, num_segments=n_nodes)

        def _batchnorm(x, gamma, beta):
            m = jnp.mean(x, axis=0)
            v = jnp.mean((x - m) ** 2, axis=0)
            return (x - m) * jax.lax.rsqrt(v + EPS) * gamma + beta
        n_nodes = x.shape[0]
        loops = jnp.arange(n_nodes, dtype=es.dtype)
        row = jnp.concatenate([es[0], loops])
        col = jnp.concatenate([es[1], loops])
        res = x
        h = _gcn_conv(x, W1, row, col, n_nodes)
        h = jax.nn.relu(_batchnorm(h, g1, b1))
        h = _gcn_conv(h, W2, row, col, n_nodes)
        h = _batchnorm(h, g2, b2)
        return jax.nn.relu(h + res)

    def _L0_mix_ref(x, Wqkv, Wout, bout):
        import jax, jax.numpy as jnp
        import numpy as np
        HEADS = 8
        DIM_HEAD = 64
        EPS = 1e-05

        def _inst_norm_lastdim(t):
            mu = jnp.mean(t, axis=-1, keepdims=True)
            var = jnp.mean(jnp.square(t - mu), axis=-1, keepdims=True)
            return (t - mu) * jax.lax.rsqrt(var + EPS)
        b, n, dim = x.shape
        qkv = jnp.einsum('bnc,fc->bnf', x, Wqkv)
        q, k, v = jnp.split(qkv, 3, axis=-1)

        def to_heads(t):
            return t.reshape(b, n, HEADS, DIM_HEAD).transpose(0, 2, 1, 3)
        q, k, v = (to_heads(q), to_heads(k), to_heads(v))
        k = _inst_norm_lastdim(k)
        v = _inst_norm_lastdim(v)
        dots = jnp.einsum('bhnd,bhne->bhde', k, v)
        out = jnp.einsum('bhnd,bhde->bhne', q, dots) / n
        out = out.transpose(0, 2, 1, 3).reshape(b, n, HEADS * DIM_HEAD)
        return jnp.einsum('bnf,cf->bnc', out, Wout) + bout

    def _L0_ffn_ref(x, Wg, bg, W1, b1, W2, b2):
        import jax, jax.numpy as jnp
        import numpy as np
        B, S, D, E, H, K = (4, 512, 256, 8, 512, 2)
        Bv, Sv, Dv = x.shape
        gate_scores = x @ Wg + bg
        _, idx = jax.lax.top_k(gate_scores, K)
        mask = jax.nn.one_hot(idx, E, dtype=x.dtype).sum(axis=-2)
        xf = x.reshape(-1, Dv)
        mf = mask.reshape(-1, E)
        h = jax.nn.gelu(jnp.einsum('td,edh->teh', xf, W1) + b1[None], approximate=False)
        y = jnp.einsum('teh,ehd->ted', h, W2) + b2[None]
        out = jnp.einsum('ted,te->td', y, mf)
        return out.reshape(Bv, Sv, Dv)

    def _L1_gnn_ref(x, edge_index, edge_attr, W1, b1, W2, b2, gamma, beta):
        import jax, jax.numpy as jnp
        import numpy as np
        N = 6250
        H = 256
        E = 100000
        F = 3
        DIST_SCALE = 4.0
        LN_EPS = 1e-05
        src = edge_index[0]
        dst = edge_index[1]
        n_nodes = x.shape[0]
        feat = edge_attr.astype(jnp.float32)
        feat_norm = jnp.sqrt(jnp.sum(feat * feat, axis=1) + 1e-12)
        w = jnp.exp(-DIST_SCALE * feat_norm).astype(x.dtype)
        w = jnp.maximum(w, 0.0)
        weighted = x[src] * w[:, None]
        agg = jax.ops.segment_sum(weighted, dst, num_segments=n_nodes)
        wsum = jax.ops.segment_sum(w, dst, num_segments=n_nodes)
        agg = agg / jnp.maximum(wsum, 1e-06)[:, None]
        h = jax.nn.gelu(jnp.dot(agg, W1.T) + b1, approximate=False)
        msg = jnp.dot(h, W2.T) + b2
        y = x + msg
        mu = jnp.mean(y, axis=-1, keepdims=True)
        var = jnp.mean(jnp.square(y - mu), axis=-1, keepdims=True)
        return (y - mu) * jax.lax.rsqrt(var + LN_EPS) * gamma + beta

    def _L1_mix_ref(x, Wq, Wkv, Wproj, bproj):
        import jax, jax.numpy as jnp
        import numpy as np
        NUM_HEADS = 8
        B, N, C = x.shape
        h = NUM_HEADS
        d = C // h
        q = jnp.einsum('bnc,oc->bno', x, Wq).reshape(B, N, h, d).transpose(0, 2, 1, 3)
        kv = jnp.einsum('bnc,oc->bno', x, Wkv).reshape(B, N, 2, h, d)
        k = kv[:, :, 0].transpose(0, 2, 1, 3)
        v = kv[:, :, 1].transpose(0, 2, 1, 3)
        q = jax.nn.elu(q) + 1.0
        k = jax.nn.elu(k) + 1.0
        k_sum = k.sum(axis=2)
        D_inv = 1.0 / jnp.maximum(jnp.einsum('bhnd,bhd->bhn', q, k_sum), 1e-06)
        context = jnp.einsum('bhnd,bhne->bhde', k, v)
        attn = jnp.einsum('bhnd,bhde->bhne', q, context) * D_inv[..., None]
        out = attn.transpose(0, 2, 1, 3).reshape(B, N, C)
        out = jnp.einsum('bnc,oc->bno', out, Wproj) + bproj
        return out

    def _L1_ffn_ref(x, sW1, sb1, sW2, sb2, sW3, sb3, eW1, eb1, eW2, eb2, eW3, eb3, gW, gb):
        import jax, jax.numpy as jnp
        import numpy as np
        B, A = (512, 8)
        IN, OUT = (256, 256)
        SH1, SH2 = (256, 128)
        EH1, EH2 = (128, 64)
        E, TOPK = (4, 2)

        def _shared_mlp(x, W1, b1, W2, b2, W3, b3):
            h = jax.nn.relu(x @ W1 + b1)
            h = jax.nn.relu(h @ W2 + b2)
            return h @ W3 + b3

        def _experts_mlp(x, eW1, eb1, eW2, eb2, eW3, eb3):
            h = jax.nn.relu(jnp.einsum('baf,efh->ebah', x, eW1) + eb1[:, None, None, :])
            h = jax.nn.relu(jnp.einsum('ebah,ehg->ebag', h, eW2) + eb2[:, None, None, :])
            o = jnp.einsum('ebag,ego->ebao', h, eW3) + eb3[:, None, None, :]
            return jnp.moveaxis(o, 0, -1)
        all_out = _experts_mlp(x, eW1, eb1, eW2, eb2, eW3, eb3)
        shared = _shared_mlp(x, sW1, sb1, sW2, sb2, sW3, sb3)
        gates = jax.nn.softmax(x @ gW + gb, axis=-1)
        topv, topi = jax.lax.top_k(gates, TOPK)
        topw = jax.nn.softmax(topv, axis=-1)
        sel = jnp.take_along_axis(all_out, topi[:, :, None, :], axis=-1)
        gated = jnp.sum(sel * topw[:, :, None, :], axis=-1)
        return shared + gated
    edge_index = jnp.stack([src, dst])
    xn = _layernorm(x, axis=-1)
    x = x + _L0_gnn_ref(xn, edge_index, L0_gnn_W1, L0_gnn_g1, L0_gnn_b1, L0_gnn_W2, L0_gnn_g2, L0_gnn_b2) + _L0_mix_ref(xn[None], L0_mix_Wqkv, L0_mix_Wout, L0_mix_bout)[0]
    x = x + _L0_ffn_ref(_layernorm(x, axis=-1)[None], L0_ffn_Wg, L0_ffn_bg, L0_ffn_W1, L0_ffn_b1, L0_ffn_W2, L0_ffn_b2)[0]
    xn = _layernorm(x, axis=-1)
    x = x + _L1_gnn_ref(xn, edge_index, edge_attr_3, L1_gnn_W1, L1_gnn_b1, L1_gnn_W2, L1_gnn_b2, L1_gnn_gamma, L1_gnn_beta) + _L1_mix_ref(xn[None], L1_mix_Wq, L1_mix_Wkv, L1_mix_Wproj, L1_mix_bproj)[0]
    x = x + _L1_ffn_ref(_layernorm(x, axis=-1)[None], L1_ffn_sW1, L1_ffn_sb1, L1_ffn_sW2, L1_ffn_sb2, L1_ffn_sW3, L1_ffn_sb3, L1_ffn_eW1, L1_ffn_eb1, L1_ffn_eW2, L1_ffn_eb2, L1_ffn_eW3, L1_ffn_eb3, L1_ffn_gW, L1_ffn_gb)[0]
    return x

_drawn_inputs = setup_inputs


def setup_inputs(seed=0):
    import zlib

    import numpy as np

    out = dict(_drawn_inputs(seed))
    spreads = {'L0_gnn_g1': (1.0, 0.2),
     'L0_gnn_b1': (0.0, 0.1),
     'L0_gnn_g2': (1.0, 0.2),
     'L0_gnn_b2': (0.0, 0.1),
     'L0_ffn_bg': (0.0, 0.1),
     'L0_ffn_b1': (0.0, 0.392),
     'L0_ffn_b2': (0.0, 0.1),
     'L1_gnn_b1': (0.0, 0.8),
     'L1_gnn_b2': (0.0, 0.1),
     'L1_gnn_gamma': (1.0, 0.2),
     'L1_gnn_beta': (0.0, 0.1),
     'L1_mix_bproj': (0.0, 0.1),
     'L1_ffn_sb1': (0.0, 0.8),
     'L1_ffn_sb2': (0.0, 0.598),
     'L1_ffn_sb3': (0.0, 0.1),
     'L1_ffn_eb1': (0.0, 0.8),
     'L1_ffn_eb2': (0.0, 0.8),
     'L1_ffn_eb3': (0.0, 0.328),
     'L1_ffn_gb': (0.0, 0.8)}
    factors = {'edge_attr_3': 5.343,
     'L0_mix_bout': 7.041,
     'L1_gnn_W1': 4.643,
     'L1_gnn_W2': 4.182,
     'L1_mix_Wq': 8.0,
     'L1_mix_Wkv': 8.0,
     'L1_mix_Wproj': 8.0,
     'L1_ffn_eW1': 3.607,
     'L1_ffn_eW2': 3.152}
    for name, (base, spread) in spreads.items():
        noise = np.random.default_rng([zlib.crc32(name.encode()), seed]).standard_normal(out[name].shape)
        drawn = base * np.exp(spread * noise) if base else spread * noise
        out[name] = jnp.asarray(drawn.astype(out[name].dtype))
    for name, factor in factors.items():
        out[name] = (out[name] * factor).astype(out[name].dtype)
    return out
```

```python
from contextlib import ExitStack

import concourse.bass as bass
from concourse import mybir

ALU = mybir.AluOpType
ACT = mybir.ActivationFunctionType
F32 = mybir.dt.float32
F16 = mybir.dt.float16
BF16 = mybir.dt.bfloat16
I32 = mybir.dt.int32
U32 = mybir.dt.uint32
AX = mybir.AxisListType
ds = bass.ds

P = 128
N = 6250
D = 256
E = 100000
NT = -(-N // P)
NP = NT * P
LAST = N - (NT - 1) * P
TS = 7
NS = NT // TS
SS = TS * P
HALVES = ((0, 4), (4, 3))
EPS = 1e-5

ET = 784
CT = 4
NC = ET // CT
RB = 7
RP = ET // RB
W = 128
RING = 4
NI = NC // RING

TURNED = (("L0_mix_Wqkv", 512, 1024, 256), ("L0_mix_Wout", 0, 256, 512), ("L0_gnn_W1", 0, 512, 256),
          ("L0_gnn_W2", 0, 256, 512), ("L1_gnn_W1", 0, 256, 256), ("L1_gnn_W2", 0, 256, 256),
          ("L1_mix_Wq", 0, 256, 256), ("L1_mix_Wk", 0, 256, 256), ("L1_mix_Wv", 256, 256, 256),
          ("L1_mix_Wproj", 0, 256, 256))
TURNED_AT = {}
NBLOCKS = 0
for _name, _r0, _rows, _cols in TURNED:
    TURNED_AT[_name] = NBLOCKS
    NBLOCKS += (_rows // P) * (_cols // P)


EXPERTS, HID = 8, 512
HM = HID // P
REGION = NP + P
MT = (2 * NP + EXPERTS * (P - 1)) // P
MT += MT % 2
XS, WS = 16.0, 1024.0

COLUMNS = (("L0_gnn_g1", 4), ("L0_gnn_b1", 4), ("L0_gnn_g2", 2), ("L0_gnn_b2", 2), ("L0_ffn_b1", 32),
           ("L1_gnn_b1", 2), ("L1_ffn_sb1", 2), ("L1_ffn_sb2", 1), ("L1_ffn_eb1", 4), ("L1_ffn_eb2", 2))
COLUMNS_AT = {}
NCOL = 0
for _name, _n in COLUMNS:
    COLUMNS_AT[_name] = (NCOL, _n)
    NCOL += _n


class Chain:

    def __init__(self, engine, sem, turn=0, per_turn=0, start=0):
        self.engine, self.sem, self.base, self.k = engine, sem, turn * per_turn + start, 0

    def done(self, instruction):
        instruction.then_inc(self.sem, 1)
        self.k += 1
        return instruction

    def value(self):
        return self.base + self.k

    def wait(self):
        self.engine.wait_ge(self.sem, self.value())


class Shared:

    def __init__(self, sem):
        self.sem, self.base = sem, 0

    def at(self, n):
        return self.base + n

    def end(self, n):
        self.base += n


class Carver:

    def __init__(self, region, words):
        self.region, self.words, self.at = region, words, 0

    def take(self, shape, dtype=F32):
        n = 1
        for s in shape:
            n *= s
        size = {F32: 4, I32: 4, U32: 4, BF16: 2, F16: 2}[dtype]
        words = -(-n * size // 4)
        assert self.at + words <= self.words, (self.at, words, self.words)
        view = self.region[:, self.at:self.at + words]
        self.at += words
        if dtype is not F32:
            view = view.bitcast(dtype)
        if len(shape) == 2:
            view = view.rearrange("p (a b) -> p a b", b=shape[1])
        elif len(shape) == 3:
            view = view.rearrange("p (a b c) -> p a b c", b=shape[1], c=shape[2])
        elif len(shape) == 4:
            view = view.rearrange("p (a b c d) -> p a b c d", b=shape[1], c=shape[2], d=shape[3])
        return view


class Core:

    def __init__(self, nc, ctx, inputs, out):
        self.nc, self.ctx, self.inp, self.out = nc, ctx, inputs, out

        def dram(name, shape):
            return nc.dram_tensor(name, shape, F32, kind="Internal").ap()

        self.turned = dram("turned_weights", (P, NBLOCKS * P))
        self.xn_tab = dram("xn_table", (NP, D))
        self.h_tab = dram("h_table", (NP, D))
        self.xn3_tab = dram("xn3_table", (NP, D))
        self.dis_row = dram("dis_row", (1, NP))
        self.wsum_row = dram("wsum_row", (1, NP))
        self.xn2_tab = dram("xn2_table", (NP, D))
        self.slot_x = dram("expert_rows", (EXPERTS * REGION, D))
        self.slot_y = dram("expert_results", (MT * P, D))
        self.x1_tab = dram("x1_table", (NP, D))
        self.x2_tab = dram("x2_table", (NP, D))
        self.xnT = self.sb("xnT", [P, 2, NP], F32)
        self.agg = self.sb("agg", [P, 3, NP], F32)
        self.scr = self.sb("scr", [P, SCR], F32)
        self.ident = self.sb("ident", [P, P], F32)
        self.ones = self.sb("ones", [P, P], F32)
        self.zeros = self.sb("zeros", [P, P], F32)
        self.iota = self.sb("iota", [P, W], F32)
        self.src = self.sb("src_i", [P, ET], I32)
        self.dloc = self.sb("dloc", [P, ET + CT], F32)
        self.w = self.sb("w_edge", [P, ET], F32)
        self.base = self.sb("base", [P, NC], F32)
        self.base_i = self.sb("base_i", [P, NC], I32)
        self.flag_i = self.sb("flag_i", [P, 1], I32)
        self.dis = self.sb("dis_node", [P, NT], F32)
        self.m0 = self.sb("m0", [P, 2, D], F32)
        self.idx = self.sb("index_columns", [P, RING, CT], I32)
        self.w_stat = self.sb("weight_columns", [P, RING, CT], F32)
        self.dst_now = self.sb("slow_destinations_now", [P, CT], F32)
        self.ones16 = self.sb("ones16", [P, P], BF16)
        self.iota16 = self.sb("iota16", [P, W], BF16)
        self.x_all = self.scr[:, SCR - NT * D:SCR].rearrange("p (t d) -> p t d", d=D)
        self.cols = self.sb("feature_columns", [P, NCOL], F32)
        self.scores = self.sb("expert_scores", [P, NT, EXPERTS], F32)
        self.scatter_to = self.sb("expert_row_of_node", [P, 2, NT], I32)
        self.result_at = self.sb("result_row_of_node", [P, 2, NT], I32)
        self.pad_to = self.sb("expert_pad_rows", [P, EXPERTS], I32)
        self.tile_expert = self.sb("expert_of_tile", [P, MT], I32)
        self.tile_row = self.sb("first_row_of_tile", [P, MT], I32)
        self.bd64 = self.sb("diagonal_blocks64", [P, P], F32)
        self.bd32 = self.sb("diagonal_blocks32", [P, P], F32)
        self.small1 = self.sb("small1", [P, 256], F32)
        self.psum = ctx.enter_context(nc.psum_tensor("psum", [P, 8, 512], F32))
        self.constants = Shared(self.sem("constants_loaded"))
        self.passed = self.sem("wait_passed")
        self.agg_sems = {}
        self.agg_at = {"fast": {}, "slow": {}}

    def sb(self, name, shape, dtype):
        return self.ctx.enter_context(self.nc.sbuf_tensor(name, shape, dtype))

    def sem(self, name):
        return self.ctx.enter_context(self.nc.semaphore(name))

    def agg_sem(self, name):
        if name not in self.agg_sems:
            self.agg_sems[name] = self.sem(name)
            for counts in self.agg_at.values():
                counts[name] = 0
        return self.agg_sems[name]

    def column(self, name, j=0):
        at, n = COLUMNS_AT[name]
        return self.cols[:, at + j:at + j + 1]

    def columns(self, name):
        at, n = COLUMNS_AT[name]
        return self.cols[:, at:at + n]

    def turned_part(self, name, cols):
        at = TURNED_AT[name] * P
        return self.turned[:, at:at + cols]


SCR = 16384


def turn_weights(c):
    nc = c.nc
    agg = c.agg.rearrange("p a b -> p (a b)")
    col_rows = agg[:, NBLOCKS * P:NBLOCKS * P + P]
    natural = agg[:, 0:NBLOCKS * P].rearrange("p (b n) -> p b n", n=P)
    turned = c.scr[:, 0:NBLOCKS * P]
    loaded, const = c.sem("weights_loaded"), c.sem("weights_const")
    turn, copied_v, copied_a = c.sem("weights_turned"), c.sem("weights_copied_v"), c.sem("weights_copied_a")
    stored, masks = c.sem("weights_stored"), c.sem("masks_cleared")
    groups = NBLOCKS // 4
    n_loads = sum(cols // P for _, _, _, cols in TURNED) + len(COLUMNS)
    sources = {"L1_mix_Wk": "L1_mix_Wkv", "L1_mix_Wv": "L1_mix_Wkv"}
    with nc.Block() as block:

        @block.sync
        def _(sp):
            for name, r0, rows, cols in TURNED:
                w = c.inp[sources.get(name, name)]
                nro = rows // P
                for ci in range(cols // P):
                    at = TURNED_AT[name] + ci * nro
                    sp.dma_start(natural[:, at:at + nro, :],
                                 w[r0:r0 + rows, ci * P:(ci + 1) * P].rearrange("(r p) n -> p r n", p=P)
                                 ).then_inc(loaded, 16)
            for name, n in COLUMNS:
                at = COLUMNS_AT[name][0]
                w = c.inp[name]
                flat = w.rearrange("e n -> (e n)") if len(w.shape) == 2 else w
                sp.dma_start(col_rows[at:at + n, :], flat.rearrange("(r n) -> r n", n=P)).then_inc(loaded, 16)
            sp.wait_ge(copied_v, groups // 2)
            sp.wait_ge(copied_a, groups // 2)
            sp.dma_start(c.turned, turned).then_inc(stored, 16)
            sp.wait_ge(stored, 16)

        @block.gpsimd
        def _(g):
            g.memset(c.ident[:], 0.0).then_inc(const, 1)
            g.iota(c.iota[:], pattern=[[1, W]], base=0, channel_multiplier=0,
                   allow_small_or_imprecise_dtypes=True).then_inc(const, 1)
            g.memset(c.ones[:], 1.0).then_inc(const, 1)
            g.wait_ge(const, 3)
            g.affine_select(out=c.ident[:], in_=c.ident[:], compare_op=ALU.not_equal, fill=1.0, base=0,
                            pattern=[[-1, P]], channel_multiplier=1).then_inc(const, 1)

        @block.tensor
        def _(pe):
            pe.wait_ge(const, 4)
            pe.wait_ge(loaded, 16 * n_loads)
            for q in range(groups):
                if q >= 4:
                    pe.wait_ge((copied_v, copied_a)[q % 2], (q - 4) // 2 + 1)
                for b in range(4):
                    last = pe.transpose(c.psum[:, q % 4, b * P:(b + 1) * P], natural[:, 4 * q + b, :], c.ident[:])
                last.then_inc(turn, 1)
            pe.transpose(c.psum[:, 4, 0:NCOL], col_rows[0:NCOL, :], c.ident[0:NCOL, 0:NCOL]).then_inc(turn, 1)

        @block.vector
        def _(v):
            for m, size in ((c.bd64, 64), (c.bd32, 32)):
                v.memset(m[:], 0.0).then_inc(masks, 1)
            v.wait_ge(masks, 2)
            for m, size in ((c.bd64, 64), (c.bd32, 32)):
                for j in range(0, P, size):
                    v.memset(m[j:j + size, j:j + size], 1.0)
            for q in range(0, groups, 2):
                v.wait_ge(turn, q + 1)
                v.tensor_copy(turned[:, q * 512:(q + 1) * 512], c.psum[:, q % 4, :]).then_inc(copied_v, 1)
            v.wait_ge(turn, groups + 1)
            v.tensor_copy(c.cols[:], c.psum[:, 4, 0:NCOL])

        @block.scalar
        def _(a):
            for q in range(1, groups, 2):
                a.wait_ge(turn, q + 1)
                a.activation(turned[:, q * 512:(q + 1) * 512], c.psum[:, q % 4, :], ACT.Copy).then_inc(copied_a, 1)


def prepare_edges(c):
    nc = c.nc
    part = Carver(c.agg.rearrange("p a b -> p (a b)"), 2 * NP)
    rows = ET // RB
    full = E // P - (RB - 1) * RP
    rest = E % P
    dst_r, src_r = part.take([RB, P], I32), part.take([RB, P], I32)
    att_r = part.take([RB, P * 3])
    att_v = att_r.rearrange("p b (j f) -> p b j f", f=3)
    lists = part.take([3, RB * P])
    norm = part.take([RB, P])
    dstT = part.take([ET])
    ends = part.take([2, NC])
    ends_all = part.take([2, NC])
    spread, flag = part.take([NC]), part.take([1])
    fill, loaded, x_loaded = c.sem("edges_filled"), c.sem("edges_loaded"), c.sem("x_loaded")
    vec, root, turn, most = c.sem("edges_vec"), c.sem("edges_root"), c.sem("edges_turned"), c.sem("edges_most")
    n_dst = (RB - 1) * RP * P
    with nc.Block() as block:

        @block.sync
        def _(sp):
            sp.wait_ge(fill, 3)
            for r, source in ((dst_r, c.inp["dst"]), (src_r, c.inp["src"])):
                sp.dma_start(r[0:RP, 0:RB - 1, :], source[0:n_dst].rearrange("(b p j) -> p b j", p=RP, j=P)
                             ).then_inc(loaded, 16)
                sp.dma_start(r[0:full, RB - 1, :], source[n_dst:E - rest].rearrange("(p j) -> p j", j=P)
                             ).then_inc(loaded, 16)
                sp.dma_start(r[full:full + 1, RB - 1, 0:rest], source[E - rest:E].rearrange("(p j) -> p j", p=1)
                             ).then_inc(loaded, 16)

        @block.scalar
        def _(a):
            att = c.inp["edge_attr_3"]
            a.wait_ge(fill, 3)
            a.dma_start(att_r[0:RP, 0:RB - 1, :],
                        att[0:n_dst, :].rearrange("(b p j) f -> p b (j f)", p=RP, j=P)).then_inc(loaded, 16)
            a.dma_start(att_r[0:full, RB - 1, :],
                        att[n_dst:E - rest, :].rearrange("(p j) f -> p (j f)", j=P)).then_inc(loaded, 16)
            a.dma_start(att_r[full:full + 1, RB - 1, 0:rest * 3],
                        att[E - rest:E, :].rearrange("(p j) f -> p (j f)", p=1)).then_inc(loaded, 16)
            x, whole = c.inp["x"], (NT - 1) * P
            a.dma_start(c.x_all[:, 0:NT - 1, :], x[0:whole, :].rearrange("(t p) d -> p t d", p=P)).then_inc(x_loaded, 16)
            a.wait_ge(fill, 4)
            a.dma_start(c.x_all[0:LAST, NT - 1, :], x[whole:N, :]).then_inc(x_loaded, 16)
            a.wait_ge(vec, 4)
            a.activation(norm[0:RP], norm[0:RP], ACT.Sqrt).then_inc(root, 1)
            a.wait_ge(root, 1)
            a.activation(norm[0:RP], norm[0:RP], ACT.Exp, scale=-4.0).then_inc(root, 1)
            a.wait_ge(x_loaded, 32)

        @block.vector
        def _(v):
            v.memset(dst_r[0:RP, RB - 1, :], N).then_inc(fill, 1)
            v.memset(src_r[0:RP, RB - 1, :], 0).then_inc(fill, 1)
            v.memset(att_r[0:RP, RB - 1, :], 0.0).then_inc(fill, 1)
            v.memset(c.x_all[:, NT - 1, :], 0.0).then_inc(fill, 1)
            v.memset(c.agg[:, 2, :], 0.0)
            v.memset(c.zeros[:], 0.0)
            v.memset(c.ones16[:], 1.0)
            v.tensor_copy(c.iota16[:], c.iota[:])
            step = Chain(v, vec)
            v.wait_ge(loaded, 9 * 16)
            step.done(v.tensor_tensor(att_r[0:RP], att_r[0:RP], att_r[0:RP], ALU.mult))
            step.done(v.tensor_copy(lists[0:RP, 0, :], dst_r[0:RP].rearrange("p b j -> p (b j)")))
            step.wait()
            step.done(v.tensor_reduce(norm[0:RP], att_v[0:RP], AX.X, ALU.add))
            step.wait()
            step.done(v.tensor_scalar(norm[0:RP], norm[0:RP], 1e-12, None, ALU.add))
            step.done(v.tensor_copy(lists[0:RP, 1, :], src_r[0:RP].rearrange("p b j -> p (b j)")))
            v.wait_ge(root, 2)
            step.done(v.tensor_scalar(lists[0:RP, 2, :], norm[0:RP].rearrange("p b j -> p (b j)"), 0.0, None, ALU.max))
            for n, target in enumerate((dstT, c.src, c.w)):
                v.wait_ge(turn, n + 1)
                step.done(v.tensor_copy(target[:, 0:4 * RP], c.psum[:, 2 * n, 0:4 * RP]))
                step.done(v.tensor_copy(target[:, 4 * RP:ET], c.psum[:, 2 * n + 1, 0:3 * RP]))
            step.wait()
            chunks = dstT.rearrange("p (c t) -> p c t", t=CT)
            step.done(v.tensor_reduce(ends[:, 0, :], chunks, AX.X, ALU.min, negate=True))
            step.done(v.tensor_reduce(ends[:, 1, :], chunks, AX.X, ALU.max))
            v.wait_ge(most, 1)
            step.done(v.tensor_scalar(c.base[:], ends_all[:, 0, :], float(W - NP), -1.0, ALU.max, ALU.mult))
            step.done(v.memset(c.dloc[:, ET:ET + CT], -1.0))
            step.wait()
            step.done(v.tensor_copy(c.base_i[:], c.base[:]))
            step.done(v.tensor_tensor(c.dloc[:, 0:ET].rearrange("p (c t) -> p c t", t=CT), chunks,
                                      c.base[:].unsqueeze(2).broadcast_to([P, NC, CT]), ALU.subtract))
            step.done(v.tensor_tensor(spread, ends_all[:, 1, :], c.base[:], ALU.subtract))
            step.wait()
            step.done(v.tensor_reduce(flag, spread, AX.X, ALU.max))
            step.wait()
            step.done(v.tensor_scalar(c.flag_i[:], flag, float(W), None, ALU.is_ge))

        @block.tensor
        def _(pe):
            for n, ready in enumerate((2, 5, 6)):
                pe.wait_ge(vec, ready)
                for b in range(RB):
                    out = c.psum[:, 2 * n + b // 4, (b % 4) * RP:(b % 4 + 1) * RP]
                    last = pe.transpose(out, lists[0:RP, n, b * P:(b + 1) * P], c.ident[0:RP, 0:RP])
                last.then_inc(turn, 1)

        @block.gpsimd
        def _(g):
            g.wait_ge(vec, 14)
            g.partition_all_reduce(ends_all.rearrange("p a b -> p (a b)"), ends.rearrange("p a b -> p (a b)"), P,
                                   bass.bass_isa.ReduceOp.max).then_inc(most, 1)


def aggregate(c, table=None, weighted=False, slots=(), side=None):
    nc = c.nc
    gathers = table is not None
    part = Carver(c.scr, SCR)
    hot = part.take([2, CT, W], F32 if gathers else BF16)
    rows = part.take([RING, CT, D]) if gathers else None
    iota = c.iota if gathers else c.iota16
    S = c.agg_sem
    hot_ready, summed, added = S("onehot_ready"), S("chunk_summed"), S("window_added")
    idx_ready, begun, now_ready = S("indices_ready"), c.passed, S("slow_destinations_ready")
    landed = [S(f"rows_landed{u}") for u in range(RING)]
    lo, nslot = (0 if 0 in slots else 2), len(slots)
    acc = c.agg[:, lo:lo + nslot, :]
    bank = [c.psum[:, b, 0:nslot * W].rearrange("p (s w) -> p s w", w=W) for b in range(2)]
    flag = c.flag_i[0:1, 0:1]
    side = side or {}

    class Values:

        def __init__(self, way):
            self.at = dict(c.agg_at[way])

        def hot(self, n):
            return self.at["onehot_ready"] + n

        def summed(self, n):
            return self.at["chunk_summed"] + RING + n

        def added(self, n):
            return self.at["window_added"] + 2 + n

        def idx(self, n):
            return self.at["indices_ready"] + n

        def now(self, n):
            return self.at["slow_destinations_ready"] + n

        def landed(self, u, n):
            return self.at[f"rows_landed{u}"] + 16 * CT * n

    fast, slow = Values("fast"), Values("slow")

    def products(pe, b, u, hot_b):
        for s, what in enumerate(slots):
            for t in range(CT):
                if what == "count":
                    lhs = c.ones16[:]
                elif what == "weight":
                    lhs = c.w_stat[:, u, t:t + 1].broadcast_to([P, P])
                else:
                    lhs = rows[:, u, t, what * P:(what + 1) * P]
                last = pe.matmul(bank[b][:, s, :], lhs, hot[:, hot_b, t, :], start=(t == 0), stop=(t == CT - 1))
        return last

    def run_side(engine_name, *args):
        if engine_name in side:
            side[engine_name](*args)

    def side_alone(engine, names):
        if any(n in side for n in names):
            def turn(i, last):
                for n in names:
                    if n == "vector":
                        for u in range(RING):
                            side[n](engine, i, last, u)
                    else:
                        run_side(n, engine, i, last)
            with engine.Fori(0, NI - 1) as i:
                turn(i, False)
            turn(NI - 1, True)

    with nc.Block() as block:

        @block.vector
        def _(v):
            v.sem_inc(added, 2)
            is_slow = v.value_load(flag, min_val=0, max_val=1)

            def onehots(tiles, b, dst):
                for t in range(CT):
                    if weighted:
                        last = v.tensor_scalar(hot[:, b, t, :], iota[:], dst(t), c.w[:, ds(tiles + t, 1)],
                                               ALU.is_equal, ALU.mult)
                    else:
                        last = v.tensor_scalar(hot[:, b, t, :], iota[:], dst(t), None, ALU.is_equal)
                last.then_inc(hot_ready, 1)

            def indices(ch, u):
                if gathers:
                    if "weight" in slots:
                        v.tensor_copy(c.w_stat[:, u, :], c.w[:, ds(ch * CT, CT)])
                    v.tensor_copy(c.idx[:, u, :], c.src[:, ds(ch * CT, CT)]).then_inc(idx_ready, 1)

            with v.If(is_slow < 1):
                for ch in range(RING - 1):
                    indices(ch, ch)
                onehots(0, 0, lambda t: c.dloc[:, t:t + 1])

                def turn(i, last):
                    for u in range(RING):
                        ch = i * RING + u
                        v.wait_ge(summed, fast.summed(ch))
                        if not (last and u == RING - 1):
                            onehots((ch + 1) * CT, (u + 1) % 2, lambda t: c.dloc[:, ds((ch + 1) * CT + t, 1)])
                        if not (last and u > 0):
                            indices(ch + RING - 1, (u + RING - 1) % RING)
                        if "vector" in side:
                            side["vector"](v, i, last, u)
                        first = v.value_load(c.base_i[0:1, ds(ch, 1)], min_val=0, max_val=NP - W)
                        v.wait_ge(summed, fast.summed(ch + 1))
                        v.wait_ge(added, fast.added(ch))
                        window = acc[:, :, ds(first, W)]
                        v.tensor_tensor(window, window, bank[u % 2], ALU.add).then_inc(added, 1)
                with v.Fori(0, NI - 1) as i:
                    turn(i, False)
                turn(NI - 1, True)
            with v.Else():
                side_alone(v, ["vector"])
                with v.Fori(0, NC) as ch:
                    v.wait_ge(summed, slow.summed(ch * NT))
                    indices(ch, 0)
                    v.wait_ge(now_ready, slow.now(ch * (NT + 1)))
                    v.tensor_scalar(c.dst_now[:], c.dloc[:, ds(ch * CT, CT)], c.base[:, ds(ch, 1)], None, ALU.add
                                    ).then_inc(now_ready, 1)
                    with v.Fori(0, NT) as win:
                        n = ch * NT + win
                        v.wait_ge(now_ready, slow.now(ch * (NT + 1) + win + 1))
                        v.wait_ge(summed, slow.summed(n))
                        onehots(ch * CT, 0, lambda t: c.dst_now[:, t:t + 1])
                        v.tensor_scalar(c.dst_now[:], c.dst_now[:], float(-W), None, ALU.add).then_inc(now_ready, 1)
                        v.wait_ge(summed, slow.summed(n + 1))
                        v.wait_ge(added, slow.added(n))
                        window = acc[:, :, ds(win * W, W)]
                        v.tensor_tensor(window, window, bank[0], ALU.add).then_inc(added, 1)

        @block.tensor
        def _(pe):
            pe.sem_inc(summed, RING)
            if "tensor_first" in side:
                side["tensor_first"](pe)
            is_slow = pe.value_load(flag, min_val=0, max_val=1)
            with pe.If(is_slow < 1):
                def turn(i, last):
                    run_side("tensor_begin", pe, i, last)
                    for u in range(RING):
                        ch = i * RING + u
                        pe.wait_ge(hot_ready, fast.hot(ch + 1))
                        if gathers:
                            pe.wait_ge(landed[u], fast.landed(u, i + 1))
                        if "weight" in slots:
                            pe.wait_ge(idx_ready, fast.idx(ch + 1))
                        pe.wait_ge(added, fast.added(ch - 1))
                        products(pe, u % 2, u, u % 2).then_inc(summed, 1)
                    run_side("tensor_end", pe, i, last)
                with pe.Fori(0, NI - 1) as i:
                    turn(i, False)
                turn(NI - 1, True)
            with pe.Else():
                side_alone(pe, ["tensor_begin", "tensor_end"] if "tensor_begin" in side else [])
                with pe.Fori(0, NC) as ch:
                    with pe.Fori(0, NT) as win:
                        pe.wait_ge(hot_ready, slow.hot(ch * NT + win + 1))
                        if gathers:
                            pe.wait_ge(landed[0], slow.landed(0, ch + 1))
                        if "weight" in slots:
                            pe.wait_ge(idx_ready, slow.idx(ch + 1))
                        pe.wait_ge(added, slow.added(ch * NT + win))
                        products(pe, 0, 0, 0).then_inc(summed, 1)

        if gathers:
            @block.gpsimd
            def _(g):
                is_slow = g.value_load(flag, min_val=0, max_val=1)

                def gather(u, value):
                    g.wait_ge(idx_ready, value)
                    g.sem_inc(begun, 1)
                    for t in range(CT):
                        g.indirect_dma_start(out=rows[:, u, t, :], out_offset=None, in_=table,
                                             in_offset=bass.IndirectOffsetOnAxis(ap=c.idx[:, u, t:t + 1], axis=0)
                                             ).then_inc(landed[u], 16)

                with g.If(is_slow < 1):
                    with g.Fori(0, NI) as i:
                        for u in range(RING):
                            gather(u, fast.idx(i * RING + u + 1))
                with g.Else():
                    with g.Fori(0, NC) as ch:
                        gather(0, slow.idx(ch + 1))

        if "scalar" in side:
            @block.scalar
            def _(a):
                with a.Fori(0, NI - 1) as i:
                    side["scalar"](a, i, False)
                side["scalar"](a, NI - 1, True)

        @block.sync
        def _(sp):
            if "sync_first" in side:
                side["sync_first"](sp)
            if "sync" in side:
                with sp.Fori(0, NI - 1) as i:
                    side["sync"](sp, i, False)
                side["sync"](sp, NI - 1, True)

    windows = {"fast": NC, "slow": NC * NT}
    for way, counts in c.agg_at.items():
        counts["onehot_ready"] += windows[way]
        counts["chunk_summed"] += windows[way] + RING
        counts["window_added"] += windows[way] + 2
        if way == "slow":
            counts["slow_destinations_ready"] += NC * (NT + 1)
        if gathers:
            counts["indices_ready"] += NC
            for u in range(RING):
                counts[f"rows_landed{u}"] += 16 * CT * (NC if way == "slow" and u == 0 else
                                                        0 if way == "slow" else NI)


def count_degrees(c):
    aggregate(c, slots=("count",))


def first_norm(c):
    nc = c.nc
    part = Carver(c.scr, SCR - NT * D)
    xn = part.take([TS, D])
    dis49 = part.take([P])
    stats, moments, rstd = c.small1[:, 0:TS * 6], c.small1[:, TS * 6:TS * 8], c.small1[:, TS * 8:TS * 9]
    vec, act, turned = c.sem("norm1_vec"), c.sem("norm1_act"), c.sem("norm1_turned")
    cp_v, cp_a = c.sem("norm1_agg_copied"), c.sem("norm1_xnT_copied")
    stored, row = c.sem("norm1_stored"), c.sem("dis_row_moved")
    own, begun = c.sem("dis_ready"), c.passed
    tab = part.take([TS, D])
    st_v = stats.rearrange("p (t s) -> p t s", s=6)
    mo_v = moments.rearrange("p (t s) -> p t s", s=2)
    dis_all = c.agg[:, 2, :]
    PER = TS + TS + 1 + 1 + TS + TS
    with nc.Block() as block:

        @block.vector
        def _(v):
            v.tensor_scalar(dis_all, dis_all, 1.0, None, ALU.add).then_inc(own, 1)
            v.wait_ge(own, 2)
            v.reciprocal(dis_all, dis_all).then_inc(own, 1)
            v.wait_ge(own, 4)
            v.tensor_copy(c.dis[:], c.psum[:, 7, 0:NT]).then_inc(own, 1)
            v.wait_ge(own, 5)
            v.memset(dis_all, 0.0)
            with v.Fori(0, NS) as s:
                step = Chain(v, vec, s, PER)
                step.wait()
                for t in range(TS):
                    step.done(v.bn_stats(st_v[:, t, :], c.x_all[:, ds(s * TS + t, 1), :].rearrange("p t d -> p (t d)")))
                step.wait()
                v.sem_inc(begun, 1)
                for t in range(TS):
                    step.done(v.bn_aggr(mo_v[:, t, :], st_v[:, t, :]))
                step.wait()
                step.done(v.tensor_scalar(rstd, mo_v[:, :, 1], EPS, None, ALU.add))
                v.wait_ge(act, s + 1)
                step.done(v.reciprocal(rstd, rstd))
                step.wait()
                v.wait_ge(turned, s * 4)
                v.wait_ge(stored, s * 16)
                for t in range(TS):
                    step.done(v.tensor_scalar(xn[:, t, :], c.x_all[:, ds(s * TS + t, 1), :].rearrange("p t d -> p (t d)"),
                                              mo_v[:, t, 0:1], rstd[:, t:t + 1], ALU.subtract, ALU.mult))
                step.wait()
                for t in range(TS):
                    step.done(v.tensor_scalar(tab[:, t, :], xn[:, t, :], c.dis[:, ds(s * TS + t, 1)], None, ALU.mult))
                for k in range(2):
                    for h, (t0, nt) in enumerate(HALVES):
                        if h == 0:
                            v.wait_ge(turned, s * 4 + 3 + k)
                        v.tensor_copy(c.agg[:, k, ds(s * SS + t0 * P, nt * P)], c.psum[:, 4 + 2 * k + h, 0:nt * P]
                                      ).then_inc(cp_v, 1)

        @block.scalar
        def _(a):
            a.wait_ge(own, 1)
            a.activation(dis_all, dis_all, ACT.Sqrt).then_inc(own, 1)
            with a.Fori(0, NS) as s:
                a.wait_ge(vec, s * PER + 2 * TS + 1)
                a.activation(rstd, rstd, ACT.Sqrt).then_inc(act, 1)
                for k in range(2):
                    for h, (t0, nt) in enumerate(HALVES):
                        if h == 0:
                            a.wait_ge(turned, s * 4 + 1 + k)
                        a.activation(c.xnT[:, k, ds(s * SS + t0 * P, nt * P)], c.psum[:, 2 * k + h, 0:nt * P],
                                     ACT.Copy).then_inc(cp_a, 1)

        @block.tensor
        def _(pe):
            pe.wait_ge(row, 32)
            pe.transpose(c.psum[:, 7, 0:NT], dis49[0:NT, :], c.ident[0:NT, 0:NT]).then_inc(own, 1)
            pe.wait_ge(own, 5)
            with pe.Fori(0, NS) as s:
                for n, rows in enumerate((xn, tab)):
                    pe.wait_ge(vec, s * PER + (3 + n) * TS + 2)
                    pe.wait_ge((cp_a, cp_v)[n], s * 4)
                    for k in range(2):
                        for t in range(TS):
                            h = t // 4
                            last = pe.transpose(c.psum[:, 4 * n + 2 * k + h, (t % 4) * P:(t % 4 + 1) * P],
                                                rows[:, t, k * P:(k + 1) * P], c.ident[:])
                        last.then_inc(turned, 1)

        @block.sync
        def _(sp):
            sp.wait_ge(own, 3)
            sp.dma_start(c.dis_row, dis_all[0:1, :]).then_inc(row, 16)
            sp.wait_ge(row, 16)
            sp.dma_start(dis49[0:NT, :], c.dis_row.rearrange("a (t n) -> (a t) n", n=P)).then_inc(row, 16)
            with sp.Fori(0, NS) as s:
                sp.wait_ge(vec, s * PER + PER)
                sp.dma_start(c.xn_tab[ds(s * SS, SS), :].rearrange("(t p) d -> p t d", p=P), tab).then_inc(stored, 16)
            sp.wait_ge(stored, 16 * NS)


HEADS0, DH0 = 8, 64
PAIRS = HEADS0 // 2


def gather_first(c):
    part = Carver(c.scr, SCR)
    part.at = (2 * CT * W) + RING * CT * D
    wkv = part.take([2, 2 * HEADS0 * DH0])
    tile = part.take([2, P])
    G = 2 * HEADS0
    cen, sq, kv = part.take([G, DH0]), part.take([G, DH0]), part.take([G, DH0])
    mean, var = part.take([G]), part.take([G])
    flat = "p a b -> p (a b)"
    w_loaded, tile_ready, kv_ready = c.constants.sem, c.sem("kv_tile_ready"), c.sem("kv_ready")
    vec, act, dots = c.sem("kv_vec"), c.sem("kv_act"), c.sem("dots_done")
    both = c.psum[:, 2:4, :].rearrange("p a b -> p (a b)").rearrange("p (g d) -> p g d", d=DH0)
    sums = c.psum[:, 4, :]
    PER = 7

    def first(pe):
        pe.matmul(sums, c.zeros[:], c.ones[:, 0:1].broadcast_to([P, 512]), start=True, stop=False,
                  skip_group_check=True)
        pe.wait_ge(w_loaded, c.constants.at(16))

    def products_begin(pe, i, last):
        pe.wait_ge(tile_ready, i + 1)
        pe.wait_ge(vec, i * PER)
        for half in range(2):
            for k in range(2):
                ins = pe.matmul(c.psum[:, 2 + half, :], tile[:, k, :], wkv[:, k, half * 512:(half + 1) * 512],
                                start=(k == 0), stop=(k == 1))
        ins.then_inc(kv_ready, 1)

    def products_end(pe, i, last):
        pe.wait_ge(vec, (i + 1) * PER)
        for q in range(PAIRS):
            ins = pe.matmul(sums[:, q * P:(q + 1) * P],
                            kv.rearrange(flat)[:, 512 + q * P:512 + (q + 1) * P],
                            kv.rearrange(flat)[:, q * P:(q + 1) * P], start=False, stop=last,
                            skip_group_check=True)
        ins.then_inc(dots, 1)

    def vector(v, i, last, u):
        if u == 0:
            return
        step = Chain(v, vec, i, PER)
        if u == 1:
            v.wait_ge(kv_ready, i + 1)
            step.done(v.tensor_reduce(mean, both, AX.X, ALU.add))
            step.wait()
            step.done(v.tensor_scalar(mean, mean, 1.0 / DH0, None, ALU.mult))
            step.wait()
            v.wait_ge(act, i * 3)
            step.done(v.tensor_tensor(cen, both, mean.unsqueeze(2).broadcast_to([P, G, DH0]), ALU.subtract))
        if u == 2:
            step.k = 3
            v.wait_ge(act, i * 3 + 2)
            step.done(v.tensor_reduce(var, sq, AX.X, ALU.add))
            step.wait()
            step.done(v.tensor_scalar(var, var, 1.0 / DH0, EPS, ALU.mult, ALU.add))
        if u == 3:
            step.k = 5
            v.wait_ge(act, i * 3 + 3)
            step.done(v.reciprocal(var, var))
            step.wait()
            v.wait_ge(dots, i)
            step.done(v.tensor_tensor(kv, cen, var.unsqueeze(2).broadcast_to([P, G, DH0]), ALU.mult))

    def scalar(a, i, last):
        a.wait_ge(kv_ready, i)
        a.activation(tile[:], c.xnT[:, :, ds(i * P, P)], ACT.Copy).then_inc(tile_ready, 1)
        a.wait_ge(vec, i * PER + 3)
        a.activation(sq.rearrange(flat), cen.rearrange(flat), ACT.Square).then_inc(act, 2)
        a.wait_ge(vec, i * PER + 5)
        a.activation(var, var, ACT.Sqrt).then_inc(act, 1)

    def sync_first(sp):
        sp.dma_start(wkv.rearrange(flat), c.turned_part("L0_mix_Wqkv", 2 * 1024)).then_inc(w_loaded, 16)

    side = dict(tensor_first=first, tensor_begin=products_begin, tensor_end=products_end, vector=vector,
                scalar=scalar, sync_first=sync_first)
    aggregate(c, table=c.xn_tab, slots=(0, 1, "weight"), side=side)
    c.constants.end(16)


def fold_attention(c):
    nc = c.nc
    part = Carver(c.scr, SCR)
    woutT, wq = part.take([PAIRS, D]), part.take([PAIRS, D])
    dots, t_sb = part.take([PAIRS, P]), part.take([PAIRS, D])
    stored, loaded, wide = c.sem("fold0_stored"), c.constants.sem, c.sem("dis_broadcast")
    vec, pe_done = c.sem("fold0_vec"), c.sem("fold0_products")
    with nc.Block() as block:

        @block.sync
        def _(sp):
            sp.dma_start(c.wsum_row, c.agg[0:1, 2, :]).then_inc(stored, 16)
            sp.dma_start(woutT.rearrange("p a b -> p (a b)"), c.turned_part("L0_mix_Wout", PAIRS * D)).then_inc(loaded, 16)
            sp.dma_start(wq[:], c.inp["L0_mix_Wqkv"][0:PAIRS * P, :].rearrange("(q p) n -> p q n", p=P)).then_inc(loaded, 16)
            sp.wait_ge(stored, 16)
            sp.dma_start(c.agg[:, 2, :], c.dis_row.partition_broadcast(P)).then_inc(wide, 16)

        @block.vector
        def _(v):
            v.scalar_tensor_tensor(dots[:], c.psum[:, 4, :].rearrange("p (q d) -> p q d", d=P), 1.0 / N,
                                   c.bd64[:].unsqueeze(1).broadcast_to([P, PAIRS, P]), ALU.mult, ALU.mult
                                   ).then_inc(vec, 1)
            v.wait_ge(pe_done, 1)
            v.tensor_copy(t_sb[:], c.psum[:, 0:2, :].rearrange("p a b -> p (a b)").rearrange("p (q d) -> p q d", d=D)
                          ).then_inc(vec, 1)
            v.wait_ge(pe_done, 2)
            v.tensor_copy(c.m0[:], c.psum[:, 2, :].rearrange("p (k d) -> p k d", d=D))
            v.wait_ge(wide, 16)
            for k in range(2):
                v.tensor_tensor(c.agg[:, k, :], c.agg[:, k, :], c.agg[:, 2, :], ALU.mult)

        @block.tensor
        def _(pe):
            pe.wait_ge(vec, 1)
            pe.wait_ge(loaded, c.constants.at(32))
            for q in range(PAIRS):
                last = pe.matmul(c.psum[:, q // 2, (q % 2) * D:(q % 2 + 1) * D], dots[:, q, :], woutT[:, q, :],
                                 start=True, stop=True)
            last.then_inc(pe_done, 1)
            pe.wait_ge(vec, 2)
            for k in range(2):
                for q in range(PAIRS):
                    last = pe.matmul(c.psum[:, 2, k * D:(k + 1) * D], wq[:, q, k * P:(k + 1) * P], t_sb[:, q, :],
                                     start=(q == 0), stop=(q == PAIRS - 1))
            last.then_inc(pe_done, 1)
    c.constants.end(32)


H1 = 4


def first_conv(c):
    nc = c.nc
    part = Carver(c.scr, SCR)
    w1T, w2T = part.take([2, H1 * P]), part.take([H1, D])
    stats = part.take([H1, NS * 2, 6])
    moments = part.take([H1, 2])
    rstd, scale, bias = part.take([H1]), part.take([H1]), part.take([H1])
    h1r = part.take([2, H1, 512])
    rows = part.take([2, 4, D])
    loaded, ready, read = c.constants.sem, c.sem("conv1_h1_ready"), c.sem("conv1_h1_read")
    with nc.Block() as block:

        @block.sync
        def _(sp):
            sp.dma_start(w1T.rearrange("p a b -> p (a b)"), c.turned_part("L0_gnn_W1", 2 * H1 * P)).then_inc(loaded, 16)
            sp.dma_start(w2T.rearrange("p a b -> p (a b)"), c.turned_part("L0_gnn_W2", H1 * D)).then_inc(loaded, 16)
            sp.wait_ge(loaded, c.constants.at(32))

        @block.tensor
        def _(pe):
            pe.wait_ge(loaded, c.constants.at(32))
            with pe.Fori(0, NS) as s:
                for h, (t0, nt) in enumerate(HALVES):
                    pe.wait_ge(read, s * 2 + h)
                    for m in range(H1):
                        for k in range(2):
                            last = pe.matmul(c.psum[:, 4 * h + m, 0:nt * P], w1T[:, k, m * P:(m + 1) * P],
                                             c.agg[:, k, ds(s * SS + t0 * P, nt * P)], start=(k == 0), stop=(k == 1))
                    last.then_inc(ready, 1)

        @block.vector
        def _(v):
            def turn(s, last_step):
                for h, (t0, nt) in enumerate(HALVES):
                    cols = nt * P
                    if last_step and h == 1:
                        cols = (nt - 1) * P + LAST
                    v.wait_ge(ready, s * 2 + h + 1)
                    for m in range(H1):
                        last = v.bn_stats(stats[:, m, ds(s * 2 + h, 1), :].rearrange("p a b -> p (a b)"),
                                          c.psum[:, 4 * h + m, 0:cols])
                    last.then_inc(read, 1)
            with v.Fori(0, NS - 1) as s:
                turn(s, False)
            turn(NS - 1, True)

    vec, root = c.sem("conv1_bn_vec"), c.sem("conv1_bn_root")
    h_ready, relu, tiles = c.sem("conv1_part_ready"), c.sem("conv1_relu_done"), c.sem("conv1_rows_ready")
    scaled, turned, copied = c.sem("conv1_rows_scaled"), c.sem("conv1_rows_turned"), c.sem("conv1_agg_copied")
    stored = [c.sem(f"conv1_stored{h}") for h in range(2)]
    with nc.Block() as block:

        @block.vector
        def _(v):
            step = Chain(v, vec)
            for m in range(H1):
                step.done(v.bn_aggr(moments[:, m, :], stats[:, m, :, :].rearrange("p a b -> p (a b)")))
            step.wait()
            step.done(v.tensor_scalar(rstd, moments[:, :, 1], EPS, None, ALU.add))
            v.wait_ge(root, 1)
            step.done(v.reciprocal(rstd, rstd))
            step.wait()
            step.done(v.tensor_tensor(scale, rstd, c.columns("L0_gnn_g1"), ALU.mult))
            step.wait()
            step.done(v.tensor_tensor(bias, moments[:, :, 0], scale, ALU.mult))
            step.wait()
            step.done(v.tensor_tensor(bias, c.columns("L0_gnn_b1"), bias, ALU.subtract))
            with v.Fori(0, NS) as s:
                for h, (t0, nt) in enumerate(HALVES):
                    v.wait_ge(stored[h], s * 16)
                    v.wait_ge(turned, s * 4)
                    v.wait_ge(tiles, s * 2 + h + 1)
                    for t in range(nt):
                        last = v.tensor_scalar(rows[:, h, t, :], c.psum[:, 4 + t // 2, (t % 2) * D:(t % 2 + 1) * D],
                                               c.dis[:, ds(s * TS + t0 + t, 1)], None, ALU.mult)
                    last.then_inc(scaled, 1)
                    for k in range(2):
                        v.wait_ge(turned, (s * 2 + h) * 2 + k + 1)
                        v.tensor_copy(c.agg[:, k, ds(s * SS + t0 * P, nt * P)], c.psum[:, 6 + k, 0:nt * P]
                                      ).then_inc(copied, 1)

        @block.scalar
        def _(a):
            a.wait_ge(vec, H1 + 1)
            a.activation(rstd, rstd, ACT.Sqrt).then_inc(root, 1)
            a.wait_ge(vec, H1 + 5)
            with a.Fori(0, NS) as s:
                for h, (t0, nt) in enumerate(HALVES):
                    for m in range(H1):
                        a.wait_ge(h_ready, (s * 2 + h) * H1 + m + 1)
                        if m == 0:
                            a.wait_ge(tiles, s * 2)
                        a.activation(h1r[:, h, m, 0:nt * P], c.psum[:, m, 0:nt * P], ACT.Relu, bias=bias[:, m:m + 1],
                                     scale=scale[:, m:m + 1]).then_inc(relu, 1)

        @block.tensor
        def _(pe):
            def h1(s, h):
                t0, nt = HALVES[h]
                for m in range(H1):
                    pe.wait_ge(relu, (s * 2 + h - 1) * H1 + m + 1 if h else s * 2 * H1)
                    for k in range(2):
                        last = pe.matmul(c.psum[:, m, 0:nt * P], w1T[:, k, m * P:(m + 1) * P],
                                         c.agg[:, k, ds(s * SS + t0 * P, nt * P)], start=(k == 0), stop=(k == 1))
                    last.then_inc(h_ready, 1)

            def node_rows(s, h):
                t0, nt = HALVES[h]
                pe.wait_ge(scaled, s * 2 + h)
                for m in range(H1):
                    pe.wait_ge(relu, (s * 2 + h) * H1 + m + 1)
                    for t in range(nt):
                        last = pe.matmul(c.psum[:, 4 + t // 2, (t % 2) * D:(t % 2 + 1) * D],
                                         h1r[:, h, m, t * P:(t + 1) * P], w2T[:, m, :],
                                         start=(m == 0 and t % 2 == 0), stop=(m == H1 - 1), skip_group_check=True)
                last.then_inc(tiles, 1)

            def turn_rows(s, h):
                t0, nt = HALVES[h]
                pe.wait_ge(scaled, s * 2 + h + 1)
                pe.wait_ge(copied, (s * 2 + h) * 2)
                for k in range(2):
                    for t in range(nt):
                        last = pe.transpose(c.psum[:, 6 + k, t * P:(t + 1) * P], rows[:, h, t, k * P:(k + 1) * P], c.ident[:])
                    last.then_inc(turned, 1)

            with pe.Fori(0, NS) as s:
                h1(s, 0)
                node_rows(s, 0)
                h1(s, 1)
                turn_rows(s, 0)
                node_rows(s, 1)
                turn_rows(s, 1)

        @block.sync
        def _(sp):
            with sp.Fori(0, NS) as s:
                for h, (t0, nt) in enumerate(HALVES):
                    sp.wait_ge(scaled, s * 2 + h + 1)
                    sp.dma_start(c.h_tab[ds(s * SS + t0 * P, nt * P), :].rearrange("(t p) d -> p t d", p=P),
                                 rows[:, h, 0:nt, :]).then_inc(stored[h], 16)
            for q in stored:
                sp.wait_ge(q, 16 * NS)
    c.constants.end(32)


def gather_second(c):
    aggregate(c, table=c.h_tab, slots=(0, 1))


def first_layer_sum(c):
    nc = c.nc
    part = Carver(c.scr, SCR)
    pre = part.take([2, 2, 512])
    xs = part.take([2, 2, 512])
    x_in = part.take([2, 4, D])
    x1 = part.take([2, 4, D])
    xn2 = part.take([2, 4, D])
    xn2T = part.take([2, 2, 512])
    wg, bg, bout = part.take([2, EXPERTS]), part.take([EXPERTS]), part.take([D])
    chunks = -(-N // 512)
    stats = part.take([2, chunks, 6])
    moments, rstd2, scale, bias = part.take([2, 2]), part.take([2]), part.take([2]), part.take([2])
    st, mo, rstd = part.take([2, 4, 6]), part.take([2, 4, 2]), part.take([2, 4])
    loaded, bn, root2 = c.constants.sem, c.sem("sum_bn_vec"), c.sem("sum_bn_root")
    x_in_ready = [c.sem(f"sum_x_loaded{h}") for h in range(2)]
    pre_ready, relu, xs_ready = c.sem("sum_pre_ready"), c.sem("sum_relu_done"), c.sem("sum_xn_copied")
    x1_psum, x1_ready, vec, root = c.sem("sum_x1_products"), c.sem("sum_x1_ready"), c.sem("sum_vec"), c.sem("sum_root")
    begun, xn2_ready, turned, copied = c.sem("sum_moments_begun"), c.sem("sum_xn2_ready"), c.sem("sum_turned"), c.sem("sum_xn2T_copied")
    scored, scores_ready = c.sem("sum_scored"), c.sem("sum_scores_ready")
    stored = [c.sem(f"sum_stored{h}") for h in range(2)]
    with nc.Block() as block:

        @block.sync
        def _(sp):
            sp.dma_start(wg[:], c.inp["L0_ffn_Wg"].rearrange("(k p) e -> p k e", p=P)).then_inc(loaded, 16)
            sp.dma_start(bg, c.inp["L0_ffn_bg"].unsqueeze(0).partition_broadcast(P)).then_inc(loaded, 16)
            sp.dma_start(bout[0:1, :], c.inp["L0_mix_bout"].unsqueeze(0)).then_inc(loaded, 16)

            def load(s, h, last):
                t0, nt = HALVES[h]
                sp.wait_ge(x1_ready, s * 2)
                if last and h == 1:
                    full = nt - 1
                    r0 = (NS - 1) * SS + t0 * P
                    sp.dma_start(x_in[:, h, 0:full, :], c.inp["x"][r0:r0 + full * P, :].rearrange("(t p) d -> p t d", p=P)
                                 ).then_inc(x_in_ready[h], 16)
                    sp.dma_start(x_in[0:LAST, h, full, :], c.inp["x"][r0 + full * P:N, :]).then_inc(x_in_ready[h], 16)
                else:
                    sp.dma_start(x_in[:, h, 0:nt, :],
                                 c.inp["x"][ds(s * SS + t0 * P, nt * P), :].rearrange("(t p) d -> p t d", p=P)
                                 ).then_inc(x_in_ready[h], 16)

            def store(s, h):
                t0, nt = HALVES[h]
                sp.wait_ge(xn2_ready, s * 2 + h + 1)
                for table, rows in ((c.x1_tab, x1), (c.xn2_tab, xn2)):
                    sp.dma_start(table[ds(s * SS + t0 * P, nt * P), :].rearrange("(t p) d -> p t d", p=P),
                                 rows[:, h, 0:nt, :]).then_inc(stored[h], 16)

            def turn(s, last):
                for h in range(2):
                    load(s, h, last)
                for h in range(2):
                    store(s, h)
            with sp.Fori(0, NS - 1) as s:
                turn(s, False)
            turn(NS - 1, True)
            sp.wait_ge(loaded, c.constants.at(48))
            for q in stored:
                sp.wait_ge(q, 32 * NS)

        @block.vector
        def _(v):
            step = Chain(v, bn)
            for k in range(2):
                step.done(v.tensor_tensor(c.agg[:, k, :], c.agg[:, k, :], c.agg[:, 2, :], ALU.mult))
            step.wait()
            for k in range(2):
                for j in range(chunks):
                    ins = v.bn_stats(stats[:, k, j, :], c.agg[:, k, j * 512:min(N, j * 512 + 512)])
            step.done(ins)
            step.wait()
            for k in range(2):
                step.done(v.bn_aggr(moments[:, k, :], stats[:, k, :, :].rearrange("p a b -> p (a b)")))
            step.wait()
            step.done(v.tensor_scalar(rstd2, moments[:, :, 1], EPS, None, ALU.add))
            v.wait_ge(root2, 1)
            step.done(v.reciprocal(rstd2, rstd2))
            step.wait()
            step.done(v.tensor_tensor(scale, rstd2, c.columns("L0_gnn_g2"), ALU.mult))
            step.wait()
            step.done(v.tensor_tensor(bias, moments[:, :, 0], scale, ALU.mult))
            step.wait()
            step.done(v.tensor_tensor(bias, c.columns("L0_gnn_b2"), bias, ALU.subtract))
            step.wait()
            v.wait_ge(loaded, c.constants.at(48))

            def norm(s, h, last):
                t0, nt = HALVES[h]
                per = 3
                chain = Chain(v, vec, s, 2 * per, h * per)
                x_count = s * 16 + 16 if not (last and h == 1) else s * 16 + 32
                v.wait_ge(x_in_ready[h], x_count)
                v.wait_ge(x1_psum, s * 2 + h + 1)
                v.wait_ge(stored[h], s * 32)
                v.wait_ge(turned, s * 4 + 2 * h)
                for t in range(nt):
                    ins = v.tensor_tensor(x1[:, h, t, :], c.psum[:, t // 2, (t % 2) * D:(t % 2 + 1) * D],
                                          x_in[:, h, t, :], ALU.add)
                ins.then_inc(x1_ready, 1)
                v.wait_ge(x1_ready, s * 2 + h + 1)
                for t in range(nt):
                    ins = v.bn_stats(st[:, h, t, :], x1[:, h, t, :])
                chain.done(ins)
                chain.wait()
                v.sem_inc(begun, 1)
                for t in range(nt):
                    ins = v.bn_aggr(mo[:, h, t, :], st[:, h, t, :])
                chain.done(ins)
                chain.wait()
                v.tensor_scalar(rstd[:, h, 0:nt], mo[:, h, 0:nt, 1], EPS, None, ALU.add).then_inc(begun, 1)
                v.wait_ge(root, s * 2 + h + 1)
                chain.done(v.reciprocal(rstd[:, h, 0:nt], rstd[:, h, 0:nt]))
                chain.wait()
                for t in range(nt):
                    ins = v.tensor_scalar(xn2[:, h, t, :], x1[:, h, t, :], mo[:, h, t, 0:1], rstd[:, h, t:t + 1],
                                          ALU.subtract, ALU.mult)
                ins.then_inc(xn2_ready, 1)

            def turn(s, last):
                for h, (t0, nt) in enumerate(HALVES):
                    v.wait_ge(x1_psum, s * 2)
                    for k in range(2):
                        at = ds(s * SS + t0 * P, nt * P)
                        v.scalar_tensor_tensor(pre[:, h, k, 0:nt * P], c.agg[:, k, at], scale[:, k:k + 1], c.xnT[:, k, at],
                                               ALU.mult, ALU.add).then_inc(pre_ready, 1)
                for h in range(2):
                    norm(s, h, last)
                for h, (t0, nt) in enumerate(HALVES):
                    v.wait_ge(scored, s * 2 + h + 1)
                    v.tensor_tensor(c.scores[:, ds(s * TS + t0, nt), :],
                                    c.psum[:, 7, h * 64:h * 64 + nt * EXPERTS].rearrange("p (t e) -> p t e", e=EXPERTS),
                                    bg.unsqueeze(1).broadcast_to([P, nt, EXPERTS]), ALU.add).then_inc(scores_ready, 1)
            with v.Fori(0, NS - 1) as s:
                turn(s, False)
            turn(NS - 1, True)

        @block.scalar
        def _(a):
            a.wait_ge(bn, 6)
            a.activation(rstd2, rstd2, ACT.Sqrt).then_inc(root2, 1)
            a.wait_ge(bn, 9)
            with a.Fori(0, NS) as s:
                for h, (t0, nt) in enumerate(HALVES):
                    a.wait_ge(x1_psum, s * 2)
                    a.activation(xs[:, h, :, 0:nt * P], c.xnT[:, :, ds(s * SS + t0 * P, nt * P)], ACT.Copy).then_inc(xs_ready, 1)
                    for k in range(2):
                        a.wait_ge(pre_ready, (s * 2 + h) * 2 + k + 1)
                        a.activation(pre[:, h, k, 0:nt * P], pre[:, h, k, 0:nt * P], ACT.Relu, bias=bias[:, k:k + 1]
                                     ).then_inc(relu, 1)
                for h, (t0, nt) in enumerate(HALVES):
                    a.wait_ge(begun, (s * 2 + h) * 2 + 2)
                    a.activation(rstd[:, h, 0:nt], rstd[:, h, 0:nt], ACT.Sqrt).then_inc(root, 1)
                    a.wait_ge(scored, s * 2 + h)
                    for k in range(2):
                        a.wait_ge(turned, (s * 2 + h) * 2 + k + 1)
                        a.activation(xn2T[:, h, k, 0:nt * P], c.psum[:, 5 + k, 0:nt * P], ACT.Copy).then_inc(copied, 1)

        @block.tensor
        def _(pe):
            pe.wait_ge(loaded, c.constants.at(48))

            def x1_rows(s, h):
                t0, nt = HALVES[h]
                pe.wait_ge(x1_ready, s * 2 + h)
                pe.wait_ge(xs_ready, s * 2 + h + 1)
                pe.wait_ge(relu, (s * 2 + h) * 2 + 2)
                for t in range(nt):
                    bank, col = t // 2, (t % 2) * D
                    cols = slice(t * P, (t + 1) * P)
                    for k in range(2):
                        pe.matmul(c.psum[:, bank, col + k * P:col + (k + 1) * P], pre[:, h, k, cols], c.ident[:],
                                  start=(k == 0), stop=False, skip_group_check=True)
                    for k in range(2):
                        pe.matmul(c.psum[:, bank, col:col + D], xs[:, h, k, cols], c.m0[:, k, :], start=False,
                                  stop=False, skip_group_check=True)
                    last = pe.matmul(c.psum[:, bank, col:col + D], c.ones[0:1, :], bout[0:1, :], start=False, stop=True,
                                     skip_group_check=True)
                last.then_inc(x1_psum, 1)

            def turn_rows(s, h):
                t0, nt = HALVES[h]
                pe.wait_ge(xn2_ready, s * 2 + h + 1)
                pe.wait_ge(copied, (s * 2 + h) * 2)
                for k in range(2):
                    for t in range(nt):
                        last = pe.transpose(c.psum[:, 5 + k, t * P:(t + 1) * P], xn2[:, h, t, k * P:(k + 1) * P], c.ident[:])
                    last.then_inc(turned, 1)

            def score(s, h):
                t0, nt = HALVES[h]
                pe.wait_ge(copied, (s * 2 + h) * 2 + 2)
                pe.wait_ge(scores_ready, s * 2 + h)
                for t in range(nt):
                    col = h * 64 + t * EXPERTS
                    for k in range(2):
                        last = pe.matmul(c.psum[:, 7, col:col + EXPERTS], xn2T[:, h, k, t * P:(t + 1) * P], wg[:, k, :],
                                         start=(k == 0), stop=(k == 1))
                last.then_inc(scored, 1)

            with pe.Fori(0, NS) as s:
                x1_rows(s, 0)
                x1_rows(s, 1)
                for h in range(2):
                    turn_rows(s, h)
                    score(s, h)
    c.constants.end(48)


def route(c):
    nc = c.nc
    part = Carver(c.scr, SCR)
    T8 = [NT, EXPERTS]
    rev, eq, cand = part.take([EXPERTS]), part.take(T8), part.take(T8)
    mask = [part.take(T8), part.take(T8)]
    rest = part.take(T8)
    top, code = part.take([NT]), [part.take([NT]), part.take([NT])]
    both = part.take(T8, BF16)
    tri, ones_b = part.take([P], BF16), part.take([NT])
    total, upto = part.take([EXPERTS, NT]), part.take([EXPERTS, NT])
    rank = part.take(T8)
    picked, rank_of = part.take(T8), [part.take([NT]), part.take([NT])]
    start_of = part.take([NT])
    count_i, ntile = part.take([EXPERTS], I32), part.take([EXPERTS])
    end, first = part.take([EXPERTS]), part.take([EXPERTS])
    where = part.take([EXPERTS])
    node, tile_no = part.take([1]), part.take([MT])
    inside, later = part.take([MT]), part.take([MT])
    t_expert, t_row = part.take([MT]), part.take([MT])
    const, vec, pe_done = c.sem("route_const"), c.sem("route_vec"), c.sem("route_counts")
    w_loaded = c.sem("expert_weights_loaded")
    raw = c.agg.rearrange("p a b -> p (a b)")
    words = EXPERTS * 2 * HID
    marks = {}
    with nc.Block() as block:

        @block.sync
        def _(sp):
            w1, w2 = raw[:, 0:words], raw[:, words:2 * words]
            for e in range(EXPERTS):
                sp.dma_start(w1[:, e * 2 * HID:(e + 1) * 2 * HID].rearrange("p (k n) -> p k n", n=HID),
                             c.inp["L0_ffn_W1"][e].rearrange("(k p) n -> p k n", p=P)).then_inc(w_loaded, 16)
                sp.dma_start(w2[:, e * HM * D:(e + 1) * HM * D].rearrange("p (m n) -> p m n", n=D),
                             c.inp["L0_ffn_W2"][e].rearrange("(m p) n -> p m n", p=P)).then_inc(w_loaded, 16)
            sp.wait_ge(w_loaded, 16 * 2 * EXPERTS)

        @block.gpsimd
        def _(g):
            small = dict(allow_small_or_imprecise_dtypes=True)
            g.iota(rev, pattern=[[-1, EXPERTS]], base=EXPERTS, channel_multiplier=0, **small).then_inc(const, 1)
            g.iota(node, pattern=[[0, 1]], base=0, channel_multiplier=1, **small).then_inc(const, 1)
            g.iota(tile_no, pattern=[[1, MT]], base=0, channel_multiplier=0, **small).then_inc(const, 1)
            g.memset(tri, 1.0).then_inc(const, 1)
            g.wait_ge(const, 4)
            g.affine_select(out=tri, in_=tri, compare_op=ALU.is_gt, fill=0.0, base=0, pattern=[[1, P]],
                            channel_multiplier=-1).then_inc(const, 1)

        @block.vector
        def _(v):
            step = Chain(v, vec)

            def do(instruction):
                step.done(instruction)
                step.wait()

            def wide(x):
                return x.unsqueeze(2).broadcast_to([P, NT, EXPERTS])

            def over(x):
                return x.unsqueeze(1).broadcast_to([P, NT, EXPERTS])

            v.wait_ge(const, 5)
            scores = c.scores[:]
            for n in range(2):
                do(v.tensor_reduce(top, scores, AX.X, ALU.max))
                do(v.tensor_tensor(eq, scores, wide(top), ALU.is_equal))
                do(v.tensor_tensor(cand, eq, over(rev), ALU.mult))
                do(v.tensor_reduce(code[n], cand, AX.X, ALU.max))
                do(v.tensor_tensor(mask[n], over(rev), wide(code[n]), ALU.is_equal))
                if n == 0:
                    do(v.scalar_tensor_tensor(rest, mask[0], -1e30, scores, ALU.mult, ALU.add))
                    scores = rest
            do(v.tensor_tensor(both, mask[0], mask[1], ALU.add))
            marks["both"] = step.value()
            do(v.memset(ones_b, 1.0))
            v.wait_ge(pe_done, 1)
            in_tile = c.psum[:, 0, 0:NT * EXPERTS].rearrange("p (t e) -> p t e", e=EXPERTS)
            tile_sum = c.psum[:, 1, 0:NT * EXPERTS].rearrange("p (t e) -> p e t", e=EXPERTS)
            do(v.tensor_copy(total, tile_sum))
            for e in range(EXPERTS):
                ins = v.tensor_tensor_scan(upto[:, e, :], ones_b, total[:, e, :], 0.0, ALU.mult, ALU.add)
            do(ins)
            do(v.tensor_tensor(total, upto, total, ALU.subtract))
            do(v.tensor_tensor(rank, in_tile, total.rearrange("p e t -> p t e"), ALU.add))
            do(v.tensor_scalar(where, upto[:, :, NT - 1], float(P - 1), None, ALU.add))
            do(v.tensor_copy(count_i, where))
            do(v.tensor_scalar(count_i, count_i, 7, None, ALU.arith_shift_right))
            do(v.tensor_copy(ntile, count_i))
            do(v.tensor_tensor_scan(end, ones_b[:, 0:EXPERTS], ntile, 0.0, ALU.mult, ALU.add))
            do(v.tensor_tensor(first, end, ntile, ALU.subtract))
            for n in range(2):
                do(v.tensor_tensor(picked, mask[n], rank, ALU.mult))
                do(v.tensor_reduce(rank_of[n], picked, AX.X, ALU.add))
                do(v.tensor_scalar(start_of, code[n], -float(REGION), float(EXPERTS * REGION), ALU.mult, ALU.add))
                do(v.tensor_tensor(c.scatter_to[:, n, :], start_of, rank_of[n], ALU.add))
                do(v.tensor_tensor(picked, mask[n], over(first), ALU.mult))
                do(v.tensor_reduce(start_of, picked, AX.X, ALU.add))
                do(v.scalar_tensor_tensor(c.result_at[:, n, :], start_of, float(P), rank_of[n], ALU.mult, ALU.add))
            do(v.tensor_scalar(where, rev, -float(REGION), float(EXPERTS * REGION), ALU.mult, ALU.add))
            do(v.tensor_tensor(where, where, upto[:, :, NT - 1], ALU.add))
            do(v.tensor_scalar(c.pad_to[:], where, node[:, 0:1], None, ALU.add))
            do(v.memset(t_expert, 0.0))
            do(v.memset(t_row, 0.0))
            for e in range(EXPERTS):
                do(v.tensor_scalar(inside, tile_no, first[:, e:e + 1], None, ALU.is_ge))
                do(v.tensor_scalar(later, tile_no, end[:, e:e + 1], None, ALU.is_lt))
                do(v.tensor_tensor(inside, inside, later, ALU.mult))
                do(v.scalar_tensor_tensor(t_expert, inside, float(e), t_expert, ALU.mult, ALU.add))
                do(v.tensor_scalar(later, tile_no, first[:, e:e + 1], None, ALU.subtract))
                do(v.tensor_scalar(later, later, float(P), float(e * REGION), ALU.mult, ALU.add))
                do(v.tensor_tensor(later, later, inside, ALU.mult))
                do(v.tensor_tensor(t_row, t_row, later, ALU.add))
            do(v.tensor_copy(c.tile_expert[:], t_expert))
            do(v.tensor_copy(c.tile_row[:], t_row))

        @block.tensor
        def _(pe):
            pe.wait_ge(const, 5)
            pe.wait_ge(vec, marks["both"])
            flat = both.rearrange("p t e -> p (t e)")
            pe.matmul(c.psum[:, 0, 0:NT * EXPERTS], tri, flat, start=True, stop=True)
            pe.matmul(c.psum[:, 1, 0:NT * EXPERTS], c.ones16[:], flat, start=True, stop=True).then_inc(pe_done, 1)


def send_to_experts(c):
    nc = c.nc
    part = Carver(c.scr, SCR)
    part.at = EXPERTS * HM * D
    rows = part.take([2, 4, D])
    zero_rows = part.take([D])
    to = part.take([2, 2, 4], I32)
    raw = c.agg.rearrange("p a b -> p (a b)")
    words = EXPERTS * 2 * HID
    xnT = c.xnT.rearrange("p a b -> p (a b)")
    c.w1_16 = xnT[:, 0:words].bitcast(F16).rearrange("p (e k h n) -> p e k h n", k=2, h=2, n=HID)
    c.w2_16 = c.scr[:, 0:words].bitcast(F16).rearrange("p (e k h n) -> p e k h n", k=HM, h=2, n=D)
    w1 = raw[:, 0:words].rearrange("p (e k n) -> p e k n", k=2, n=HID)
    w2 = raw[:, words:2 * words].rearrange("p (e k n) -> p e k n", k=HM, n=D)
    zero, landed = c.sem("pad_rows_zeroed"), [c.sem(f"send_rows_landed{h}") for h in range(2)]
    idx_ready, begun, sent = c.sem("send_indices_ready"), c.passed, [c.sem(f"rows_sent{h}") for h in range(2)]
    padded, high = c.sem("pads_sent"), c.sem("weights_high")
    with nc.Block() as block:

        @block.sync
        def _(sp):
            with sp.Fori(0, NS) as s:
                for h, (t0, nt) in enumerate(HALVES):
                    sp.wait_ge(sent[h], s * (2 * nt * 16))
                    sp.dma_start(rows[:, h, 0:nt, :],
                                 c.xn2_tab[ds(s * SS + t0 * P, nt * P), :].rearrange("(t p) d -> p t d", p=P)
                                 ).then_inc(landed[h], 16)

        @block.vector
        def _(v):
            v.memset(zero_rows, 0.0).then_inc(zero, 1)
            for e in range(EXPERTS):
                for n, (w, parts) in enumerate(((w1, c.w1_16), (w2, c.w2_16))):
                    v.wait_ge(high, 2 * e + n + 1)
                    v.scalar_tensor_tensor(parts[:, e, :, 1, :], w[:, e, :, :], WS, parts[:, e, :, 0, :],
                                           ALU.mult, ALU.subtract)

        @block.scalar
        def _(a):
            def indices(s):
                for h, (t0, nt) in enumerate(HALVES):
                    a.wait_ge(sent[h], s * (2 * nt * 16))
                    a.activation(to[:, h, :, 0:nt], c.scatter_to[:, :, ds(s * TS + t0, nt)], ACT.Copy).then_inc(idx_ready, 1)

            for e in range(EXPERTS):
                for w, parts in ((w1, c.w1_16), (w2, c.w2_16)):
                    a.activation(parts[:, e, :, 0, :], w[:, e, :, :], ACT.Copy, scale=WS).then_inc(high, 1)
                if e < NS:
                    indices(e)

        @block.gpsimd
        def _(g):
            g.wait_ge(zero, 1)
            for e in range(EXPERTS):
                g.indirect_dma_start(out=c.slot_x, in_=zero_rows, in_offset=None,
                                     out_offset=bass.IndirectOffsetOnAxis(ap=c.pad_to[:, e:e + 1], axis=0)
                                     ).then_inc(padded, 16)
            with g.Fori(0, NS) as s:
                for h, (t0, nt) in enumerate(HALVES):
                    g.wait_ge(landed[h], s * 16 + 16)
                    g.sem_inc(begun, 1)
                    g.wait_ge(idx_ready, s * 2 + h + 1)
                    g.sem_inc(begun, 1)
                    for n in range(2):
                        for t in range(nt):
                            g.indirect_dma_start(out=c.slot_x, in_=rows[:, h, t, :], in_offset=None,
                                                 out_offset=bass.IndirectOffsetOnAxis(ap=to[:, h, n, t:t + 1], axis=0)
                                                 ).then_inc(sent[h], 16)
            g.wait_ge(padded, 16 * EXPERTS)
            for h, (t0, nt) in enumerate(HALVES):
                g.wait_ge(sent[h], 32 * nt * NS)


def experts(c):
    nc = c.nc
    part = Carver(c.scr, SCR)
    part.at = EXPERTS * HM * D
    x = part.take([2, D])
    xT = part.take([2, 2, D], F16)
    g = part.take([2, HID])
    gT = part.take([2, 2, HID], F16)
    y = part.take([2, D])
    b2 = part.take([EXPERTS, D])
    agg = c.agg.rearrange("p a b -> p (a b)")
    loaded, x_ready = c.constants.sem, [c.sem(f"moe_x_loaded{b}") for b in range(2)]
    turned, x_high, x_low = c.sem("moe_turned"), c.sem("moe_x_high"), c.sem("moe_x_low")
    h_ready, g_ready = c.sem("moe_h_ready"), c.sem("moe_gelu_done")
    g_high, g_low = c.sem("moe_g_high"), c.sem("moe_g_low")
    begun = c.passed
    y_ready, y_out = c.sem("moe_y_products"), c.sem("moe_y_ready")
    stored = [c.sem(f"moe_stored{b}") for b in range(2)]
    PARTS = ((0, 0), (0, 1), (1, 0))

    def turns(engine, body):
        body(0, True, False)
        with engine.Fori(1, MT // 2 - 1) as q:
            body(q, False, False)
        body(MT // 2 - 1, False, True)

    with nc.Block() as block:

        @block.sync
        def _(sp):
            sp.dma_start(b2.rearrange("p e d -> p (e d)"),
                         c.inp["L0_ffn_b2"].rearrange("e d -> (e d)").unsqueeze(0).partition_broadcast(P)).then_inc(loaded, 16)
            sp.wait_ge(loaded, c.constants.at(16))

            def load(q, b):
                sp.wait_ge(turned, (q - 1) * 2 + b + 1)
                row = sp.value_load(c.tile_row[0:1, ds(q * 2 + b, 1)], min_val=0, max_val=EXPERTS * REGION - P)
                sp.dma_start(x[:, b, :], c.slot_x[ds(row, P), :]).then_inc(x_ready[b], 16)

            def store(q, b):
                sp.wait_ge(y_out, q * 2 + b + 1)
                sp.dma_start(c.slot_y[ds((q * 2 + b) * P, P), :], y[:, b, :]).then_inc(stored[b], 16)

            for b in range(2):
                row = sp.value_load(c.tile_row[0:1, b:b + 1], min_val=0, max_val=EXPERTS * REGION - P)
                sp.dma_start(x[:, b, :], c.slot_x[ds(row, P), :]).then_inc(x_ready[b], 16)
            with sp.Fori(1, MT // 2) as q:
                for b in range(2):
                    load(q, b)
                for b in range(2):
                    store(q - 1, b)
            for b in range(2):
                store(MT // 2 - 1, b)
            for b in range(2):
                sp.wait_ge(stored[b], 16 * (MT // 2))

        @block.scalar
        def _(a):
            def body(q, first, last):
                for b in range(2):
                    i = q * 2 + b
                    a.wait_ge(turned, i + 1)
                    if not first:
                        a.wait_ge(h_ready, i - 1)
                    a.activation(xT[:, b, 0, :], c.psum[:, b, 0:D], ACT.Copy, scale=XS).then_inc(x_high, 1)
                    if not (first and b == 0):
                        gelu(i - 1, 1 - b, first)

            def gelu(i, b, first):
                a.wait_ge(h_ready, i + 1)
                if not first:
                    a.wait_ge(g_low, i - 1)
                e = a.value_load(c.tile_expert[0:1, ds(i, 1)], min_val=0, max_val=EXPERTS - 1)
                at = COLUMNS_AT["L0_ffn_b1"][0]
                for m in range(HM):
                    ins = a.activation(g[:, b, m * P:(m + 1) * P], c.psum[:, 2 + b, m * P:(m + 1) * P], ACT.Gelu,
                                       bias=c.cols[:, ds(e * HM + (at + m), 1)], scale=1.0 / (XS * WS))
                ins.then_inc(g_ready, 1)
            turns(a, body)
            gelu(MT - 1, 1, False)

        @block.vector
        def _(v):
            def x_split(i, b):
                v.wait_ge(x_high, i + 1)
                v.scalar_tensor_tensor(xT[:, b, 1, :], c.psum[:, b, 0:D], XS, xT[:, b, 0, :], ALU.mult, ALU.subtract
                                       ).then_inc(x_low, 1)

            def g_split(i, b, first):
                v.wait_ge(g_ready, i + 1)
                if not first:
                    v.wait_ge(y_ready, i - 1)
                v.tensor_scalar(gT[:, b, 0, :], g[:, b, :], XS, None, ALU.mult).then_inc(g_high, 1)
                v.wait_ge(g_high, i + 1)
                v.scalar_tensor_tensor(gT[:, b, 1, :], g[:, b, :], XS, gT[:, b, 0, :], ALU.mult, ALU.subtract
                                       ).then_inc(g_low, 1)

            def y_rows(i, b, q, first):
                v.wait_ge(y_ready, i + 1)
                if not first:
                    v.wait_ge(stored[b], q * 16)
                e = v.value_load(c.tile_expert[0:1, ds(i, 1)], min_val=0, max_val=EXPERTS - 1)
                v.scalar_tensor_tensor(y[:, b, :], c.psum[:, 4 + b, 0:D], 1.0 / (XS * WS),
                                       b2[:, ds(e, 1), :].rearrange("p e d -> p (e d)"), ALU.mult, ALU.add
                                       ).then_inc(y_out, 1)

            v.wait_ge(loaded, c.constants.at(16))

            def body(q, first, last):
                for b in range(2):
                    i = q * 2 + b
                    x_split(i, b)
                    if not (first and b == 0):
                        g_split(i - 1, 1 - b, first)
                    if not first:
                        y_rows(i - 2, b, q - 1, False) if b == 0 else y_rows(i - 2, b, q - 1, False)
            turns(v, body)
            y_rows(MT - 2, 0, MT // 2 - 1, False)
            g_split(MT - 1, 1, False)
            y_rows(MT - 1, 1, MT // 2 - 1, False)

        @block.tensor
        def _(pe):
            def turn_x(i, b, q, first):
                pe.wait_ge(x_ready[b], (q + 1) * 16)
                if not first:
                    pe.wait_ge(x_low, i - 1)
                for k in range(2):
                    last = pe.transpose(c.psum[:, b, k * P:(k + 1) * P], x[:, b, k * P:(k + 1) * P], c.ident[:])
                last.then_inc(turned, 1)

            def hidden(i, b, first):
                pe.wait_ge(x_low, i + 1)
                if not first:
                    pe.wait_ge(g_ready, i - 1)
                pe.sem_inc(begun, 1)
                e = pe.value_load(c.tile_expert[0:1, ds(i, 1)], min_val=0, max_val=EXPERTS - 1)
                for m in range(HM):
                    n = 0
                    for k in range(2):
                        for wp, xp in PARTS:
                            n += 1
                            last = pe.matmul(c.psum[:, 2 + b, m * P:(m + 1) * P],
                                             c.w1_16[:, ds(e, 1), k, wp, m * P:(m + 1) * P].rearrange("p e n -> p (e n)"),
                                             xT[:, b, xp, k * P:(k + 1) * P], start=(n == 1), stop=(n == 6))
                last.then_inc(h_ready, 1)

            def result(i, b, first):
                pe.wait_ge(g_low, i + 1)
                if not first:
                    pe.wait_ge(y_out, i - 1)
                pe.sem_inc(begun, 1)
                e = pe.value_load(c.tile_expert[0:1, ds(i, 1)], min_val=0, max_val=EXPERTS - 1)
                n = 0
                for m in range(HM):
                    for wp, gp in PARTS:
                        n += 1
                        last = pe.matmul(c.psum[:, 4 + b, 0:D], gT[:, b, gp, m * P:(m + 1) * P],
                                         c.w2_16[:, ds(e, 1), m, wp, :].rearrange("p e n -> p (e n)"),
                                         start=(n == 1), stop=(n == 3 * HM))
                last.then_inc(y_ready, 1)

            turn_x(0, 0, 0, True)

            def body(q, first, last):
                for b in range(2):
                    i = q * 2 + b
                    if b == 0:
                        turn_x(i + 1, 1, q, first)
                    elif not last:
                        turn_x(i + 1, 0, q + 1, False)
                    hidden(i, b, first)
                    if not (first and b == 0):
                        result(i - 1, 1 - b, first or False)
            turns(pe, body)
            result(MT - 1, 1, False)
    c.constants.end(16)


def second_norm(c):
    nc = c.nc
    part = Carver(c.scr, SCR)
    x2, xn3 = part.take([2, 4, D]), part.take([2, 4, D])
    y = part.take([2, 2, 4, D])
    at = part.take([2, 2, 4], I32)
    st, mo, rstd = part.take([2, 4, 6]), part.take([2, 4, 2]), part.take([2, 4])
    wsum = part.take([P])
    w_in, w_vec, w_out = c.sem("norm3_wsum_loaded"), c.sem("norm3_wsum_inverted"), c.sem("norm3_wsum_moved")
    x_in = [c.sem(f"norm3_x1_loaded{h}") for h in range(2)]
    y_in = [c.sem(f"norm3_results_landed{h}") for h in range(2)]
    at_ready, begun, vec, root = c.sem("norm3_indices_ready"), c.passed, c.sem("norm3_vec"), c.sem("norm3_root")
    moments = c.passed
    turned, copied = c.sem("norm3_turned"), c.sem("norm3_copied")
    stored = [c.sem(f"norm3_stored{h}") for h in range(2)]
    PER = 7
    with nc.Block() as block:

        @block.sync
        def _(sp):
            sp.dma_start(wsum[0:NT, :], c.wsum_row.rearrange("a (t n) -> (a t) n", n=P)).then_inc(w_in, 16)
            sp.wait_ge(w_vec, 2)
            sp.dma_start(c.wsum_row.rearrange("a (t n) -> (a t) n", n=P), wsum[0:NT, :]).then_inc(w_out, 16)
            sp.wait_ge(w_out, 16)
            sp.dma_start(c.agg[:, 2, :], c.wsum_row.partition_broadcast(P)).then_inc(w_out, 16)
            with sp.Fori(0, NS) as s:
                for h, (t0, nt) in enumerate(HALVES):
                    sp.wait_ge(stored[h], s * 32)
                    sp.dma_start(x2[:, h, 0:nt, :], c.x1_tab[ds(s * SS + t0 * P, nt * P), :].rearrange("(t p) d -> p t d", p=P)
                                 ).then_inc(x_in[h], 16)
                for h, (t0, nt) in enumerate(HALVES):
                    sp.wait_ge(vec, s * (2 * PER) + (h + 1) * PER)
                    for table, rows in ((c.x2_tab, x2), (c.xn3_tab, xn3)):
                        sp.dma_start(table[ds(s * SS + t0 * P, nt * P), :].rearrange("(t p) d -> p t d", p=P),
                                     rows[:, h, 0:nt, :]).then_inc(stored[h], 16)
            sp.wait_ge(w_out, 32)
            for q in stored:
                sp.wait_ge(q, 32 * NS)

        @block.gpsimd
        def _(g):
            with g.Fori(0, NS) as s:
                for h, (t0, nt) in enumerate(HALVES):
                    g.wait_ge(at_ready, s * 2 + h + 1)
                    g.sem_inc(begun, 1)
                    for n in range(2):
                        for t in range(nt):
                            g.indirect_dma_start(out=y[:, h, n, t, :], out_offset=None, in_=c.slot_y,
                                                 in_offset=bass.IndirectOffsetOnAxis(ap=at[:, h, n, t:t + 1], axis=0)
                                                 ).then_inc(y_in[h], 16)

        @block.vector
        def _(v):
            v.memset(c.agg[:, 0:2, :], 0.0)
            v.wait_ge(w_in, 16)
            v.tensor_scalar(wsum[0:NT, :], wsum[0:NT, :], 1e-6, None, ALU.max).then_inc(w_vec, 1)
            v.wait_ge(w_vec, 1)
            v.reciprocal(wsum[0:NT, :], wsum[0:NT, :]).then_inc(w_vec, 1)
            with v.Fori(0, NS) as s:
                for h, (t0, nt) in enumerate(HALVES):
                    chain = Chain(v, vec, s, 2 * PER, h * PER)
                    v.wait_ge(x_in[h], s * 16 + 16)
                    v.wait_ge(y_in[h], (s + 1) * (2 * nt * 16))
                    chain.done(v.tensor_tensor(x2[:, h, 0:nt, :], x2[:, h, 0:nt, :], y[:, h, 0, 0:nt, :], ALU.add))
                    chain.wait()
                    chain.done(v.tensor_tensor(x2[:, h, 0:nt, :], x2[:, h, 0:nt, :], y[:, h, 1, 0:nt, :], ALU.add))
                    chain.wait()
                    for t in range(nt):
                        ins = v.bn_stats(st[:, h, t, :], x2[:, h, t, :])
                    chain.done(ins)
                    chain.wait()
                    v.sem_inc(moments, 1)
                    for t in range(nt):
                        ins = v.bn_aggr(mo[:, h, t, :], st[:, h, t, :])
                    chain.done(ins)
                    chain.wait()
                    chain.done(v.tensor_scalar(rstd[:, h, 0:nt], mo[:, h, 0:nt, 1], EPS, None, ALU.add))
                    v.wait_ge(root, s * 2 + h + 1)
                    chain.done(v.reciprocal(rstd[:, h, 0:nt], rstd[:, h, 0:nt]))
                    chain.wait()
                    v.wait_ge(turned, s * 2)
                    for t in range(nt):
                        ins = v.tensor_scalar(xn3[:, h, t, :], x2[:, h, t, :], mo[:, h, t, 0:1], rstd[:, h, t:t + 1],
                                              ALU.subtract, ALU.mult)
                    chain.done(ins)

        @block.scalar
        def _(a):
            with a.Fori(0, NS) as s:
                for h, (t0, nt) in enumerate(HALVES):
                    a.wait_ge(vec, s * (2 * PER))
                    a.wait_ge(y_in[h], s * (2 * nt * 16))
                    a.activation(at[:, h, :, 0:nt], c.result_at[:, :, ds(s * TS + t0, nt)], ACT.Copy).then_inc(at_ready, 1)
                for h, (t0, nt) in enumerate(HALVES):
                    a.wait_ge(vec, s * (2 * PER) + h * PER + 5)
                    a.activation(rstd[:, h, 0:nt], rstd[:, h, 0:nt], ACT.Sqrt).then_inc(root, 1)
                    a.wait_ge(turned, s * 2 + h + 1)
                    for k in range(2):
                        last = a.activation(c.xnT[:, k, ds(s * SS + t0 * P, nt * P)], c.psum[:, 2 * h + k, 0:nt * P], ACT.Copy)
                    last.then_inc(copied, 1)

        @block.tensor
        def _(pe):
            with pe.Fori(0, NS) as s:
                for h, (t0, nt) in enumerate(HALVES):
                    pe.wait_ge(vec, s * (2 * PER) + (h + 1) * PER)
                    pe.wait_ge(copied, s * 2)
                    for k in range(2):
                        for t in range(nt):
                            last = pe.transpose(c.psum[:, 2 * h + k, t * P:(t + 1) * P], xn3[:, h, t, k * P:(k + 1) * P],
                                                c.ident[:])
                    last.then_inc(turned, 1)


def gather_third(c):
    part = Carver(c.scr, SCR)
    part.at = (2 * CT * W) + RING * CT * D
    wk, tile, rows = part.take([2, D]), part.take([2, P]), part.take([D])
    low, e, kk = part.take([D]), part.take([D]), part.take([D])
    w_loaded, tile_ready, z_ready = c.constants.sem, c.sem("k_tile_ready"), c.sem("k_products")
    rows_ready, vec, act, sums_done = c.sem("k_rows_loaded"), c.sem("k_vec"), c.sem("k_exp_done"), c.sem("k_sums_done")
    z, sums, ksum = c.psum[:, 2, 0:D], c.psum[:, 3, :], c.psum[:, 4, 0:2]
    PER = 2

    def first(pe):
        pe.matmul(sums, c.zeros[:], c.ones[:, 0:1].broadcast_to([P, 512]), start=True, stop=False, skip_group_check=True)
        pe.matmul(ksum, c.zeros[:], c.ones[:, 0:2], start=True, stop=False, skip_group_check=True)
        pe.wait_ge(w_loaded, c.constants.at(16))

    def products_begin(pe, i, last):
        pe.wait_ge(tile_ready, i + 1)
        pe.wait_ge(vec, i * PER)
        for k in range(2):
            ins = pe.matmul(z, tile[:, k, :], wk[:, k, :], start=(k == 0), stop=(k == 1))
        ins.then_inc(z_ready, 1)

    def products_end(pe, i, last):
        pe.wait_ge(vec, (i + 1) * PER)
        pe.wait_ge(rows_ready, i * 16 + 16)
        n = LAST if last else P
        for k in range(2):
            pe.matmul(sums[:, k * D:(k + 1) * D], rows[0:n, k * P:(k + 1) * P], kk[0:n, :], start=False, stop=last,
                      skip_group_check=True)
        for j in range(2):
            ins = pe.matmul(ksum[:, j:j + 1], kk[0:n, j * P:(j + 1) * P], c.ones[0:n, 0:1], start=False, stop=last,
                            skip_group_check=True)
        ins.then_inc(sums_done, 1)

    def vector(v, i, last, u):
        step = Chain(v, vec, i, PER)
        if u == 1:
            v.wait_ge(z_ready, i + 1)
            v.wait_ge(act, i)
            step.done(v.tensor_scalar(low, z, 0.0, None, ALU.min))
        if u == 3:
            step.k = 1
            v.wait_ge(act, i + 1)
            v.wait_ge(sums_done, i)
            step.done(v.scalar_tensor_tensor(kk, z, 0.0, e, ALU.max, ALU.add))

    def scalar(a, i, last):
        a.wait_ge(z_ready, i)
        a.activation(tile[:], c.xnT[:, :, ds(i * P, P)], ACT.Copy).then_inc(tile_ready, 1)
        a.wait_ge(vec, i * PER + 1)
        a.activation(e, low, ACT.Exp).then_inc(act, 1)

    def sync_first(sp):
        sp.dma_start(wk.rearrange("p a b -> p (a b)"), c.turned_part("L1_mix_Wk", 2 * D)).then_inc(w_loaded, 16)

    def sync(sp, i, last):
        sp.wait_ge(sums_done, i)
        sp.dma_start(rows, c.xn3_tab[ds(i * P, P), :]).then_inc(rows_ready, 16)

    side = dict(tensor_first=first, tensor_begin=products_begin, tensor_end=products_end, vector=vector,
                scalar=scalar, sync_first=sync_first, sync=sync)
    aggregate(c, table=c.xn3_tab, weighted=True, slots=(0, 1), side=side)
    c.constants.end(16)


def fold_second_attention(c):
    nc = c.nc
    part = Carver(c.scr, SCR)
    wvT, wprojT = part.take([2, D]), part.take([2, D])
    kxT, ctxT = part.take([2, D]), part.take([2, P])
    ksum = part.take([2])
    loaded, vec, pe_done = c.constants.sem, c.sem("fold1_vec"), c.sem("fold1_products")
    with nc.Block() as block:

        @block.sync
        def _(sp):
            for w, name in ((wvT, "L1_mix_Wv"), (wprojT, "L1_mix_Wproj")):
                sp.dma_start(w.rearrange("p a b -> p (a b)"), c.turned_part(name, 2 * D)).then_inc(loaded, 16)

        @block.vector
        def _(v):
            v.tensor_copy(kxT.rearrange("p a b -> p (a b)"), c.psum[:, 3, :]).then_inc(vec, 1)
            v.tensor_copy(ksum, c.psum[:, 4, 0:2]).then_inc(vec, 1)
            v.wait_ge(vec, 2)
            for j in range(2):
                v.tensor_scalar(c.small1[:, j * P:(j + 1) * P], c.bd32[:], ksum[:, j:j + 1], None, ALU.mult)
            v.wait_ge(pe_done, 1)
            v.tensor_tensor(ctxT[:], c.psum[:, 0, 0:2 * P].rearrange("p (j d) -> p j d", d=P),
                            c.bd32[:].unsqueeze(1).broadcast_to([P, 2, P]), ALU.mult).then_inc(vec, 1)
            v.wait_ge(pe_done, 2)
            v.tensor_copy(c.m0[:], c.psum[:, 1, :].rearrange("p (k d) -> p k d", d=D))

        @block.tensor
        def _(pe):
            pe.wait_ge(vec, 2)
            pe.wait_ge(loaded, c.constants.at(32))
            for j in range(2):
                for k in range(2):
                    last = pe.matmul(c.psum[:, 0, j * P:(j + 1) * P], wvT[:, k, j * P:(j + 1) * P],
                                     kxT[:, k, j * P:(j + 1) * P], start=(k == 0), stop=(k == 1))
            last.then_inc(pe_done, 1)
            pe.wait_ge(vec, 3)
            for j in range(2):
                last = pe.matmul(c.psum[:, 1, j * D:(j + 1) * D], ctxT[:, j, :], wprojT[:, j, :], start=True, stop=True)
            last.then_inc(pe_done, 1)
    c.constants.end(32)


def second_layer_sum(c):
    nc = c.nc
    part = Carver(c.scr, SCR)
    w1T, w2T, wqT = part.take([2, D]), part.take([2, D]), part.take([2, D])
    g1T, qT = part.take([2, 2, 512]), part.take([2, 2, 512])
    low = part.take([2, 512])
    y, x2 = part.take([2, 4, D]), part.take([2, 4, D])
    xn4T = part.take([2, 2, 512])
    b2, gamma, beta, bproj = part.take([D]), part.take([D]), part.take([D]), part.take([D])
    gw, gb = part.take([2, GATES]), part.take([GATES])
    st, mo, rstd = part.take([2, 4, 6]), part.take([2, 4, 2]), part.take([2, 4])
    loaded, consts = c.constants.sem, c.sem("last_shift_ready")
    rows_in = [c.sem(f"last_rows_loaded{h}") for h in range(2)]
    scaled, shifted, moved = c.sem("agg_scaled"), c.sem("last_rows_shifted"), c.sem("x3_moved")
    g_pre, gelu_done, q_pre, q_vec, q_exp = (c.sem("last_gelu_products"), c.sem("last_gelu_done"), c.sem("q_products"),
                                             c.sem("q_vec"), c.sem("q_exp_done"))
    div_pre, y_pre, y_read, m_pre, m_read = (c.sem("divisor_products"), c.sem("y_products"), c.sem("y_read"),
                                             c.sem("attention_products"), c.sem("attention_read"))
    vec, root, turned, copied = c.sem("last_vec"), c.sem("last_root"), c.sem("last_turned"), c.sem("last_copied")
    gate_pre, gate_read = c.sem("gate_products"), c.sem("gate_read")
    QV, YV, XV = 5, 5, 6
    PER = YV + XV
    flat = "p a b -> p (a b)"

    def turns(engine, body):
        body(0, True)
        with engine.Fori(1, NS) as s:
            body(s, False)

    def columns(s, h):
        t0, nt = HALVES[h]
        return ds(s * SS + t0 * P, nt * P)

    with nc.Block() as block:

        @block.sync
        def _(sp):
            for w, name in ((w1T, "L1_gnn_W1"), (w2T, "L1_gnn_W2"), (wqT, "L1_mix_Wq")):
                sp.dma_start(w.rearrange(flat), c.turned_part(name, 2 * D)).then_inc(loaded, 16)
            for b, name in ((b2, "L1_gnn_b2"), (gamma, "L1_gnn_gamma"), (beta, "L1_gnn_beta"), (bproj, "L1_mix_bproj"),
                            (gb, "L1_ffn_gb")):
                sp.dma_start(b, c.inp[name].unsqueeze(0).partition_broadcast(P)).then_inc(loaded, 16)
            sp.dma_start(gw, c.inp["L1_ffn_gW"].rearrange("(k p) e -> p k e", p=P)).then_inc(loaded, 16)

            def body(s, first):
                for h, (t0, nt) in enumerate(HALVES):
                    at = ds(s * SS + t0 * P, nt * P)
                    if not first:
                        sp.wait_ge(moved, s * 4 - 3 + 2 * h)
                        sp.wait_ge(turned, s * 2 - 1 + h)
                    for rows, table in ((y, c.xn3_tab), (x2, c.x2_tab)):
                        sp.dma_start(rows[:, h, 0:nt, :], table[at, :].rearrange("(t p) d -> p t d", p=P)).then_inc(rows_in[h], 16)
            turns(sp, body)
            sp.wait_ge(loaded, c.constants.at(144))

        @block.gpsimd
        def _(g):
            g.wait_ge(loaded, c.constants.at(144))
            g.tensor_tensor(beta, beta, bproj, ALU.add).then_inc(consts, 1)
            g.wait_ge(consts, 1)

            def prepare(s, h):
                t0, nt = HALVES[h]
                acc = c.agg[:, 0:2, columns(s, h)]
                g.tensor_tensor(acc, acc, c.agg[:, 2:3, columns(s, h)].broadcast_to([P, 2, nt * P]), ALU.mult
                                ).then_inc(scaled, 1)
                g.wait_ge(rows_in[h], s * 32 + 32)
                for rows, shift in ((y, b2), (x2, beta)):
                    last = g.tensor_tensor(rows[:, h, 0:nt, :], rows[:, h, 0:nt, :],
                                           shift.unsqueeze(1).broadcast_to([P, nt, D]), ALU.add)
                last.then_inc(shifted, 1)

            def move_x3(s, h):
                t0, nt = HALVES[h]
                g.wait_ge(vec, s * (2 * PER) + h * PER + YV + 1)
                g.sem_inc(c.passed, 1)
                g.tensor_copy(c.agg[:, 0:2, columns(s, h)].rearrange("p k (t n) -> p t k n", n=P),
                              y[:, h, 0:nt, :].rearrange("p t (k n) -> p t k n", n=P)).then_inc(moved, 1)

            def move_xn4(s, h):
                t0, nt = HALVES[h]
                g.wait_ge(copied, s * 2 + h + 1)
                g.sem_inc(c.passed, 1)
                g.tensor_copy(c.xnT[:, :, columns(s, h)], xn4T[:, h, :, 0:nt * P]).then_inc(moved, 1)

            def body(s, first):
                prepare(s, 0)
                if not first:
                    move_xn4(s - 1, 1)
                prepare(s, 1)
                move_x3(s, 0)
                move_xn4(s, 0)
                move_x3(s, 1)
            turns(g, body)
            move_xn4(NS - 1, 1)

        @block.vector
        def _(v):
            v.wait_ge(loaded, c.constants.at(144))

            def q_chain(s, h):
                return Chain(v, q_vec, s, 2 * QV, h * QV)

            def q_rows(s, h):
                t0, nt = HALVES[h]
                z = c.psum[:, 2:4, 0:nt * P]
                chain = q_chain(s, h)
                v.wait_ge(q_pre, s * 2 + h + 1)
                chain.wait()
                chain.done(v.tensor_scalar(low[:, :, 0:nt * P], z, 0.0, None, ALU.min))
                v.wait_ge(q_exp, s * 2 + h + 1)
                v.wait_ge(m_pre, s * 2)
                chain.done(v.scalar_tensor_tensor(qT[:, h, :, 0:nt * P], z, 0.0, low[:, :, 0:nt * P], ALU.max, ALU.add))

            def q_divided(s, h):
                t0, nt = HALVES[h]
                chain = q_chain(s, h)
                chain.k = 2
                v.wait_ge(div_pre, s * 2 + h + 1)
                chain.wait()
                chain.done(v.tensor_scalar(low[:, :, 0:nt * P], c.psum[:, 2:4, 0:nt * P], 1e-6, None, ALU.max))
                chain.wait()
                chain.done(v.reciprocal(low[:, :, 0:nt * P], low[:, :, 0:nt * P]))
                chain.wait()
                q = qT[:, h, :, 0:nt * P]
                chain.done(v.tensor_tensor(q, q, low[:, :, 0:nt * P], ALU.mult))

            def moments(chain, s, h, which):
                t0, nt = HALVES[h]
                for t in range(nt):
                    ins = v.bn_stats(st[:, h, t, :], y[:, h, t, :])
                chain.done(ins)
                chain.wait()
                v.sem_inc(c.passed, 1)
                for t in range(nt):
                    ins = v.bn_aggr(mo[:, h, t, :], st[:, h, t, :])
                chain.done(ins)
                chain.wait()
                chain.done(v.tensor_scalar(rstd[:, h, 0:nt], mo[:, h, 0:nt, 1], EPS, None, ALU.add))
                v.wait_ge(root, s * 4 + h * 2 + which + 1)
                chain.done(v.reciprocal(rstd[:, h, 0:nt], rstd[:, h, 0:nt]))
                chain.wait()

            def y_rows(s, h):
                t0, nt = HALVES[h]
                chain = Chain(v, vec, s, 2 * PER, h * PER)
                v.wait_ge(y_pre, s * 2 + h + 1)
                v.wait_ge(shifted, s * 2 + h + 1)
                rows = y[:, h, 0:nt, :]
                v.tensor_tensor(rows, rows, c.psum[:, 4:6, :].rearrange(flat)[:, 0:nt * D].rearrange("p (t d) -> p t d", d=D),
                                ALU.add).then_inc(y_read, 1)
                v.wait_ge(y_read, s * 2 + h + 1)
                moments(chain, s, h, 0)
                for t in range(nt):
                    ins = v.scalar_tensor_tensor(y[:, h, t, :], y[:, h, t, :], mo[:, h, t, 0:1], gamma, ALU.subtract, ALU.mult)
                chain.done(ins)

            def x3_rows(s, h):
                t0, nt = HALVES[h]
                chain = Chain(v, vec, s, 2 * PER, h * PER + YV)
                v.wait_ge(m_pre, s * 2 + h + 1)
                chain.wait()
                mix = c.psum[:, 6:8, :].rearrange(flat)
                for t in range(nt):
                    ins = v.scalar_tensor_tensor(y[:, h, t, :], y[:, h, t, :], rstd[:, h, t:t + 1], mix[:, t * D:(t + 1) * D],
                                                 ALU.mult, ALU.add)
                ins.then_inc(m_read, 1)
                v.wait_ge(m_read, s * 2 + h + 1)
                rows = y[:, h, 0:nt, :]
                chain.done(v.tensor_tensor(rows, rows, x2[:, h, 0:nt, :], ALU.add))
                chain.wait()
                moments(chain, s, h, 1)
                for t in range(nt):
                    ins = v.tensor_scalar(x2[:, h, t, :], y[:, h, t, :], mo[:, h, t, 0:1], rstd[:, h, t:t + 1],
                                          ALU.subtract, ALU.mult)
                chain.done(ins)

            def gates_read(s, h):
                t0, nt = HALVES[h]
                v.wait_ge(gate_pre, s * 2 + h + 1)
                v.tensor_tensor(c.scores[:, ds(s * TS + t0, nt), 0:GATES],
                                c.psum[:, 4, 0:nt * GATES].rearrange("p (t e) -> p t e", e=GATES),
                                gb.unsqueeze(1).broadcast_to([P, nt, GATES]), ALU.add).then_inc(gate_read, 1)

            def body(s, first):
                q_rows(s, 0)
                if not first:
                    gates_read(s - 1, 1)
                y_rows(s, 0)
                q_divided(s, 0)
                q_rows(s, 1)
                x3_rows(s, 0)
                y_rows(s, 1)
                q_divided(s, 1)
                x3_rows(s, 1)
                gates_read(s, 0)
            turns(v, body)
            gates_read(NS - 1, 1)

        @block.scalar
        def _(a):
            def gelu(s, h):
                t0, nt = HALVES[h]
                a.wait_ge(g_pre, s * 2 + h + 1)
                a.wait_ge(y_pre, s * 2)
                for m in range(2):
                    last = a.activation(g1T[:, h, m, 0:nt * P], c.psum[:, m, 0:nt * P], ACT.Gelu, bias=c.column("L1_gnn_b1", m))
                last.then_inc(gelu_done, 1)

            def exp(s, h):
                t0, nt = HALVES[h]
                a.wait_ge(q_vec, s * (2 * QV) + h * QV + 1)
                a.activation(low[:, :, 0:nt * P], low[:, :, 0:nt * P], ACT.Exp).then_inc(q_exp, 1)

            def rooted(s, h, which):
                t0, nt = HALVES[h]
                a.wait_ge(vec, s * (2 * PER) + h * PER + (YV + 4 if which else 3))
                a.activation(rstd[:, h, 0:nt], rstd[:, h, 0:nt], ACT.Sqrt).then_inc(root, 1)

            def copy(s, h):
                t0, nt = HALVES[h]
                a.wait_ge(turned, s * 2 + h + 1)
                a.wait_ge(gate_pre, s * 2)
                a.wait_ge(moved, s * 4)
                for k in range(2):
                    last = a.activation(xn4T[:, h, k, 0:nt * P], c.psum[:, 4 + k, 0:nt * P], ACT.Copy)
                last.then_inc(copied, 1)

            def body(s, first):
                gelu(s, 0)
                exp(s, 0)
                if not first:
                    copy(s - 1, 1)
                gelu(s, 1)
                rooted(s, 0, 0)
                exp(s, 1)
                rooted(s, 0, 1)
                rooted(s, 1, 0)
                copy(s, 0)
                rooted(s, 1, 1)
            turns(a, body)
            copy(NS - 1, 1)

        @block.tensor
        def _(pe):
            pe.wait_ge(loaded, c.constants.at(144))

            def gelu_products(s, h):
                t0, nt = HALVES[h]
                pe.wait_ge(scaled, s * 2 + h + 1)
                pe.wait_ge(gelu_done, s * 2 + h)
                for m in range(2):
                    for k in range(2):
                        last = pe.matmul(c.psum[:, m, 0:nt * P], w1T[:, k, m * P:(m + 1) * P], c.agg[:, k, columns(s, h)],
                                         start=(k == 0), stop=(k == 1))
                last.then_inc(g_pre, 1)

            def q_products(s, h):
                t0, nt = HALVES[h]
                pe.wait_ge(q_vec, s * (2 * QV) + (3 if h else 0))
                for m in range(2):
                    for k in range(2):
                        last = pe.matmul(c.psum[:, 2 + m, 0:nt * P], wqT[:, k, m * P:(m + 1) * P], c.xnT[:, k, columns(s, h)],
                                         start=(k == 0), stop=(k == 1))
                last.then_inc(q_pre, 1)

            def divisors(s, h):
                t0, nt = HALVES[h]
                pe.wait_ge(q_vec, s * (2 * QV) + h * QV + 2)
                for j in range(2):
                    last = pe.matmul(c.psum[:, 2 + j, 0:nt * P], c.small1[:, j * P:(j + 1) * P], qT[:, h, j, 0:nt * P],
                                     start=True, stop=True)
                last.then_inc(div_pre, 1)

            def node_rows(bank, lhs, h, w):
                t0, nt = HALVES[h]
                for t in range(nt):
                    for k in range(2):
                        last = pe.matmul(c.psum[:, bank + t // 2, (t % 2) * D:(t % 2 + 1) * D], lhs[:, h, k, t * P:(t + 1) * P],
                                         w[:, k, :], start=(k == 0), stop=(k == 1))
                return last

            def y_products(s, h, first):
                pe.wait_ge(gelu_done, s * 2 + h + 1)
                pe.wait_ge(y_read, s * 2 + h)
                if not (first and h == 0):
                    pe.wait_ge(gate_read, s * 2)
                node_rows(4, g1T, h, w2T).then_inc(y_pre, 1)

            def attention(s, h):
                pe.wait_ge(q_vec, s * (2 * QV) + h * QV + QV)
                pe.wait_ge(m_read, s * 2 + h)
                node_rows(6, qT, h, c.m0).then_inc(m_pre, 1)

            def turn_rows(s, h):
                t0, nt = HALVES[h]
                pe.wait_ge(vec, s * (2 * PER) + (h + 1) * PER)
                pe.wait_ge(y_read, s * 2 + 2)
                pe.wait_ge(gate_read, s * 2 + h)
                for k in range(2):
                    for t in range(nt):
                        last = pe.transpose(c.psum[:, 4 + k, t * P:(t + 1) * P], x2[:, h, t, k * P:(k + 1) * P], c.ident[:])
                last.then_inc(turned, 1)

            def gate_products(s, h):
                t0, nt = HALVES[h]
                pe.wait_ge(copied, s * 2 + h + 1)
                for t in range(nt):
                    for k in range(2):
                        last = pe.matmul(c.psum[:, 4, t * GATES:(t + 1) * GATES], xn4T[:, h, k, t * P:(t + 1) * P], gw[:, k, :],
                                         start=(k == 0), stop=(k == 1))
                last.then_inc(gate_pre, 1)

            def body(s, first):
                gelu_products(s, 0)
                q_products(s, 0)
                if not first:
                    turn_rows(s - 1, 1)
                gelu_products(s, 1)
                if not first:
                    gate_products(s - 1, 1)
                y_products(s, 0, first)
                divisors(s, 0)
                q_products(s, 1)
                attention(s, 0)
                y_products(s, 1, first)
                divisors(s, 1)
                turn_rows(s, 0)
                attention(s, 1)
                gate_products(s, 0)
            turns(pe, body)
            turn_rows(NS - 1, 1)
            gate_products(NS - 1, 1)
    c.constants.end(144)


GATES = 4
EH1, EH2 = 128, 64
SH1, SH2 = 256, 128


class LastWeights:

    def __init__(self, part):
        self.s1, self.s2, self.s3 = part.take([2, SH1]), part.take([2, SH2]), part.take([D])
        self.e1 = part.take([GATES, 2, EH1])
        self.e2 = part.take([GATES, P])
        self.e3 = part.take([GATES // 2, D])
        self.b3 = part.take([D])
        self.pick = part.take([GATES // 2, P])


def gates(c):
    nc = c.nc
    part = Carver(c.scr, SCR)
    w = c.last = LastWeights(part)
    G4 = [NT, GATES]
    rev, p, eq, cand, rest = part.take([GATES]), part.take(G4), part.take(G4), part.take(G4), part.take(G4)
    mask = [part.take(G4), part.take(G4)]
    top, code, weight = part.take([NT]), part.take([NT]), [part.take([NT]), part.take([NT])]
    second = part.take([NT])
    gate5 = part.take([NT, GATES + 1])
    logits = c.scores[:, :, 0:GATES]
    cleared, vec, act = c.sem("last_weights_cleared"), c.sem("gates_vec"), c.sem("gates_exp")
    turned, copied = c.sem("gates_turned"), c.sem("gates_copied")
    groups = -(-NT // 4)
    marks = {}
    n_loads = 3 + 2 * GATES + GATES // 2 + 2
    with nc.Block() as block:

        @block.sync
        def _(sp):
            inp = {n: c.inp["L1_ffn_" + n] for n in ("sW1", "sW2", "sW3", "eW1", "eW2", "eW3", "eb3", "sb3")}
            done = c.constants.sem
            sp.dma_start(w.s1, inp["sW1"].rearrange("(k p) n -> p k n", p=P)).then_inc(done, 16)
            sp.dma_start(w.s2, inp["sW2"].rearrange("(k p) n -> p k n", p=P)).then_inc(done, 16)
            sp.dma_start(w.s3, inp["sW3"]).then_inc(done, 16)
            for e in range(GATES):
                sp.dma_start(w.e1[:, e, :, :], inp["eW1"][e, :, :].rearrange("(k p) n -> p k n", p=P)).then_inc(done, 16)
            for q in range(GATES // 2):
                sp.dma_start(w.e3[:, q, :], inp["eW3"][2 * q:2 * q + 2, :, :].rearrange("e g o -> (e g) o")).then_inc(done, 16)
            sp.dma_start(w.b3[0:GATES, :], inp["eb3"]).then_inc(done, 16)
            sp.dma_start(w.b3[GATES:GATES + 1, :], inp["sb3"].unsqueeze(0)).then_inc(done, 16)
            sp.wait_ge(cleared, 1)
            for e in range(GATES):
                at = (e % 2) * EH2
                sp.dma_start(w.e2[:, e, at:at + EH2], inp["eW2"][e, :, :]).then_inc(done, 16)
            sp.wait_ge(done, c.constants.at(16 * n_loads))

        @block.vector
        def _(v):
            v.memset(w.e2, 0.0).then_inc(cleared, 1)
            for q in range(GATES // 2):
                for b in range(2):
                    e = 2 * q + b
                    v.tensor_copy(w.pick[0:GATES, q, b * EH2:(b + 1) * EH2],
                                  c.ident[0:GATES, e:e + 1].broadcast_to([GATES, EH2]))
            chain = Chain(v, vec)

            def do(ins):
                chain.done(ins)
                chain.wait()

            def over(x):
                return x.unsqueeze(2).broadcast_to([P, NT, GATES])
            rev_b = rev.unsqueeze(1).broadcast_to([P, NT, GATES])
            do(v.tensor_scalar(rev, c.iota[:, 0:GATES], -1.0, float(GATES), ALU.mult, ALU.add))
            do(v.tensor_reduce(top, logits, AX.X, ALU.max))
            do(v.tensor_tensor(p, logits, over(top), ALU.subtract))
            marks["shifted"] = chain.value()
            v.wait_ge(act, 1)
            do(v.tensor_reduce(top, p, AX.X, ALU.add))
            do(v.reciprocal(top, top))
            do(v.tensor_tensor(p, p, over(top), ALU.mult))
            for n, values in enumerate((p, rest)):
                best = (top, second)[n]
                do(v.tensor_reduce(best, values, AX.X, ALU.max))
                do(v.tensor_tensor(eq, values, over(best), ALU.is_equal))
                do(v.tensor_tensor(cand, eq, rev_b, ALU.mult))
                do(v.tensor_reduce(code, cand, AX.X, ALU.max))
                do(v.tensor_tensor(mask[n], rev_b, over(code), ALU.is_equal))
                if n == 0:
                    do(v.scalar_tensor_tensor(rest, mask[0], -2.0, p, ALU.mult, ALU.add))
            do(v.tensor_tensor(second, second, top, ALU.subtract))
            marks["second"] = chain.value()
            v.wait_ge(act, 2)
            do(v.tensor_scalar(top, second, 1.0, None, ALU.add))
            do(v.reciprocal(weight[0], top))
            do(v.tensor_tensor(weight[1], second, weight[0], ALU.mult))
            for n in range(2):
                do(v.tensor_tensor(mask[n], mask[n], over(weight[n]), ALU.mult))
            do(v.memset(gate5[:, :, GATES:GATES + 1], 1.0))
            do(v.tensor_tensor(gate5[:, :, 0:GATES], mask[0], mask[1], ALU.add))
            marks["gates"] = chain.value()

        @block.scalar
        def _(a):
            a.wait_ge(vec, marks["shifted"])
            a.activation(p, p, ACT.Exp).then_inc(act, 1)
            a.wait_ge(vec, marks["second"])
            a.activation(second, second, ACT.Exp).then_inc(act, 1)
            for q in range(groups):
                n = min(4, NT - 4 * q) * P
                a.wait_ge(turned, q + 1)
                a.activation(c.agg[0:GATES + 1, 2, q * 4 * P:q * 4 * P + n], c.psum[0:GATES + 1, q % 8, 0:n], ACT.Copy
                             ).then_inc(copied, 1)

        @block.tensor
        def _(pe):
            pe.wait_ge(vec, marks["gates"])
            for q in range(groups):
                if q >= 8:
                    pe.wait_ge(copied, q - 7)
                for t in range(min(4, NT - 4 * q)):
                    last = pe.transpose(c.psum[0:GATES + 1, q % 8, t * P:(t + 1) * P], gate5[:, 4 * q + t, :], c.ident[:])
                last.then_inc(turned, 1)
    c.constants.end(16 * n_loads)


def second_mixture(c):
    nc = c.nc
    part = Carver(c.scr, SCR)
    LastWeights(part)
    w = c.last
    s1, e1, e2 = part.take([2, 512]), part.take([GATES, 512]), part.take([2, 512])
    s2, e2w = part.take([2, 512]), part.take([2, 2, 512])
    gate = part.take([2, 512])
    rows = part.take([2, 4, D])
    pre, relu = c.sem("mixture_products"), c.sem("mixture_relu_done")
    gate_ready, spread, gated = c.sem("mixture_gates_copied"), c.sem("mixture_gates_spread"), c.sem("mixture_gated")
    out_pre, out_ready = c.sem("out_products"), c.sem("out_rows_ready")
    stored = [c.sem(f"out_stored{h}") for h in range(2)]
    K = 9
    G1 = GATES + 1

    def turns(engine, body):
        body(0, True, False)
        with engine.Fori(1, NS - 1) as s:
            body(s, False, False)
        body(NS - 1, False, True)

    def columns(s, h):
        t0, nt = HALVES[h]
        return ds(s * SS + t0 * P, nt * P)

    with nc.Block() as block:

        @block.sync
        def _(sp):
            def body(s, first, last):
                for h, (t0, nt) in enumerate(HALVES):
                    sp.wait_ge(out_ready, s * 2 + h + 1)
                    if last and h == 1:
                        r0 = (NS - 1) * SS + t0 * P
                        full = nt - 1
                        sp.dma_start(c.out[r0:r0 + full * P, :].rearrange("(t p) d -> p t d", p=P), rows[:, h, 0:full, :]
                                     ).then_inc(stored[h], 16)
                        sp.dma_start(c.out[r0 + full * P:N, :], rows[0:LAST, h, full, :]).then_inc(stored[h], 16)
                    else:
                        sp.dma_start(c.out[columns(s, h), :].rearrange("(t p) d -> p t d", p=P), rows[:, h, 0:nt, :]
                                     ).then_inc(stored[h], 16)
            turns(sp, body)
            sp.wait_ge(stored[0], 16 * NS)
            sp.wait_ge(stored[1], 16 * NS + 16)

        @block.scalar
        def _(a):
            def body(s, first, last):
                for h, (t0, nt) in enumerate(HALVES):
                    n, u = nt * P, s * 2 + h
                    if not first:
                        a.wait_ge(out_pre, u - 1)
                    a.activation(gate[0:G1, h, 0:n], c.agg[0:G1, 2, columns(s, h)], ACT.Copy).then_inc(gate_ready, 1)
                    outs = ([(s1[:, m, :], m, "L1_ffn_sb1", m) for m in range(2)] +
                            [(e1[:, e, :], (2, 3, 0, 1)[e], "L1_ffn_eb1", e) for e in range(GATES)] +
                            [(s2[:, h, :], 2, "L1_ffn_sb2", 0)] + [(e2[:, q, :], q, "L1_ffn_eb2", q) for q in range(2)])
                    for i, (to, bank, bias, j) in enumerate(outs):
                        a.wait_ge(pre, u * K + i + 1)
                        if bias == "L1_ffn_eb2":
                            a.wait_ge(gated, u)
                        a.activation(to[:, 0:n], c.psum[:, bank, 0:n], ACT.Relu, bias=c.column(bias, j)).then_inc(relu, 1)
            turns(a, body)

        @block.vector
        def _(v):
            def gate_rows(s, h):
                t0, nt = HALVES[h]
                u = s * 2 + h
                v.wait_ge(relu, (u + 1) * K)
                v.wait_ge(spread, u + 1)
                v.tensor_tensor(e2w[:, h, :, 0:nt * P], e2[:, :, 0:nt * P], c.psum[:, 4:6, 0:nt * P], ALU.mult
                                ).then_inc(gated, 1)

            def out_rows(s, h):
                t0, nt = HALVES[h]
                v.wait_ge(out_pre, s * 2 + h + 1)
                v.wait_ge(stored[h], s * 16)
                v.tensor_tensor(rows[:, h, 0:nt, :].rearrange("p t (k n) -> p t k n", n=P),
                                c.psum[:, 6:8, :].rearrange("p a b -> p (a b)")[:, 0:nt * D].rearrange(
                                    "p (t k n) -> p t k n", n=P, k=2),
                                c.agg[:, 0:2, columns(s, h)].rearrange("p k (t n) -> p t k n", n=P), ALU.add
                                ).then_inc(out_ready, 1)

            def body(s, first, last):
                if not first:
                    out_rows(s - 1, 1)
                gate_rows(s, 0)
                out_rows(s, 0)
                gate_rows(s, 1)
            turns(v, body)
            out_rows(NS - 1, 1)

        @block.tensor
        def _(pe):
            def hidden(s, h):
                t0, nt = HALVES[h]
                n, u = nt * P, s * 2 + h
                x = [c.xnT[:, k, columns(s, h)] for k in range(2)]
                pe.wait_ge(relu, u * K)
                for m in range(2):
                    for k in range(2):
                        last = pe.matmul(c.psum[:, m, 0:n], w.s1[:, k, m * P:(m + 1) * P], x[k], start=(k == 0), stop=(k == 1))
                    last.then_inc(pre, 1)
                for e in range(GATES):
                    if e >= 2:
                        pe.wait_ge(relu, u * K + e - 1)
                    for k in range(2):
                        last = pe.matmul(c.psum[:, (2, 3, 0, 1)[e], 0:n], w.e1[:, e, k, :], x[k], start=(k == 0), stop=(k == 1))
                    last.then_inc(pre, 1)

            def second(s, h):
                t0, nt = HALVES[h]
                n, u = nt * P, s * 2 + h
                pe.wait_ge(relu, u * K + 3)
                for k in range(2):
                    last = pe.matmul(c.psum[:, 2, 0:n], w.s2[:, k, :], s1[:, k, 0:n], start=(k == 0), stop=(k == 1))
                last.then_inc(pre, 1)
                pe.wait_ge(gate_ready, u + 1)
                pe.wait_ge(gated, u)
                for q in range(2):
                    last = pe.matmul(c.psum[:, 4 + q, 0:n], w.pick[0:GATES, q, :], gate[0:GATES, h, 0:n], start=True, stop=True)
                last.then_inc(spread, 1)
                for q in range(2):
                    pe.wait_ge(relu, u * K + 5 + q)
                    for b in range(2):
                        last = pe.matmul(c.psum[:, q, 0:n], w.e2[:, 2 * q + b, :], e1[:, 2 * q + b, 0:n],
                                         start=(b == 0), stop=(b == 1))
                    last.then_inc(pre, 1)

            def out_products(s, h):
                t0, nt = HALVES[h]
                u = s * 2 + h
                pe.wait_ge(gated, u + 1)
                pe.wait_ge(out_ready, u)
                for t in range(nt):
                    bank = c.psum[:, 6 + t // 2, (t % 2) * D:(t % 2 + 1) * D]
                    at = slice(t * P, (t + 1) * P)
                    pe.matmul(bank, s2[:, h, at], w.s3, start=True, stop=False)
                    for q in range(2):
                        pe.matmul(bank, e2w[:, h, q, at], w.e3[:, q, :], start=False, stop=False)
                    last = pe.matmul(bank, gate[0:G1, h, at], w.b3[0:G1, :], start=False, stop=True)
                last.then_inc(out_pre, 1)

            def body(s, first, last):
                hidden(s, 0)
                if not first:
                    out_products(s - 1, 1)
                second(s, 0)
                hidden(s, 1)
                out_products(s, 0)
                second(s, 1)
            turns(pe, body)
            out_products(NS - 1, 1)


PHASES = (turn_weights, prepare_edges, count_degrees, first_norm, gather_first, fold_attention, first_conv,
          gather_second, first_layer_sum, route, send_to_experts, experts, second_norm, gather_third,
          fold_second_attention, second_layer_sum, gates, second_mixture)


def build(nc, inputs, out):
    with ExitStack() as ctx:
        core = Core(nc, ctx, inputs, out)
        for phase in PHASES:
            phase(core)


def kernel(**inputs):
    import numpy as _np
    import concourse.bacc as _bacc
    from concourse import mybir as _mybir
    from concourse.bass_utils import run_bass_kernel_spmd as _run

    nc = _bacc.Bacc("TRN2", target_bir_lowering=False, num_devices=1)
    arrays = {name: _np.ascontiguousarray(a) for name, a in inputs.items()}
    dram = {name: nc.dram_tensor("in_" + name, a.shape, _mybir.dt.from_np(a.dtype), kind="ExternalInput").ap()
            for name, a in arrays.items()}
    out = nc.dram_tensor("out", arrays["x"].shape, _mybir.dt.float32, kind="ExternalOutput").ap()
    build(nc, dram, out)
    got = _run(nc, [{"in_" + name: a for name, a in arrays.items()}], core_ids=[0])
    return got.results[0]["out"]
```

```python
from contextlib import ExitStack

import concourse.bass as bass
from concourse import mybir

ALU = mybir.AluOpType
ACT = mybir.ActivationFunctionType
F32 = mybir.dt.float32
F16 = mybir.dt.float16
BF16 = mybir.dt.bfloat16
I32 = mybir.dt.int32
U32 = mybir.dt.uint32
AX = mybir.AxisListType
ds = bass.ds

P = 128
N = 6250
D = 256
E = 100000
NT = -(-N // P)
NP = NT * P
LAST = N - (NT - 1) * P
TS = 7
NS = NT // TS
SS = TS * P
HALVES = ((0, 4), (4, 3))
EPS = 1e-5

ET = 784
CT = 4
NC = ET // CT
RB = 7
RP = ET // RB
W = 128
RING = 4
NI = NC // RING

TURNED = (("L0_mix_Wqkv", 512, 1024, 256), ("L0_mix_Wout", 0, 256, 512), ("L0_gnn_W1", 0, 512, 256),
          ("L0_gnn_W2", 0, 256, 512), ("L1_gnn_W1", 0, 256, 256), ("L1_gnn_W2", 0, 256, 256),
          ("L1_mix_Wq", 0, 256, 256), ("L1_mix_Wk", 0, 256, 256), ("L1_mix_Wv", 256, 256, 256),
          ("L1_mix_Wproj", 0, 256, 256))
TURNED_AT = {}
NBLOCKS = 0
for _name, _r0, _rows, _cols in TURNED:
    TURNED_AT[_name] = NBLOCKS
    NBLOCKS += (_rows // P) * (_cols // P)


EXPERTS, HID = 8, 512
HM = HID // P
REGION = NP + P
MT = (2 * NP + EXPERTS * (P - 1)) // P
MT += MT % 2
XS, WS = 16.0, 1024.0

COLUMNS = (("L0_gnn_g1", 4), ("L0_gnn_b1", 4), ("L0_gnn_g2", 2), ("L0_gnn_b2", 2), ("L0_ffn_b1", 32),
           ("L1_gnn_b1", 2), ("L1_ffn_sb1", 2), ("L1_ffn_sb2", 1), ("L1_ffn_eb1", 4), ("L1_ffn_eb2", 2))
COLUMNS_AT = {}
NCOL = 0
for _name, _n in COLUMNS:
    COLUMNS_AT[_name] = (NCOL, _n)
    NCOL += _n


class Chain:

    def __init__(self, engine, sem, turn=0, per_turn=0, start=0):
        self.engine, self.sem, self.base, self.k = engine, sem, turn * per_turn + start, 0

    def done(self, instruction):
        instruction.then_inc(self.sem, 1)
        self.k += 1
        return instruction

    def value(self):
        return self.base + self.k

    def wait(self):
        self.engine.wait_ge(self.sem, self.value())


class Shared:

    def __init__(self, sem):
        self.sem, self.base = sem, 0

    def at(self, n):
        return self.base + n

    def end(self, n):
        self.base += n


class Carver:

    def __init__(self, region, words):
        self.region, self.words, self.at = region, words, 0

    def take(self, shape, dtype=F32):
        n = 1
        for s in shape:
            n *= s
        size = {F32: 4, I32: 4, U32: 4, BF16: 2, F16: 2}[dtype]
        words = -(-n * size // 4)
        assert self.at + words <= self.words, (self.at, words, self.words)
        view = self.region[:, self.at:self.at + words]
        self.at += words
        if dtype is not F32:
            view = view.bitcast(dtype)
        if len(shape) == 2:
            view = view.rearrange("p (a b) -> p a b", b=shape[1])
        elif len(shape) == 3:
            view = view.rearrange("p (a b c) -> p a b c", b=shape[1], c=shape[2])
        elif len(shape) == 4:
            view = view.rearrange("p (a b c d) -> p a b c d", b=shape[1], c=shape[2], d=shape[3])
        return view


class Core:

    def __init__(self, nc, ctx, inputs, out):
        self.nc, self.ctx, self.inp, self.out = nc, ctx, inputs, out

        def dram(name, shape):
            return nc.dram_tensor(name, shape, F32, kind="Internal").ap()

        self.turned = dram("turned_weights", (P, NBLOCKS * P))
        self.xn_tab = dram("xn_table", (NP, D))
        self.h_tab = dram("h_table", (NP, D))
        self.xn3_tab = dram("xn3_table", (NP, D))
        self.dis_row = dram("dis_row", (1, NP))
        self.wsum_row = dram("wsum_row", (1, NP))
        self.xn2_tab = dram("xn2_table", (NP, D))
        self.slot_x = dram("expert_rows", (EXPERTS * REGION, D))
        self.slot_y = dram("expert_results", (MT * P, D))
        self.x1_tab = dram("x1_table", (NP, D))
        self.x2_tab = dram("x2_table", (NP, D))
        self.xnT = self.sb("xnT", [P, 2, NP], F32)
        self.agg = self.sb("agg", [P, 3, NP], F32)
        self.scr = self.sb("scr", [P, SCR], F32)
        self.ident = self.sb("ident", [P, P], F32)
        self.ones = self.sb("ones", [P, P], F32)
        self.zeros = self.sb("zeros", [P, P], F32)
        self.iota = self.sb("iota", [P, W], F32)
        self.src = self.sb("src_i", [P, ET], I32)
        self.dloc = self.sb("dloc", [P, ET + CT], F32)
        self.w = self.sb("w_edge", [P, ET], F32)
        self.base = self.sb("base", [P, NC], F32)
        self.base_i = self.sb("base_i", [P, NC], I32)
        self.flag_i = self.sb("flag_i", [P, 1], I32)
        self.dis = self.sb("dis_node", [P, NT], F32)
        self.m0 = self.sb("m0", [P, 2, D], F32)
        self.idx = self.sb("index_columns", [P, RING, CT], I32)
        self.w_stat = self.sb("weight_columns", [P, RING, CT], F32)
        self.dst_now = self.sb("slow_destinations_now", [P, CT], F32)
        self.ones16 = self.sb("ones16", [P, P], BF16)
        self.iota16 = self.sb("iota16", [P, W], BF16)
        self.x_all = self.scr[:, SCR - NT * D:SCR].rearrange("p (t d) -> p t d", d=D)
        self.cols = self.sb("feature_columns", [P, NCOL], F32)
        self.scores = self.sb("expert_scores", [P, NT, EXPERTS], F32)
        self.scatter_to = self.sb("expert_row_of_node", [P, 2, NT], I32)
        self.result_at = self.sb("result_row_of_node", [P, 2, NT], I32)
        self.pad_to = self.sb("expert_pad_rows", [P, EXPERTS], I32)
        self.tile_expert = self.sb("expert_of_tile", [P, MT], I32)
        self.tile_row = self.sb("first_row_of_tile", [P, MT], I32)
        self.bd64 = self.sb("diagonal_blocks64", [P, P], F32)
        self.bd32 = self.sb("diagonal_blocks32", [P, P], F32)
        self.small1 = self.sb("small1", [P, 256], F32)
        self.psum = ctx.enter_context(nc.psum_tensor("psum", [P, 8, 512], F32))
        self.constants = Shared(self.sem("constants_loaded"))
        self.passed = self.sem("wait_passed")
        self.agg_sems = {}
        self.agg_at = {"fast": {}, "slow": {}}

    def sb(self, name, shape, dtype):
        return self.ctx.enter_context(self.nc.sbuf_tensor(name, shape, dtype))

    def sem(self, name):
        return self.ctx.enter_context(self.nc.semaphore(name))

    def agg_sem(self, name):
        if name not in self.agg_sems:
            self.agg_sems[name] = self.sem(name)
            for counts in self.agg_at.values():
                counts[name] = 0
        return self.agg_sems[name]

    def column(self, name, j=0):
        at, n = COLUMNS_AT[name]
        return self.cols[:, at + j:at + j + 1]

    def columns(self, name):
        at, n = COLUMNS_AT[name]
        return self.cols[:, at:at + n]

    def turned_part(self, name, cols):
        at = TURNED_AT[name] * P
        return self.turned[:, at:at + cols]


SCR = 16384


def turn_weights(c):
    nc = c.nc
    agg = c.agg.rearrange("p a b -> p (a b)")
    col_rows = agg[:, NBLOCKS * P:NBLOCKS * P + P]
    natural = agg[:, 0:NBLOCKS * P].rearrange("p (b n) -> p b n", n=P)
    turned = c.scr[:, 0:NBLOCKS * P]
    loaded, const = c.constants.sem, c.sem("weights_const")
    turn, copied_v, copied_a = c.sem("weights_turned"), c.sem("weights_copied_v"), c.sem("weights_copied_a")
    stored, masks = c.sem("weights_stored"), c.sem("masks_cleared")
    groups = NBLOCKS // 4
    n_loads = sum(cols // P for _, _, _, cols in TURNED) + len(COLUMNS)
    sources = {"L1_mix_Wk": "L1_mix_Wkv", "L1_mix_Wv": "L1_mix_Wkv"}
    with nc.Block() as block:

        @block.sync
        def _(sp):
            for name, r0, rows, cols in TURNED:
                w = c.inp[sources.get(name, name)]
                nro = rows // P
                for ci in range(cols // P):
                    at = TURNED_AT[name] + ci * nro
                    sp.dma_start(natural[:, at:at + nro, :],
                                 w[r0:r0 + rows, ci * P:(ci + 1) * P].rearrange("(r p) n -> p r n", p=P)
                                 ).then_inc(loaded, 16)
            for name, n in COLUMNS:
                at = COLUMNS_AT[name][0]
                w = c.inp[name]
                flat = w.rearrange("e n -> (e n)") if len(w.shape) == 2 else w
                sp.dma_start(col_rows[at:at + n, :], flat.rearrange("(r n) -> r n", n=P)).then_inc(loaded, 16)
            sp.wait_ge(copied_v, groups // 2)
            sp.wait_ge(copied_a, groups // 2)
            sp.dma_start(c.turned, turned).then_inc(stored, 16)
            sp.wait_ge(stored, 16)

        @block.gpsimd
        def _(g):
            g.memset(c.ident[:], 0.0).then_inc(const, 1)
            g.iota(c.iota[:], pattern=[[1, W]], base=0, channel_multiplier=0,
                   allow_small_or_imprecise_dtypes=True).then_inc(const, 1)
            g.memset(c.ones[:], 1.0).then_inc(const, 1)
            g.wait_ge(const, 3)
            g.affine_select(out=c.ident[:], in_=c.ident[:], compare_op=ALU.not_equal, fill=1.0, base=0,
                            pattern=[[-1, P]], channel_multiplier=1).then_inc(const, 1)

        @block.tensor
        def _(pe):
            pe.wait_ge(const, 4)
            pe.wait_ge(loaded, c.constants.at(16 * n_loads))
            for q in range(groups):
                if q >= 4:
                    pe.wait_ge((copied_v, copied_a)[q % 2], (q - 4) // 2 + 1)
                for b in range(4):
                    last = pe.transpose(c.psum[:, q % 4, b * P:(b + 1) * P], natural[:, 4 * q + b, :], c.ident[:])
                last.then_inc(turn, 1)
            pe.transpose(c.psum[:, 4, 0:NCOL], col_rows[0:NCOL, :], c.ident[0:NCOL, 0:NCOL]).then_inc(turn, 1)

        @block.vector
        def _(v):
            for m, size in ((c.bd64, 64), (c.bd32, 32)):
                v.memset(m[:], 0.0).then_inc(masks, 1)
            v.wait_ge(masks, 2)
            for m, size in ((c.bd64, 64), (c.bd32, 32)):
                for j in range(0, P, size):
                    v.memset(m[j:j + size, j:j + size], 1.0)
            for q in range(0, groups, 2):
                v.wait_ge(turn, q + 1)
                v.tensor_copy(turned[:, q * 512:(q + 1) * 512], c.psum[:, q % 4, :]).then_inc(copied_v, 1)
            v.wait_ge(turn, groups + 1)
            v.tensor_copy(c.cols[:], c.psum[:, 4, 0:NCOL])

        @block.scalar
        def _(a):
            for q in range(1, groups, 2):
                a.wait_ge(turn, q + 1)
                a.activation(turned[:, q * 512:(q + 1) * 512], c.psum[:, q % 4, :], ACT.Copy).then_inc(copied_a, 1)
    c.constants.end(16 * n_loads)


def prepare_edges(c):
    nc = c.nc
    part = Carver(c.agg.rearrange("p a b -> p (a b)"), 2 * NP)
    rows = ET // RB
    full = E // P - (RB - 1) * RP
    rest = E % P
    dst_r, src_r = part.take([RB, P], I32), part.take([RB, P], I32)
    att_r = part.take([RB, P * 3])
    att_v = att_r.rearrange("p b (j f) -> p b j f", f=3)
    lists = part.take([3, RB * P])
    norm = part.take([RB, P])
    dstT = part.take([ET])
    ends = part.take([2, NC])
    ends_all = part.take([2, NC])
    spread, flag = part.take([NC]), part.take([1])
    fill, loaded, x_loaded = c.sem("edges_filled"), c.constants.sem, c.sem("x_loaded")
    vec, root, turn, most = c.sem("edges_vec"), c.sem("edges_root"), c.sem("edges_turned"), c.sem("edges_most")
    n_dst = (RB - 1) * RP * P
    with nc.Block() as block:

        @block.sync
        def _(sp):
            sp.wait_ge(fill, 3)
            for r, source in ((dst_r, c.inp["dst"]), (src_r, c.inp["src"])):
                sp.dma_start(r[0:RP, 0:RB - 1, :], source[0:n_dst].rearrange("(b p j) -> p b j", p=RP, j=P)
                             ).then_inc(loaded, 16)
                sp.dma_start(r[0:full, RB - 1, :], source[n_dst:E - rest].rearrange("(p j) -> p j", j=P)
                             ).then_inc(loaded, 16)
                sp.dma_start(r[full:full + 1, RB - 1, 0:rest], source[E - rest:E].rearrange("(p j) -> p j", p=1)
                             ).then_inc(loaded, 16)

        @block.scalar
        def _(a):
            att = c.inp["edge_attr_3"]
            a.wait_ge(fill, 3)
            a.dma_start(att_r[0:RP, 0:RB - 1, :],
                        att[0:n_dst, :].rearrange("(b p j) f -> p b (j f)", p=RP, j=P)).then_inc(loaded, 16)
            a.dma_start(att_r[0:full, RB - 1, :],
                        att[n_dst:E - rest, :].rearrange("(p j) f -> p (j f)", j=P)).then_inc(loaded, 16)
            a.dma_start(att_r[full:full + 1, RB - 1, 0:rest * 3],
                        att[E - rest:E, :].rearrange("(p j) f -> p (j f)", p=1)).then_inc(loaded, 16)
            x, whole = c.inp["x"], (NT - 1) * P
            a.dma_start(c.x_all[:, 0:NT - 1, :], x[0:whole, :].rearrange("(t p) d -> p t d", p=P)).then_inc(x_loaded, 16)
            a.wait_ge(fill, 4)
            a.dma_start(c.x_all[0:LAST, NT - 1, :], x[whole:N, :]).then_inc(x_loaded, 16)
            a.wait_ge(vec, 4)
            a.activation(norm[0:RP], norm[0:RP], ACT.Sqrt).then_inc(root, 1)
            a.wait_ge(root, 1)
            a.activation(norm[0:RP], norm[0:RP], ACT.Exp, scale=-4.0).then_inc(root, 1)
            a.wait_ge(x_loaded, 32)

        @block.vector
        def _(v):
            v.memset(dst_r[0:RP, RB - 1, :], N).then_inc(fill, 1)
            v.memset(src_r[0:RP, RB - 1, :], 0).then_inc(fill, 1)
            v.memset(att_r[0:RP, RB - 1, :], 0.0).then_inc(fill, 1)
            v.memset(c.x_all[:, NT - 1, :], 0.0).then_inc(fill, 1)
            v.memset(c.agg[:, 2, :], 0.0)
            v.memset(c.zeros[:], 0.0)
            v.memset(c.ones16[:], 1.0)
            v.tensor_copy(c.iota16[:], c.iota[:])
            step = Chain(v, vec)
            v.wait_ge(loaded, c.constants.at(9 * 16))
            step.done(v.tensor_tensor(att_r[0:RP], att_r[0:RP], att_r[0:RP], ALU.mult))
            step.done(v.tensor_copy(lists[0:RP, 0, :], dst_r[0:RP].rearrange("p b j -> p (b j)")))
            step.wait()
            step.done(v.tensor_reduce(norm[0:RP], att_v[0:RP], AX.X, ALU.add))
            step.wait()
            step.done(v.tensor_scalar(norm[0:RP], norm[0:RP], 1e-12, None, ALU.add))
            step.done(v.tensor_copy(lists[0:RP, 1, :], src_r[0:RP].rearrange("p b j -> p (b j)")))
            v.wait_ge(root, 2)
            step.done(v.tensor_scalar(lists[0:RP, 2, :], norm[0:RP].rearrange("p b j -> p (b j)"), 0.0, None, ALU.max))
            for n, target in enumerate((dstT, c.src, c.w)):
                v.wait_ge(turn, n + 1)
                step.done(v.tensor_copy(target[:, 0:4 * RP], c.psum[:, 2 * n, 0:4 * RP]))
                step.done(v.tensor_copy(target[:, 4 * RP:ET], c.psum[:, 2 * n + 1, 0:3 * RP]))
            step.wait()
            chunks = dstT.rearrange("p (c t) -> p c t", t=CT)
            step.done(v.tensor_reduce(ends[:, 0, :], chunks, AX.X, ALU.min, negate=True))
            step.done(v.tensor_reduce(ends[:, 1, :], chunks, AX.X, ALU.max))
            v.wait_ge(most, 1)
            step.done(v.tensor_scalar(c.base[:], ends_all[:, 0, :], float(W - NP), -1.0, ALU.max, ALU.mult))
            step.done(v.memset(c.dloc[:, ET:ET + CT], -1.0))
            step.wait()
            step.done(v.tensor_copy(c.base_i[:], c.base[:]))
            step.done(v.tensor_tensor(c.dloc[:, 0:ET].rearrange("p (c t) -> p c t", t=CT), chunks,
                                      c.base[:].unsqueeze(2).broadcast_to([P, NC, CT]), ALU.subtract))
            step.done(v.tensor_tensor(spread, ends_all[:, 1, :], c.base[:], ALU.subtract))
            step.wait()
            step.done(v.tensor_reduce(flag, spread, AX.X, ALU.max))
            step.wait()
            step.done(v.tensor_scalar(c.flag_i[:], flag, float(W), None, ALU.is_ge))

        @block.tensor
        def _(pe):
            for n, ready in enumerate((2, 5, 6)):
                pe.wait_ge(vec, ready)
                for b in range(RB):
                    out = c.psum[:, 2 * n + b // 4, (b % 4) * RP:(b % 4 + 1) * RP]
                    last = pe.transpose(out, lists[0:RP, n, b * P:(b + 1) * P], c.ident[0:RP, 0:RP])
                last.then_inc(turn, 1)

        @block.gpsimd
        def _(g):
            g.wait_ge(vec, 14)
            g.partition_all_reduce(ends_all.rearrange("p a b -> p (a b)"), ends.rearrange("p a b -> p (a b)"), P,
                                   bass.bass_isa.ReduceOp.max).then_inc(most, 1)
    c.constants.end(9 * 16)


def aggregate(c, table=None, weighted=False, slots=(), side=None):
    nc = c.nc
    gathers = table is not None
    part = Carver(c.scr, SCR)
    hot = part.take([2, CT, W], F32 if gathers else BF16)
    rows = part.take([RING, CT, D]) if gathers else None
    iota = c.iota if gathers else c.iota16
    S = c.agg_sem
    hot_ready, summed, added = S("onehot_ready"), S("chunk_summed"), S("window_added")
    idx_ready, begun, now_ready = S("indices_ready"), c.passed, S("slow_destinations_ready")
    landed = [S(f"rows_landed{u}") for u in range(RING)]
    lo, nslot = (0 if 0 in slots else 2), len(slots)
    acc = c.agg[:, lo:lo + nslot, :]
    bank = [c.psum[:, b, 0:nslot * W].rearrange("p (s w) -> p s w", w=W) for b in range(2)]
    flag = c.flag_i[0:1, 0:1]
    side = side or {}

    class Values:

        def __init__(self, way):
            self.at = dict(c.agg_at[way])

        def hot(self, n):
            return self.at["onehot_ready"] + n

        def summed(self, n):
            return self.at["chunk_summed"] + RING + n

        def added(self, n):
            return self.at["window_added"] + 2 + n

        def idx(self, n):
            return self.at["indices_ready"] + n

        def now(self, n):
            return self.at["slow_destinations_ready"] + n

        def landed(self, u, n):
            return self.at[f"rows_landed{u}"] + 16 * CT * n

    fast, slow = Values("fast"), Values("slow")

    def products(pe, b, u, hot_b):
        for s, what in enumerate(slots):
            for t in range(CT):
                if what == "count":
                    lhs = c.ones16[:]
                elif what == "weight":
                    lhs = c.w_stat[:, u, t:t + 1].broadcast_to([P, P])
                else:
                    lhs = rows[:, u, t, what * P:(what + 1) * P]
                last = pe.matmul(bank[b][:, s, :], lhs, hot[:, hot_b, t, :], start=(t == 0), stop=(t == CT - 1))
        return last

    def run_side(engine_name, *args):
        if engine_name in side:
            side[engine_name](*args)

    def side_alone(engine, names):
        if any(n in side for n in names):
            def turn(i, last):
                for n in names:
                    if n == "vector":
                        for u in range(RING):
                            side[n](engine, i, last, u)
                    else:
                        run_side(n, engine, i, last)
            with engine.Fori(0, NI - 1) as i:
                turn(i, False)
            turn(NI - 1, True)

    with nc.Block() as block:

        @block.vector
        def _(v):
            v.sem_inc(added, 2)
            is_slow = v.value_load(flag, min_val=0, max_val=1)

            def onehots(tiles, b, dst):
                for t in range(CT):
                    if weighted:
                        last = v.tensor_scalar(hot[:, b, t, :], iota[:], dst(t), c.w[:, ds(tiles + t, 1)],
                                               ALU.is_equal, ALU.mult)
                    else:
                        last = v.tensor_scalar(hot[:, b, t, :], iota[:], dst(t), None, ALU.is_equal)
                last.then_inc(hot_ready, 1)

            def indices(ch, u):
                if gathers:
                    if "weight" in slots:
                        v.tensor_copy(c.w_stat[:, u, :], c.w[:, ds(ch * CT, CT)])
                    v.tensor_copy(c.idx[:, u, :], c.src[:, ds(ch * CT, CT)]).then_inc(idx_ready, 1)

            with v.If(is_slow < 1):
                for ch in range(RING - 1):
                    indices(ch, ch)
                onehots(0, 0, lambda t: c.dloc[:, t:t + 1])

                def turn(i, last):
                    _, firsts = nc.values_load_multi_w_load_instructions(c.base_i[0:1, ds(i * RING, RING)],
                                                                         engines=[v.engine], min_val=0, max_val=NP - W)
                    for u in range(RING):
                        ch = i * RING + u
                        v.wait_ge(summed, fast.summed(ch))
                        if not (last and u == RING - 1):
                            onehots((ch + 1) * CT, (u + 1) % 2, lambda t: c.dloc[:, ds((ch + 1) * CT + t, 1)])
                        if not (last and u > 0):
                            indices(ch + RING - 1, (u + RING - 1) % RING)
                        if "vector" in side:
                            side["vector"](v, i, last, u)
                        v.wait_ge(summed, fast.summed(ch + 1))
                        v.wait_ge(added, fast.added(ch))
                        window = acc[:, :, ds(firsts[u], W)]
                        v.tensor_tensor(window, window, bank[u % 2], ALU.add).then_inc(added, 1)
                with v.Fori(0, NI - 1) as i:
                    turn(i, False)
                turn(NI - 1, True)
            with v.Else():
                side_alone(v, ["vector"])
                with v.Fori(0, NC) as ch:
                    v.wait_ge(summed, slow.summed(ch * NT))
                    indices(ch, 0)
                    v.wait_ge(now_ready, slow.now(ch * (NT + 1)))
                    v.tensor_scalar(c.dst_now[:], c.dloc[:, ds(ch * CT, CT)], c.base[:, ds(ch, 1)], None, ALU.add
                                    ).then_inc(now_ready, 1)
                    with v.Fori(0, NT) as win:
                        n = ch * NT + win
                        v.wait_ge(now_ready, slow.now(ch * (NT + 1) + win + 1))
                        v.wait_ge(summed, slow.summed(n))
                        onehots(ch * CT, 0, lambda t: c.dst_now[:, t:t + 1])
                        v.tensor_scalar(c.dst_now[:], c.dst_now[:], float(-W), None, ALU.add).then_inc(now_ready, 1)
                        v.wait_ge(summed, slow.summed(n + 1))
                        v.wait_ge(added, slow.added(n))
                        window = acc[:, :, ds(win * W, W)]
                        v.tensor_tensor(window, window, bank[0], ALU.add).then_inc(added, 1)

        @block.tensor
        def _(pe):
            pe.sem_inc(summed, RING)
            if "tensor_first" in side:
                side["tensor_first"](pe)
            is_slow = pe.value_load(flag, min_val=0, max_val=1)
            with pe.If(is_slow < 1):
                def turn(i, last):
                    run_side("tensor_begin", pe, i, last)
                    for u in range(RING):
                        ch = i * RING + u
                        pe.wait_ge(hot_ready, fast.hot(ch + 1))
                        if gathers:
                            pe.wait_ge(landed[u], fast.landed(u, i + 1))
                        if "weight" in slots:
                            pe.wait_ge(idx_ready, fast.idx(ch + 1))
                        pe.wait_ge(added, fast.added(ch - 1))
                        products(pe, u % 2, u, u % 2).then_inc(summed, 1)
                    run_side("tensor_end", pe, i, last)
                with pe.Fori(0, NI - 1) as i:
                    turn(i, False)
                turn(NI - 1, True)
            with pe.Else():
                side_alone(pe, [n for n in ("tensor_begin", "tensor_end") if n in side])
                with pe.Fori(0, NC) as ch:
                    with pe.Fori(0, NT) as win:
                        pe.wait_ge(hot_ready, slow.hot(ch * NT + win + 1))
                        if gathers:
                            pe.wait_ge(landed[0], slow.landed(0, ch + 1))
                        if "weight" in slots:
                            pe.wait_ge(idx_ready, slow.idx(ch + 1))
                        pe.wait_ge(added, slow.added(ch * NT + win))
                        products(pe, 0, 0, 0).then_inc(summed, 1)

        if gathers:
            @block.gpsimd
            def _(g):
                is_slow = g.value_load(flag, min_val=0, max_val=1)

                def gather(u, value):
                    g.wait_ge(idx_ready, value)
                    g.sem_inc(begun, 1)
                    for t in range(CT):
                        g.indirect_dma_start(out=rows[:, u, t, :], out_offset=None, in_=table,
                                             in_offset=bass.IndirectOffsetOnAxis(ap=c.idx[:, u, t:t + 1], axis=0)
                                             ).then_inc(landed[u], 16)

                with g.If(is_slow < 1):
                    with g.Fori(0, NI) as i:
                        for u in range(RING):
                            gather(u, fast.idx(i * RING + u + 1))
                with g.Else():
                    with g.Fori(0, NC) as ch:
                        gather(0, slow.idx(ch + 1))

        if "gpsimd" in side:
            @block.gpsimd
            def _(g):
                with g.Fori(0, NI) as i:
                    side["gpsimd"](g, i, False)

        if "scalar" in side:
            @block.scalar
            def _(a):
                with a.Fori(0, NI - 1) as i:
                    side["scalar"](a, i, False)
                side["scalar"](a, NI - 1, True)

        @block.sync
        def _(sp):
            if "sync_first" in side:
                side["sync_first"](sp)
            if "sync" in side:
                with sp.Fori(0, NI - 1) as i:
                    side["sync"](sp, i, False)
                side["sync"](sp, NI - 1, True)

    windows = {"fast": NC, "slow": NC * NT}
    for way, counts in c.agg_at.items():
        counts["onehot_ready"] += windows[way]
        counts["chunk_summed"] += windows[way] + RING
        counts["window_added"] += windows[way] + 2
        if way == "slow":
            counts["slow_destinations_ready"] += NC * (NT + 1)
        if gathers:
            counts["indices_ready"] += NC
            for u in range(RING):
                counts[f"rows_landed{u}"] += 16 * CT * (NC if way == "slow" and u == 0 else
                                                        0 if way == "slow" else NI)


def count_degrees(c):
    part = Carver(c.scr, SCR - NT * D)
    part.at = 2 * CT * W // 2
    xn = part.take([D])
    stats, moments, rstd = c.small1[:, 0:6], c.small1[:, 6:8], c.small1[:, 8:9]
    vec, root, turned = c.sem("norm1_vec"), c.sem("norm1_root"), c.sem("norm1_turned")
    copied, moved = c.sem("norm1_xnT_copied"), c.sem("norm1_xn_moved")
    PER = 5

    def vector(v, i, last, u):
        step = Chain(v, vec, i, PER)
        x = c.x_all[:, ds(i, 1), :].rearrange("p t d -> p (t d)")
        if u == 0:
            step.wait()
            step.done(v.bn_stats(stats, x))
        if u == 1:
            step.k = 1
            step.wait()
            v.sem_inc(c.passed, 1)
            step.done(v.bn_aggr(moments, stats))
            step.wait()
            step.done(v.tensor_scalar(rstd, moments[:, 1:2], EPS, None, ALU.add))
        if u == 2:
            step.k = 3
            v.wait_ge(root, i + 1)
            step.done(v.reciprocal(rstd, rstd))
        if u == 3:
            step.k = 4
            step.wait()
            v.wait_ge(turned, i)
            v.wait_ge(moved, i)
            step.done(v.tensor_scalar(xn, x, moments[:, 0:1], rstd, ALU.subtract, ALU.mult))

    def scalar(a, i, last):
        a.wait_ge(vec, i * PER + 3)
        a.activation(rstd, rstd, ACT.Sqrt).then_inc(root, 1)
        a.wait_ge(turned, i + 1)
        a.activation(c.xnT[:, :, ds(i * P, P)], c.psum[:, 3, 0:D].rearrange("p (k n) -> p k n", n=P), ACT.Copy
                     ).then_inc(copied, 1)

    def tensor(pe, i, last):
        pe.wait_ge(vec, (i + 1) * PER)
        pe.wait_ge(copied, i)
        for k in range(2):
            ins = pe.transpose(c.psum[:, 3, k * P:(k + 1) * P], xn[:, k * P:(k + 1) * P], c.ident[:])
        ins.then_inc(turned, 1)

    def gpsimd(g, i, last):
        g.wait_ge(vec, (i + 1) * PER)
        g.sem_inc(c.passed, 1)
        g.tensor_copy(c.x_all[:, ds(i, 1), :].rearrange("p t d -> p (t d)"), xn).then_inc(moved, 1)

    aggregate(c, slots=("count",), side=dict(vector=vector, scalar=scalar, tensor_end=tensor, gpsimd=gpsimd))


def scale_by_degrees(c):
    nc = c.nc
    part = Carver(c.scr, SCR - NT * D)
    dis49 = part.take([P])[0:NT, :]
    row, own, wide = c.sem("dis_row_moved"), c.sem("dis_steps"), c.constants.sem
    stored, scaled_a, scaled_v = c.sem("xn_table_stored"), c.sem("xn_scaled_a"), c.sem("xn_scaled_v")
    by_tile = c.dis_row.rearrange("a (t n) -> (a t) n", n=P)
    table = c.xn_tab.rearrange("(t p) d -> p t d", p=P)
    PIECES = ((0, 14), (14, 28), (28, 39), (39, NT))
    with nc.Block() as block:

        @block.sync
        def _(sp):
            sp.dma_start(c.dis_row, c.agg[0:1, 2, :]).then_inc(row, 16)
            sp.wait_ge(row, 16)
            sp.dma_start(dis49, by_tile).then_inc(row, 16)
            sp.wait_ge(own, 3)
            sp.dma_start(by_tile, dis49).then_inc(row, 16)
            sp.wait_ge(row, 48)
            sp.dma_start(c.agg[:, 2, :], c.dis_row.partition_broadcast(P)).then_inc(wide, 16)
            for n, (a, b) in enumerate(PIECES):
                sp.wait_ge(scaled_v if n < 2 else scaled_a, n % 2 + 1)
                sp.dma_start(table[:, a:b, :], c.x_all[:, a:b, :]).then_inc(stored, 16)
            sp.wait_ge(stored, 16 * len(PIECES))

        @block.vector
        def _(v):
            v.wait_ge(row, 32)
            v.tensor_scalar(dis49, dis49, 1.0, None, ALU.add).then_inc(own, 1)
            v.wait_ge(own, 2)
            v.reciprocal(dis49, dis49).then_inc(own, 1)
            v.wait_ge(own, 4)
            v.tensor_copy(c.dis[:], c.psum[:, 7, 0:NT]).then_inc(own, 1)
            v.wait_ge(own, 5)
            for a, b in PIECES[:2]:
                v.tensor_tensor(c.x_all[:, a:b, :], c.x_all[:, a:b, :], c.dis[:, a:b].unsqueeze(2).broadcast_to([P, b - a, D]),
                                ALU.mult).then_inc(scaled_v, 1)
            v.wait_ge(wide, c.constants.at(16))
            for k in range(2):
                v.tensor_tensor(c.agg[:, k, :], c.xnT[:, k, :], c.agg[:, 2, :], ALU.mult)

        @block.scalar
        def _(s):
            s.wait_ge(own, 1)
            s.activation(dis49, dis49, ACT.Sqrt).then_inc(own, 1)
            s.wait_ge(own, 5)
            for a, b in PIECES[2:]:
                for t in range(a, b):
                    last = s.activation(c.x_all[:, t, :], c.x_all[:, t, :], ACT.Copy, scale=c.dis[:, t:t + 1])
                last.then_inc(scaled_a, 1)

        @block.tensor
        def _(pe):
            pe.wait_ge(own, 3)
            pe.transpose(c.psum[:, 7, 0:NT], dis49, c.ident[0:NT, 0:NT]).then_inc(own, 1)
    c.constants.end(16)


HEADS0, DH0 = 8, 64
PAIRS = HEADS0 // 2


def gather_first(c):
    part = Carver(c.scr, SCR)
    part.at = (2 * CT * W) + RING * CT * D
    wkv = part.take([2, 2 * HEADS0 * DH0])
    tile = part.take([2, P])
    G = 2 * HEADS0
    cen, sq, kv = part.take([G, DH0]), part.take([G, DH0]), part.take([G, DH0])
    mean, var = part.take([G]), part.take([G])
    flat = "p a b -> p (a b)"
    w_loaded, tile_ready, kv_ready = c.constants.sem, c.sem("kv_tile_ready"), c.sem("kv_ready")
    vec, act, dots = c.sem("kv_vec"), c.sem("kv_act"), c.sem("dots_done")
    both = c.psum[:, 2:4, :].rearrange("p a b -> p (a b)").rearrange("p (g d) -> p g d", d=DH0)
    sums = c.psum[:, 4, :]
    PER = 7

    def first(pe):
        pe.matmul(sums, c.zeros[:], c.ones[:, 0:1].broadcast_to([P, 512]), start=True, stop=False,
                  skip_group_check=True)
        pe.wait_ge(w_loaded, c.constants.at(16))

    def products_begin(pe, i, last):
        pe.wait_ge(tile_ready, i + 1)
        pe.wait_ge(vec, i * PER)
        for half in range(2):
            for k in range(2):
                ins = pe.matmul(c.psum[:, 2 + half, :], tile[:, k, :], wkv[:, k, half * 512:(half + 1) * 512],
                                start=(k == 0), stop=(k == 1))
        ins.then_inc(kv_ready, 1)

    def products_end(pe, i, last):
        pe.wait_ge(vec, (i + 1) * PER)
        for q in range(PAIRS):
            ins = pe.matmul(sums[:, q * P:(q + 1) * P],
                            kv.rearrange(flat)[:, 512 + q * P:512 + (q + 1) * P],
                            kv.rearrange(flat)[:, q * P:(q + 1) * P], start=False, stop=last,
                            skip_group_check=True)
        ins.then_inc(dots, 1)

    def vector(v, i, last, u):
        if u == 0:
            return
        step = Chain(v, vec, i, PER)
        if u == 1:
            v.wait_ge(kv_ready, i + 1)
            step.done(v.tensor_reduce(mean, both, AX.X, ALU.add))
            step.wait()
            step.done(v.tensor_scalar(mean, mean, 1.0 / DH0, None, ALU.mult))
            step.wait()
            v.wait_ge(act, i * 3)
            step.done(v.tensor_tensor(cen, both, mean.unsqueeze(2).broadcast_to([P, G, DH0]), ALU.subtract))
        if u == 2:
            step.k = 3
            v.wait_ge(act, i * 3 + 2)
            step.done(v.tensor_reduce(var, sq, AX.X, ALU.add))
            step.wait()
            step.done(v.tensor_scalar(var, var, 1.0 / DH0, EPS, ALU.mult, ALU.add))
        if u == 3:
            step.k = 5
            v.wait_ge(act, i * 3 + 3)
            step.done(v.reciprocal(var, var))
            step.wait()
            v.wait_ge(dots, i)
            step.done(v.tensor_tensor(kv, cen, var.unsqueeze(2).broadcast_to([P, G, DH0]), ALU.mult))

    def scalar(a, i, last):
        a.wait_ge(kv_ready, i)
        a.activation(tile[:], c.xnT[:, :, ds(i * P, P)], ACT.Copy).then_inc(tile_ready, 1)
        a.wait_ge(vec, i * PER + 3)
        a.activation(sq.rearrange(flat), cen.rearrange(flat), ACT.Square).then_inc(act, 2)
        a.wait_ge(vec, i * PER + 5)
        a.activation(var, var, ACT.Sqrt).then_inc(act, 1)

    def sync_first(sp):
        sp.dma_start(wkv.rearrange(flat), c.turned_part("L0_mix_Wqkv", 2 * 1024)).then_inc(w_loaded, 16)

    side = dict(tensor_first=first, tensor_begin=products_begin, tensor_end=products_end, vector=vector,
                scalar=scalar, sync_first=sync_first)
    aggregate(c, table=c.xn_tab, slots=(0, 1), side=side)
    c.constants.end(16)


def fold_attention(c):
    nc = c.nc
    part = Carver(c.scr, SCR)
    woutT, wq = part.take([PAIRS, D]), part.take([PAIRS, D])
    dots, t_sb = part.take([PAIRS, P]), part.take([PAIRS, D])
    loaded = c.constants.sem
    vec, pe_done = c.sem("fold0_vec"), c.sem("fold0_products")
    with nc.Block() as block:

        @block.sync
        def _(sp):
            sp.dma_start(woutT.rearrange("p a b -> p (a b)"), c.turned_part("L0_mix_Wout", PAIRS * D)).then_inc(loaded, 16)
            sp.dma_start(wq[:], c.inp["L0_mix_Wqkv"][0:PAIRS * P, :].rearrange("(q p) n -> p q n", p=P)).then_inc(loaded, 16)

        @block.vector
        def _(v):
            v.scalar_tensor_tensor(dots[:], c.psum[:, 4, :].rearrange("p (q d) -> p q d", d=P), 1.0 / N,
                                   c.bd64[:].unsqueeze(1).broadcast_to([P, PAIRS, P]), ALU.mult, ALU.mult
                                   ).then_inc(vec, 1)
            v.wait_ge(pe_done, 1)
            v.tensor_copy(t_sb[:], c.psum[:, 0:2, :].rearrange("p a b -> p (a b)").rearrange("p (q d) -> p q d", d=D)
                          ).then_inc(vec, 1)
            v.wait_ge(pe_done, 2)
            v.tensor_copy(c.m0[:], c.psum[:, 2, :].rearrange("p (k d) -> p k d", d=D))
            for k in range(2):
                v.tensor_tensor(c.agg[:, k, :], c.agg[:, k, :], c.agg[:, 2, :], ALU.mult)

        @block.tensor
        def _(pe):
            pe.wait_ge(vec, 1)
            pe.wait_ge(loaded, c.constants.at(32))
            for q in range(PAIRS):
                last = pe.matmul(c.psum[:, q // 2, (q % 2) * D:(q % 2 + 1) * D], dots[:, q, :], woutT[:, q, :],
                                 start=True, stop=True)
            last.then_inc(pe_done, 1)
            pe.wait_ge(vec, 2)
            for k in range(2):
                for q in range(PAIRS):
                    last = pe.matmul(c.psum[:, 2, k * D:(k + 1) * D], wq[:, q, k * P:(k + 1) * P], t_sb[:, q, :],
                                     start=(q == 0), stop=(q == PAIRS - 1))
            last.then_inc(pe_done, 1)
    c.constants.end(32)


H1 = 4


def first_conv(c):
    nc = c.nc
    part = Carver(c.scr, SCR)
    w1T, w2T = part.take([2, H1 * P]), part.take([H1, D])
    stats = part.take([H1, NS * 2, 6])
    moments = part.take([H1, 2])
    rstd, scale, bias = part.take([H1]), part.take([H1]), part.take([H1])
    h1r = part.take([2, H1, 512])
    rows = part.take([2, 4, D])
    loaded, ready, read = c.constants.sem, c.sem("conv1_h1_ready"), c.sem("conv1_h1_read")
    with nc.Block() as block:

        @block.sync
        def _(sp):
            sp.dma_start(w1T.rearrange("p a b -> p (a b)"), c.turned_part("L0_gnn_W1", 2 * H1 * P)).then_inc(loaded, 16)
            sp.dma_start(w2T.rearrange("p a b -> p (a b)"), c.turned_part("L0_gnn_W2", H1 * D)).then_inc(loaded, 16)
            sp.wait_ge(loaded, c.constants.at(32))

        @block.gpsimd
        def _(g):
            g.memset(c.agg[:, 2, :], 0.0)

        @block.tensor
        def _(pe):
            pe.wait_ge(loaded, c.constants.at(32))
            with pe.Fori(0, NS) as s:
                for h, (t0, nt) in enumerate(HALVES):
                    pe.wait_ge(read, s * 2 + h)
                    for m in range(H1):
                        for k in range(2):
                            last = pe.matmul(c.psum[:, 4 * h + m, 0:nt * P], w1T[:, k, m * P:(m + 1) * P],
                                             c.agg[:, k, ds(s * SS + t0 * P, nt * P)], start=(k == 0), stop=(k == 1))
                    last.then_inc(ready, 1)

        @block.vector
        def _(v):
            def turn(s, last_step):
                for h, (t0, nt) in enumerate(HALVES):
                    cols = nt * P
                    if last_step and h == 1:
                        cols = (nt - 1) * P + LAST
                    v.wait_ge(ready, s * 2 + h + 1)
                    for m in range(H1):
                        last = v.bn_stats(stats[:, m, ds(s * 2 + h, 1), :].rearrange("p a b -> p (a b)"),
                                          c.psum[:, 4 * h + m, 0:cols])
                    last.then_inc(read, 1)
            with v.Fori(0, NS - 1) as s:
                turn(s, False)
            turn(NS - 1, True)

    vec, root = c.sem("conv1_bn_vec"), c.sem("conv1_bn_root")
    h_ready, relu, tiles = c.sem("conv1_part_ready"), c.sem("conv1_relu_done"), c.sem("conv1_rows_ready")
    scaled, turned, copied = c.sem("conv1_rows_scaled"), c.sem("conv1_rows_turned"), c.sem("conv1_agg_copied")
    stored = [c.sem(f"conv1_stored{h}") for h in range(2)]
    with nc.Block() as block:

        @block.vector
        def _(v):
            step = Chain(v, vec)
            for m in range(H1):
                step.done(v.bn_aggr(moments[:, m, :], stats[:, m, :, :].rearrange("p a b -> p (a b)")))
            step.wait()
            step.done(v.tensor_scalar(rstd, moments[:, :, 1], EPS, None, ALU.add))
            v.wait_ge(root, 1)
            step.done(v.reciprocal(rstd, rstd))
            step.wait()
            step.done(v.tensor_tensor(scale, rstd, c.columns("L0_gnn_g1"), ALU.mult))
            step.wait()
            step.done(v.tensor_tensor(bias, moments[:, :, 0], scale, ALU.mult))
            step.wait()
            step.done(v.tensor_tensor(bias, c.columns("L0_gnn_b1"), bias, ALU.subtract))
            with v.Fori(0, NS) as s:
                for h, (t0, nt) in enumerate(HALVES):
                    v.wait_ge(stored[h], s * 16)
                    v.wait_ge(turned, s * 4)
                    v.wait_ge(tiles, s * 2 + h + 1)
                    for t in range(nt):
                        last = v.tensor_scalar(rows[:, h, t, :], c.psum[:, 4 + t // 2, (t % 2) * D:(t % 2 + 1) * D],
                                               c.dis[:, ds(s * TS + t0 + t, 1)], None, ALU.mult)
                    last.then_inc(scaled, 1)
                    for k in range(2):
                        v.wait_ge(turned, (s * 2 + h) * 2 + k + 1)
                        v.tensor_copy(c.agg[:, k, ds(s * SS + t0 * P, nt * P)], c.psum[:, 6 + k, 0:nt * P]
                                      ).then_inc(copied, 1)

        @block.scalar
        def _(a):
            a.wait_ge(vec, H1 + 1)
            a.activation(rstd, rstd, ACT.Sqrt).then_inc(root, 1)
            a.wait_ge(vec, H1 + 5)
            with a.Fori(0, NS) as s:
                for h, (t0, nt) in enumerate(HALVES):
                    for m in range(H1):
                        a.wait_ge(h_ready, (s * 2 + h) * H1 + m + 1)
                        if m == 0:
                            a.wait_ge(tiles, s * 2)
                        a.activation(h1r[:, h, m, 0:nt * P], c.psum[:, m, 0:nt * P], ACT.Relu, bias=bias[:, m:m + 1],
                                     scale=scale[:, m:m + 1]).then_inc(relu, 1)

        @block.tensor
        def _(pe):
            def h1(s, h):
                t0, nt = HALVES[h]
                for m in range(H1):
                    pe.wait_ge(relu, (s * 2 + h - 1) * H1 + m + 1 if h else s * 2 * H1)
                    for k in range(2):
                        last = pe.matmul(c.psum[:, m, 0:nt * P], w1T[:, k, m * P:(m + 1) * P],
                                         c.agg[:, k, ds(s * SS + t0 * P, nt * P)], start=(k == 0), stop=(k == 1))
                    last.then_inc(h_ready, 1)

            def node_rows(s, h):
                t0, nt = HALVES[h]
                pe.wait_ge(scaled, s * 2 + h)
                for m in range(H1):
                    pe.wait_ge(relu, (s * 2 + h) * H1 + m + 1)
                    for t in range(nt):
                        last = pe.matmul(c.psum[:, 4 + t // 2, (t % 2) * D:(t % 2 + 1) * D],
                                         h1r[:, h, m, t * P:(t + 1) * P], w2T[:, m, :],
                                         start=(m == 0 and t % 2 == 0), stop=(m == H1 - 1), skip_group_check=True)
                last.then_inc(tiles, 1)

            def turn_rows(s, h):
                t0, nt = HALVES[h]
                pe.wait_ge(scaled, s * 2 + h + 1)
                pe.wait_ge(copied, (s * 2 + h) * 2)
                for k in range(2):
                    for t in range(nt):
                        last = pe.transpose(c.psum[:, 6 + k, t * P:(t + 1) * P], rows[:, h, t, k * P:(k + 1) * P], c.ident[:])
                    last.then_inc(turned, 1)

            with pe.Fori(0, NS) as s:
                h1(s, 0)
                node_rows(s, 0)
                h1(s, 1)
                turn_rows(s, 0)
                node_rows(s, 1)
                turn_rows(s, 1)

        @block.sync
        def _(sp):
            with sp.Fori(0, NS) as s:
                for h, (t0, nt) in enumerate(HALVES):
                    sp.wait_ge(scaled, s * 2 + h + 1)
                    sp.dma_start(c.h_tab[ds(s * SS + t0 * P, nt * P), :].rearrange("(t p) d -> p t d", p=P),
                                 rows[:, h, 0:nt, :]).then_inc(stored[h], 16)
            for q in stored:
                sp.wait_ge(q, 16 * NS)
    c.constants.end(32)


def gather_second(c):
    nc = c.nc
    dis_all = c.scr[:, SCR - NP:]
    done = c.constants.sem

    def sync_first(sp):
        sp.dma_start(dis_all, c.dis_row.partition_broadcast(P)).then_inc(done, 16)
        sp.wait_ge(done, c.constants.at(16))

    aggregate(c, table=c.h_tab, slots=(0, 1, "weight"), side=dict(sync_first=sync_first))
    with nc.Block() as block:

        @block.sync
        def _(sp):
            sp.dma_start(c.wsum_row, c.agg[0:1, 2, :]).then_inc(done, 16)
            sp.wait_ge(done, c.constants.at(32))

        @block.vector
        def _(v):
            for k in range(2):
                v.tensor_tensor(c.agg[:, k, :], c.agg[:, k, :], dis_all, ALU.mult)
    c.constants.end(32)


def first_layer_sum(c):
    nc = c.nc
    part = Carver(c.scr, SCR)
    pre = part.take([2, 2, 512])
    xs = part.take([2, 2, 512])
    x_in = part.take([2, 4, D])
    x1 = part.take([2, 4, D])
    xn2 = part.take([2, 4, D])
    xn2T = part.take([2, 2, 512])
    wg, bg, bout = part.take([2, EXPERTS]), part.take([EXPERTS]), part.take([D])
    chunks = -(-N // 512)
    stats = part.take([2, chunks, 6])
    moments, rstd2, scale, bias = part.take([2, 2]), part.take([2]), part.take([2]), part.take([2])
    st, mo, rstd = part.take([2, 4, 6]), part.take([2, 4, 2]), part.take([2, 4])
    loaded, bn, root2 = c.constants.sem, c.sem("sum_bn_vec"), c.sem("sum_bn_root")
    x_in_ready = [c.sem(f"sum_x_loaded{h}") for h in range(2)]
    pre_ready, relu, xs_ready = c.sem("sum_pre_ready"), c.sem("sum_relu_done"), c.sem("sum_xn_copied")
    x1_psum, x1_ready, vec, root = c.sem("sum_x1_products"), c.sem("sum_x1_ready"), c.sem("sum_vec"), c.sem("sum_root")
    begun, xn2_ready, turned, copied = c.sem("sum_moments_begun"), c.sem("sum_xn2_ready"), c.sem("sum_turned"), c.sem("sum_xn2T_copied")
    scored, scores_ready = c.sem("sum_scored"), c.sem("sum_scores_ready")
    stored = [c.sem(f"sum_stored{h}") for h in range(2)]
    with nc.Block() as block:

        @block.sync
        def _(sp):
            sp.dma_start(wg[:], c.inp["L0_ffn_Wg"].rearrange("(k p) e -> p k e", p=P)).then_inc(loaded, 16)
            sp.dma_start(bg, c.inp["L0_ffn_bg"].unsqueeze(0).partition_broadcast(P)).then_inc(loaded, 16)
            sp.dma_start(bout[0:1, :], c.inp["L0_mix_bout"].unsqueeze(0)).then_inc(loaded, 16)

            def load(s, h, last):
                t0, nt = HALVES[h]
                sp.wait_ge(x1_ready, s * 2)
                if last and h == 1:
                    full = nt - 1
                    r0 = (NS - 1) * SS + t0 * P
                    sp.dma_start(x_in[:, h, 0:full, :], c.inp["x"][r0:r0 + full * P, :].rearrange("(t p) d -> p t d", p=P)
                                 ).then_inc(x_in_ready[h], 16)
                    sp.dma_start(x_in[0:LAST, h, full, :], c.inp["x"][r0 + full * P:N, :]).then_inc(x_in_ready[h], 16)
                else:
                    sp.dma_start(x_in[:, h, 0:nt, :],
                                 c.inp["x"][ds(s * SS + t0 * P, nt * P), :].rearrange("(t p) d -> p t d", p=P)
                                 ).then_inc(x_in_ready[h], 16)

            def store(s, h):
                t0, nt = HALVES[h]
                sp.wait_ge(xn2_ready, s * 2 + h + 1)
                for table, rows in ((c.x1_tab, x1), (c.xn2_tab, xn2)):
                    sp.dma_start(table[ds(s * SS + t0 * P, nt * P), :].rearrange("(t p) d -> p t d", p=P),
                                 rows[:, h, 0:nt, :]).then_inc(stored[h], 16)

            def turn(s, last):
                for h in range(2):
                    load(s, h, last)
                for h in range(2):
                    store(s, h)
            with sp.Fori(0, NS - 1) as s:
                turn(s, False)
            turn(NS - 1, True)
            sp.wait_ge(loaded, c.constants.at(48))
            for q in stored:
                sp.wait_ge(q, 32 * NS)

        @block.vector
        def _(v):
            step = Chain(v, bn)
            for k in range(2):
                for j in range(chunks):
                    ins = v.bn_stats(stats[:, k, j, :], c.agg[:, k, j * 512:min(N, j * 512 + 512)])
            step.done(ins)
            step.wait()
            for k in range(2):
                step.done(v.bn_aggr(moments[:, k, :], stats[:, k, :, :].rearrange("p a b -> p (a b)")))
            step.wait()
            step.done(v.tensor_scalar(rstd2, moments[:, :, 1], EPS, None, ALU.add))
            v.wait_ge(root2, 1)
            step.done(v.reciprocal(rstd2, rstd2))
            step.wait()
            step.done(v.tensor_tensor(scale, rstd2, c.columns("L0_gnn_g2"), ALU.mult))
            step.wait()
            step.done(v.tensor_tensor(bias, moments[:, :, 0], scale, ALU.mult))
            step.wait()
            step.done(v.tensor_tensor(bias, c.columns("L0_gnn_b2"), bias, ALU.subtract))
            step.wait()
            v.wait_ge(loaded, c.constants.at(48))

            def norm(s, h, last):
                t0, nt = HALVES[h]
                per = 3
                chain = Chain(v, vec, s, 2 * per, h * per)
                x_count = s * 16 + 16 if not (last and h == 1) else s * 16 + 32
                v.wait_ge(x_in_ready[h], x_count)
                v.wait_ge(x1_psum, s * 2 + h + 1)
                v.wait_ge(stored[h], s * 32)
                v.wait_ge(turned, s * 4 + 2 * h)
                for t in range(nt):
                    ins = v.tensor_tensor(x1[:, h, t, :], c.psum[:, t // 2, (t % 2) * D:(t % 2 + 1) * D],
                                          x_in[:, h, t, :], ALU.add)
                ins.then_inc(x1_ready, 1)
                v.wait_ge(x1_ready, s * 2 + h + 1)
                for t in range(nt):
                    ins = v.bn_stats(st[:, h, t, :], x1[:, h, t, :])
                chain.done(ins)
                chain.wait()
                v.sem_inc(begun, 1)
                for t in range(nt):
                    ins = v.bn_aggr(mo[:, h, t, :], st[:, h, t, :])
                chain.done(ins)
                chain.wait()
                v.tensor_scalar(rstd[:, h, 0:nt], mo[:, h, 0:nt, 1], EPS, None, ALU.add).then_inc(begun, 1)
                v.wait_ge(root, s * 2 + h + 1)
                chain.done(v.reciprocal(rstd[:, h, 0:nt], rstd[:, h, 0:nt]))
                chain.wait()
                for t in range(nt):
                    ins = v.tensor_scalar(xn2[:, h, t, :], x1[:, h, t, :], mo[:, h, t, 0:1], rstd[:, h, t:t + 1],
                                          ALU.subtract, ALU.mult)
                ins.then_inc(xn2_ready, 1)

            def turn(s, last):
                for h, (t0, nt) in enumerate(HALVES):
                    v.wait_ge(x1_psum, s * 2)
                    for k in range(2):
                        at = ds(s * SS + t0 * P, nt * P)
                        v.scalar_tensor_tensor(pre[:, h, k, 0:nt * P], c.agg[:, k, at], scale[:, k:k + 1], c.xnT[:, k, at],
                                               ALU.mult, ALU.add).then_inc(pre_ready, 1)
                for h in range(2):
                    norm(s, h, last)
                for h, (t0, nt) in enumerate(HALVES):
                    v.wait_ge(scored, s * 2 + h + 1)
                    v.tensor_tensor(c.scores[:, ds(s * TS + t0, nt), :],
                                    c.psum[:, 7, h * 64:h * 64 + nt * EXPERTS].rearrange("p (t e) -> p t e", e=EXPERTS),
                                    bg.unsqueeze(1).broadcast_to([P, nt, EXPERTS]), ALU.add).then_inc(scores_ready, 1)
            with v.Fori(0, NS - 1) as s:
                turn(s, False)
            turn(NS - 1, True)

        @block.scalar
        def _(a):
            a.wait_ge(bn, 4)
            a.activation(rstd2, rstd2, ACT.Sqrt).then_inc(root2, 1)
            a.wait_ge(bn, 7)
            with a.Fori(0, NS) as s:
                for h, (t0, nt) in enumerate(HALVES):
                    a.wait_ge(x1_psum, s * 2)
                    a.activation(xs[:, h, :, 0:nt * P], c.xnT[:, :, ds(s * SS + t0 * P, nt * P)], ACT.Copy).then_inc(xs_ready, 1)
                    for k in range(2):
                        a.wait_ge(pre_ready, (s * 2 + h) * 2 + k + 1)
                        a.activation(pre[:, h, k, 0:nt * P], pre[:, h, k, 0:nt * P], ACT.Relu, bias=bias[:, k:k + 1]
                                     ).then_inc(relu, 1)
                for h, (t0, nt) in enumerate(HALVES):
                    a.wait_ge(begun, (s * 2 + h) * 2 + 2)
                    a.activation(rstd[:, h, 0:nt], rstd[:, h, 0:nt], ACT.Sqrt).then_inc(root, 1)
                    a.wait_ge(scored, s * 2 + h)
                    for k in range(2):
                        a.wait_ge(turned, (s * 2 + h) * 2 + k + 1)
                        a.activation(xn2T[:, h, k, 0:nt * P], c.psum[:, 5 + k, 0:nt * P], ACT.Copy).then_inc(copied, 1)

        @block.tensor
        def _(pe):
            pe.wait_ge(loaded, c.constants.at(48))

            def x1_rows(s, h):
                t0, nt = HALVES[h]
                pe.wait_ge(x1_ready, s * 2 + h)
                pe.wait_ge(xs_ready, s * 2 + h + 1)
                pe.wait_ge(relu, (s * 2 + h) * 2 + 2)
                for t in range(nt):
                    bank, col = t // 2, (t % 2) * D
                    cols = slice(t * P, (t + 1) * P)
                    for k in range(2):
                        pe.matmul(c.psum[:, bank, col + k * P:col + (k + 1) * P], pre[:, h, k, cols], c.ident[:],
                                  start=(k == 0), stop=False, skip_group_check=True)
                    for k in range(2):
                        pe.matmul(c.psum[:, bank, col:col + D], xs[:, h, k, cols], c.m0[:, k, :], start=False,
                                  stop=False, skip_group_check=True)
                    last = pe.matmul(c.psum[:, bank, col:col + D], c.ones[0:1, :], bout[0:1, :], start=False, stop=True,
                                     skip_group_check=True)
                last.then_inc(x1_psum, 1)

            def turn_rows(s, h):
                t0, nt = HALVES[h]
                pe.wait_ge(xn2_ready, s * 2 + h + 1)
                pe.wait_ge(copied, (s * 2 + h) * 2)
                for k in range(2):
                    for t in range(nt):
                        last = pe.transpose(c.psum[:, 5 + k, t * P:(t + 1) * P], xn2[:, h, t, k * P:(k + 1) * P], c.ident[:])
                    last.then_inc(turned, 1)

            def score(s, h):
                t0, nt = HALVES[h]
                pe.wait_ge(copied, (s * 2 + h) * 2 + 2)
                pe.wait_ge(scores_ready, s * 2 + h)
                for t in range(nt):
                    col = h * 64 + t * EXPERTS
                    for k in range(2):
                        last = pe.matmul(c.psum[:, 7, col:col + EXPERTS], xn2T[:, h, k, t * P:(t + 1) * P], wg[:, k, :],
                                         start=(k == 0), stop=(k == 1))
                last.then_inc(scored, 1)

            with pe.Fori(0, NS) as s:
                x1_rows(s, 0)
                x1_rows(s, 1)
                for h in range(2):
                    turn_rows(s, h)
                    score(s, h)
    c.constants.end(48)


def route(c):
    nc = c.nc
    part = Carver(c.scr, SCR)
    T8 = [NT, EXPERTS]
    rev, eq, cand = part.take([EXPERTS]), part.take(T8), part.take(T8)
    mask = [part.take(T8), part.take(T8)]
    rest = part.take(T8)
    top, code = part.take([NT]), [part.take([NT]), part.take([NT])]
    both = part.take(T8, BF16)
    tri, ones_b = part.take([P], BF16), part.take([NT])
    total, upto = part.take([EXPERTS, NT]), part.take([EXPERTS, NT])
    rank = part.take(T8)
    picked, rank_of = part.take(T8), [part.take([NT]), part.take([NT])]
    start_of = part.take([NT])
    count_i, ntile = part.take([EXPERTS], I32), part.take([EXPERTS])
    end, first = part.take([EXPERTS]), part.take([EXPERTS])
    where = part.take([EXPERTS])
    node, tile_no = part.take([1]), part.take([MT])
    inside, later = part.take([MT]), part.take([MT])
    t_expert, t_row = part.take([MT]), part.take([MT])
    const, vec, pe_done = c.sem("route_const"), c.sem("route_vec"), c.sem("route_counts")
    w_loaded = c.sem("expert_weights_loaded")
    raw = c.agg.rearrange("p a b -> p (a b)")
    words = EXPERTS * 2 * HID
    marks = {}
    with nc.Block() as block:

        @block.sync
        def _(sp):
            w1, w2 = raw[:, 0:words], raw[:, words:2 * words]
            for e in range(EXPERTS):
                sp.dma_start(w1[:, e * 2 * HID:(e + 1) * 2 * HID].rearrange("p (k n) -> p k n", n=HID),
                             c.inp["L0_ffn_W1"][e].rearrange("(k p) n -> p k n", p=P)).then_inc(w_loaded, 16)
                sp.dma_start(w2[:, e * HM * D:(e + 1) * HM * D].rearrange("p (m n) -> p m n", n=D),
                             c.inp["L0_ffn_W2"][e].rearrange("(m p) n -> p m n", p=P)).then_inc(w_loaded, 16)
            sp.wait_ge(w_loaded, 16 * 2 * EXPERTS)

        @block.gpsimd
        def _(g):
            small = dict(allow_small_or_imprecise_dtypes=True)
            g.iota(rev, pattern=[[-1, EXPERTS]], base=EXPERTS, channel_multiplier=0, **small).then_inc(const, 1)
            g.iota(node, pattern=[[0, 1]], base=0, channel_multiplier=1, **small).then_inc(const, 1)
            g.iota(tile_no, pattern=[[1, MT]], base=0, channel_multiplier=0, **small).then_inc(const, 1)
            g.memset(tri, 1.0).then_inc(const, 1)
            g.wait_ge(const, 4)
            g.affine_select(out=tri, in_=tri, compare_op=ALU.is_gt, fill=0.0, base=0, pattern=[[1, P]],
                            channel_multiplier=-1).then_inc(const, 1)

        @block.vector
        def _(v):
            step = Chain(v, vec)

            def do(instruction):
                step.done(instruction)
                step.wait()

            def wide(x):
                return x.unsqueeze(2).broadcast_to([P, NT, EXPERTS])

            def over(x):
                return x.unsqueeze(1).broadcast_to([P, NT, EXPERTS])

            v.wait_ge(const, 5)
            scores = c.scores[:]
            for n in range(2):
                do(v.tensor_reduce(top, scores, AX.X, ALU.max))
                do(v.tensor_tensor(eq, scores, wide(top), ALU.is_equal))
                do(v.tensor_tensor(cand, eq, over(rev), ALU.mult))
                do(v.tensor_reduce(code[n], cand, AX.X, ALU.max))
                do(v.tensor_tensor(mask[n], over(rev), wide(code[n]), ALU.is_equal))
                if n == 0:
                    do(v.scalar_tensor_tensor(rest, mask[0], -1e30, scores, ALU.mult, ALU.add))
                    scores = rest
            do(v.tensor_tensor(both, mask[0], mask[1], ALU.add))
            marks["both"] = step.value()
            do(v.memset(ones_b, 1.0))
            v.wait_ge(pe_done, 1)
            in_tile = c.psum[:, 0, 0:NT * EXPERTS].rearrange("p (t e) -> p t e", e=EXPERTS)
            tile_sum = c.psum[:, 1, 0:NT * EXPERTS].rearrange("p (t e) -> p e t", e=EXPERTS)
            do(v.tensor_copy(total, tile_sum))
            for e in range(EXPERTS):
                ins = v.tensor_tensor_scan(upto[:, e, :], ones_b, total[:, e, :], 0.0, ALU.mult, ALU.add)
            do(ins)
            do(v.tensor_tensor(total, upto, total, ALU.subtract))
            do(v.tensor_tensor(rank, in_tile, total.rearrange("p e t -> p t e"), ALU.add))
            do(v.tensor_scalar(where, upto[:, :, NT - 1], float(P - 1), None, ALU.add))
            do(v.tensor_copy(count_i, where))
            do(v.tensor_scalar(count_i, count_i, 7, None, ALU.arith_shift_right))
            do(v.tensor_copy(ntile, count_i))
            do(v.tensor_tensor_scan(end, ones_b[:, 0:EXPERTS], ntile, 0.0, ALU.mult, ALU.add))
            do(v.tensor_tensor(first, end, ntile, ALU.subtract))
            for n in range(2):
                do(v.tensor_tensor(picked, mask[n], rank, ALU.mult))
                do(v.tensor_reduce(rank_of[n], picked, AX.X, ALU.add))
                do(v.tensor_scalar(start_of, code[n], -float(REGION), float(EXPERTS * REGION), ALU.mult, ALU.add))
                do(v.tensor_tensor(c.scatter_to[:, n, :], start_of, rank_of[n], ALU.add))
                do(v.tensor_tensor(picked, mask[n], over(first), ALU.mult))
                do(v.tensor_reduce(start_of, picked, AX.X, ALU.add))
                do(v.scalar_tensor_tensor(c.result_at[:, n, :], start_of, float(P), rank_of[n], ALU.mult, ALU.add))
            do(v.tensor_scalar(where, rev, -float(REGION), float(EXPERTS * REGION), ALU.mult, ALU.add))
            do(v.tensor_tensor(where, where, upto[:, :, NT - 1], ALU.add))
            do(v.tensor_scalar(c.pad_to[:], where, node[:, 0:1], None, ALU.add))
            do(v.memset(t_expert, 0.0))
            do(v.memset(t_row, 0.0))
            for e in range(EXPERTS):
                do(v.tensor_scalar(inside, tile_no, first[:, e:e + 1], None, ALU.is_ge))
                do(v.tensor_scalar(later, tile_no, end[:, e:e + 1], None, ALU.is_lt))
                do(v.tensor_tensor(inside, inside, later, ALU.mult))
                do(v.scalar_tensor_tensor(t_expert, inside, float(e), t_expert, ALU.mult, ALU.add))
                do(v.tensor_scalar(later, tile_no, first[:, e:e + 1], None, ALU.subtract))
                do(v.tensor_scalar(later, later, float(P), float(e * REGION), ALU.mult, ALU.add))
                do(v.tensor_tensor(later, later, inside, ALU.mult))
                do(v.tensor_tensor(t_row, t_row, later, ALU.add))
            do(v.tensor_copy(c.tile_expert[:], t_expert))
            do(v.tensor_copy(c.tile_row[:], t_row))

        @block.tensor
        def _(pe):
            pe.wait_ge(const, 5)
            pe.wait_ge(vec, marks["both"])
            flat = both.rearrange("p t e -> p (t e)")
            pe.matmul(c.psum[:, 0, 0:NT * EXPERTS], tri, flat, start=True, stop=True)
            pe.matmul(c.psum[:, 1, 0:NT * EXPERTS], c.ones16[:], flat, start=True, stop=True).then_inc(pe_done, 1)


def send_to_experts(c):
    nc = c.nc
    part = Carver(c.scr, SCR)
    part.at = EXPERTS * HM * D
    rows = part.take([2, 4, D])
    zero_rows = part.take([D])
    to = part.take([2, 2, 4], I32)
    raw = c.agg.rearrange("p a b -> p (a b)")
    words = EXPERTS * 2 * HID
    xnT = c.xnT.rearrange("p a b -> p (a b)")
    c.w1_16 = xnT[:, 0:words].bitcast(F16).rearrange("p (e k h n) -> p e k h n", k=2, h=2, n=HID)
    c.w2_16 = c.scr[:, 0:words].bitcast(F16).rearrange("p (e k h n) -> p e k h n", k=HM, h=2, n=D)
    w1 = raw[:, 0:words].rearrange("p (e k n) -> p e k n", k=2, n=HID)
    w2 = raw[:, words:2 * words].rearrange("p (e k n) -> p e k n", k=HM, n=D)
    zero, landed = c.sem("pad_rows_zeroed"), [c.sem(f"send_rows_landed{h}") for h in range(2)]
    idx_ready, begun, sent = c.sem("send_indices_ready"), c.passed, [c.sem(f"rows_sent{h}") for h in range(2)]
    padded, high = c.sem("pads_sent"), c.sem("weights_high")
    with nc.Block() as block:

        @block.sync
        def _(sp):
            with sp.Fori(0, NS) as s:
                for h, (t0, nt) in enumerate(HALVES):
                    sp.wait_ge(sent[h], s * (2 * nt * 16))
                    sp.dma_start(rows[:, h, 0:nt, :],
                                 c.xn2_tab[ds(s * SS + t0 * P, nt * P), :].rearrange("(t p) d -> p t d", p=P)
                                 ).then_inc(landed[h], 16)

        @block.vector
        def _(v):
            v.memset(zero_rows, 0.0).then_inc(zero, 1)
            for e in range(EXPERTS):
                for n, (w, parts) in enumerate(((w1, c.w1_16), (w2, c.w2_16))):
                    v.wait_ge(high, 2 * e + n + 1)
                    v.scalar_tensor_tensor(parts[:, e, :, 1, :], w[:, e, :, :], WS, parts[:, e, :, 0, :],
                                           ALU.mult, ALU.subtract)

        @block.scalar
        def _(a):
            def indices(s):
                for h, (t0, nt) in enumerate(HALVES):
                    a.wait_ge(sent[h], s * (2 * nt * 16))
                    a.activation(to[:, h, :, 0:nt], c.scatter_to[:, :, ds(s * TS + t0, nt)], ACT.Copy).then_inc(idx_ready, 1)

            for e in range(EXPERTS):
                for w, parts in ((w1, c.w1_16), (w2, c.w2_16)):
                    a.activation(parts[:, e, :, 0, :], w[:, e, :, :], ACT.Copy, scale=WS).then_inc(high, 1)
                if e < NS:
                    indices(e)

        @block.gpsimd
        def _(g):
            g.wait_ge(zero, 1)
            for e in range(EXPERTS):
                g.indirect_dma_start(out=c.slot_x, in_=zero_rows, in_offset=None,
                                     out_offset=bass.IndirectOffsetOnAxis(ap=c.pad_to[:, e:e + 1], axis=0)
                                     ).then_inc(padded, 16)
            with g.Fori(0, NS) as s:
                for h, (t0, nt) in enumerate(HALVES):
                    g.wait_ge(landed[h], s * 16 + 16)
                    g.sem_inc(begun, 1)
                    g.wait_ge(idx_ready, s * 2 + h + 1)
                    g.sem_inc(begun, 1)
                    for n in range(2):
                        for t in range(nt):
                            g.indirect_dma_start(out=c.slot_x, in_=rows[:, h, t, :], in_offset=None,
                                                 out_offset=bass.IndirectOffsetOnAxis(ap=to[:, h, n, t:t + 1], axis=0)
                                                 ).then_inc(sent[h], 16)
            g.wait_ge(padded, 16 * EXPERTS)
            for h, (t0, nt) in enumerate(HALVES):
                g.wait_ge(sent[h], 32 * nt * NS)


def experts(c):
    nc = c.nc
    part = Carver(c.scr, SCR)
    part.at = EXPERTS * HM * D
    x = part.take([2, D])
    xT = part.take([2, 2, D], F16)
    g = part.take([2, HID])
    gT = part.take([2, 2, HID], F16)
    y = part.take([2, D])
    b2 = part.take([EXPERTS, D])
    agg = c.agg.rearrange("p a b -> p (a b)")
    loaded, x_ready = c.constants.sem, [c.sem(f"moe_x_loaded{b}") for b in range(2)]
    turned, x_high, x_low = c.sem("moe_turned"), c.sem("moe_x_high"), c.sem("moe_x_low")
    h_ready, g_ready = c.sem("moe_h_ready"), c.sem("moe_gelu_done")
    g_high, g_low = c.sem("moe_g_high"), c.sem("moe_g_low")
    y_ready, y_out = c.sem("moe_y_products"), c.sem("moe_y_ready")
    stored = [c.sem(f"moe_stored{b}") for b in range(2)]
    PARTS = ((0, 0), (0, 1), (1, 0))

    def turns(engine, body):
        body(0, True, False)
        with engine.Fori(1, MT // 2 - 1) as q:
            body(q, False, False)
        body(MT // 2 - 1, False, True)

    def experts_of(engine, tile, n):
        _, regs = nc.values_load_multi_w_load_instructions(c.tile_expert[0:1, ds(tile, n)], engines=[engine.engine],
                                                           min_val=0, max_val=EXPERTS - 1)
        return regs

    with nc.Block() as block:

        @block.sync
        def _(sp):
            sp.dma_start(b2.rearrange("p e d -> p (e d)"),
                         c.inp["L0_ffn_b2"].rearrange("e d -> (e d)").unsqueeze(0).partition_broadcast(P)).then_inc(loaded, 16)

            def load(i, b):
                row = sp.value_load(c.tile_row[0:1, ds(i, 1)], min_val=0, max_val=EXPERTS * REGION - P)
                sp.dma_start(x[:, b, :], c.slot_x[ds(row, P), :]).then_inc(x_ready[b], 16)

            for b in range(2):
                load(b, b)
            with sp.Fori(0, MT // 2 - 1) as q:
                for b in range(2):
                    sp.wait_ge(turned, q * 2 + b + 1)
                    load(q * 2 + 2 + b, b)
            sp.wait_ge(loaded, c.constants.at(16))

        @block.gpsimd
        def _(gp):
            with gp.Fori(0, MT // 2) as q:
                for b in range(2):
                    gp.wait_ge(y_out, q * 2 + b + 1)
                    gp.sem_inc(c.passed, 1)
                    gp.dma_start(c.slot_y[ds((q * 2 + b) * P, P), :], y[:, b, :]).then_inc(stored[b], 16)
            for b in range(2):
                gp.wait_ge(stored[b], 16 * (MT // 2))

        @block.scalar
        def _(a):
            def x_high_part(i, b):
                a.wait_ge(turned, i + 1)
                a.activation(xT[:, b, 0, :], c.psum[:, b, 0:D], ACT.Copy, scale=XS).then_inc(x_high, 1)

            def gelu(i, b, first, e):
                a.wait_ge(h_ready, i + 1)
                if not first:
                    a.wait_ge(g_low, i - 1)
                at = COLUMNS_AT["L0_ffn_b1"][0]
                for m in range(HM):
                    ins = a.activation(g[:, b, m * P:(m + 1) * P], c.psum[:, 2 + b, m * P:(m + 1) * P], ACT.Gelu,
                                       bias=c.cols[:, ds(e * HM + (at + m), 1)], scale=1.0 / (XS * WS))
                ins.then_inc(g_ready, 1)

            x_high_part(0, 0)
            x_high_part(1, 1)

            def body(q, first, last):
                e = experts_of(a, q * 2, 2)
                for b in range(2):
                    gelu(q * 2 + b, b, first, e[b])
                    if not last:
                        x_high_part(q * 2 + b + 2, b)
            turns(a, body)

        @block.vector
        def _(v):
            def x_split(i, b):
                v.wait_ge(x_high, i + 1)
                v.scalar_tensor_tensor(xT[:, b, 1, :], c.psum[:, b, 0:D], XS, xT[:, b, 0, :], ALU.mult, ALU.subtract
                                       ).then_inc(x_low, 1)

            def g_split(i, b, first):
                v.wait_ge(g_ready, i + 1)
                if not first:
                    v.wait_ge(y_ready, i - 1)
                v.tensor_scalar(gT[:, b, 0, :], g[:, b, :], XS, None, ALU.mult).then_inc(g_high, 1)
                v.wait_ge(g_high, i + 1)
                v.scalar_tensor_tensor(gT[:, b, 1, :], g[:, b, :], XS, gT[:, b, 0, :], ALU.mult, ALU.subtract
                                       ).then_inc(g_low, 1)

            def y_rows(i, b, pair, e):
                v.wait_ge(y_ready, i + 1)
                v.wait_ge(stored[b], pair * 16)
                v.scalar_tensor_tensor(y[:, b, :], c.psum[:, 4 + b, 0:D], 1.0 / (XS * WS),
                                       b2[:, ds(e, 1), :].rearrange("p e d -> p (e d)"), ALU.mult, ALU.add
                                       ).then_inc(y_out, 1)

            v.wait_ge(loaded, c.constants.at(16))
            x_split(0, 0)
            x_split(1, 1)

            def body(q, first, last):
                if not first:
                    e = experts_of(v, q * 2 - 2, 2)
                for b in range(2):
                    i = q * 2 + b
                    if not first:
                        y_rows(i - 2, b, q - 1, e[b])
                    g_split(i, b, first)
                    if not last:
                        x_split(i + 2, b)
            turns(v, body)
            e = experts_of(v, MT - 2, 2)
            for b in range(2):
                y_rows(MT - 2 + b, b, MT // 2 - 1, e[b])

        @block.tensor
        def _(pe):
            def turn_x(i, b, pair):
                pe.wait_ge(x_ready[b], (pair + 1) * 16)
                for k in range(2):
                    last = pe.transpose(c.psum[:, b, k * P:(k + 1) * P], x[:, b, k * P:(k + 1) * P], c.ident[:])
                last.then_inc(turned, 1)

            def hidden(i, b, first, e):
                pe.wait_ge(x_low, i + 1)
                if not first:
                    pe.wait_ge(g_ready, i - 1)
                for m in range(HM):
                    n = 0
                    for k in range(2):
                        for wp, xp in PARTS:
                            n += 1
                            last = pe.matmul(c.psum[:, 2 + b, m * P:(m + 1) * P],
                                             c.w1_16[:, ds(e, 1), k, wp, m * P:(m + 1) * P].rearrange("p e n -> p (e n)"),
                                             xT[:, b, xp, k * P:(k + 1) * P], start=(n == 1), stop=(n == 6))
                last.then_inc(h_ready, 1)

            def result(i, b, pair, e):
                pe.wait_ge(g_low, i + 1)
                pe.wait_ge(y_out, pair * 2)
                n = 0
                for m in range(HM):
                    for wp, gp in PARTS:
                        n += 1
                        last = pe.matmul(c.psum[:, 4 + b, 0:D], gT[:, b, gp, m * P:(m + 1) * P],
                                         c.w2_16[:, ds(e, 1), m, wp, :].rearrange("p e n -> p (e n)"),
                                         start=(n == 1), stop=(n == 3 * HM))
                last.then_inc(y_ready, 1)

            turn_x(0, 0, 0)
            turn_x(1, 1, 0)

            def body(q, first, last):
                e = experts_of(pe, 0, 2) if first else experts_of(pe, q * 2 - 2, 4)
                for b in range(2):
                    i = q * 2 + b
                    hidden(i, b, first, e[b] if first else e[2 + b])
                    if not first:
                        result(i - 2, b, q - 1, e[b])
                    if not last:
                        turn_x(i + 2, b, q + 1)
            turns(pe, body)
            e = experts_of(pe, MT - 2, 2)
            for b in range(2):
                result(MT - 2 + b, b, MT // 2 - 1, e[b])
    c.constants.end(16)


def second_norm(c):
    nc = c.nc
    part = Carver(c.scr, SCR)
    x2, xn3 = part.take([2, 4, D]), part.take([2, 4, D])
    y = part.take([2, 2, 4, D])
    at = part.take([2, 2, 4], I32)
    st, mo, rstd = part.take([2, 4, 6]), part.take([2, 4, 2]), part.take([2, 4])
    wsum = part.take([P])
    w_in, w_vec, w_out = c.sem("norm3_wsum_loaded"), c.sem("norm3_wsum_inverted"), c.sem("norm3_wsum_moved")
    x_in = [c.sem(f"norm3_x1_loaded{h}") for h in range(2)]
    y_in = [c.sem(f"norm3_results_landed{h}") for h in range(2)]
    at_ready, begun, vec, root = c.sem("norm3_indices_ready"), c.passed, c.sem("norm3_vec"), c.sem("norm3_root")
    moments = c.passed
    turned, copied = c.sem("norm3_turned"), c.sem("norm3_copied")
    stored = [c.sem(f"norm3_stored{h}") for h in range(2)]
    PER = 7
    with nc.Block() as block:

        @block.sync
        def _(sp):
            sp.dma_start(wsum[0:NT, :], c.wsum_row.rearrange("a (t n) -> (a t) n", n=P)).then_inc(w_in, 16)
            sp.wait_ge(w_vec, 2)
            sp.dma_start(c.wsum_row.rearrange("a (t n) -> (a t) n", n=P), wsum[0:NT, :]).then_inc(w_out, 16)
            sp.wait_ge(w_out, 16)
            sp.dma_start(c.agg[:, 2, :], c.wsum_row.partition_broadcast(P)).then_inc(w_out, 16)
            with sp.Fori(0, NS) as s:
                for h, (t0, nt) in enumerate(HALVES):
                    sp.wait_ge(stored[h], s * 32)
                    sp.dma_start(x2[:, h, 0:nt, :], c.x1_tab[ds(s * SS + t0 * P, nt * P), :].rearrange("(t p) d -> p t d", p=P)
                                 ).then_inc(x_in[h], 16)
                for h, (t0, nt) in enumerate(HALVES):
                    sp.wait_ge(vec, s * (2 * PER) + (h + 1) * PER)
                    for table, rows in ((c.x2_tab, x2), (c.xn3_tab, xn3)):
                        sp.dma_start(table[ds(s * SS + t0 * P, nt * P), :].rearrange("(t p) d -> p t d", p=P),
                                     rows[:, h, 0:nt, :]).then_inc(stored[h], 16)
            sp.wait_ge(w_out, 32)
            for q in stored:
                sp.wait_ge(q, 32 * NS)

        @block.gpsimd
        def _(g):
            with g.Fori(0, NS) as s:
                for h, (t0, nt) in enumerate(HALVES):
                    g.wait_ge(at_ready, s * 2 + h + 1)
                    g.sem_inc(begun, 1)
                    for n in range(2):
                        for t in range(nt):
                            g.indirect_dma_start(out=y[:, h, n, t, :], out_offset=None, in_=c.slot_y,
                                                 in_offset=bass.IndirectOffsetOnAxis(ap=at[:, h, n, t:t + 1], axis=0)
                                                 ).then_inc(y_in[h], 16)

        @block.vector
        def _(v):
            v.memset(c.agg[:, 0:2, :], 0.0)
            v.wait_ge(w_in, 16)
            v.tensor_scalar(wsum[0:NT, :], wsum[0:NT, :], 1e-6, None, ALU.max).then_inc(w_vec, 1)
            v.wait_ge(w_vec, 1)
            v.reciprocal(wsum[0:NT, :], wsum[0:NT, :]).then_inc(w_vec, 1)
            with v.Fori(0, NS) as s:
                for h, (t0, nt) in enumerate(HALVES):
                    chain = Chain(v, vec, s, 2 * PER, h * PER)
                    v.wait_ge(x_in[h], s * 16 + 16)
                    v.wait_ge(y_in[h], (s + 1) * (2 * nt * 16))
                    chain.done(v.tensor_tensor(x2[:, h, 0:nt, :], x2[:, h, 0:nt, :], y[:, h, 0, 0:nt, :], ALU.add))
                    chain.wait()
                    chain.done(v.tensor_tensor(x2[:, h, 0:nt, :], x2[:, h, 0:nt, :], y[:, h, 1, 0:nt, :], ALU.add))
                    chain.wait()
                    for t in range(nt):
                        ins = v.bn_stats(st[:, h, t, :], x2[:, h, t, :])
                    chain.done(ins)
                    chain.wait()
                    v.sem_inc(moments, 1)
                    for t in range(nt):
                        ins = v.bn_aggr(mo[:, h, t, :], st[:, h, t, :])
                    chain.done(ins)
                    chain.wait()
                    chain.done(v.tensor_scalar(rstd[:, h, 0:nt], mo[:, h, 0:nt, 1], EPS, None, ALU.add))
                    v.wait_ge(root, s * 2 + h + 1)
                    chain.done(v.reciprocal(rstd[:, h, 0:nt], rstd[:, h, 0:nt]))
                    chain.wait()
                    v.wait_ge(turned, s * 2)
                    for t in range(nt):
                        ins = v.tensor_scalar(xn3[:, h, t, :], x2[:, h, t, :], mo[:, h, t, 0:1], rstd[:, h, t:t + 1],
                                              ALU.subtract, ALU.mult)
                    chain.done(ins)

        @block.scalar
        def _(a):
            def indices(s, h):
                t0, nt = HALVES[h]
                a.activation(at[:, h, :, 0:nt], c.result_at[:, :, ds(s * TS + t0, nt)], ACT.Copy).then_inc(at_ready, 1)

            def body(s, last):
                for h, (t0, nt) in enumerate(HALVES):
                    a.wait_ge(vec, s * (2 * PER) + h * PER + 5)
                    a.activation(rstd[:, h, 0:nt], rstd[:, h, 0:nt], ACT.Sqrt).then_inc(root, 1)
                    if not last:
                        indices(s + 1, h)
                    a.wait_ge(turned, s * 2 + h + 1)
                    for k in range(2):
                        ins = a.activation(c.xnT[:, k, ds(s * SS + t0 * P, nt * P)], c.psum[:, 2 * h + k, 0:nt * P], ACT.Copy)
                    ins.then_inc(copied, 1)
            for h in range(2):
                indices(0, h)
            with a.Fori(0, NS - 1) as s:
                body(s, False)
            body(NS - 1, True)

        @block.tensor
        def _(pe):
            with pe.Fori(0, NS) as s:
                for h, (t0, nt) in enumerate(HALVES):
                    pe.wait_ge(vec, s * (2 * PER) + (h + 1) * PER)
                    pe.wait_ge(copied, s * 2)
                    for k in range(2):
                        for t in range(nt):
                            last = pe.transpose(c.psum[:, 2 * h + k, t * P:(t + 1) * P], xn3[:, h, t, k * P:(k + 1) * P],
                                                c.ident[:])
                    last.then_inc(turned, 1)


def gather_third(c):
    part = Carver(c.scr, SCR)
    part.at = (2 * CT * W) + RING * CT * D
    wk, tile, rows = part.take([2, D]), part.take([2, P]), part.take([D])
    low, e, kk = part.take([D]), part.take([D]), part.take([D])
    w_loaded, tile_ready, z_ready = c.constants.sem, c.sem("k_tile_ready"), c.sem("k_products")
    rows_ready, vec, act, sums_done = c.sem("k_rows_loaded"), c.sem("k_vec"), c.sem("k_exp_done"), c.sem("k_sums_done")
    z, sums, ksum = c.psum[:, 2, 0:D], c.psum[:, 3, :], c.psum[:, 4, 0:2]
    PER = 2

    def first(pe):
        pe.matmul(sums, c.zeros[:], c.ones[:, 0:1].broadcast_to([P, 512]), start=True, stop=False, skip_group_check=True)
        pe.matmul(ksum, c.zeros[:], c.ones[:, 0:2], start=True, stop=False, skip_group_check=True)
        pe.wait_ge(w_loaded, c.constants.at(16))

    def products_begin(pe, i, last):
        pe.wait_ge(tile_ready, i + 1)
        pe.wait_ge(vec, i * PER)
        for k in range(2):
            ins = pe.matmul(z, tile[:, k, :], wk[:, k, :], start=(k == 0), stop=(k == 1))
        ins.then_inc(z_ready, 1)

    def products_end(pe, i, last):
        pe.wait_ge(vec, (i + 1) * PER)
        pe.wait_ge(rows_ready, i * 16 + 16)
        n = LAST if last else P
        for k in range(2):
            pe.matmul(sums[:, k * D:(k + 1) * D], rows[0:n, k * P:(k + 1) * P], kk[0:n, :], start=False, stop=last,
                      skip_group_check=True)
        for j in range(2):
            ins = pe.matmul(ksum[:, j:j + 1], kk[0:n, j * P:(j + 1) * P], c.ones[0:n, 0:1], start=False, stop=last,
                            skip_group_check=True)
        ins.then_inc(sums_done, 1)

    def vector(v, i, last, u):
        step = Chain(v, vec, i, PER)
        if u == 1:
            v.wait_ge(z_ready, i + 1)
            v.wait_ge(act, i)
            step.done(v.tensor_scalar(low, z, 0.0, None, ALU.min))
        if u == 3:
            step.k = 1
            v.wait_ge(act, i + 1)
            v.wait_ge(sums_done, i)
            step.done(v.scalar_tensor_tensor(kk, z, 0.0, e, ALU.max, ALU.add))

    def scalar(a, i, last):
        a.wait_ge(z_ready, i)
        a.activation(tile[:], c.xnT[:, :, ds(i * P, P)], ACT.Copy).then_inc(tile_ready, 1)
        a.wait_ge(vec, i * PER + 1)
        a.activation(e, low, ACT.Exp).then_inc(act, 1)

    def sync_first(sp):
        sp.dma_start(wk.rearrange("p a b -> p (a b)"), c.turned_part("L1_mix_Wk", 2 * D)).then_inc(w_loaded, 16)

    def sync(sp, i, last):
        sp.wait_ge(sums_done, i)
        sp.dma_start(rows, c.xn3_tab[ds(i * P, P), :]).then_inc(rows_ready, 16)

    side = dict(tensor_first=first, tensor_begin=products_begin, tensor_end=products_end, vector=vector,
                scalar=scalar, sync_first=sync_first, sync=sync)
    aggregate(c, table=c.xn3_tab, weighted=True, slots=(0, 1), side=side)
    c.constants.end(16)


HEADS1, DH1 = 8, 32


def fold_second_attention(c):
    nc = c.nc
    part = Carver(c.scr, SCR)
    wvT, wprojT = part.take([2, D]), part.take([2, D])
    kxT, ctxT = part.take([2, D]), part.take([2, P])
    ksum = part.take([2])
    loaded, vec, pe_done = c.constants.sem, c.sem("fold1_vec"), c.sem("fold1_products")
    with nc.Block() as block:

        @block.sync
        def _(sp):
            for w, name in ((wvT, "L1_mix_Wv"), (wprojT, "L1_mix_Wproj")):
                sp.dma_start(w.rearrange("p a b -> p (a b)"), c.turned_part(name, 2 * D)).then_inc(loaded, 16)

        @block.vector
        def _(v):
            v.tensor_copy(kxT.rearrange("p a b -> p (a b)"), c.psum[:, 3, :]).then_inc(vec, 1)
            v.tensor_copy(ksum, c.psum[:, 4, 0:2]).then_inc(vec, 1)
            v.wait_ge(vec, 2)
            v.memset(c.small1[:, 0:2 * HEADS1], 0.0).then_inc(vec, 1)
            v.wait_ge(vec, 3)
            of_head = c.bd32.rearrange("p (g d) -> p g d", d=DH1)[:, :, 0]
            for j in range(2):
                at = j * HEADS1 + j * P // DH1
                v.tensor_scalar(c.small1[:, at:at + P // DH1], of_head, ksum[:, j:j + 1], None, ALU.mult)
            v.wait_ge(pe_done, 1)
            v.tensor_tensor(ctxT[:], c.psum[:, 0, 0:2 * P].rearrange("p (j d) -> p j d", d=P),
                            c.bd32[:].unsqueeze(1).broadcast_to([P, 2, P]), ALU.mult).then_inc(vec, 1)
            v.wait_ge(pe_done, 2)
            v.tensor_copy(c.m0[:], c.psum[:, 1, :].rearrange("p (k d) -> p k d", d=D))

        @block.tensor
        def _(pe):
            pe.wait_ge(vec, 2)
            pe.wait_ge(loaded, c.constants.at(32))
            for j in range(2):
                for k in range(2):
                    last = pe.matmul(c.psum[:, 0, j * P:(j + 1) * P], wvT[:, k, j * P:(j + 1) * P],
                                     kxT[:, k, j * P:(j + 1) * P], start=(k == 0), stop=(k == 1))
            last.then_inc(pe_done, 1)
            pe.wait_ge(vec, 4)
            for j in range(2):
                last = pe.matmul(c.psum[:, 1, j * D:(j + 1) * D], ctxT[:, j, :], wprojT[:, j, :], start=True, stop=True)
            last.then_inc(pe_done, 1)
    c.constants.end(32)


def second_layer_sum(c):
    nc = c.nc
    part = Carver(c.scr, SCR)
    w1T, w2T, wqT = part.take([2, D]), part.take([2, D]), part.take([2, D])
    g1T, qT = part.take([2, 2, 512]), part.take([2, 2, 512])
    e, divisor, inverse = part.take([2, 512]), part.take([2, 4 * HEADS1]), part.take([P])
    spread = part.take([4 * HEADS1, DH1])
    y, x2 = part.take([2, 4, D]), part.take([2, 4, D])
    xn4T = part.take([2, 2, 512])
    b2, gamma, beta, bproj = part.take([D]), part.take([D]), part.take([D]), part.take([D])
    gw, gb = part.take([2, GATES]), part.take([GATES])
    st, mo, rstd = part.take([2, 4, 6]), part.take([2, 4, 2]), part.take([2, 4])
    loaded, consts = c.constants.sem, c.sem("last_shift_ready")
    rows_in = [c.sem(f"last_rows_loaded{h}") for h in range(2)]
    scaled, shifted, moved = c.sem("agg_scaled"), c.sem("last_rows_shifted"), c.sem("x3_and_xn4_moved")
    g_pre, gelu_done, q_pre, q_vec, q_exp = (c.sem("last_gelu_products"), c.sem("last_gelu_done"), c.sem("q_products"),
                                             c.sem("q_vec"), c.sem("q_exp_done"))
    div_pre, y_pre, y_read, m_pre, m_read = (c.sem("divisor_products"), c.sem("y_products"), c.sem("y_read"),
                                             c.sem("attention_products"), c.sem("attention_read"))
    vec, root, turned, copied = c.sem("last_vec"), c.sem("last_root"), c.sem("last_turned"), c.sem("last_copied")
    gate_pre, gate_read = c.sem("gate_products"), c.sem("gate_read")
    inverse_copied = c.sem("inverse_copied")
    QV = 4
    DV = 3
    PER = 11
    Y_VAR, Y_DONE, X3, X_VAR = 3, 5, 6, 9
    flat = "p a b -> p (a b)"

    def former(s, h):
        return (s, 0) if h else (s - 1, 1)

    def columns(s, h):
        t0, nt = HALVES[h]
        return ds(s * SS + t0 * P, nt * P)

    def pipeline(engine, slot):
        slot((0, 0), None, None, True)
        slot((0, 1), (0, 0), None, True)
        with engine.Fori(1, NS) as s:
            for h in range(2):
                slot((s, h), former(s, h), (s - 1, h), False)
        slot(None, (NS - 1, 1), (NS - 1, 0), False)
        slot(None, None, (NS - 1, 1), False)

    with nc.Block() as block:

        @block.sync
        def _(sp):
            for w, name in ((w1T, "L1_gnn_W1"), (w2T, "L1_gnn_W2"), (wqT, "L1_mix_Wq")):
                sp.dma_start(w.rearrange(flat), c.turned_part(name, 2 * D)).then_inc(loaded, 16)
            for b, name in ((b2, "L1_gnn_b2"), (gamma, "L1_gnn_gamma"), (beta, "L1_gnn_beta"), (bproj, "L1_mix_bproj"),
                            (gb, "L1_ffn_gb")):
                sp.dma_start(b, c.inp[name].unsqueeze(0).partition_broadcast(P)).then_inc(loaded, 16)
            sp.dma_start(gw, c.inp["L1_ffn_gW"].rearrange("(k p) e -> p k e", p=P)).then_inc(loaded, 16)

            def load(s, h, first):
                t0, nt = HALVES[h]
                if not first:
                    sp.wait_ge(moved, s * 4 - 3 + 2 * h)
                    sp.wait_ge(turned, s * 2 - 1 + h)
                for rows, table in ((y, c.xn3_tab), (x2, c.x2_tab)):
                    sp.dma_start(rows[:, h, 0:nt, :], table[columns(s, h), :].rearrange("(t p) d -> p t d", p=P)
                                 ).then_inc(rows_in[h], 16)
            for h in range(2):
                load(0, h, True)
            with sp.Fori(1, NS) as s:
                for h in range(2):
                    load(s, h, False)
            sp.wait_ge(loaded, c.constants.at(144))

        @block.gpsimd
        def _(g):
            def scale(s, h):
                acc = c.agg[:, 0:2, columns(s, h)]
                g.tensor_tensor(acc, acc, c.agg[:, 2:3, columns(s, h)].broadcast_to([P, 2, HALVES[h][1] * P]), ALU.mult
                                ).then_inc(scaled, 1)

            def shift(s, h):
                t0, nt = HALVES[h]
                g.wait_ge(rows_in[h], s * 32 + 32)
                for rows, by in ((y, b2), (x2, beta)):
                    last = g.tensor_tensor(rows[:, h, 0:nt, :], rows[:, h, 0:nt, :],
                                           by.unsqueeze(1).broadcast_to([P, nt, D]), ALU.add)
                last.then_inc(shifted, 1)

            def move_x3(s, h):
                t0, nt = HALVES[h]
                g.wait_ge(vec, (s * 2 + h) * PER + X3)
                g.sem_inc(c.passed, 1)
                g.tensor_copy(c.agg[:, 0:2, columns(s, h)].rearrange("p k (t n) -> p t k n", n=P),
                              y[:, h, 0:nt, :].rearrange("p t (k n) -> p t k n", n=P)).then_inc(moved, 1)

            def move_xn4(s, h):
                g.wait_ge(copied, s * 2 + h + 1)
                g.sem_inc(c.passed, 1)
                g.tensor_copy(c.xnT[:, :, columns(s, h)], xn4T[:, h, :, 0:HALVES[h][1] * P]).then_inc(moved, 1)

            scale(0, 0)
            g.wait_ge(loaded, c.constants.at(144))
            g.tensor_tensor(beta, beta, bproj, ALU.add).then_inc(consts, 1)
            g.wait_ge(consts, 2)

            def ahead(s, h):
                scale(*((s + 1, 0) if h else (s, 1)))

            def slot(a, b, c_, first):
                if b is not None:
                    move_x3(*b)
                if c_ is not None:
                    move_xn4(*c_)
                if a is not None:
                    shift(*a)

            ahead(0, 0)
            slot((0, 0), None, None, True)
            ahead(0, 1)
            slot((0, 1), (0, 0), None, True)
            with g.Fori(1, NS - 1) as s:
                for h in range(2):
                    ahead(s, h)
                    slot((s, h), former(s, h), (s - 1, h), False)
            s = NS - 1
            ahead(s, 0)
            slot((s, 0), (s - 1, 1), (s - 1, 0), False)
            slot((s, 1), (s, 0), (s - 1, 1), False)
            slot(None, (s, 1), (s, 0), False)
            slot(None, None, (s, 1), False)

        @block.vector
        def _(v):
            v.wait_ge(loaded, c.constants.at(144))
            rows = 4 * HEADS1
            v.tensor_copy(spread[0:rows, :, :], c.ident[0:rows, 0:rows].unsqueeze(2).broadcast_to([rows, rows, DH1])
                          ).then_inc(consts, 1)

            def q_rows(s, h):
                n = HALVES[h][1] * P
                v.wait_ge(q_exp, (s * 2 + h) * 2 + 2)
                v.scalar_tensor_tensor(qT[:, h, :, 0:n], e[:, :, 0:n], 1.0, qT[:, h, :, 0:n], ALU.min, ALU.add
                                       ).then_inc(q_vec, 1)

            def inverses(s, h):
                n = HALVES[h][1] * HEADS1
                chain = Chain(v, q_vec, s * 2 + h, QV, 1)
                v.wait_ge(div_pre, (s * 2 + h) * DV + 1)
                chain.done(v.tensor_scalar(divisor[:, h, 0:n], c.psum[:, 2, 0:n], 1e-6, None, ALU.max))
                chain.wait()
                chain.done(v.reciprocal(divisor[:, h, 0:n], divisor[:, h, 0:n]))

            def q_divided(s, h):
                n = HALVES[h][1] * P
                v.wait_ge(div_pre, (s * 2 + h) * DV + DV)
                q = qT[:, h, :, 0:n]
                v.tensor_tensor(q, q, c.psum[:, 2:4, 0:n], ALU.mult).then_inc(q_vec, 1)

            def variances(chain, h):
                t0, nt = HALVES[h]
                for t in range(nt):
                    ins = v.bn_stats(st[:, h, t, :], y[:, h, t, :])
                chain.done(ins)
                chain.wait()
                v.sem_inc(c.passed, 1)
                for t in range(nt):
                    ins = v.bn_aggr(mo[:, h, t, :], st[:, h, t, :])
                chain.done(ins)
                chain.wait()
                chain.done(v.tensor_scalar(rstd[:, h, 0:nt], mo[:, h, 0:nt, 1], EPS, None, ALU.add))

            def deviations(chain, s, h, which):
                nt = HALVES[h][1]
                v.wait_ge(root, (s * 2 + h) * 2 + which + 1)
                chain.done(v.reciprocal(rstd[:, h, 0:nt], rstd[:, h, 0:nt]))
                chain.wait()

            def y_rows(s, h):
                nt = HALVES[h][1]
                v.wait_ge(y_pre, s * 2 + h + 1)
                v.wait_ge(shifted, s * 2 + h + 1)
                rows = y[:, h, 0:nt, :]
                v.tensor_tensor(rows, rows, c.psum[:, 4:6, :].rearrange(flat)[:, 0:nt * D].rearrange("p (t d) -> p t d", d=D),
                                ALU.add).then_inc(y_read, 1)
                v.wait_ge(y_read, s * 2 + h + 1)
                variances(Chain(v, vec, s * 2 + h, PER), h)

            def y_normed(s, h):
                chain = Chain(v, vec, s * 2 + h, PER, Y_VAR)
                deviations(chain, s, h, 0)
                for t in range(HALVES[h][1]):
                    ins = v.scalar_tensor_tensor(y[:, h, t, :], y[:, h, t, :], mo[:, h, t, 0:1], gamma, ALU.subtract, ALU.mult)
                chain.done(ins)

            def x3_rows(s, h):
                nt = HALVES[h][1]
                chain = Chain(v, vec, s * 2 + h, PER, Y_DONE)
                v.wait_ge(m_pre, s * 2 + h + 1)
                chain.wait()
                mix = c.psum[:, 6:8, :].rearrange(flat)
                for t in range(nt):
                    ins = v.scalar_tensor_tensor(y[:, h, t, :], y[:, h, t, :], rstd[:, h, t:t + 1], mix[:, t * D:(t + 1) * D],
                                                 ALU.mult, ALU.add)
                ins.then_inc(m_read, 1)
                v.wait_ge(m_read, s * 2 + h + 1)
                rows = y[:, h, 0:nt, :]
                chain.done(v.tensor_tensor(rows, rows, x2[:, h, 0:nt, :], ALU.add))
                chain.wait()
                variances(chain, h)

            def xn4_rows(s, h):
                chain = Chain(v, vec, s * 2 + h, PER, X_VAR)
                deviations(chain, s, h, 1)
                for t in range(HALVES[h][1]):
                    ins = v.tensor_scalar(x2[:, h, t, :], y[:, h, t, :], mo[:, h, t, 0:1], rstd[:, h, t:t + 1],
                                          ALU.subtract, ALU.mult)
                chain.done(ins)

            def gates_read(s, h):
                t0, nt = HALVES[h]
                v.wait_ge(gate_pre, s * 2 + h + 1)
                v.tensor_tensor(c.scores[:, ds(s * TS + t0, nt), 0:GATES],
                                c.psum[:, 0, 0:nt * GATES].rearrange("p (t e) -> p t e", e=GATES),
                                gb.unsqueeze(1).broadcast_to([P, nt, GATES]), ALU.add).then_inc(gate_read, 1)

            def slot(a, b, c_, first):
                if a is not None:
                    q_rows(*a)
                    inverses(*a)
                if b is not None:
                    y_rows(*b)
                    y_normed(*b)
                if a is not None:
                    q_divided(*a)
                if b is not None:
                    x3_rows(*b)
                if c_ is not None:
                    gates_read(*c_)
                if b is not None:
                    xn4_rows(*b)
            pipeline(v, slot)

        @block.scalar
        def _(a_):
            def gelu(s, h):
                n = HALVES[h][1] * P
                a_.wait_ge(g_pre, s * 2 + h + 1)
                for m in range(2):
                    last = a_.activation(g1T[:, h, m, 0:n], c.psum[:, m, 0:n], ACT.Gelu, bias=c.column("L1_gnn_b1", m))
                last.then_inc(gelu_done, 1)

            def exp_and_relu(s, h, first):
                n, u = HALVES[h][1] * P, s * 2 + h
                a_.wait_ge(q_pre, u + 1)
                if not (first and h == 0):
                    a_.wait_ge(q_vec, u * QV - QV + 1)
                a_.activation(e[:, :, 0:n], c.psum[:, 2:4, 0:n], ACT.Exp).then_inc(q_exp, 1)
                a_.activation(qT[:, h, :, 0:n], c.psum[:, 2:4, 0:n], ACT.Relu).then_inc(q_exp, 1)

            def rooted(s, h, at):
                nt = HALVES[h][1]
                a_.wait_ge(vec, (s * 2 + h) * PER + at)
                a_.activation(rstd[:, h, 0:nt], rstd[:, h, 0:nt], ACT.Sqrt).then_inc(root, 1)

            def copy(s, h, early):
                n, u = HALVES[h][1] * P, s * 2 + h
                a_.wait_ge(turned, u + 1)
                if not early:
                    a_.wait_ge(moved, u * 2 - 1)
                for k in range(2):
                    last = a_.activation(xn4T[:, h, k, 0:n], c.psum[:, 4 + k, 0:n], ACT.Copy)
                last.then_inc(copied, 1)

            def copy_inverses(s, h):
                n = HALVES[h][1] * HEADS1
                a_.wait_ge(div_pre, (s * 2 + h) * DV + 2)
                a_.activation(inverse[0:n, :], c.psum[0:n, 3, 0:P], ACT.Copy).then_inc(inverse_copied, 1)

            def slot(a, b, c_, first, early=False):
                if a is not None:
                    exp_and_relu(*a, first)
                    gelu(*a)
                if b is not None:
                    rooted(*b, Y_VAR)
                if a is not None:
                    copy_inverses(*a)
                if c_ is not None:
                    copy(*c_, early)
                if b is not None:
                    rooted(*b, X_VAR)
            slot((0, 0), None, None, True)
            slot((0, 1), (0, 0), None, True)
            for h in range(2):
                slot((1, h), former(1, h), (0, h), False, early=True)
            with a_.Fori(2, NS) as s:
                for h in range(2):
                    slot((s, h), former(s, h), (s - 1, h), False)
            slot(None, (NS - 1, 1), (NS - 1, 0), False)
            slot(None, None, (NS - 1, 1), False)

        @block.tensor
        def _(pe):
            pe.wait_ge(loaded, c.constants.at(144))

            def gelu_products(s, h, first):
                n, u = HALVES[h][1] * P, s * 2 + h
                pe.wait_ge(scaled, u + 1)
                pe.wait_ge(gelu_done, u)
                if not first:
                    pe.wait_ge(gate_read, u - 2)
                for m in range(2):
                    for k in range(2):
                        last = pe.matmul(c.psum[:, m, 0:n], w1T[:, k, m * P:(m + 1) * P], c.agg[:, k, columns(s, h)],
                                         start=(k == 0), stop=(k == 1))
                last.then_inc(g_pre, 1)

            def q_products(s, h):
                n, u = HALVES[h][1] * P, s * 2 + h
                pe.wait_ge(q_vec, u * QV)
                for m in range(2):
                    for k in range(2):
                        last = pe.matmul(c.psum[:, 2 + m, 0:n], wqT[:, k, m * P:(m + 1) * P], c.xnT[:, k, columns(s, h)],
                                         start=(k == 0), stop=(k == 1))
                last.then_inc(q_pre, 1)

            def divisors(s, h):
                pe.wait_ge(q_vec, (s * 2 + h) * QV + 1)
                for t in range(HALVES[h][1]):
                    for j in range(2):
                        last = pe.matmul(c.psum[:, 2, t * HEADS1:(t + 1) * HEADS1], qT[:, h, j, t * P:(t + 1) * P],
                                         c.small1[:, j * HEADS1:(j + 1) * HEADS1], start=(j == 0), stop=(j == 1))
                last.then_inc(div_pre, 1)

            def turn_inverses(s, h):
                n = HALVES[h][1] * HEADS1
                pe.wait_ge(q_vec, (s * 2 + h) * QV + 3)
                pe.transpose(c.psum[0:n, 3, 0:P], divisor[:, h, 0:n], c.ident[:]).then_inc(div_pre, 1)

            def spread_inverses(s, h):
                nt = HALVES[h][1]
                n = nt * HEADS1
                heads = P // DH1
                pe.wait_ge(inverse_copied, s * 2 + h + 1)
                for t in range(nt):
                    for j in range(2):
                        at = t * HEADS1 + j * heads
                        last = pe.matmul(c.psum[:, 2 + j, t * P:(t + 1) * P],
                                         spread[0:n, at:at + heads, :].rearrange("p g d -> p (g d)"), inverse[0:n, :],
                                         start=True, stop=True)
                last.then_inc(div_pre, 1)

            def node_rows(bank, lhs, h, w):
                for t in range(HALVES[h][1]):
                    for k in range(2):
                        last = pe.matmul(c.psum[:, bank + t // 2, (t % 2) * D:(t % 2 + 1) * D], lhs[:, h, k, t * P:(t + 1) * P],
                                         w[:, k, :], start=(k == 0), stop=(k == 1))
                return last

            def y_products(s, h, first):
                u = s * 2 + h
                pe.wait_ge(gelu_done, u + 1)
                pe.wait_ge(y_read, u)
                if not first:
                    pe.wait_ge(copied, u - 1)
                node_rows(4, g1T, h, w2T).then_inc(y_pre, 1)

            def attention(s, h, first):
                u = s * 2 + h
                pe.wait_ge(q_vec, u * QV + QV)
                pe.wait_ge(m_read, u)
                node_rows(6, qT, h, c.m0).then_inc(m_pre, 1)

            def turn_rows(s, h, y_rows_read):
                nt, u = HALVES[h][1], s * 2 + h
                pe.wait_ge(vec, (u + 1) * PER)
                pe.wait_ge(y_read, y_rows_read)
                for k in range(2):
                    for t in range(nt):
                        last = pe.transpose(c.psum[:, 4 + k, t * P:(t + 1) * P], x2[:, h, t, k * P:(k + 1) * P], c.ident[:])
                last.then_inc(turned, 1)

            def gate_products(s, h, behind):
                u = s * 2 + h
                pe.wait_ge(copied, u + 1)
                pe.wait_ge(gelu_done, 2 * NS if behind else u + 3)
                if behind:
                    pe.wait_ge(gate_read, u)
                for t in range(HALVES[h][1]):
                    for k in range(2):
                        last = pe.matmul(c.psum[:, 0, t * GATES:(t + 1) * GATES], xn4T[:, h, k, t * P:(t + 1) * P], gw[:, k, :],
                                         start=(k == 0), stop=(k == 1))
                last.then_inc(gate_pre, 1)

            def slot(a, b, c_, first):
                if a is not None:
                    q_products(*a)
                    gelu_products(*a, first)
                    divisors(*a)
                if b is not None:
                    y_products(*b, first)
                if a is not None:
                    turn_inverses(*a)
                if b is not None:
                    attention(*b, first)
                if a is not None:
                    spread_inverses(*a)
                if c_ is not None:
                    turn_rows(*c_, c_[0] * 2 + c_[1] + (2 if b is not None else 1))
                if c_ is not None:
                    gate_products(*c_, a is None)
            pipeline(pe, slot)
    c.constants.end(144)


GATES = 4
EH1, EH2 = 128, 64
SH1, SH2 = 256, 128


class LastWeights:

    def __init__(self, part):
        self.s1, self.s2, self.s3 = part.take([2, SH1]), part.take([2, SH2]), part.take([D])
        self.e1 = part.take([GATES, 2, EH1])
        self.e2 = part.take([GATES, P])
        self.e3 = part.take([GATES // 2, D])
        self.b3 = part.take([D])
        self.pick = part.take([GATES // 2, P])


def gates(c):
    nc = c.nc
    part = Carver(c.scr, SCR)
    w = c.last = LastWeights(part)
    G4 = [NT, GATES]
    rev, p, eq, cand, rest = part.take([GATES]), part.take(G4), part.take(G4), part.take(G4), part.take(G4)
    mask = [part.take(G4), part.take(G4)]
    top, code, weight = part.take([NT]), part.take([NT]), [part.take([NT]), part.take([NT])]
    second = part.take([NT])
    gate5 = part.take([NT, GATES + 1])
    logits = c.scores[:, :, 0:GATES]
    cleared, vec, act = c.sem("last_weights_cleared"), c.sem("gates_vec"), c.sem("gates_exp")
    turned, copied = c.sem("gates_turned"), c.sem("gates_copied")
    groups = -(-NT // 4)
    marks = {}
    n_loads = 3 + 2 * GATES + GATES // 2 + 2
    with nc.Block() as block:

        @block.sync
        def _(sp):
            inp = {n: c.inp["L1_ffn_" + n] for n in ("sW1", "sW2", "sW3", "eW1", "eW2", "eW3", "eb3", "sb3")}
            done = c.constants.sem
            sp.dma_start(w.s1, inp["sW1"].rearrange("(k p) n -> p k n", p=P)).then_inc(done, 16)
            sp.dma_start(w.s2, inp["sW2"].rearrange("(k p) n -> p k n", p=P)).then_inc(done, 16)
            sp.dma_start(w.s3, inp["sW3"]).then_inc(done, 16)
            for e in range(GATES):
                sp.dma_start(w.e1[:, e, :, :], inp["eW1"][e, :, :].rearrange("(k p) n -> p k n", p=P)).then_inc(done, 16)
            for q in range(GATES // 2):
                sp.dma_start(w.e3[:, q, :], inp["eW3"][2 * q:2 * q + 2, :, :].rearrange("e g o -> (e g) o")).then_inc(done, 16)
            sp.dma_start(w.b3[0:GATES, :], inp["eb3"]).then_inc(done, 16)
            sp.dma_start(w.b3[GATES:GATES + 1, :], inp["sb3"].unsqueeze(0)).then_inc(done, 16)
            sp.wait_ge(cleared, 1)
            for e in range(GATES):
                at = (e % 2) * EH2
                sp.dma_start(w.e2[:, e, at:at + EH2], inp["eW2"][e, :, :]).then_inc(done, 16)
            sp.wait_ge(done, c.constants.at(16 * n_loads))

        @block.vector
        def _(v):
            v.memset(w.e2, 0.0).then_inc(cleared, 1)
            for q in range(GATES // 2):
                for b in range(2):
                    e = 2 * q + b
                    v.tensor_copy(w.pick[0:GATES, q, b * EH2:(b + 1) * EH2],
                                  c.ident[0:GATES, e:e + 1].broadcast_to([GATES, EH2]))
            chain = Chain(v, vec)

            def do(ins):
                chain.done(ins)
                chain.wait()

            def over(x):
                return x.unsqueeze(2).broadcast_to([P, NT, GATES])
            rev_b = rev.unsqueeze(1).broadcast_to([P, NT, GATES])
            do(v.tensor_scalar(rev, c.iota[:, 0:GATES], -1.0, float(GATES), ALU.mult, ALU.add))
            do(v.tensor_reduce(top, logits, AX.X, ALU.max))
            do(v.tensor_tensor(p, logits, over(top), ALU.subtract))
            marks["shifted"] = chain.value()
            v.wait_ge(act, 1)
            do(v.tensor_reduce(top, p, AX.X, ALU.add))
            do(v.reciprocal(top, top))
            do(v.tensor_tensor(p, p, over(top), ALU.mult))
            for n, values in enumerate((p, rest)):
                best = (top, second)[n]
                do(v.tensor_reduce(best, values, AX.X, ALU.max))
                do(v.tensor_tensor(eq, values, over(best), ALU.is_equal))
                do(v.tensor_tensor(cand, eq, rev_b, ALU.mult))
                do(v.tensor_reduce(code, cand, AX.X, ALU.max))
                do(v.tensor_tensor(mask[n], rev_b, over(code), ALU.is_equal))
                if n == 0:
                    do(v.scalar_tensor_tensor(rest, mask[0], -2.0, p, ALU.mult, ALU.add))
            do(v.tensor_tensor(second, second, top, ALU.subtract))
            marks["second"] = chain.value()
            v.wait_ge(act, 2)
            do(v.tensor_scalar(top, second, 1.0, None, ALU.add))
            do(v.reciprocal(weight[0], top))
            do(v.tensor_tensor(weight[1], second, weight[0], ALU.mult))
            for n in range(2):
                do(v.tensor_tensor(mask[n], mask[n], over(weight[n]), ALU.mult))
            do(v.memset(gate5[:, :, GATES:GATES + 1], 1.0))
            do(v.tensor_tensor(gate5[:, :, 0:GATES], mask[0], mask[1], ALU.add))
            marks["gates"] = chain.value()

        @block.scalar
        def _(a):
            a.wait_ge(vec, marks["shifted"])
            a.activation(p, p, ACT.Exp).then_inc(act, 1)
            a.wait_ge(vec, marks["second"])
            a.activation(second, second, ACT.Exp).then_inc(act, 1)
            for q in range(groups):
                n = min(4, NT - 4 * q) * P
                a.wait_ge(turned, q + 1)
                a.activation(c.agg[0:GATES + 1, 2, q * 4 * P:q * 4 * P + n], c.psum[0:GATES + 1, q % 8, 0:n], ACT.Copy
                             ).then_inc(copied, 1)

        @block.tensor
        def _(pe):
            pe.wait_ge(vec, marks["gates"])
            for q in range(groups):
                if q >= 8:
                    pe.wait_ge(copied, q - 7)
                for t in range(min(4, NT - 4 * q)):
                    last = pe.transpose(c.psum[0:GATES + 1, q % 8, t * P:(t + 1) * P], gate5[:, 4 * q + t, :], c.ident[:])
                last.then_inc(turned, 1)
    c.constants.end(16 * n_loads)


def second_mixture(c):
    nc = c.nc
    part = Carver(c.scr, SCR)
    LastWeights(part)
    w = c.last
    s1, e1, e2 = part.take([2, 512]), part.take([GATES, 512]), part.take([2, 512])
    s2, e2w = part.take([2, 512]), part.take([2, 2, 512])
    gate = part.take([2, 512])
    rows = part.take([2, 4, D])
    pre, relu = c.sem("mixture_products"), c.sem("mixture_relu_done")
    gate_ready, spread, gated = c.sem("mixture_gates_copied"), c.sem("mixture_gates_spread"), c.sem("mixture_gated")
    out_pre, out_ready = c.sem("out_products"), c.sem("out_rows_ready")
    stored = [c.sem(f"out_stored{h}") for h in range(2)]
    K = 9
    G1 = GATES + 1

    def turns(engine, body):
        body(0, True, False)
        with engine.Fori(1, NS - 1) as s:
            body(s, False, False)
        body(NS - 1, False, True)

    def columns(s, h):
        t0, nt = HALVES[h]
        return ds(s * SS + t0 * P, nt * P)

    with nc.Block() as block:

        @block.sync
        def _(sp):
            def body(s, first, last):
                for h, (t0, nt) in enumerate(HALVES):
                    sp.wait_ge(out_ready, s * 2 + h + 1)
                    if last and h == 1:
                        r0 = (NS - 1) * SS + t0 * P
                        full = nt - 1
                        sp.dma_start(c.out[r0:r0 + full * P, :].rearrange("(t p) d -> p t d", p=P), rows[:, h, 0:full, :]
                                     ).then_inc(stored[h], 16)
                        sp.dma_start(c.out[r0 + full * P:N, :], rows[0:LAST, h, full, :]).then_inc(stored[h], 16)
                    else:
                        sp.dma_start(c.out[columns(s, h), :].rearrange("(t p) d -> p t d", p=P), rows[:, h, 0:nt, :]
                                     ).then_inc(stored[h], 16)
            turns(sp, body)
            sp.wait_ge(stored[0], 16 * NS)
            sp.wait_ge(stored[1], 16 * NS + 16)

        @block.scalar
        def _(a):
            def body(s, first, last):
                for h, (t0, nt) in enumerate(HALVES):
                    n, u = nt * P, s * 2 + h
                    if not first:
                        a.wait_ge(out_pre, u - 1)
                    a.activation(gate[0:G1, h, 0:n], c.agg[0:G1, 2, columns(s, h)], ACT.Copy).then_inc(gate_ready, 1)
                    outs = ([(s1[:, m, :], m, "L1_ffn_sb1", m) for m in range(2)] +
                            [(e1[:, e, :], (2, 3, 0, 1)[e], "L1_ffn_eb1", e) for e in range(GATES)] +
                            [(s2[:, h, :], 2, "L1_ffn_sb2", 0)] + [(e2[:, q, :], q, "L1_ffn_eb2", q) for q in range(2)])
                    for i, (to, bank, bias, j) in enumerate(outs):
                        a.wait_ge(pre, u * K + i + 1)
                        if bias == "L1_ffn_eb2":
                            a.wait_ge(gated, u)
                        a.activation(to[:, 0:n], c.psum[:, bank, 0:n], ACT.Relu, bias=c.column(bias, j)).then_inc(relu, 1)
            turns(a, body)

        @block.vector
        def _(v):
            def gate_rows(s, h):
                t0, nt = HALVES[h]
                u = s * 2 + h
                v.wait_ge(relu, (u + 1) * K)
                v.wait_ge(spread, u + 1)
                v.tensor_tensor(e2w[:, h, :, 0:nt * P], e2[:, :, 0:nt * P], c.psum[:, 4:6, 0:nt * P], ALU.mult
                                ).then_inc(gated, 1)

            def out_rows(s, h):
                t0, nt = HALVES[h]
                v.wait_ge(out_pre, s * 2 + h + 1)
                v.wait_ge(stored[h], s * 16)
                v.tensor_tensor(rows[:, h, 0:nt, :].rearrange("p t (k n) -> p t k n", n=P),
                                c.psum[:, 6:8, :].rearrange("p a b -> p (a b)")[:, 0:nt * D].rearrange(
                                    "p (t k n) -> p t k n", n=P, k=2),
                                c.agg[:, 0:2, columns(s, h)].rearrange("p k (t n) -> p t k n", n=P), ALU.add
                                ).then_inc(out_ready, 1)

            def body(s, first, last):
                if not first:
                    out_rows(s - 1, 1)
                gate_rows(s, 0)
                out_rows(s, 0)
                gate_rows(s, 1)
            turns(v, body)
            out_rows(NS - 1, 1)

        @block.tensor
        def _(pe):
            def hidden(s, h):
                t0, nt = HALVES[h]
                n, u = nt * P, s * 2 + h
                x = [c.xnT[:, k, columns(s, h)] for k in range(2)]
                pe.wait_ge(relu, u * K)
                for m in range(2):
                    for k in range(2):
                        last = pe.matmul(c.psum[:, m, 0:n], w.s1[:, k, m * P:(m + 1) * P], x[k], start=(k == 0), stop=(k == 1))
                    last.then_inc(pre, 1)
                for e in range(GATES):
                    if e >= 2:
                        pe.wait_ge(relu, u * K + e - 1)
                    for k in range(2):
                        last = pe.matmul(c.psum[:, (2, 3, 0, 1)[e], 0:n], w.e1[:, e, k, :], x[k], start=(k == 0), stop=(k == 1))
                    last.then_inc(pre, 1)

            def second(s, h):
                t0, nt = HALVES[h]
                n, u = nt * P, s * 2 + h
                pe.wait_ge(relu, u * K + 3)
                for k in range(2):
                    last = pe.matmul(c.psum[:, 2, 0:n], w.s2[:, k, :], s1[:, k, 0:n], start=(k == 0), stop=(k == 1))
                last.then_inc(pre, 1)
                pe.wait_ge(gate_ready, u + 1)
                pe.wait_ge(gated, u)
                for q in range(2):
                    last = pe.matmul(c.psum[:, 4 + q, 0:n], w.pick[0:GATES, q, :], gate[0:GATES, h, 0:n], start=True, stop=True)
                last.then_inc(spread, 1)
                for q in range(2):
                    pe.wait_ge(relu, u * K + 5 + q)
                    for b in range(2):
                        last = pe.matmul(c.psum[:, q, 0:n], w.e2[:, 2 * q + b, :], e1[:, 2 * q + b, 0:n],
                                         start=(b == 0), stop=(b == 1))
                    last.then_inc(pre, 1)

            def out_products(s, h):
                t0, nt = HALVES[h]
                u = s * 2 + h
                pe.wait_ge(gated, u + 1)
                pe.wait_ge(out_ready, u)
                for t in range(nt):
                    bank = c.psum[:, 6 + t // 2, (t % 2) * D:(t % 2 + 1) * D]
                    at = slice(t * P, (t + 1) * P)
                    pe.matmul(bank, s2[:, h, at], w.s3, start=True, stop=False)
                    for q in range(2):
                        pe.matmul(bank, e2w[:, h, q, at], w.e3[:, q, :], start=False, stop=False)
                    last = pe.matmul(bank, gate[0:G1, h, at], w.b3[0:G1, :], start=False, stop=True)
                last.then_inc(out_pre, 1)

            def body(s, first, last):
                hidden(s, 0)
                if not first:
                    out_products(s - 1, 1)
                second(s, 0)
                hidden(s, 1)
                out_products(s, 0)
                second(s, 1)
            turns(pe, body)
            out_products(NS - 1, 1)


PHASES = (turn_weights, prepare_edges, count_degrees, scale_by_degrees, gather_first, fold_attention, first_conv,
          gather_second, first_layer_sum, route, send_to_experts, experts, second_norm, gather_third,
          fold_second_attention, second_layer_sum, gates, second_mixture)


def build(nc, inputs, out):
    with ExitStack() as ctx:
        core = Core(nc, ctx, inputs, out)
        for phase in PHASES:
            phase(core)


def kernel(**inputs):
    import numpy as _np
    import concourse.bacc as _bacc
    from concourse import mybir as _mybir
    from concourse.bass_utils import run_bass_kernel_spmd as _run

    nc = _bacc.Bacc("TRN2", target_bir_lowering=False, num_devices=1)
    arrays = {name: _np.ascontiguousarray(a) for name, a in inputs.items()}
    dram = {name: nc.dram_tensor("in_" + name, a.shape, _mybir.dt.from_np(a.dtype), kind="ExternalInput").ap()
            for name, a in arrays.items()}
    out = nc.dram_tensor("out", arrays["x"].shape, _mybir.dt.float32, kind="ExternalOutput").ap()
    build(nc, dram, out)
    got = _run(nc, [{"in_" + name: a for name, a in arrays.items()}], core_ids=[0])
    return got.results[0]["out"]
```

```python
from contextlib import ExitStack

import concourse.bass as bass
from concourse import mybir

ALU = mybir.AluOpType
ACT = mybir.ActivationFunctionType
F32 = mybir.dt.float32
F16 = mybir.dt.float16
BF16 = mybir.dt.bfloat16
I32 = mybir.dt.int32
U32 = mybir.dt.uint32
AX = mybir.AxisListType
ds = bass.ds

P = 128
N = 6250
D = 256
E = 100000
NT = -(-N // P)
NP = NT * P
LAST = N - (NT - 1) * P
TS = 7
NS = NT // TS
SS = TS * P
HALVES = ((0, 4), (4, 3))
EPS = 1e-5

ET = 784
CT = 4
NC = ET // CT
RB = 7
RP = ET // RB
W = 128
RING = 4
NI = NC // RING

TURNED = (("L0_mix_Wqkv", 512, 1024, 256), ("L0_mix_Wout", 0, 256, 512), ("L0_gnn_W1", 0, 512, 256),
          ("L0_gnn_W2", 0, 256, 512), ("L1_gnn_W1", 0, 256, 256), ("L1_gnn_W2", 0, 256, 256),
          ("L1_mix_Wq", 0, 256, 256), ("L1_mix_Wk", 0, 256, 256), ("L1_mix_Wv", 256, 256, 256),
          ("L1_mix_Wproj", 0, 256, 256))
TURNED_AT = {}
NBLOCKS = 0
for _name, _r0, _rows, _cols in TURNED:
    TURNED_AT[_name] = NBLOCKS
    NBLOCKS += (_rows // P) * (_cols // P)


EXPERTS, HID = 8, 512
HM = HID // P
REGION = NP + P
MT = (2 * NP + EXPERTS * (P - 1)) // P
MT += MT % 2
XS, WS = 16.0, 1024.0

COLUMNS = (("L0_gnn_g1", 4), ("L0_gnn_b1", 4), ("L0_gnn_g2", 2), ("L0_gnn_b2", 2), ("L0_ffn_b1", 32),
           ("L1_gnn_b1", 2), ("L1_ffn_sb1", 2), ("L1_ffn_sb2", 1), ("L1_ffn_eb1", 4), ("L1_ffn_eb2", 2))
COLUMNS_AT = {}
NCOL = 0
for _name, _n in COLUMNS:
    COLUMNS_AT[_name] = (NCOL, _n)
    NCOL += _n


class Chain:

    def __init__(self, engine, sem, turn=0, per_turn=0, start=0):
        self.engine, self.sem, self.base, self.k = engine, sem, turn * per_turn + start, 0

    def done(self, instruction):
        instruction.then_inc(self.sem, 1)
        self.k += 1
        return instruction

    def value(self):
        return self.base + self.k

    def wait(self):
        self.engine.wait_ge(self.sem, self.value())


class Shared:

    def __init__(self, sem):
        self.sem, self.base = sem, 0

    def at(self, n):
        return self.base + n

    def end(self, n):
        self.base += n


class Carver:

    def __init__(self, region, words):
        self.region, self.words, self.at = region, words, 0

    def take(self, shape, dtype=F32):
        n = 1
        for s in shape:
            n *= s
        size = {F32: 4, I32: 4, U32: 4, BF16: 2, F16: 2}[dtype]
        words = -(-n * size // 4)
        assert self.at + words <= self.words, (self.at, words, self.words)
        view = self.region[:, self.at:self.at + words]
        self.at += words
        if dtype is not F32:
            view = view.bitcast(dtype)
        if len(shape) == 2:
            view = view.rearrange("p (a b) -> p a b", b=shape[1])
        elif len(shape) == 3:
            view = view.rearrange("p (a b c) -> p a b c", b=shape[1], c=shape[2])
        elif len(shape) == 4:
            view = view.rearrange("p (a b c d) -> p a b c d", b=shape[1], c=shape[2], d=shape[3])
        return view


class Core:

    def __init__(self, nc, ctx, inputs, out):
        self.nc, self.ctx, self.inp, self.out = nc, ctx, inputs, out

        def dram(name, shape):
            return nc.dram_tensor(name, shape, F32, kind="Internal").ap()

        self.turned = dram("turned_weights", (P, NBLOCKS * P))
        self.xn_tab = dram("xn_table", (NP, D))
        self.h_tab = dram("h_table", (NP, D))
        self.xn3_tab = dram("xn3_table", (NP, D))
        self.dis_row = dram("dis_row", (1, NP))
        self.wsum_row = dram("wsum_row", (1, NP))
        self.xn2_tab = dram("xn2_table", (NP, D))
        self.slot_x = dram("expert_rows", (EXPERTS * REGION, D))
        self.slot_y = dram("expert_results", (MT * P, D))
        self.x1_tab = dram("x1_table", (NP, D))
        self.x2_tab = dram("x2_table", (NP, D))
        self.xnT = self.sb("xnT", [P, 2, NP], F32)
        self.agg = self.sb("agg", [P, 3, NP], F32)
        self.scr = self.sb("scr", [P, SCR], F32)
        self.ident = self.sb("ident", [P, P], F32)
        self.ones = self.sb("ones", [P, P], F32)
        self.zeros = self.sb("zeros", [P, P], F32)
        self.iota = self.sb("iota", [P, W], F32)
        self.src = self.sb("src_i", [P, ET], I32)
        self.dloc = self.sb("dloc", [P, ET + CT], F32)
        self.w = self.sb("w_edge", [P, ET], F32)
        self.base = self.sb("base", [P, NC], F32)
        self.base_i = self.sb("base_i", [P, NC], I32)
        self.flag_i = self.sb("flag_i", [P, 1], I32)
        self.dis = self.sb("dis_node", [P, NT], F32)
        self.m0 = self.sb("m0", [P, 2, D], F32)
        self.idx = self.sb("index_columns", [P, RING, CT], I32)
        self.w_stat = self.sb("weight_columns", [P, RING, CT], F32)
        self.dst_now = self.sb("slow_destinations_now", [P, CT], F32)
        self.ones16 = self.sb("ones16", [P, P], BF16)
        self.iota16 = self.sb("iota16", [P, W], BF16)
        tail = Carver(self.agg.rearrange("p a b -> p (a b)"), 3 * NP)
        tail.at = 3 * NP - ET
        self.dst_high, self.dst_low = tail.take([ET], BF16), tail.take([ET], BF16)
        self.x_all = self.scr[:, SCR - NT * D:SCR].rearrange("p (t d) -> p t d", d=D)
        self.cols = self.sb("feature_columns", [P, NCOL], F32)
        self.scores = self.sb("expert_scores", [P, NT, EXPERTS], F32)
        self.scatter_to = self.sb("expert_row_of_node", [P, 2, NT], I32)
        self.result_at = self.sb("result_row_of_node", [P, 2, NT], I32)
        self.pad_to = self.sb("expert_pad_rows", [P, EXPERTS], I32)
        self.tile_expert = self.sb("expert_of_tile", [P, MT], I32)
        self.tile_row = self.sb("first_row_of_tile", [P, MT], I32)
        self.bd64 = self.sb("diagonal_blocks64", [P, P], F32)
        self.bd32 = self.sb("diagonal_blocks32", [P, P], F32)
        self.small1 = self.sb("small1", [P, 256], F32)
        self.psum = ctx.enter_context(nc.psum_tensor("psum", [P, 8, 512], F32))
        self.constants = Shared(self.sem("constants_loaded"))
        self.moves = Shared(self.sem("phase_data_moved"))
        self.passed = self.sem("wait_passed")
        self.agg_sems = {}
        self.agg_at = {"fast": {}, "slow": {}}

    def sb(self, name, shape, dtype):
        return self.ctx.enter_context(self.nc.sbuf_tensor(name, shape, dtype))

    def sem(self, name):
        return self.ctx.enter_context(self.nc.semaphore(name))

    def agg_sem(self, name):
        if name not in self.agg_sems:
            self.agg_sems[name] = self.sem(name)
            for counts in self.agg_at.values():
                counts[name] = 0
        return self.agg_sems[name]

    def column(self, name, j=0):
        at, n = COLUMNS_AT[name]
        return self.cols[:, at + j:at + j + 1]

    def columns(self, name):
        at, n = COLUMNS_AT[name]
        return self.cols[:, at:at + n]

    def turned_part(self, name, cols):
        at = TURNED_AT[name] * P
        return self.turned[:, at:at + cols]


SCR = 16384


def make_constants(c):
    nc = c.nc
    const, masks = c.sem("constants_made"), c.sem("masks_cleared")
    with nc.Block() as block:

        @block.gpsimd
        def _(g):
            g.memset(c.ident[:], 0.0).then_inc(const, 1)
            g.iota(c.iota[:], pattern=[[1, W]], base=0, channel_multiplier=0,
                   allow_small_or_imprecise_dtypes=True).then_inc(const, 1)
            g.memset(c.ones[:], 1.0).then_inc(const, 1)
            g.wait_ge(const, 3)
            g.affine_select(out=c.ident[:], in_=c.ident[:], compare_op=ALU.not_equal, fill=1.0, base=0,
                            pattern=[[-1, P]], channel_multiplier=1).then_inc(const, 1)

        @block.vector
        def _(v):
            for m, size in ((c.bd64, 64), (c.bd32, 32)):
                v.memset(m[:], 0.0).then_inc(masks, 1)
            v.wait_ge(masks, 2)
            for m, size in ((c.bd64, 64), (c.bd32, 32)):
                for j in range(0, P, size):
                    v.memset(m[j:j + size, j:j + size], 1.0)


class WeightTurning:

    GROUPS = NBLOCKS // 4
    BANKS = (4, 5, 6)

    def __init__(self, c, words):
        self.c = c
        self.col_rows = words[:, NBLOCKS * P:NBLOCKS * P + P]
        self.flat = words[:, 0:NBLOCKS * P]
        self.blocks = self.flat.rearrange("p (b n) -> p b n", n=P)
        self.turned, self.copied = c.sem("weights_turned"), c.sem("weights_copied")
        self.n_loads = sum(cols // P for _, _, _, cols in TURNED) + len(COLUMNS)

    def sync(self, sp):
        c = self.c
        sources = {"L1_mix_Wk": "L1_mix_Wkv", "L1_mix_Wv": "L1_mix_Wkv"}
        for name, r0, rows, cols in TURNED:
            w = c.inp[sources.get(name, name)]
            nro = rows // P
            for ci in range(cols // P):
                at = TURNED_AT[name] + ci * nro
                sp.dma_start(self.blocks[:, at:at + nro, :],
                             w[r0:r0 + rows, ci * P:(ci + 1) * P].rearrange("(r p) n -> p r n", p=P)
                             ).then_inc(c.constants.sem, 16)
        for name, n in COLUMNS:
            at = COLUMNS_AT[name][0]
            w = c.inp[name]
            flat = w.rearrange("e n -> (e n)") if len(w.shape) == 2 else w
            sp.dma_start(self.col_rows[at:at + n, :], flat.rearrange("(r n) -> r n", n=P)).then_inc(c.constants.sem, 16)
        sp.wait_ge(self.copied, self.GROUPS)
        sp.dma_start(c.turned, self.flat).then_inc(c.moves.sem, 16)
        sp.wait_ge(c.moves.sem, c.moves.at(16))

    def tensor(self, pe):
        c = self.c
        pe.wait_ge(c.constants.sem, c.constants.at(16 * self.n_loads))
        for q in range(self.GROUPS + 1):
            bank = self.BANKS[q % len(self.BANKS)]
            if q >= len(self.BANKS):
                pe.wait_ge(self.copied, q - len(self.BANKS) + 1)
            if q < self.GROUPS:
                for b in range(4):
                    last = pe.transpose(c.psum[:, bank, b * P:(b + 1) * P], self.blocks[:, 4 * q + b, :], c.ident[:])
            else:
                last = pe.transpose(c.psum[:, bank, 0:NCOL], self.col_rows[0:NCOL, :], c.ident[0:NCOL, 0:NCOL])
            last.then_inc(self.turned, 1)

    def scalar(self, a):
        c = self.c
        for q in range(self.GROUPS + 1):
            bank = self.BANKS[q % len(self.BANKS)]
            a.wait_ge(self.turned, q + 1)
            if q < self.GROUPS:
                a.activation(self.flat[:, q * 512:(q + 1) * 512], c.psum[:, bank, :], ACT.Copy).then_inc(self.copied, 1)
            else:
                a.activation(c.cols[:], c.psum[:, bank, 0:NCOL], ACT.Copy)


def prepare_edges(c):
    nc = c.nc
    part = Carver(c.agg.rearrange("p a b -> p (a b)"), 2 * NP)
    rows = ET // RB
    full = E // P - (RB - 1) * RP
    rest = E % P
    dst_r, src_r = part.take([RB, P], I32), part.take([RB, P], I32)
    att_r = part.take([RB, P * 3])
    att_v = att_r.rearrange("p b (j f) -> p b j f", f=3)
    lists = part.take([3, RB * P])
    norm = part.take([RB, P])
    dstT = part.take([ET])
    ends = part.take([2, NC])
    ends_all = part.take([2, NC])
    spread, flag = part.take([NC]), part.take([1])
    dst_i, high, splits = part.take([ET], I32), part.take([ET]), c.sem("destinations_split")
    fill, loaded, x_loaded = c.sem("edges_filled"), c.constants.sem, c.moves.sem
    vec, root, turn, most = c.sem("edges_vec"), c.sem("edges_root"), c.sem("edges_turned"), c.sem("edges_most")
    n_dst = (RB - 1) * RP * P
    with nc.Block() as block:

        @block.sync
        def _(sp):
            sp.wait_ge(fill, 3)
            for r, source in ((dst_r, c.inp["dst"]), (src_r, c.inp["src"])):
                sp.dma_start(r[0:RP, 0:RB - 1, :], source[0:n_dst].rearrange("(b p j) -> p b j", p=RP, j=P)
                             ).then_inc(loaded, 16)
                sp.dma_start(r[0:full, RB - 1, :], source[n_dst:E - rest].rearrange("(p j) -> p j", j=P)
                             ).then_inc(loaded, 16)
                sp.dma_start(r[full:full + 1, RB - 1, 0:rest], source[E - rest:E].rearrange("(p j) -> p j", p=1)
                             ).then_inc(loaded, 16)

        @block.scalar
        def _(a):
            att = c.inp["edge_attr_3"]
            a.wait_ge(fill, 3)
            a.dma_start(att_r[0:RP, 0:RB - 1, :],
                        att[0:n_dst, :].rearrange("(b p j) f -> p b (j f)", p=RP, j=P)).then_inc(loaded, 16)
            a.dma_start(att_r[0:full, RB - 1, :],
                        att[n_dst:E - rest, :].rearrange("(p j) f -> p (j f)", j=P)).then_inc(loaded, 16)
            a.dma_start(att_r[full:full + 1, RB - 1, 0:rest * 3],
                        att[E - rest:E, :].rearrange("(p j) f -> p (j f)", p=1)).then_inc(loaded, 16)
            x, whole = c.inp["x"], (NT - 1) * P
            a.dma_start(c.x_all[:, 0:NT - 1, :], x[0:whole, :].rearrange("(t p) d -> p t d", p=P)).then_inc(x_loaded, 16)
            a.wait_ge(fill, 4)
            a.dma_start(c.x_all[0:LAST, NT - 1, :], x[whole:N, :]).then_inc(x_loaded, 16)
            a.wait_ge(vec, 4)
            a.activation(norm[0:RP], norm[0:RP], ACT.Sqrt).then_inc(root, 1)
            a.wait_ge(root, 1)
            a.activation(norm[0:RP], norm[0:RP], ACT.Exp, scale=-4.0).then_inc(root, 1)
            a.wait_ge(x_loaded, c.moves.at(32))

        @block.vector
        def _(v):
            v.memset(dst_r[0:RP, RB - 1, :], N).then_inc(fill, 1)
            v.memset(src_r[0:RP, RB - 1, :], 0).then_inc(fill, 1)
            v.memset(att_r[0:RP, RB - 1, :], 0.0).then_inc(fill, 1)
            v.memset(c.x_all[:, NT - 1, :], 0.0).then_inc(fill, 1)
            v.memset(c.zeros[:], 0.0)
            v.memset(c.ones16[:], 1.0)
            v.tensor_copy(c.iota16[:], c.iota[:])
            step, split = Chain(v, vec), Chain(v, splits)
            v.wait_ge(loaded, c.constants.at(9 * 16))
            step.done(v.tensor_tensor(att_r[0:RP], att_r[0:RP], att_r[0:RP], ALU.mult))
            step.done(v.tensor_copy(lists[0:RP, 0, :], dst_r[0:RP].rearrange("p b j -> p (b j)")))
            step.wait()
            step.done(v.tensor_reduce(norm[0:RP], att_v[0:RP], AX.X, ALU.add))
            step.wait()
            step.done(v.tensor_scalar(norm[0:RP], norm[0:RP], 1e-12, None, ALU.add))
            step.done(v.tensor_copy(lists[0:RP, 1, :], src_r[0:RP].rearrange("p b j -> p (b j)")))
            v.wait_ge(root, 2)
            step.done(v.tensor_scalar(lists[0:RP, 2, :], norm[0:RP].rearrange("p b j -> p (b j)"), 0.0, None, ALU.max))
            for n, target in enumerate((dstT, c.src, c.w)):
                v.wait_ge(turn, n + 1)
                step.done(v.tensor_copy(target[:, 0:4 * RP], c.psum[:, 2 * n, 0:4 * RP]))
                step.done(v.tensor_copy(target[:, 4 * RP:ET], c.psum[:, 2 * n + 1, 0:3 * RP]))
            step.wait()
            split.done(v.tensor_copy(dst_i, dstT))
            split.wait()
            split.done(v.tensor_single_scalar(dst_i, dst_i, 7, ALU.arith_shift_right))
            split.wait()
            split.done(v.tensor_copy(c.dst_high, dst_i))
            split.done(v.tensor_copy(high, dst_i))
            split.wait()
            v.scalar_tensor_tensor(c.dst_low, high, -float(P), dstT, ALU.mult, ALU.add)
            chunks = dstT.rearrange("p (c t) -> p c t", t=CT)
            step.done(v.tensor_reduce(ends[:, 0, :], chunks, AX.X, ALU.min, negate=True))
            step.done(v.tensor_reduce(ends[:, 1, :], chunks, AX.X, ALU.max))
            v.wait_ge(most, 1)
            step.done(v.tensor_scalar(c.base[:], ends_all[:, 0, :], float(W - NP), -1.0, ALU.max, ALU.mult))
            step.done(v.memset(c.dloc[:, ET:ET + CT], -1.0))
            step.wait()
            step.done(v.tensor_copy(c.base_i[:], c.base[:]))
            step.done(v.tensor_tensor(c.dloc[:, 0:ET].rearrange("p (c t) -> p c t", t=CT), chunks,
                                      c.base[:].unsqueeze(2).broadcast_to([P, NC, CT]), ALU.subtract))
            step.done(v.tensor_tensor(spread, ends_all[:, 1, :], c.base[:], ALU.subtract))
            step.wait()
            step.done(v.tensor_reduce(flag, spread, AX.X, ALU.max))
            step.wait()
            step.done(v.tensor_scalar(c.flag_i[:], flag, float(W), None, ALU.is_ge))

        @block.tensor
        def _(pe):
            for n, ready in enumerate((2, 5, 6)):
                pe.wait_ge(vec, ready)
                for b in range(RB):
                    out = c.psum[:, 2 * n + b // 4, (b % 4) * RP:(b % 4 + 1) * RP]
                    last = pe.transpose(out, lists[0:RP, n, b * P:(b + 1) * P], c.ident[0:RP, 0:RP])
                last.then_inc(turn, 1)

        @block.gpsimd
        def _(g):
            g.wait_ge(vec, 14)
            g.partition_all_reduce(ends_all.rearrange("p a b -> p (a b)"), ends.rearrange("p a b -> p (a b)"), P,
                                   bass.bass_isa.ReduceOp.max).then_inc(most, 1)
    c.constants.end(9 * 16)
    c.moves.end(32)


def aggregate(c, table, weighted=False, slots=(), side=None):
    nc = c.nc
    part = Carver(c.scr, SCR)
    hot, rows, iota = part.take([2, CT, W]), part.take([RING, CT, D]), c.iota
    S = c.agg_sem
    hot_ready, summed, added = S("onehot_ready"), S("chunk_summed"), S("window_added")
    idx_ready, begun, now_ready = S("indices_ready"), c.passed, S("slow_destinations_ready")
    landed = [S(f"rows_landed{u}") for u in range(RING)]
    nslot = len(slots)
    acc = c.agg[:, 0:nslot, :]
    bank = [c.psum[:, b, 0:nslot * W].rearrange("p (s w) -> p s w", w=W) for b in range(2)]
    flag = c.flag_i[0:1, 0:1]
    side = side or {}

    class Values:

        def __init__(self, way):
            self.at = dict(c.agg_at[way])

        def hot(self, n):
            return self.at["onehot_ready"] + n

        def summed(self, n):
            return self.at["chunk_summed"] + RING + n

        def added(self, n):
            return self.at["window_added"] + 2 + n

        def idx(self, n):
            return self.at["indices_ready"] + n

        def now(self, n):
            return self.at["slow_destinations_ready"] + n

        def landed(self, u, n):
            return self.at[f"rows_landed{u}"] + 16 * CT * n

    fast, slow = Values("fast"), Values("slow")

    def products(pe, b, u, hot_b):
        for s, what in enumerate(slots):
            for t in range(CT):
                if what == "weight":
                    lhs = c.w_stat[:, u, t:t + 1].broadcast_to([P, P])
                else:
                    lhs = rows[:, u, t, what * P:(what + 1) * P]
                last = pe.matmul(bank[b][:, s, :], lhs, hot[:, hot_b, t, :], start=(t == 0), stop=(t == CT - 1))
        return last

    def run_side(engine_name, *args):
        if engine_name in side:
            side[engine_name](*args)

    def side_alone(engine, names):
        if any(n in side for n in names):
            def turn(i, last):
                for n in names:
                    if n == "vector":
                        for u in range(RING):
                            side[n](engine, i, last, u)
                    else:
                        run_side(n, engine, i, last)
            with engine.Fori(0, NI - 1) as i:
                turn(i, False)
            turn(NI - 1, True)

    with nc.Block() as block:

        @block.vector
        def _(v):
            v.sem_inc(added, 2)
            is_slow = v.value_load(flag, min_val=0, max_val=1)

            def onehots(tiles, b, dst):
                for t in range(CT):
                    if weighted:
                        last = v.tensor_scalar(hot[:, b, t, :], iota[:], dst(t), c.w[:, ds(tiles + t, 1)],
                                               ALU.is_equal, ALU.mult)
                    else:
                        last = v.tensor_scalar(hot[:, b, t, :], iota[:], dst(t), None, ALU.is_equal)
                last.then_inc(hot_ready, 1)

            def indices(ch, u):
                if "weight" in slots:
                    v.tensor_copy(c.w_stat[:, u, :], c.w[:, ds(ch * CT, CT)])
                v.tensor_copy(c.idx[:, u, :], c.src[:, ds(ch * CT, CT)]).then_inc(idx_ready, 1)

            with v.If(is_slow < 1):
                for ch in range(RING - 1):
                    indices(ch, ch)
                onehots(0, 0, lambda t: c.dloc[:, t:t + 1])

                def turn(i, last):
                    _, firsts = nc.values_load_multi_w_load_instructions(c.base_i[0:1, ds(i * RING, RING)],
                                                                         engines=[v.engine], min_val=0, max_val=NP - W)
                    for u in range(RING):
                        ch = i * RING + u
                        v.wait_ge(summed, fast.summed(ch))
                        if not (last and u == RING - 1):
                            onehots((ch + 1) * CT, (u + 1) % 2, lambda t: c.dloc[:, ds((ch + 1) * CT + t, 1)])
                        if not (last and u > 0):
                            indices(ch + RING - 1, (u + RING - 1) % RING)
                        if "vector" in side:
                            side["vector"](v, i, last, u)
                        v.wait_ge(summed, fast.summed(ch + 1))
                        v.wait_ge(added, fast.added(ch))
                        window = acc[:, :, ds(firsts[u], W)]
                        v.tensor_tensor(window, window, bank[u % 2], ALU.add).then_inc(added, 1)
                with v.Fori(0, NI - 1) as i:
                    turn(i, False)
                turn(NI - 1, True)
            with v.Else():
                side_alone(v, ["vector"])
                with v.Fori(0, NC) as ch:
                    v.wait_ge(summed, slow.summed(ch * NT))
                    indices(ch, 0)
                    v.wait_ge(now_ready, slow.now(ch * (NT + 1)))
                    v.tensor_scalar(c.dst_now[:], c.dloc[:, ds(ch * CT, CT)], c.base[:, ds(ch, 1)], None, ALU.add
                                    ).then_inc(now_ready, 1)
                    with v.Fori(0, NT) as win:
                        n = ch * NT + win
                        v.wait_ge(now_ready, slow.now(ch * (NT + 1) + win + 1))
                        v.wait_ge(summed, slow.summed(n))
                        onehots(ch * CT, 0, lambda t: c.dst_now[:, t:t + 1])
                        v.tensor_scalar(c.dst_now[:], c.dst_now[:], float(-W), None, ALU.add).then_inc(now_ready, 1)
                        v.wait_ge(summed, slow.summed(n + 1))
                        v.wait_ge(added, slow.added(n))
                        window = acc[:, :, ds(win * W, W)]
                        v.tensor_tensor(window, window, bank[0], ALU.add).then_inc(added, 1)

        @block.tensor
        def _(pe):
            pe.sem_inc(summed, RING)
            if "tensor_first" in side:
                side["tensor_first"](pe)
            is_slow = pe.value_load(flag, min_val=0, max_val=1)
            with pe.If(is_slow < 1):
                def turn(i, last):
                    run_side("tensor_begin", pe, i, last)
                    for u in range(RING):
                        ch = i * RING + u
                        pe.wait_ge(hot_ready, fast.hot(ch + 1))
                        pe.wait_ge(landed[u], fast.landed(u, i + 1))
                        if "weight" in slots:
                            pe.wait_ge(idx_ready, fast.idx(ch + 1))
                        pe.wait_ge(added, fast.added(ch - 1))
                        products(pe, u % 2, u, u % 2).then_inc(summed, 1)
                    run_side("tensor_end", pe, i, last)
                with pe.Fori(0, NI - 1) as i:
                    turn(i, False)
                turn(NI - 1, True)
            with pe.Else():
                side_alone(pe, [n for n in ("tensor_begin", "tensor_end") if n in side])
                with pe.Fori(0, NC) as ch:
                    with pe.Fori(0, NT) as win:
                        pe.wait_ge(hot_ready, slow.hot(ch * NT + win + 1))
                        pe.wait_ge(landed[0], slow.landed(0, ch + 1))
                        if "weight" in slots:
                            pe.wait_ge(idx_ready, slow.idx(ch + 1))
                        pe.wait_ge(added, slow.added(ch * NT + win))
                        products(pe, 0, 0, 0).then_inc(summed, 1)

        @block.gpsimd
        def _(g):
            is_slow = g.value_load(flag, min_val=0, max_val=1)

            def gather(u, value):
                g.wait_ge(idx_ready, value)
                g.sem_inc(begun, 1)
                for t in range(CT):
                    g.indirect_dma_start(out=rows[:, u, t, :], out_offset=None, in_=table,
                                         in_offset=bass.IndirectOffsetOnAxis(ap=c.idx[:, u, t:t + 1], axis=0)
                                         ).then_inc(landed[u], 16)

            with g.If(is_slow < 1):
                with g.Fori(0, NI) as i:
                    for u in range(RING):
                        gather(u, fast.idx(i * RING + u + 1))
            with g.Else():
                with g.Fori(0, NC) as ch:
                    gather(0, slow.idx(ch + 1))

        if "scalar" in side:
            @block.scalar
            def _(a):
                with a.Fori(0, NI - 1) as i:
                    side["scalar"](a, i, False)
                side["scalar"](a, NI - 1, True)

        @block.sync
        def _(sp):
            if "sync_first" in side:
                side["sync_first"](sp)
            if "sync" in side:
                with sp.Fori(0, NI - 1) as i:
                    side["sync"](sp, i, False)
                side["sync"](sp, NI - 1, True)

    windows = {"fast": NC, "slow": NC * NT}
    for way, counts in c.agg_at.items():
        counts["onehot_ready"] += windows[way]
        counts["chunk_summed"] += windows[way] + RING
        counts["window_added"] += windows[way] + 2
        if way == "slow":
            counts["slow_destinations_ready"] += NC * (NT + 1)
        counts["indices_ready"] += NC
        for u in range(RING):
            counts[f"rows_landed{u}"] += 16 * CT * (NC if way == "slow" and u == 0 else 0 if way == "slow" else NI)


BT = 14
BLOCKS = ET // BT // NS


def count_degrees(c):
    nc = c.nc
    words = c.agg.rearrange("p a b -> p (a b)")
    weights = WeightTurning(c, words)
    part = Carver(words, 3 * NP - ET)
    part.at = NBLOCKS * P + P
    tiles, places = part.take([2, BT, NT], BF16), part.take([2, BT, P], BF16)
    xn = part.take([TS, D])
    st, mo, rstd = part.take([TS, 6]), part.take([TS, 2]), part.take([TS])
    hot, used = c.sem("count_onehots"), c.sem("onehots_used")
    vec, root, turned, copied = c.sem("norm1_vec"), c.sem("norm1_root"), c.sem("norm1_turned"), c.sem("norm1_copied")
    PER = 5
    MIDDLE = NS // 2
    counts = c.psum[0:NT, 7, 0:P]

    def onehots(v, s, n):
        v.wait_ge(used, s * BLOCKS + n)
        for out, dst, width in ((tiles, c.dst_high, NT), (places, c.dst_low, P)):
            last = v.tensor_tensor(out[:, n % 2, :, :], c.iota16[:, 0:width].unsqueeze(1).broadcast_to([P, BT, width]),
                                   dst[:, ds((s * BLOCKS + n) * BT, BT)].unsqueeze(2).broadcast_to([P, BT, width]),
                                   ALU.is_equal)
        last.then_inc(hot, 1)

    with nc.Block() as block:

        @block.vector
        def _(v):
            with v.Fori(0, NS) as s:
                step = Chain(v, vec, s, PER)
                for n in range(BLOCKS):
                    onehots(v, s, n)
                    if n == 0:
                        step.wait()
                        for t in range(TS):
                            ins = v.bn_stats(st[:, t, :], c.x_all[:, ds(s * TS + t, 1), :].rearrange("p t d -> p (t d)"))
                        step.done(ins)
                    if n == 1:
                        step.wait()
                        v.sem_inc(c.passed, 1)
                        for t in range(TS):
                            ins = v.bn_aggr(mo[:, t, :], st[:, t, :])
                        step.done(ins)
                        step.wait()
                        step.done(v.tensor_scalar(rstd, mo[:, :, 1], EPS, None, ALU.add))
                    if n == 2:
                        v.wait_ge(root, s + 1)
                        step.done(v.reciprocal(rstd, rstd))
                        step.wait()
                        v.wait_ge(turned, s)
                        v.wait_ge(copied, s)
                        for t in range(TS):
                            ins = v.tensor_scalar(xn[:, t, :], c.x_all[:, ds(s * TS + t, 1), :].rearrange("p t d -> p (t d)"),
                                                  mo[:, t, 0:1], rstd[:, t:t + 1], ALU.subtract, ALU.mult)
                        step.done(ins)

        @block.scalar
        def _(a):
            def step(s):
                a.wait_ge(vec, s * PER + 3)
                a.activation(rstd, rstd, ACT.Sqrt).then_inc(root, 1)
                a.wait_ge(vec, s * PER + PER)
                a.activation(c.x_all[:, ds(s * TS, TS), :], xn, ACT.Copy)
                a.wait_ge(turned, s + 1)
                for k in range(2):
                    for h, (t0, nt) in enumerate(HALVES):
                        ins = a.activation(c.xnT[:, k, ds(s * SS + t0 * P, nt * P)], c.psum[:, 2 * k + h, 0:nt * P], ACT.Copy)
                ins.then_inc(copied, 1)

            with a.Fori(0, MIDDLE) as s:
                step(s)
            weights.scalar(a)
            with a.Fori(MIDDLE, NS) as s:
                step(s)

        @block.tensor
        def _(pe):
            pe.matmul(counts, c.zeros[:, 0:NT], c.zeros[:], start=True, stop=False, skip_group_check=True
                      ).then_inc(used, 1)

            def step(s):
                for n in range(BLOCKS):
                    pe.wait_ge(hot, s * BLOCKS + n + 1)
                    for t in range(BT):
                        last = pe.matmul(counts, tiles[:, n % 2, t, :], places[:, n % 2, t, :], start=False, stop=False,
                                         skip_group_check=True)
                    last.then_inc(used, 1)
                    if n == 4:
                        pe.wait_ge(vec, s * PER + PER)
                        pe.wait_ge(copied, s)
                        for k in range(2):
                            for t in range(TS):
                                last = pe.transpose(c.psum[:, 2 * k + t // 4, (t % 4) * P:(t % 4 + 1) * P],
                                                    xn[:, t, k * P:(k + 1) * P], c.ident[:])
                        last.then_inc(turned, 1)

            with pe.Fori(0, MIDDLE) as s:
                step(s)
            weights.tensor(pe)
            with pe.Fori(MIDDLE, NS) as s:
                step(s)

        @block.sync
        def _(sp):
            weights.sync(sp)
    c.constants.end(16 * weights.n_loads)
    c.moves.end(16)


def scale_by_degrees(c):
    nc = c.nc
    part = Carver(c.scr, SCR - NT * D)
    dis49 = part.take([P])[0:NT, :]
    row, own, wide = c.sem("dis_row_moved"), c.sem("dis_steps"), c.constants.sem
    stored, scaled_a, scaled_v = c.moves.sem, c.sem("xn_scaled_a"), c.sem("xn_scaled_v")
    by_tile = c.dis_row.rearrange("a (t n) -> (a t) n", n=P)
    table = c.xn_tab.rearrange("(t p) d -> p t d", p=P)
    PIECES = ((0, 14), (14, 28), (28, 39), (39, NT))
    with nc.Block() as block:

        @block.sync
        def _(sp):
            sp.wait_ge(own, 3)
            sp.dma_start(by_tile, dis49).then_inc(row, 16)
            sp.wait_ge(row, 16)
            sp.dma_start(c.agg[:, 2, :], c.dis_row.partition_broadcast(P)).then_inc(wide, 16)
            for n, (a, b) in enumerate(PIECES):
                sp.wait_ge(scaled_v if n < 2 else scaled_a, n % 2 + 1)
                sp.dma_start(table[:, a:b, :], c.x_all[:, a:b, :]).then_inc(stored, 16)
            sp.wait_ge(stored, c.moves.at(16 * len(PIECES)))

        @block.vector
        def _(v):
            v.tensor_scalar(dis49, c.psum[0:NT, 7, 0:P], 1.0, None, ALU.add).then_inc(own, 1)
            v.wait_ge(own, 2)
            v.reciprocal(dis49, dis49).then_inc(own, 1)
            v.wait_ge(own, 4)
            v.tensor_copy(c.dis[:], c.psum[:, 6, 0:NT]).then_inc(own, 1)
            v.wait_ge(own, 5)
            for a, b in PIECES[:2]:
                v.tensor_tensor(c.x_all[:, a:b, :], c.x_all[:, a:b, :], c.dis[:, a:b].unsqueeze(2).broadcast_to([P, b - a, D]),
                                ALU.mult).then_inc(scaled_v, 1)
            v.wait_ge(wide, c.constants.at(16))
            for k in range(2):
                v.tensor_tensor(c.agg[:, k, :], c.xnT[:, k, :], c.agg[:, 2, :], ALU.mult)

        @block.scalar
        def _(s):
            s.wait_ge(own, 1)
            s.activation(dis49, dis49, ACT.Sqrt).then_inc(own, 1)
            s.wait_ge(own, 5)
            for a, b in PIECES[2:]:
                for t in range(a, b):
                    last = s.activation(c.x_all[:, t, :], c.x_all[:, t, :], ACT.Copy, scale=c.dis[:, t:t + 1])
                last.then_inc(scaled_a, 1)

        @block.tensor
        def _(pe):
            pe.wait_ge(own, 3)
            pe.transpose(c.psum[:, 6, 0:NT], dis49, c.ident[0:NT, 0:NT]).then_inc(own, 1)
    c.constants.end(16)
    c.moves.end(16 * len(PIECES))


HEADS0, DH0 = 8, 64
PAIRS = HEADS0 // 2


def gather_first(c):
    part = Carver(c.scr, SCR)
    part.at = (2 * CT * W) + RING * CT * D
    wkv = part.take([2, 2 * HEADS0 * DH0])
    tile = part.take([2, P])
    G = 2 * HEADS0
    cen, sq, kv = part.take([G, DH0]), part.take([G, DH0]), part.take([G, DH0])
    mean, var = part.take([G]), part.take([G])
    flat = "p a b -> p (a b)"
    w_loaded, tile_ready, kv_ready = c.constants.sem, c.sem("kv_tile_ready"), c.sem("kv_ready")
    vec, act, dots = c.sem("kv_vec"), c.sem("kv_act"), c.sem("dots_done")
    both = c.psum[:, 2:4, :].rearrange("p a b -> p (a b)").rearrange("p (g d) -> p g d", d=DH0)
    sums = c.psum[:, 4, :]
    PER = 7

    def first(pe):
        pe.matmul(sums, c.zeros[:], c.ones[:, 0:1].broadcast_to([P, 512]), start=True, stop=False,
                  skip_group_check=True)
        pe.wait_ge(w_loaded, c.constants.at(16))

    def products_begin(pe, i, last):
        pe.wait_ge(tile_ready, i + 1)
        pe.wait_ge(vec, i * PER)
        for half in range(2):
            for k in range(2):
                ins = pe.matmul(c.psum[:, 2 + half, :], tile[:, k, :], wkv[:, k, half * 512:(half + 1) * 512],
                                start=(k == 0), stop=(k == 1))
        ins.then_inc(kv_ready, 1)

    def products_end(pe, i, last):
        pe.wait_ge(vec, (i + 1) * PER)
        for q in range(PAIRS):
            ins = pe.matmul(sums[:, q * P:(q + 1) * P],
                            kv.rearrange(flat)[:, 512 + q * P:512 + (q + 1) * P],
                            kv.rearrange(flat)[:, q * P:(q + 1) * P], start=False, stop=last,
                            skip_group_check=True)
        ins.then_inc(dots, 1)

    def vector(v, i, last, u):
        if u == 0:
            return
        step = Chain(v, vec, i, PER)
        if u == 1:
            v.wait_ge(kv_ready, i + 1)
            step.done(v.tensor_reduce(mean, both, AX.X, ALU.add))
            step.wait()
            step.done(v.tensor_scalar(mean, mean, 1.0 / DH0, None, ALU.mult))
            step.wait()
            v.wait_ge(act, i * 3)
            step.done(v.tensor_tensor(cen, both, mean.unsqueeze(2).broadcast_to([P, G, DH0]), ALU.subtract))
        if u == 2:
            step.k = 3
            v.wait_ge(act, i * 3 + 2)
            step.done(v.tensor_reduce(var, sq, AX.X, ALU.add))
            step.wait()
            step.done(v.tensor_scalar(var, var, 1.0 / DH0, EPS, ALU.mult, ALU.add))
        if u == 3:
            step.k = 5
            v.wait_ge(act, i * 3 + 3)
            step.done(v.reciprocal(var, var))
            step.wait()
            v.wait_ge(dots, i)
            step.done(v.tensor_tensor(kv, cen, var.unsqueeze(2).broadcast_to([P, G, DH0]), ALU.mult))

    def scalar(a, i, last):
        a.wait_ge(kv_ready, i)
        a.activation(tile[:], c.xnT[:, :, ds(i * P, P)], ACT.Copy).then_inc(tile_ready, 1)
        a.wait_ge(vec, i * PER + 3)
        a.activation(sq.rearrange(flat), cen.rearrange(flat), ACT.Square).then_inc(act, 2)
        a.wait_ge(vec, i * PER + 5)
        a.activation(var, var, ACT.Sqrt).then_inc(act, 1)

    def sync_first(sp):
        sp.dma_start(wkv.rearrange(flat), c.turned_part("L0_mix_Wqkv", 2 * 1024)).then_inc(w_loaded, 16)

    side = dict(tensor_first=first, tensor_begin=products_begin, tensor_end=products_end, vector=vector,
                scalar=scalar, sync_first=sync_first)
    aggregate(c, table=c.xn_tab, slots=(0, 1), side=side)
    c.constants.end(16)


def fold_attention(c):
    nc = c.nc
    part = Carver(c.scr, SCR)
    woutT, wq = part.take([PAIRS, D]), part.take([PAIRS, D])
    dots, t_sb = part.take([PAIRS, P]), part.take([PAIRS, D])
    loaded = c.constants.sem
    vec, pe_done = c.sem("fold0_vec"), c.sem("fold0_products")
    with nc.Block() as block:

        @block.sync
        def _(sp):
            sp.dma_start(woutT.rearrange("p a b -> p (a b)"), c.turned_part("L0_mix_Wout", PAIRS * D)).then_inc(loaded, 16)
            sp.dma_start(wq[:], c.inp["L0_mix_Wqkv"][0:PAIRS * P, :].rearrange("(q p) n -> p q n", p=P)).then_inc(loaded, 16)

        @block.vector
        def _(v):
            v.scalar_tensor_tensor(dots[:], c.psum[:, 4, :].rearrange("p (q d) -> p q d", d=P), 1.0 / N,
                                   c.bd64[:].unsqueeze(1).broadcast_to([P, PAIRS, P]), ALU.mult, ALU.mult
                                   ).then_inc(vec, 1)
            v.wait_ge(pe_done, 1)
            v.tensor_copy(t_sb[:], c.psum[:, 0:2, :].rearrange("p a b -> p (a b)").rearrange("p (q d) -> p q d", d=D)
                          ).then_inc(vec, 1)
            v.wait_ge(pe_done, 2)
            v.tensor_copy(c.m0[:], c.psum[:, 2, :].rearrange("p (k d) -> p k d", d=D))
            for k in range(2):
                v.tensor_tensor(c.agg[:, k, :], c.agg[:, k, :], c.agg[:, 2, :], ALU.mult)

        @block.tensor
        def _(pe):
            pe.wait_ge(vec, 1)
            pe.wait_ge(loaded, c.constants.at(32))
            for q in range(PAIRS):
                last = pe.matmul(c.psum[:, q // 2, (q % 2) * D:(q % 2 + 1) * D], dots[:, q, :], woutT[:, q, :],
                                 start=True, stop=True)
            last.then_inc(pe_done, 1)
            pe.wait_ge(vec, 2)
            for k in range(2):
                for q in range(PAIRS):
                    last = pe.matmul(c.psum[:, 2, k * D:(k + 1) * D], wq[:, q, k * P:(k + 1) * P], t_sb[:, q, :],
                                     start=(q == 0), stop=(q == PAIRS - 1))
            last.then_inc(pe_done, 1)
    c.constants.end(32)


H1 = 4


def first_conv(c):
    nc = c.nc
    part = Carver(c.scr, SCR)
    w1T, w2T = part.take([2, H1 * P]), part.take([H1, D])
    stats = part.take([H1, NS * 2, 6])
    moments = part.take([H1, 2])
    rstd, scale, bias = part.take([H1]), part.take([H1]), part.take([H1])
    h1r = part.take([2, H1, 512])
    rows = part.take([2, 4, D])
    loaded, ready, read = c.constants.sem, c.sem("conv1_h1_ready"), c.sem("conv1_h1_read")
    with nc.Block() as block:

        @block.sync
        def _(sp):
            sp.dma_start(w1T.rearrange("p a b -> p (a b)"), c.turned_part("L0_gnn_W1", 2 * H1 * P)).then_inc(loaded, 16)
            sp.dma_start(w2T.rearrange("p a b -> p (a b)"), c.turned_part("L0_gnn_W2", H1 * D)).then_inc(loaded, 16)
            sp.wait_ge(loaded, c.constants.at(32))

        @block.gpsimd
        def _(g):
            g.memset(c.agg[:, 2, :], 0.0)

        @block.tensor
        def _(pe):
            pe.wait_ge(loaded, c.constants.at(32))

            def step(s, first):
                for h, (t0, nt) in enumerate(HALVES):
                    if not first:
                        pe.wait_ge(read, s * 2 - 1 + h)
                    for m in range(H1):
                        for k in range(2):
                            last = pe.matmul(c.psum[:, 4 * h + m, 0:nt * P], w1T[:, k, m * P:(m + 1) * P],
                                             c.agg[:, k, ds(s * SS + t0 * P, nt * P)], start=(k == 0), stop=(k == 1))
                    last.then_inc(ready, 1)
            step(0, True)
            with pe.Fori(1, NS) as s:
                step(s, False)

        @block.vector
        def _(v):
            def turn(s, last_step):
                for h, (t0, nt) in enumerate(HALVES):
                    cols = nt * P
                    if last_step and h == 1:
                        cols = (nt - 1) * P + LAST
                    v.wait_ge(ready, s * 2 + h + 1)
                    for m in range(H1):
                        last = v.bn_stats(stats[:, m, ds(s * 2 + h, 1), :].rearrange("p a b -> p (a b)"),
                                          c.psum[:, 4 * h + m, 0:cols])
                    last.then_inc(read, 1)
            with v.Fori(0, NS - 1) as s:
                turn(s, False)
            turn(NS - 1, True)

    vec, root = c.sem("conv1_bn_vec"), c.sem("conv1_bn_root")
    h_ready, relu, tiles = c.sem("conv1_part_ready"), c.sem("conv1_relu_done"), c.sem("conv1_rows_ready")
    scaled, turned, copied = c.sem("conv1_rows_scaled"), c.sem("conv1_rows_turned"), c.sem("conv1_agg_copied")
    stored = [c.sem(f"conv1_stored{h}") for h in range(2)]
    with nc.Block() as block:

        @block.vector
        def _(v):
            step = Chain(v, vec)
            for m in range(H1):
                step.done(v.bn_aggr(moments[:, m, :], stats[:, m, :, :].rearrange("p a b -> p (a b)")))
            step.wait()
            step.done(v.tensor_scalar(rstd, moments[:, :, 1], EPS, None, ALU.add))
            v.wait_ge(root, 1)
            step.done(v.reciprocal(rstd, rstd))
            step.wait()
            step.done(v.tensor_tensor(scale, rstd, c.columns("L0_gnn_g1"), ALU.mult))
            step.wait()
            step.done(v.tensor_tensor(bias, moments[:, :, 0], scale, ALU.mult))
            step.wait()
            step.done(v.tensor_tensor(bias, c.columns("L0_gnn_b1"), bias, ALU.subtract))
            with v.Fori(0, NS) as s:
                for h, (t0, nt) in enumerate(HALVES):
                    v.wait_ge(stored[h], s * 16)
                    v.wait_ge(turned, s * 4)
                    v.wait_ge(tiles, s * 2 + h + 1)
                    for t in range(nt):
                        last = v.tensor_scalar(rows[:, h, t, :], c.psum[:, 4 + t // 2, (t % 2) * D:(t % 2 + 1) * D],
                                               c.dis[:, ds(s * TS + t0 + t, 1)], None, ALU.mult)
                    last.then_inc(scaled, 1)
                    for k in range(2):
                        v.wait_ge(turned, (s * 2 + h) * 2 + k + 1)
                        v.tensor_copy(c.agg[:, k, ds(s * SS + t0 * P, nt * P)], c.psum[:, 6 + k, 0:nt * P]
                                      ).then_inc(copied, 1)

        @block.scalar
        def _(a):
            a.wait_ge(vec, H1 + 1)
            a.activation(rstd, rstd, ACT.Sqrt).then_inc(root, 1)
            a.wait_ge(vec, H1 + 5)
            with a.Fori(0, NS) as s:
                for h, (t0, nt) in enumerate(HALVES):
                    for m in range(H1):
                        a.wait_ge(h_ready, (s * 2 + h) * H1 + m + 1)
                        if m == 0:
                            a.wait_ge(tiles, s * 2)
                        a.activation(h1r[:, h, m, 0:nt * P], c.psum[:, m, 0:nt * P], ACT.Relu, bias=bias[:, m:m + 1],
                                     scale=scale[:, m:m + 1]).then_inc(relu, 1)

        @block.tensor
        def _(pe):
            def h1(s, h):
                t0, nt = HALVES[h]
                for m in range(H1):
                    pe.wait_ge(relu, (s * 2 + h - 1) * H1 + m + 1 if h else s * 2 * H1)
                    for k in range(2):
                        last = pe.matmul(c.psum[:, m, 0:nt * P], w1T[:, k, m * P:(m + 1) * P],
                                         c.agg[:, k, ds(s * SS + t0 * P, nt * P)], start=(k == 0), stop=(k == 1))
                    last.then_inc(h_ready, 1)

            def node_rows(s, h):
                t0, nt = HALVES[h]
                pe.wait_ge(scaled, s * 2 + h)
                for m in range(H1):
                    pe.wait_ge(relu, (s * 2 + h) * H1 + m + 1)
                    for t in range(nt):
                        last = pe.matmul(c.psum[:, 4 + t // 2, (t % 2) * D:(t % 2 + 1) * D],
                                         h1r[:, h, m, t * P:(t + 1) * P], w2T[:, m, :],
                                         start=(m == 0 and t % 2 == 0), stop=(m == H1 - 1), skip_group_check=True)
                last.then_inc(tiles, 1)

            def turn_rows(s, h):
                t0, nt = HALVES[h]
                pe.wait_ge(scaled, s * 2 + h + 1)
                pe.wait_ge(copied, (s * 2 + h) * 2)
                for k in range(2):
                    for t in range(nt):
                        last = pe.transpose(c.psum[:, 6 + k, t * P:(t + 1) * P], rows[:, h, t, k * P:(k + 1) * P], c.ident[:])
                    last.then_inc(turned, 1)

            with pe.Fori(0, NS) as s:
                h1(s, 0)
                node_rows(s, 0)
                h1(s, 1)
                turn_rows(s, 0)
                node_rows(s, 1)
                turn_rows(s, 1)

        @block.sync
        def _(sp):
            with sp.Fori(0, NS) as s:
                for h, (t0, nt) in enumerate(HALVES):
                    sp.wait_ge(scaled, s * 2 + h + 1)
                    sp.dma_start(c.h_tab[ds(s * SS + t0 * P, nt * P), :].rearrange("(t p) d -> p t d", p=P),
                                 rows[:, h, 0:nt, :]).then_inc(stored[h], 16)
            for q in stored:
                sp.wait_ge(q, 16 * NS)
    c.constants.end(32)


def gather_second(c):
    nc = c.nc
    dis_all = c.scr[:, SCR - NP:]
    done = c.constants.sem

    def sync_first(sp):
        sp.dma_start(dis_all, c.dis_row.partition_broadcast(P)).then_inc(done, 16)
        sp.wait_ge(done, c.constants.at(16))

    aggregate(c, table=c.h_tab, slots=(0, 1, "weight"), side=dict(sync_first=sync_first))
    with nc.Block() as block:

        @block.sync
        def _(sp):
            sp.dma_start(c.wsum_row, c.agg[0:1, 2, :]).then_inc(done, 16)
            sp.wait_ge(done, c.constants.at(32))

        @block.vector
        def _(v):
            for k in range(2):
                v.tensor_tensor(c.agg[:, k, :], c.agg[:, k, :], dis_all, ALU.mult)
    c.constants.end(32)


def first_layer_sum(c):
    nc = c.nc
    part = Carver(c.scr, SCR)
    pre = part.take([2, 2, 512])
    xs = part.take([2, 2, 512])
    x_in = part.take([2, 4, D])
    x1 = part.take([2, 4, D])
    xn2 = part.take([2, 4, D])
    xn2T = part.take([2, 2, 512])
    wg, bg, bout = part.take([2, EXPERTS]), part.take([EXPERTS]), part.take([D])
    chunks = -(-N // 512)
    stats = part.take([2, chunks, 6])
    moments, rstd2, scale, bias = part.take([2, 2]), part.take([2]), part.take([2]), part.take([2])
    st, mo, rstd = part.take([2, 4, 6]), part.take([2, 4, 2]), part.take([2, 4])
    loaded, bn, root2 = c.constants.sem, c.sem("sum_bn_vec"), c.sem("sum_bn_root")
    x_in_ready = [c.sem(f"sum_x_loaded{h}") for h in range(2)]
    pre_ready, relu, xs_ready = c.sem("sum_pre_ready"), c.sem("sum_relu_done"), c.sem("sum_xn_copied")
    x1_psum, x1_ready, vec, root = c.sem("sum_x1_products"), c.sem("sum_x1_ready"), c.sem("sum_vec"), c.sem("sum_root")
    begun, xn2_ready, turned, copied = c.sem("sum_moments_begun"), c.sem("sum_xn2_ready"), c.sem("sum_turned"), c.sem("sum_xn2T_copied")
    shifted = c.sem("sum_x_shifted")
    scored, scores_ready = c.sem("sum_scored"), c.sem("sum_scores_ready")
    stored = [c.sem(f"sum_stored{h}") for h in range(2)]

    def pipeline(engine, slot):
        def step(s, first, last):
            slot((s, 0), (s, 1), None if first else (s - 1, 1))
            slot((s, 1), None if last else (s + 1, 0), (s, 0))
        step(0, True, False)
        with engine.Fori(1, NS - 1) as s:
            step(s, False, False)
        step(NS - 1, False, True)

    def unit(s, h):
        return s * 2 + h

    with nc.Block() as block:

        @block.sync
        def _(sp):
            sp.dma_start(wg[:], c.inp["L0_ffn_Wg"].rearrange("(k p) e -> p k e", p=P)).then_inc(loaded, 16)
            sp.dma_start(bg, c.inp["L0_ffn_bg"].unsqueeze(0).partition_broadcast(P)).then_inc(loaded, 16)
            sp.dma_start(bout, c.inp["L0_mix_bout"].unsqueeze(0).partition_broadcast(P)).then_inc(loaded, 16)

            def load(s, h):
                t0, nt = HALVES[h]
                if not (isinstance(s, int) and s == 0):
                    sp.wait_ge(x1_ready, unit(s, h) - 1)
                if isinstance(s, int) and s == NS - 1 and h == 1:
                    full = nt - 1
                    r0 = (NS - 1) * SS + t0 * P
                    sp.dma_start(x_in[:, h, 0:full, :], c.inp["x"][r0:r0 + full * P, :].rearrange("(t p) d -> p t d", p=P)
                                 ).then_inc(x_in_ready[h], 16)
                    sp.dma_start(x_in[0:LAST, h, full, :], c.inp["x"][r0 + full * P:N, :]).then_inc(x_in_ready[h], 16)
                else:
                    sp.dma_start(x_in[:, h, 0:nt, :],
                                 c.inp["x"][ds(s * SS + t0 * P, nt * P), :].rearrange("(t p) d -> p t d", p=P)
                                 ).then_inc(x_in_ready[h], 16)

            def store(s, h):
                t0, nt = HALVES[h]
                sp.wait_ge(xn2_ready, unit(s, h) + 1)
                for table, rows in ((c.x1_tab, x1), (c.xn2_tab, xn2)):
                    sp.dma_start(table[ds(s * SS + t0 * P, nt * P), :].rearrange("(t p) d -> p t d", p=P),
                                 rows[:, h, 0:nt, :]).then_inc(stored[h], 16)

            def slot(now, ahead, behind):
                if ahead is not None:
                    load(*ahead)
                store(*now)
            load(0, 0)
            pipeline(sp, slot)
            sp.wait_ge(loaded, c.constants.at(48))
            for q in stored:
                sp.wait_ge(q, 32 * NS)

        @block.gpsimd
        def _(g):
            g.wait_ge(loaded, c.constants.at(48))

            def shift(s, h):
                nt = HALVES[h][1]
                last = isinstance(s, int) and s == NS - 1 and h == 1
                g.wait_ge(x_in_ready[h], s * 16 + (32 if last else 16))
                g.tensor_tensor(x_in[:, h, 0:nt, :], x_in[:, h, 0:nt, :], bout.unsqueeze(1).broadcast_to([P, nt, D]), ALU.add
                                ).then_inc(shifted, 1)

            def slot(now, ahead, behind):
                if ahead is not None:
                    shift(*ahead)
            shift(0, 0)
            pipeline(g, slot)

        @block.vector
        def _(v):
            step = Chain(v, bn)
            for k in range(2):
                for j in range(chunks):
                    ins = v.bn_stats(stats[:, k, j, :], c.agg[:, k, j * 512:min(N, j * 512 + 512)])
            step.done(ins)
            step.wait()
            for k in range(2):
                step.done(v.bn_aggr(moments[:, k, :], stats[:, k, :, :].rearrange("p a b -> p (a b)")))
            step.wait()
            step.done(v.tensor_scalar(rstd2, moments[:, :, 1], EPS, None, ALU.add))
            v.wait_ge(root2, 1)
            step.done(v.reciprocal(rstd2, rstd2))
            step.wait()
            step.done(v.tensor_tensor(scale, rstd2, c.columns("L0_gnn_g2"), ALU.mult))
            step.wait()
            step.done(v.tensor_tensor(bias, moments[:, :, 0], scale, ALU.mult))
            step.wait()
            step.done(v.tensor_tensor(bias, c.columns("L0_gnn_b2"), bias, ALU.subtract))
            step.wait()
            v.wait_ge(loaded, c.constants.at(48))

            def norm(s, h):
                t0, nt = HALVES[h]
                per = 3
                chain = Chain(v, vec, s, 2 * per, h * per)
                v.wait_ge(shifted, unit(s, h) + 1)
                v.wait_ge(x1_psum, s * 2 + h + 1)
                v.wait_ge(stored[h], s * 32)
                for t in range(nt):
                    ins = v.tensor_tensor(x1[:, h, t, :], c.psum[:, t // 2, (t % 2) * D:(t % 2 + 1) * D],
                                          x_in[:, h, t, :], ALU.add)
                ins.then_inc(x1_ready, 1)
                v.wait_ge(x1_ready, s * 2 + h + 1)
                for t in range(nt):
                    ins = v.bn_stats(st[:, h, t, :], x1[:, h, t, :])
                chain.done(ins)
                chain.wait()
                v.sem_inc(begun, 1)
                for t in range(nt):
                    ins = v.bn_aggr(mo[:, h, t, :], st[:, h, t, :])
                chain.done(ins)
                chain.wait()
                v.tensor_scalar(rstd[:, h, 0:nt], mo[:, h, 0:nt, 1], EPS, None, ALU.add).then_inc(begun, 1)
                v.wait_ge(root, s * 2 + h + 1)
                chain.done(v.reciprocal(rstd[:, h, 0:nt], rstd[:, h, 0:nt]))
                chain.wait()
                for t in range(nt):
                    ins = v.tensor_scalar(xn2[:, h, t, :], x1[:, h, t, :], mo[:, h, t, 0:1], rstd[:, h, t:t + 1],
                                          ALU.subtract, ALU.mult)
                ins.then_inc(xn2_ready, 1)

            def before_relu(s, h):
                t0, nt = HALVES[h]
                if not (isinstance(s, int) and s == 0):
                    v.wait_ge(x1_psum, unit(s, h) - 1)
                for k in range(2):
                    at = ds(s * SS + t0 * P, nt * P)
                    v.scalar_tensor_tensor(pre[:, h, k, 0:nt * P], c.agg[:, k, at], scale[:, k:k + 1], c.xnT[:, k, at],
                                           ALU.mult, ALU.add).then_inc(pre_ready, 1)

            def read_scores(s, h):
                t0, nt = HALVES[h]
                v.wait_ge(scored, unit(s, h) + 1)
                v.tensor_tensor(c.scores[:, ds(s * TS + t0, nt), :],
                                c.psum[:, 7, h * 64:h * 64 + nt * EXPERTS].rearrange("p (t e) -> p t e", e=EXPERTS),
                                bg.unsqueeze(1).broadcast_to([P, nt, EXPERTS]), ALU.add).then_inc(scores_ready, 1)

            def slot(now, ahead, behind):
                if ahead is not None:
                    before_relu(*ahead)
                norm(*now)
                if behind is not None:
                    read_scores(*behind)
            before_relu(0, 0)
            pipeline(v, slot)
            read_scores(NS - 1, 1)

        @block.scalar
        def _(a):
            a.wait_ge(bn, 4)
            a.activation(rstd2, rstd2, ACT.Sqrt).then_inc(root2, 1)
            a.wait_ge(bn, 7)

            def relu_and_xn(s, h):
                t0, nt = HALVES[h]
                if not (isinstance(s, int) and s == 0):
                    a.wait_ge(x1_psum, unit(s, h) - 1)
                a.activation(xs[:, h, :, 0:nt * P], c.xnT[:, :, ds(s * SS + t0 * P, nt * P)], ACT.Copy).then_inc(xs_ready, 1)
                for k in range(2):
                    a.wait_ge(pre_ready, unit(s, h) * 2 + k + 1)
                    a.activation(pre[:, h, k, 0:nt * P], pre[:, h, k, 0:nt * P], ACT.Relu, bias=bias[:, k:k + 1]
                                 ).then_inc(relu, 1)

            def rooted(s, h):
                nt = HALVES[h][1]
                a.wait_ge(begun, unit(s, h) * 2 + 2)
                a.activation(rstd[:, h, 0:nt], rstd[:, h, 0:nt], ACT.Sqrt).then_inc(root, 1)

            def copy(s, h):
                nt = HALVES[h][1]
                for k in range(2):
                    a.wait_ge(turned, unit(s, h) * 2 + k + 1)
                    a.activation(xn2T[:, h, k, 0:nt * P], c.psum[:, 5 + k, 0:nt * P], ACT.Copy).then_inc(copied, 1)

            def slot(now, ahead, behind):
                if ahead is not None:
                    relu_and_xn(*ahead)
                if behind is not None:
                    copy(*behind)
                rooted(*now)
            relu_and_xn(0, 0)
            pipeline(a, slot)
            copy(NS - 1, 1)

        @block.tensor
        def _(pe):
            pe.wait_ge(loaded, c.constants.at(48))

            def x1_rows(s, h):
                t0, nt = HALVES[h]
                pe.wait_ge(x1_ready, s * 2 + h)
                pe.wait_ge(xs_ready, s * 2 + h + 1)
                pe.wait_ge(relu, (s * 2 + h) * 2 + 2)
                for t in range(nt):
                    bank, col = t // 2, (t % 2) * D
                    cols = slice(t * P, (t + 1) * P)
                    for k in range(2):
                        pe.matmul(c.psum[:, bank, col + k * P:col + (k + 1) * P], pre[:, h, k, cols], c.ident[:],
                                  start=(k == 0), stop=False, skip_group_check=True)
                    for k in range(2):
                        last = pe.matmul(c.psum[:, bank, col:col + D], xs[:, h, k, cols], c.m0[:, k, :], start=False,
                                         stop=(k == 1), skip_group_check=True)
                last.then_inc(x1_psum, 1)

            def turn_rows(s, h):
                t0, nt = HALVES[h]
                pe.wait_ge(xn2_ready, s * 2 + h + 1)
                pe.wait_ge(copied, (s * 2 + h) * 2)
                for k in range(2):
                    for t in range(nt):
                        last = pe.transpose(c.psum[:, 5 + k, t * P:(t + 1) * P], xn2[:, h, t, k * P:(k + 1) * P], c.ident[:])
                    last.then_inc(turned, 1)

            def score(s, h):
                t0, nt = HALVES[h]
                pe.wait_ge(copied, (s * 2 + h) * 2 + 2)
                pe.wait_ge(scores_ready, s * 2 + h)
                for t in range(nt):
                    col = h * 64 + t * EXPERTS
                    for k in range(2):
                        last = pe.matmul(c.psum[:, 7, col:col + EXPERTS], xn2T[:, h, k, t * P:(t + 1) * P], wg[:, k, :],
                                         start=(k == 0), stop=(k == 1))
                last.then_inc(scored, 1)

            def slot(now, ahead, behind):
                x1_rows(*now)
                if behind is not None:
                    turn_rows(*behind)
                    score(*behind)
            pipeline(pe, slot)
            turn_rows(NS - 1, 1)
            score(NS - 1, 1)
    c.constants.end(48)


def route(c):
    nc = c.nc
    part = Carver(c.scr, SCR)
    T8 = [NT, EXPERTS]
    rev, eq, cand = part.take([EXPERTS]), part.take(T8), part.take(T8)
    mask = [part.take(T8), part.take(T8)]
    rest = part.take(T8)
    top, code = part.take([NT]), [part.take([NT]), part.take([NT])]
    both = part.take(T8, BF16)
    tri, ones_b = part.take([P], BF16), part.take([NT])
    total, upto = part.take([EXPERTS, NT]), part.take([EXPERTS, NT])
    rank = part.take(T8)
    picked, rank_of = part.take(T8), [part.take([NT]), part.take([NT])]
    start_of = part.take([NT])
    count_i, ntile = part.take([EXPERTS], I32), part.take([EXPERTS])
    end, first = part.take([EXPERTS]), part.take([EXPERTS])
    where = part.take([EXPERTS])
    node, tile_no = part.take([1]), part.take([MT])
    inside, later = part.take([MT]), part.take([MT])
    t_expert, t_row = part.take([MT]), part.take([MT])
    const, vec, pe_done = c.sem("route_const"), c.sem("route_vec"), c.sem("route_counts")
    w_loaded = c.sem("expert_weights_loaded")
    raw = c.agg.rearrange("p a b -> p (a b)")
    words = EXPERTS * 2 * HID
    marks = {}
    with nc.Block() as block:

        @block.sync
        def _(sp):
            w1, w2 = raw[:, 0:words], raw[:, words:2 * words]
            for e in range(EXPERTS):
                sp.dma_start(w1[:, e * 2 * HID:(e + 1) * 2 * HID].rearrange("p (k n) -> p k n", n=HID),
                             c.inp["L0_ffn_W1"][e].rearrange("(k p) n -> p k n", p=P)).then_inc(w_loaded, 16)
                sp.dma_start(w2[:, e * HM * D:(e + 1) * HM * D].rearrange("p (m n) -> p m n", n=D),
                             c.inp["L0_ffn_W2"][e].rearrange("(m p) n -> p m n", p=P)).then_inc(w_loaded, 16)
            sp.wait_ge(w_loaded, 16 * 2 * EXPERTS)

        @block.gpsimd
        def _(g):
            small = dict(allow_small_or_imprecise_dtypes=True)
            g.iota(rev, pattern=[[-1, EXPERTS]], base=EXPERTS, channel_multiplier=0, **small).then_inc(const, 1)
            g.iota(node, pattern=[[0, 1]], base=0, channel_multiplier=1, **small).then_inc(const, 1)
            g.iota(tile_no, pattern=[[1, MT]], base=0, channel_multiplier=0, **small).then_inc(const, 1)
            g.memset(tri, 1.0).then_inc(const, 1)
            g.wait_ge(const, 4)
            g.affine_select(out=tri, in_=tri, compare_op=ALU.is_gt, fill=0.0, base=0, pattern=[[1, P]],
                            channel_multiplier=-1).then_inc(const, 1)

        @block.vector
        def _(v):
            step = Chain(v, vec)

            def do(instruction):
                step.done(instruction)
                step.wait()

            def wide(x):
                return x.unsqueeze(2).broadcast_to([P, NT, EXPERTS])

            def over(x):
                return x.unsqueeze(1).broadcast_to([P, NT, EXPERTS])

            v.wait_ge(const, 5)
            scores = c.scores[:]
            for n in range(2):
                do(v.tensor_reduce(top, scores, AX.X, ALU.max))
                do(v.tensor_tensor(eq, scores, wide(top), ALU.is_equal))
                do(v.tensor_tensor(cand, eq, over(rev), ALU.mult))
                do(v.tensor_reduce(code[n], cand, AX.X, ALU.max))
                do(v.tensor_tensor(mask[n], over(rev), wide(code[n]), ALU.is_equal))
                if n == 0:
                    do(v.scalar_tensor_tensor(rest, mask[0], -1e30, scores, ALU.mult, ALU.add))
                    scores = rest
            do(v.tensor_tensor(both, mask[0], mask[1], ALU.add))
            marks["both"] = step.value()
            do(v.memset(ones_b, 1.0))
            v.wait_ge(pe_done, 1)
            in_tile = c.psum[:, 0, 0:NT * EXPERTS].rearrange("p (t e) -> p t e", e=EXPERTS)
            tile_sum = c.psum[:, 1, 0:NT * EXPERTS].rearrange("p (t e) -> p e t", e=EXPERTS)
            do(v.tensor_copy(total, tile_sum))
            for e in range(EXPERTS):
                ins = v.tensor_tensor_scan(upto[:, e, :], ones_b, total[:, e, :], 0.0, ALU.mult, ALU.add)
            do(ins)
            do(v.tensor_tensor(total, upto, total, ALU.subtract))
            do(v.tensor_tensor(rank, in_tile, total.rearrange("p e t -> p t e"), ALU.add))
            do(v.tensor_scalar(where, upto[:, :, NT - 1], float(P - 1), None, ALU.add))
            do(v.tensor_copy(count_i, where))
            do(v.tensor_scalar(count_i, count_i, 7, None, ALU.arith_shift_right))
            do(v.tensor_copy(ntile, count_i))
            do(v.tensor_tensor_scan(end, ones_b[:, 0:EXPERTS], ntile, 0.0, ALU.mult, ALU.add))
            do(v.tensor_tensor(first, end, ntile, ALU.subtract))
            for n in range(2):
                do(v.tensor_tensor(picked, mask[n], rank, ALU.mult))
                do(v.tensor_reduce(rank_of[n], picked, AX.X, ALU.add))
                do(v.tensor_scalar(start_of, code[n], -float(REGION), float(EXPERTS * REGION), ALU.mult, ALU.add))
                do(v.tensor_tensor(c.scatter_to[:, n, :], start_of, rank_of[n], ALU.add))
                do(v.tensor_tensor(picked, mask[n], over(first), ALU.mult))
                do(v.tensor_reduce(start_of, picked, AX.X, ALU.add))
                do(v.scalar_tensor_tensor(c.result_at[:, n, :], start_of, float(P), rank_of[n], ALU.mult, ALU.add))
            do(v.tensor_scalar(where, rev, -float(REGION), float(EXPERTS * REGION), ALU.mult, ALU.add))
            do(v.tensor_tensor(where, where, upto[:, :, NT - 1], ALU.add))
            do(v.tensor_scalar(c.pad_to[:], where, node[:, 0:1], None, ALU.add))
            do(v.memset(t_expert, 0.0))
            do(v.memset(t_row, 0.0))
            for e in range(EXPERTS):
                do(v.tensor_scalar(inside, tile_no, first[:, e:e + 1], None, ALU.is_ge))
                do(v.tensor_scalar(later, tile_no, end[:, e:e + 1], None, ALU.is_lt))
                do(v.tensor_tensor(inside, inside, later, ALU.mult))
                do(v.scalar_tensor_tensor(t_expert, inside, float(e), t_expert, ALU.mult, ALU.add))
                do(v.tensor_scalar(later, tile_no, first[:, e:e + 1], None, ALU.subtract))
                do(v.tensor_scalar(later, later, float(P), float(e * REGION), ALU.mult, ALU.add))
                do(v.tensor_tensor(later, later, inside, ALU.mult))
                do(v.tensor_tensor(t_row, t_row, later, ALU.add))
            do(v.tensor_copy(c.tile_expert[:], t_expert))
            do(v.tensor_copy(c.tile_row[:], t_row))

        @block.tensor
        def _(pe):
            pe.wait_ge(const, 5)
            pe.wait_ge(vec, marks["both"])
            flat = both.rearrange("p t e -> p (t e)")
            pe.matmul(c.psum[:, 0, 0:NT * EXPERTS], tri, flat, start=True, stop=True)
            pe.matmul(c.psum[:, 1, 0:NT * EXPERTS], c.ones16[:], flat, start=True, stop=True).then_inc(pe_done, 1)


def send_to_experts(c):
    nc = c.nc
    part = Carver(c.scr, SCR)
    part.at = EXPERTS * HM * D
    rows = part.take([2, 4, D])
    zero_rows = part.take([D])
    to = part.take([2, 2, 4], I32)
    raw = c.agg.rearrange("p a b -> p (a b)")
    words = EXPERTS * 2 * HID
    xnT = c.xnT.rearrange("p a b -> p (a b)")
    c.w1_16 = xnT[:, 0:words].bitcast(F16).rearrange("p (e k h n) -> p e k h n", k=2, h=2, n=HID)
    c.w2_16 = c.scr[:, 0:words].bitcast(F16).rearrange("p (e k h n) -> p e k h n", k=HM, h=2, n=D)
    w1 = raw[:, 0:words].rearrange("p (e k n) -> p e k n", k=2, n=HID)
    w2 = raw[:, words:2 * words].rearrange("p (e k n) -> p e k n", k=HM, n=D)
    zero, landed = c.sem("pad_rows_zeroed"), [c.sem(f"send_rows_landed{h}") for h in range(2)]
    idx_ready, begun, sent = c.sem("send_indices_ready"), c.passed, [c.sem(f"rows_sent{h}") for h in range(2)]
    high = c.sem("weights_high")
    PADS = (16 * EXPERTS, 0)
    with nc.Block() as block:

        @block.sync
        def _(sp):
            with sp.Fori(0, NS) as s:
                for h, (t0, nt) in enumerate(HALVES):
                    sp.wait_ge(sent[h], s * (2 * nt * 16) + PADS[h])
                    sp.dma_start(rows[:, h, 0:nt, :],
                                 c.xn2_tab[ds(s * SS + t0 * P, nt * P), :].rearrange("(t p) d -> p t d", p=P)
                                 ).then_inc(landed[h], 16)

        @block.vector
        def _(v):
            v.memset(zero_rows, 0.0).then_inc(zero, 1)
            for e in range(EXPERTS):
                for n, (w, parts) in enumerate(((w1, c.w1_16), (w2, c.w2_16))):
                    v.wait_ge(high, 2 * e + n + 1)
                    v.scalar_tensor_tensor(parts[:, e, :, 1, :], w[:, e, :, :], WS, parts[:, e, :, 0, :],
                                           ALU.mult, ALU.subtract)

        @block.scalar
        def _(a):
            def indices(s):
                for h, (t0, nt) in enumerate(HALVES):
                    a.wait_ge(sent[h], s * (2 * nt * 16) + PADS[h])
                    a.activation(to[:, h, :, 0:nt], c.scatter_to[:, :, ds(s * TS + t0, nt)], ACT.Copy).then_inc(idx_ready, 1)

            for e in range(EXPERTS):
                for w, parts in ((w1, c.w1_16), (w2, c.w2_16)):
                    a.activation(parts[:, e, :, 0, :], w[:, e, :, :], ACT.Copy, scale=WS).then_inc(high, 1)
                if e < NS:
                    indices(e)

        @block.gpsimd
        def _(g):
            g.wait_ge(zero, 1)
            for e in range(EXPERTS):
                g.indirect_dma_start(out=c.slot_x, in_=zero_rows, in_offset=None,
                                     out_offset=bass.IndirectOffsetOnAxis(ap=c.pad_to[:, e:e + 1], axis=0)
                                     ).then_inc(sent[0], 16)
            with g.Fori(0, NS) as s:
                for h, (t0, nt) in enumerate(HALVES):
                    g.wait_ge(landed[h], s * 16 + 16)
                    g.sem_inc(begun, 1)
                    g.wait_ge(idx_ready, s * 2 + h + 1)
                    g.sem_inc(begun, 1)
                    for n in range(2):
                        for t in range(nt):
                            g.indirect_dma_start(out=c.slot_x, in_=rows[:, h, t, :], in_offset=None,
                                                 out_offset=bass.IndirectOffsetOnAxis(ap=to[:, h, n, t:t + 1], axis=0)
                                                 ).then_inc(sent[h], 16)
            for h, (t0, nt) in enumerate(HALVES):
                g.wait_ge(sent[h], 32 * nt * NS + PADS[h])


def experts(c):
    nc = c.nc
    part = Carver(c.scr, SCR)
    part.at = EXPERTS * HM * D
    x = part.take([2, D])
    xT = part.take([2, 2, D], F16)
    g = part.take([2, HID])
    gT = part.take([2, 2, HID], F16)
    y = part.take([2, D])
    b2 = part.take([EXPERTS, D])
    agg = c.agg.rearrange("p a b -> p (a b)")
    loaded, x_ready = c.constants.sem, [c.sem(f"moe_x_loaded{b}") for b in range(2)]
    turned, x_high, x_low = c.sem("moe_turned"), c.sem("moe_x_high"), c.sem("moe_x_low")
    h_ready, g_ready = c.sem("moe_h_ready"), c.sem("moe_gelu_done")
    g_high, g_low = c.sem("moe_g_high"), c.sem("moe_g_low")
    y_ready, y_out = c.sem("moe_y_products"), c.sem("moe_y_ready")
    stored = [c.sem(f"moe_stored{b}") for b in range(2)]
    PARTS = ((0, 0), (0, 1), (1, 0))

    def experts_of(engine, tile, n):
        _, regs = nc.values_load_multi_w_load_instructions(c.tile_expert[0:1, ds(tile, n)], engines=[engine.engine],
                                                           min_val=0, max_val=EXPERTS - 1)
        return list(regs)

    def turns(engine, body, back, n):
        body(0, [None] * back + experts_of(engine, 0, n - back) if n > back else None, True, False)
        with engine.Fori(0, (MT // 2 - 2) // 3) as r:
            q = r * 3 + 1
            e = experts_of(engine, q * 2 - back, 4 + n)
            for j in range(3):
                body(q + j, e[2 * j:2 * j + n], False, False)
        q = MT // 2 - 1
        body(q, experts_of(engine, q * 2 - back, n), False, True)
    assert (MT // 2 - 2) % 3 == 0

    with nc.Block() as block:

        @block.sync
        def _(sp):
            sp.dma_start(b2.rearrange("p e d -> p (e d)"),
                         c.inp["L0_ffn_b2"].rearrange("e d -> (e d)").unsqueeze(0).partition_broadcast(P)).then_inc(loaded, 16)

            def load(i, b):
                row = sp.value_load(c.tile_row[0:1, ds(i, 1)], min_val=0, max_val=EXPERTS * REGION - P)
                sp.dma_start(x[:, b, :], c.slot_x[ds(row, P), :]).then_inc(x_ready[b], 16)

            for b in range(2):
                load(b, b)
            with sp.Fori(0, MT // 2 - 1) as q:
                for b in range(2):
                    sp.wait_ge(turned, q * 2 + b + 1)
                    load(q * 2 + 2 + b, b)
            sp.wait_ge(loaded, c.constants.at(16))

        @block.gpsimd
        def _(gp):
            with gp.Fori(0, MT // 2) as q:
                for b in range(2):
                    gp.wait_ge(y_out, q * 2 + b + 1)
                    gp.sem_inc(c.passed, 1)
                    gp.dma_start(c.slot_y[ds((q * 2 + b) * P, P), :], y[:, b, :]).then_inc(stored[b], 16)
            for b in range(2):
                gp.wait_ge(stored[b], 16 * (MT // 2))

        @block.scalar
        def _(a):
            def x_high_part(i, b):
                a.wait_ge(turned, i + 1)
                a.activation(xT[:, b, 0, :], c.psum[:, b, 0:D], ACT.Copy, scale=XS).then_inc(x_high, 1)

            def gelu(i, b, first, e):
                a.wait_ge(h_ready, i + 1)
                if not first:
                    a.wait_ge(g_low, i - 1)
                at = COLUMNS_AT["L0_ffn_b1"][0]
                for m in range(HM):
                    ins = a.activation(g[:, b, m * P:(m + 1) * P], c.psum[:, 2 + b, m * P:(m + 1) * P], ACT.Gelu,
                                       bias=c.cols[:, ds(e * HM + (at + m), 1)], scale=1.0 / (XS * WS))
                ins.then_inc(g_ready, 1)

            x_high_part(0, 0)
            x_high_part(1, 1)

            def body(q, e, first, last):
                for b in range(2):
                    gelu(q * 2 + b, b, first, e[b])
                    if not last:
                        x_high_part(q * 2 + b + 2, b)
            turns(a, body, 0, 2)

        @block.vector
        def _(v):
            def x_split(i, b):
                v.wait_ge(x_high, i + 1)
                v.scalar_tensor_tensor(xT[:, b, 1, :], c.psum[:, b, 0:D], XS, xT[:, b, 0, :], ALU.mult, ALU.subtract
                                       ).then_inc(x_low, 1)

            def g_split(i, b, first):
                v.wait_ge(g_ready, i + 1)
                if not first:
                    v.wait_ge(y_ready, i - 1)
                v.tensor_scalar(gT[:, b, 0, :], g[:, b, :], XS, None, ALU.mult).then_inc(g_high, 1)
                v.wait_ge(g_high, i + 1)
                v.scalar_tensor_tensor(gT[:, b, 1, :], g[:, b, :], XS, gT[:, b, 0, :], ALU.mult, ALU.subtract
                                       ).then_inc(g_low, 1)

            def y_rows(i, b, pair, e):
                v.wait_ge(y_ready, i + 1)
                v.wait_ge(stored[b], pair * 16)
                v.scalar_tensor_tensor(y[:, b, :], c.psum[:, 4 + b, 0:D], 1.0 / (XS * WS),
                                       b2[:, ds(e, 1), :].rearrange("p e d -> p (e d)"), ALU.mult, ALU.add
                                       ).then_inc(y_out, 1)

            v.wait_ge(loaded, c.constants.at(16))
            x_split(0, 0)
            x_split(1, 1)

            def body(q, e, first, last):
                for b in range(2):
                    i = q * 2 + b
                    if not first:
                        y_rows(i - 2, b, q - 1, e[b])
                    g_split(i, b, first)
                    if not last:
                        x_split(i + 2, b)
            turns(v, body, 2, 2)
            e = experts_of(v, MT - 2, 2)
            for b in range(2):
                y_rows(MT - 2 + b, b, MT // 2 - 1, e[b])

        @block.tensor
        def _(pe):
            def turn_x(i, b, pair):
                pe.wait_ge(x_ready[b], (pair + 1) * 16)
                for k in range(2):
                    last = pe.transpose(c.psum[:, b, k * P:(k + 1) * P], x[:, b, k * P:(k + 1) * P], c.ident[:])
                last.then_inc(turned, 1)

            def hidden(i, b, first, e):
                pe.wait_ge(x_low, i + 1)
                if not first:
                    pe.wait_ge(g_ready, i - 1)
                for m in range(HM):
                    n = 0
                    for k in range(2):
                        for wp, xp in PARTS:
                            n += 1
                            last = pe.matmul(c.psum[:, 2 + b, m * P:(m + 1) * P],
                                             c.w1_16[:, ds(e, 1), k, wp, m * P:(m + 1) * P].rearrange("p e n -> p (e n)"),
                                             xT[:, b, xp, k * P:(k + 1) * P], start=(n == 1), stop=(n == 6))
                last.then_inc(h_ready, 1)

            def result(i, b, pair, e):
                pe.wait_ge(g_low, i + 1)
                pe.wait_ge(y_out, pair * 2)
                n = 0
                for m in range(HM):
                    for wp, gp in PARTS:
                        n += 1
                        last = pe.matmul(c.psum[:, 4 + b, 0:D], gT[:, b, gp, m * P:(m + 1) * P],
                                         c.w2_16[:, ds(e, 1), m, wp, :].rearrange("p e n -> p (e n)"),
                                         start=(n == 1), stop=(n == 3 * HM))
                last.then_inc(y_ready, 1)

            turn_x(0, 0, 0)
            turn_x(1, 1, 0)

            def body(q, e, first, last):
                for b in range(2):
                    i = q * 2 + b
                    hidden(i, b, first, e[2 + b])
                    if not first:
                        result(i - 2, b, q - 1, e[b])
                    if not last:
                        turn_x(i + 2, b, q + 1)
            turns(pe, body, 2, 4)
            e = experts_of(pe, MT - 2, 2)
            for b in range(2):
                result(MT - 2 + b, b, MT // 2 - 1, e[b])
    c.constants.end(16)


def second_norm(c):
    nc = c.nc
    part = Carver(c.scr, SCR)
    x2, xn3 = part.take([2, 4, D]), part.take([2, 4, D])
    y = part.take([2, 2, 4, D])
    at = part.take([2, 2, 4], I32)
    st, mo, rstd = part.take([2, 4, 6]), part.take([2, 4, 2]), part.take([2, 4])
    wsum = part.take([P])
    w_in, w_vec, w_out = c.sem("norm3_wsum_loaded"), c.sem("norm3_wsum_inverted"), c.sem("norm3_wsum_moved")
    x_in = [c.sem(f"norm3_x1_loaded{h}") for h in range(2)]
    y_in = [c.sem(f"norm3_results_landed{h}") for h in range(2)]
    at_ready, begun, vec, root = c.sem("norm3_indices_ready"), c.passed, c.sem("norm3_vec"), c.sem("norm3_root")
    moments = c.passed
    turned, copied = c.sem("norm3_turned"), c.sem("norm3_copied")
    stored = [c.sem(f"norm3_stored{h}") for h in range(2)]
    PER = 7
    with nc.Block() as block:

        @block.sync
        def _(sp):
            sp.dma_start(wsum[0:NT, :], c.wsum_row.rearrange("a (t n) -> (a t) n", n=P)).then_inc(w_in, 16)
            sp.wait_ge(w_vec, 2)
            sp.dma_start(c.wsum_row.rearrange("a (t n) -> (a t) n", n=P), wsum[0:NT, :]).then_inc(w_out, 16)
            sp.wait_ge(w_out, 16)
            sp.dma_start(c.agg[:, 2, :], c.wsum_row.partition_broadcast(P)).then_inc(w_out, 16)
            with sp.Fori(0, NS) as s:
                for h, (t0, nt) in enumerate(HALVES):
                    sp.wait_ge(stored[h], s * 32)
                    sp.dma_start(x2[:, h, 0:nt, :], c.x1_tab[ds(s * SS + t0 * P, nt * P), :].rearrange("(t p) d -> p t d", p=P)
                                 ).then_inc(x_in[h], 16)
                for h, (t0, nt) in enumerate(HALVES):
                    sp.wait_ge(vec, s * (2 * PER) + (h + 1) * PER)
                    for table, rows in ((c.x2_tab, x2), (c.xn3_tab, xn3)):
                        sp.dma_start(table[ds(s * SS + t0 * P, nt * P), :].rearrange("(t p) d -> p t d", p=P),
                                     rows[:, h, 0:nt, :]).then_inc(stored[h], 16)
            sp.wait_ge(w_out, 32)
            for q in stored:
                sp.wait_ge(q, 32 * NS)

        @block.gpsimd
        def _(g):
            with g.Fori(0, NS) as s:
                for h, (t0, nt) in enumerate(HALVES):
                    g.wait_ge(at_ready, s * 2 + h + 1)
                    g.sem_inc(begun, 1)
                    for n in range(2):
                        for t in range(nt):
                            g.indirect_dma_start(out=y[:, h, n, t, :], out_offset=None, in_=c.slot_y,
                                                 in_offset=bass.IndirectOffsetOnAxis(ap=at[:, h, n, t:t + 1], axis=0)
                                                 ).then_inc(y_in[h], 16)

        @block.vector
        def _(v):
            v.memset(c.agg[:, 0:2, :], 0.0)
            v.wait_ge(w_in, 16)
            v.tensor_scalar(wsum[0:NT, :], wsum[0:NT, :], 1e-6, None, ALU.max).then_inc(w_vec, 1)
            v.wait_ge(w_vec, 1)
            v.reciprocal(wsum[0:NT, :], wsum[0:NT, :]).then_inc(w_vec, 1)
            with v.Fori(0, NS) as s:
                for h, (t0, nt) in enumerate(HALVES):
                    chain = Chain(v, vec, s, 2 * PER, h * PER)
                    v.wait_ge(x_in[h], s * 16 + 16)
                    v.wait_ge(y_in[h], (s + 1) * (2 * nt * 16))
                    chain.done(v.tensor_tensor(x2[:, h, 0:nt, :], x2[:, h, 0:nt, :], y[:, h, 0, 0:nt, :], ALU.add))
                    chain.wait()
                    chain.done(v.tensor_tensor(x2[:, h, 0:nt, :], x2[:, h, 0:nt, :], y[:, h, 1, 0:nt, :], ALU.add))
                    chain.wait()
                    for t in range(nt):
                        ins = v.bn_stats(st[:, h, t, :], x2[:, h, t, :])
                    chain.done(ins)
                    chain.wait()
                    v.sem_inc(moments, 1)
                    for t in range(nt):
                        ins = v.bn_aggr(mo[:, h, t, :], st[:, h, t, :])
                    chain.done(ins)
                    chain.wait()
                    chain.done(v.tensor_scalar(rstd[:, h, 0:nt], mo[:, h, 0:nt, 1], EPS, None, ALU.add))
                    v.wait_ge(root, s * 2 + h + 1)
                    chain.done(v.reciprocal(rstd[:, h, 0:nt], rstd[:, h, 0:nt]))
                    chain.wait()
                    v.wait_ge(turned, s * 2)
                    for t in range(nt):
                        ins = v.tensor_scalar(xn3[:, h, t, :], x2[:, h, t, :], mo[:, h, t, 0:1], rstd[:, h, t:t + 1],
                                              ALU.subtract, ALU.mult)
                    chain.done(ins)

        @block.scalar
        def _(a):
            def indices(s, h):
                t0, nt = HALVES[h]
                a.activation(at[:, h, :, 0:nt], c.result_at[:, :, ds(s * TS + t0, nt)], ACT.Copy).then_inc(at_ready, 1)

            def body(s, last):
                for h, (t0, nt) in enumerate(HALVES):
                    if not last:
                        a.wait_ge(vec, s * (2 * PER) + h * PER + 2)
                        indices(s + 1, h)
                    a.wait_ge(vec, s * (2 * PER) + h * PER + 5)
                    a.activation(rstd[:, h, 0:nt], rstd[:, h, 0:nt], ACT.Sqrt).then_inc(root, 1)
                    a.wait_ge(turned, s * 2 + h + 1)
                    for k in range(2):
                        ins = a.activation(c.xnT[:, k, ds(s * SS + t0 * P, nt * P)], c.psum[:, 2 * h + k, 0:nt * P], ACT.Copy)
                    ins.then_inc(copied, 1)
            for h in range(2):
                indices(0, h)
            with a.Fori(0, NS - 1) as s:
                body(s, False)
            body(NS - 1, True)

        @block.tensor
        def _(pe):
            with pe.Fori(0, NS) as s:
                for h, (t0, nt) in enumerate(HALVES):
                    pe.wait_ge(vec, s * (2 * PER) + (h + 1) * PER)
                    pe.wait_ge(copied, s * 2)
                    for k in range(2):
                        for t in range(nt):
                            last = pe.transpose(c.psum[:, 2 * h + k, t * P:(t + 1) * P], xn3[:, h, t, k * P:(k + 1) * P],
                                                c.ident[:])
                    last.then_inc(turned, 1)


def gather_third(c):
    part = Carver(c.scr, SCR)
    part.at = (2 * CT * W) + RING * CT * D
    wk, tile, rows = part.take([2, D]), part.take([2, P]), part.take([D])
    low, e, kk = part.take([D]), part.take([D]), part.take([D])
    w_loaded, tile_ready, z_ready = c.constants.sem, c.sem("k_tile_ready"), c.sem("k_products")
    rows_ready, vec, act, sums_done = c.sem("k_rows_loaded"), c.sem("k_vec"), c.sem("k_exp_done"), c.sem("k_sums_done")
    z, sums, ksum = c.psum[:, 2, 0:D], c.psum[:, 3, :], c.psum[:, 4, 0:2]
    PER = 2

    def first(pe):
        pe.matmul(sums, c.zeros[:], c.ones[:, 0:1].broadcast_to([P, 512]), start=True, stop=False, skip_group_check=True)
        pe.matmul(ksum, c.zeros[:], c.ones[:, 0:2], start=True, stop=False, skip_group_check=True)
        pe.wait_ge(w_loaded, c.constants.at(16))

    def products_begin(pe, i, last):
        pe.wait_ge(tile_ready, i + 1)
        pe.wait_ge(vec, i * PER)
        for k in range(2):
            ins = pe.matmul(z, tile[:, k, :], wk[:, k, :], start=(k == 0), stop=(k == 1))
        ins.then_inc(z_ready, 1)

    def products_end(pe, i, last):
        pe.wait_ge(vec, (i + 1) * PER)
        pe.wait_ge(rows_ready, i * 16 + 16)
        n = LAST if last else P
        for k in range(2):
            pe.matmul(sums[:, k * D:(k + 1) * D], rows[0:n, k * P:(k + 1) * P], kk[0:n, :], start=False, stop=last,
                      skip_group_check=True)
        for j in range(2):
            ins = pe.matmul(ksum[:, j:j + 1], kk[0:n, j * P:(j + 1) * P], c.ones[0:n, 0:1], start=False, stop=last,
                            skip_group_check=True)
        ins.then_inc(sums_done, 1)

    def vector(v, i, last, u):
        step = Chain(v, vec, i, PER)
        if u == 1:
            v.wait_ge(z_ready, i + 1)
            v.wait_ge(act, i)
            step.done(v.tensor_scalar(low, z, 0.0, None, ALU.min))
        if u == 3:
            step.k = 1
            v.wait_ge(act, i + 1)
            v.wait_ge(sums_done, i)
            step.done(v.scalar_tensor_tensor(kk, z, 0.0, e, ALU.max, ALU.add))

    def scalar(a, i, last):
        a.wait_ge(z_ready, i)
        a.activation(tile[:], c.xnT[:, :, ds(i * P, P)], ACT.Copy).then_inc(tile_ready, 1)
        a.wait_ge(vec, i * PER + 1)
        a.activation(e, low, ACT.Exp).then_inc(act, 1)

    def sync_first(sp):
        sp.dma_start(wk.rearrange("p a b -> p (a b)"), c.turned_part("L1_mix_Wk", 2 * D)).then_inc(w_loaded, 16)

    def sync(sp, i, last):
        sp.wait_ge(sums_done, i)
        sp.dma_start(rows, c.xn3_tab[ds(i * P, P), :]).then_inc(rows_ready, 16)

    side = dict(tensor_first=first, tensor_begin=products_begin, tensor_end=products_end, vector=vector,
                scalar=scalar, sync_first=sync_first, sync=sync)
    aggregate(c, table=c.xn3_tab, weighted=True, slots=(0, 1), side=side)
    c.constants.end(16)


HEADS1, DH1 = 8, 32


def fold_second_attention(c):
    nc = c.nc
    part = Carver(c.scr, SCR)
    wvT, wprojT = part.take([2, D]), part.take([2, D])
    kxT, ctxT = part.take([2, D]), part.take([2, P])
    ksum = part.take([2])
    loaded, vec, pe_done = c.constants.sem, c.sem("fold1_vec"), c.sem("fold1_products")
    with nc.Block() as block:

        @block.sync
        def _(sp):
            for w, name in ((wvT, "L1_mix_Wv"), (wprojT, "L1_mix_Wproj")):
                sp.dma_start(w.rearrange("p a b -> p (a b)"), c.turned_part(name, 2 * D)).then_inc(loaded, 16)

        @block.vector
        def _(v):
            v.tensor_copy(kxT.rearrange("p a b -> p (a b)"), c.psum[:, 3, :]).then_inc(vec, 1)
            v.tensor_copy(ksum, c.psum[:, 4, 0:2]).then_inc(vec, 1)
            v.wait_ge(vec, 2)
            v.memset(c.small1[:, 0:2 * HEADS1], 0.0).then_inc(vec, 1)
            v.wait_ge(vec, 3)
            of_head = c.bd32.rearrange("p (g d) -> p g d", d=DH1)[:, :, 0]
            for j in range(2):
                at = j * HEADS1 + j * P // DH1
                v.tensor_scalar(c.small1[:, at:at + P // DH1], of_head, ksum[:, j:j + 1], None, ALU.mult)
            v.wait_ge(pe_done, 1)
            v.tensor_tensor(ctxT[:], c.psum[:, 0, 0:2 * P].rearrange("p (j d) -> p j d", d=P),
                            c.bd32[:].unsqueeze(1).broadcast_to([P, 2, P]), ALU.mult).then_inc(vec, 1)
            v.wait_ge(pe_done, 2)
            v.tensor_copy(c.m0[:], c.psum[:, 1, :].rearrange("p (k d) -> p k d", d=D))

        @block.tensor
        def _(pe):
            pe.wait_ge(vec, 2)
            pe.wait_ge(loaded, c.constants.at(32))
            for j in range(2):
                for k in range(2):
                    last = pe.matmul(c.psum[:, 0, j * P:(j + 1) * P], wvT[:, k, j * P:(j + 1) * P],
                                     kxT[:, k, j * P:(j + 1) * P], start=(k == 0), stop=(k == 1))
            last.then_inc(pe_done, 1)
            pe.wait_ge(vec, 4)
            for j in range(2):
                last = pe.matmul(c.psum[:, 1, j * D:(j + 1) * D], ctxT[:, j, :], wprojT[:, j, :], start=True, stop=True)
            last.then_inc(pe_done, 1)
    c.constants.end(32)


def second_layer_sum(c):
    nc = c.nc
    part = Carver(c.scr, SCR)
    w1T, w2T, wqT = part.take([2, D]), part.take([2, D]), part.take([2, D])
    g1T, qT = part.take([2, 2, 512]), part.take([2, 2, 512])
    e, divisor, inverse = part.take([2, 512]), part.take([2, 4 * HEADS1]), part.take([P])
    spread = part.take([4 * HEADS1, DH1])
    y, x2 = part.take([2, 4, D]), part.take([2, 4, D])
    xn4T = part.take([2, 2, 512])
    b2, gamma, beta, bproj = part.take([D]), part.take([D]), part.take([D]), part.take([D])
    gw, gb = part.take([2, GATES]), part.take([GATES])
    st, mo, rstd = part.take([2, 4, 6]), part.take([2, 4, 2]), part.take([2, 4])
    loaded, consts = c.constants.sem, c.sem("last_shift_ready")
    rows_in = [c.sem(f"last_rows_loaded{h}") for h in range(2)]
    scaled, shifted, moved = c.sem("agg_scaled"), c.sem("last_rows_shifted"), c.sem("x3_and_xn4_moved")
    g_pre, gelu_done, q_pre, q_vec, q_exp = (c.sem("last_gelu_products"), c.sem("last_gelu_done"), c.sem("q_products"),
                                             c.sem("q_vec"), c.sem("q_exp_done"))
    div_pre, y_pre, y_read, m_pre, m_read = (c.sem("divisor_products"), c.sem("y_products"), c.sem("y_read"),
                                             c.sem("attention_products"), c.sem("attention_read"))
    vec, root, turned, copied = c.sem("last_vec"), c.sem("last_root"), c.sem("last_turned"), c.sem("last_copied")
    gate_pre, gate_read = c.sem("gate_products"), c.sem("gate_read")
    inverse_copied = c.sem("inverse_copied")
    QV = 4
    DV = 3
    PER = 11
    Y_VAR, Y_DONE, X3, X_VAR = 3, 5, 6, 9
    flat = "p a b -> p (a b)"

    def former(s, h):
        return (s, 0) if h else (s - 1, 1)

    def columns(s, h):
        t0, nt = HALVES[h]
        return ds(s * SS + t0 * P, nt * P)

    def pipeline(engine, slot):
        slot((0, 0), None, None, True)
        slot((0, 1), (0, 0), None, True)
        with engine.Fori(1, NS) as s:
            for h in range(2):
                slot((s, h), former(s, h), (s - 1, h), False)
        slot(None, (NS - 1, 1), (NS - 1, 0), False)
        slot(None, None, (NS - 1, 1), False)

    with nc.Block() as block:

        @block.sync
        def _(sp):
            for w, name in ((w1T, "L1_gnn_W1"), (w2T, "L1_gnn_W2"), (wqT, "L1_mix_Wq")):
                sp.dma_start(w.rearrange(flat), c.turned_part(name, 2 * D)).then_inc(loaded, 16)
            for b, name in ((b2, "L1_gnn_b2"), (gamma, "L1_gnn_gamma"), (beta, "L1_gnn_beta"), (bproj, "L1_mix_bproj"),
                            (gb, "L1_ffn_gb")):
                sp.dma_start(b, c.inp[name].unsqueeze(0).partition_broadcast(P)).then_inc(loaded, 16)
            sp.dma_start(gw, c.inp["L1_ffn_gW"].rearrange("(k p) e -> p k e", p=P)).then_inc(loaded, 16)

            def load(s, h, first):
                t0, nt = HALVES[h]
                if not first:
                    sp.wait_ge(moved, s * 4 - 3 + 2 * h)
                    sp.wait_ge(turned, s * 2 - 1 + h)
                for rows, table in ((y, c.xn3_tab), (x2, c.x2_tab)):
                    sp.dma_start(rows[:, h, 0:nt, :], table[columns(s, h), :].rearrange("(t p) d -> p t d", p=P)
                                 ).then_inc(rows_in[h], 16)
            for h in range(2):
                load(0, h, True)
            with sp.Fori(1, NS) as s:
                for h in range(2):
                    load(s, h, False)
            sp.wait_ge(loaded, c.constants.at(144))

        @block.gpsimd
        def _(g):
            def scale(s, h):
                acc = c.agg[:, 0:2, columns(s, h)]
                g.tensor_tensor(acc, acc, c.agg[:, 2:3, columns(s, h)].broadcast_to([P, 2, HALVES[h][1] * P]), ALU.mult
                                ).then_inc(scaled, 1)

            def shift(s, h):
                t0, nt = HALVES[h]
                g.wait_ge(rows_in[h], s * 32 + 32)
                for rows, by in ((y, b2), (x2, beta)):
                    last = g.tensor_tensor(rows[:, h, 0:nt, :], rows[:, h, 0:nt, :],
                                           by.unsqueeze(1).broadcast_to([P, nt, D]), ALU.add)
                last.then_inc(shifted, 1)

            def move_x3(s, h):
                t0, nt = HALVES[h]
                g.wait_ge(vec, (s * 2 + h) * PER + X3)
                g.sem_inc(c.passed, 1)
                g.tensor_copy(c.agg[:, 0:2, columns(s, h)].rearrange("p k (t n) -> p t k n", n=P),
                              y[:, h, 0:nt, :].rearrange("p t (k n) -> p t k n", n=P)).then_inc(moved, 1)

            def move_xn4(s, h):
                g.wait_ge(copied, s * 2 + h + 1)
                g.sem_inc(c.passed, 1)
                g.tensor_copy(c.xnT[:, :, columns(s, h)], xn4T[:, h, :, 0:HALVES[h][1] * P]).then_inc(moved, 1)

            scale(0, 0)
            g.wait_ge(loaded, c.constants.at(144))
            g.tensor_tensor(beta, beta, bproj, ALU.add).then_inc(consts, 1)
            g.wait_ge(consts, 2)

            def ahead(s, h):
                scale(*((s + 1, 0) if h else (s, 1)))

            def slot(a, b, c_, first):
                if b is not None:
                    move_x3(*b)
                if c_ is not None:
                    move_xn4(*c_)
                if a is not None:
                    shift(*a)

            ahead(0, 0)
            slot((0, 0), None, None, True)
            ahead(0, 1)
            slot((0, 1), (0, 0), None, True)
            with g.Fori(1, NS - 1) as s:
                for h in range(2):
                    ahead(s, h)
                    slot((s, h), former(s, h), (s - 1, h), False)
            s = NS - 1
            ahead(s, 0)
            slot((s, 0), (s - 1, 1), (s - 1, 0), False)
            slot((s, 1), (s, 0), (s - 1, 1), False)
            slot(None, (s, 1), (s, 0), False)
            slot(None, None, (s, 1), False)

        @block.vector
        def _(v):
            v.wait_ge(loaded, c.constants.at(144))
            rows = 4 * HEADS1
            v.tensor_copy(spread[0:rows, :, :], c.ident[0:rows, 0:rows].unsqueeze(2).broadcast_to([rows, rows, DH1])
                          ).then_inc(consts, 1)

            def q_rows(s, h):
                n = HALVES[h][1] * P
                v.wait_ge(q_exp, (s * 2 + h) * 2 + 2)
                v.scalar_tensor_tensor(qT[:, h, :, 0:n], e[:, :, 0:n], 1.0, qT[:, h, :, 0:n], ALU.min, ALU.add
                                       ).then_inc(q_vec, 1)

            def inverses(s, h):
                n = HALVES[h][1] * HEADS1
                chain = Chain(v, q_vec, s * 2 + h, QV, 1)
                v.wait_ge(div_pre, (s * 2 + h) * DV + 1)
                chain.done(v.tensor_scalar(divisor[:, h, 0:n], c.psum[:, 2, 0:n], 1e-6, None, ALU.max))
                chain.wait()
                chain.done(v.reciprocal(divisor[:, h, 0:n], divisor[:, h, 0:n]))

            def q_divided(s, h):
                n = HALVES[h][1] * P
                v.wait_ge(div_pre, (s * 2 + h) * DV + DV)
                q = qT[:, h, :, 0:n]
                v.tensor_tensor(q, q, c.psum[:, 2:4, 0:n], ALU.mult).then_inc(q_vec, 1)

            def variances(chain, h):
                t0, nt = HALVES[h]
                for t in range(nt):
                    ins = v.bn_stats(st[:, h, t, :], y[:, h, t, :])
                chain.done(ins)
                chain.wait()
                v.sem_inc(c.passed, 1)
                for t in range(nt):
                    ins = v.bn_aggr(mo[:, h, t, :], st[:, h, t, :])
                chain.done(ins)
                chain.wait()
                chain.done(v.tensor_scalar(rstd[:, h, 0:nt], mo[:, h, 0:nt, 1], EPS, None, ALU.add))

            def deviations(chain, s, h, which):
                nt = HALVES[h][1]
                v.wait_ge(root, (s * 2 + h) * 2 + which + 1)
                chain.done(v.reciprocal(rstd[:, h, 0:nt], rstd[:, h, 0:nt]))
                chain.wait()

            def y_rows(s, h):
                nt = HALVES[h][1]
                v.wait_ge(y_pre, s * 2 + h + 1)
                v.wait_ge(shifted, s * 2 + h + 1)
                rows = y[:, h, 0:nt, :]
                v.tensor_tensor(rows, rows, c.psum[:, 4:6, :].rearrange(flat)[:, 0:nt * D].rearrange("p (t d) -> p t d", d=D),
                                ALU.add).then_inc(y_read, 1)
                v.wait_ge(y_read, s * 2 + h + 1)
                variances(Chain(v, vec, s * 2 + h, PER), h)

            def y_normed(s, h):
                chain = Chain(v, vec, s * 2 + h, PER, Y_VAR)
                deviations(chain, s, h, 0)
                for t in range(HALVES[h][1]):
                    ins = v.scalar_tensor_tensor(y[:, h, t, :], y[:, h, t, :], mo[:, h, t, 0:1], gamma, ALU.subtract, ALU.mult)
                chain.done(ins)

            def x3_rows(s, h):
                nt = HALVES[h][1]
                chain = Chain(v, vec, s * 2 + h, PER, Y_DONE)
                v.wait_ge(m_pre, s * 2 + h + 1)
                chain.wait()
                mix = c.psum[:, 6:8, :].rearrange(flat)
                for t in range(nt):
                    ins = v.scalar_tensor_tensor(y[:, h, t, :], y[:, h, t, :], rstd[:, h, t:t + 1], mix[:, t * D:(t + 1) * D],
                                                 ALU.mult, ALU.add)
                ins.then_inc(m_read, 1)
                v.wait_ge(m_read, s * 2 + h + 1)
                rows = y[:, h, 0:nt, :]
                chain.done(v.tensor_tensor(rows, rows, x2[:, h, 0:nt, :], ALU.add))
                chain.wait()
                variances(chain, h)

            def xn4_rows(s, h):
                chain = Chain(v, vec, s * 2 + h, PER, X_VAR)
                deviations(chain, s, h, 1)
                for t in range(HALVES[h][1]):
                    ins = v.tensor_scalar(x2[:, h, t, :], y[:, h, t, :], mo[:, h, t, 0:1], rstd[:, h, t:t + 1],
                                          ALU.subtract, ALU.mult)
                chain.done(ins)

            def gates_read(s, h):
                t0, nt = HALVES[h]
                v.wait_ge(gate_pre, s * 2 + h + 1)
                v.tensor_tensor(c.scores[:, ds(s * TS + t0, nt), 0:GATES],
                                c.psum[:, 0, 0:nt * GATES].rearrange("p (t e) -> p t e", e=GATES),
                                gb.unsqueeze(1).broadcast_to([P, nt, GATES]), ALU.add).then_inc(gate_read, 1)

            def slot(a, b, c_, first):
                if a is not None:
                    q_rows(*a)
                if b is not None:
                    y_rows(*b)
                if a is not None:
                    inverses(*a)
                if b is not None:
                    y_normed(*b)
                if a is not None:
                    q_divided(*a)
                if b is not None:
                    x3_rows(*b)
                if c_ is not None:
                    gates_read(*c_)
                if b is not None:
                    xn4_rows(*b)
            pipeline(v, slot)

        @block.scalar
        def _(a_):
            def gelu(s, h):
                n = HALVES[h][1] * P
                a_.wait_ge(g_pre, s * 2 + h + 1)
                for m in range(2):
                    last = a_.activation(g1T[:, h, m, 0:n], c.psum[:, m, 0:n], ACT.Gelu, bias=c.column("L1_gnn_b1", m))
                last.then_inc(gelu_done, 1)

            def exp_and_relu(s, h, first):
                n, u = HALVES[h][1] * P, s * 2 + h
                a_.wait_ge(q_pre, u + 1)
                if not (first and h == 0):
                    a_.wait_ge(q_vec, u * QV - QV + 1)
                a_.activation(e[:, :, 0:n], c.psum[:, 2:4, 0:n], ACT.Exp).then_inc(q_exp, 1)
                a_.activation(qT[:, h, :, 0:n], c.psum[:, 2:4, 0:n], ACT.Relu).then_inc(q_exp, 1)

            def rooted(s, h, at):
                nt = HALVES[h][1]
                a_.wait_ge(vec, (s * 2 + h) * PER + at)
                a_.activation(rstd[:, h, 0:nt], rstd[:, h, 0:nt], ACT.Sqrt).then_inc(root, 1)

            def copy(s, h, early):
                n, u = HALVES[h][1] * P, s * 2 + h
                a_.wait_ge(turned, u + 1)
                if not early:
                    a_.wait_ge(moved, u * 2 - 1)
                for k in range(2):
                    last = a_.activation(xn4T[:, h, k, 0:n], c.psum[:, 4 + k, 0:n], ACT.Copy)
                last.then_inc(copied, 1)

            def copy_inverses(s, h):
                n = HALVES[h][1] * HEADS1
                a_.wait_ge(div_pre, (s * 2 + h) * DV + 2)
                a_.activation(inverse[0:n, :], c.psum[0:n, 3, 0:P], ACT.Copy).then_inc(inverse_copied, 1)

            def slot(a, b, c_, first, early=False):
                if a is not None:
                    exp_and_relu(*a, first)
                    gelu(*a)
                if b is not None:
                    rooted(*b, Y_VAR)
                if a is not None:
                    copy_inverses(*a)
                if c_ is not None:
                    copy(*c_, early)
                if b is not None:
                    rooted(*b, X_VAR)
            slot((0, 0), None, None, True)
            slot((0, 1), (0, 0), None, True)
            for h in range(2):
                slot((1, h), former(1, h), (0, h), False, early=True)
            with a_.Fori(2, NS) as s:
                for h in range(2):
                    slot((s, h), former(s, h), (s - 1, h), False)
            slot(None, (NS - 1, 1), (NS - 1, 0), False)
            slot(None, None, (NS - 1, 1), False)

        @block.tensor
        def _(pe):
            pe.wait_ge(loaded, c.constants.at(144))

            def gelu_products(s, h, first):
                n, u = HALVES[h][1] * P, s * 2 + h
                pe.wait_ge(scaled, u + 1)
                pe.wait_ge(gelu_done, u)
                if not first:
                    pe.wait_ge(gate_read, u - 2)
                for m in range(2):
                    for k in range(2):
                        last = pe.matmul(c.psum[:, m, 0:n], w1T[:, k, m * P:(m + 1) * P], c.agg[:, k, columns(s, h)],
                                         start=(k == 0), stop=(k == 1))
                last.then_inc(g_pre, 1)

            def q_products(s, h):
                n, u = HALVES[h][1] * P, s * 2 + h
                pe.wait_ge(q_vec, u * QV)
                for m in range(2):
                    for k in range(2):
                        last = pe.matmul(c.psum[:, 2 + m, 0:n], wqT[:, k, m * P:(m + 1) * P], c.xnT[:, k, columns(s, h)],
                                         start=(k == 0), stop=(k == 1))
                last.then_inc(q_pre, 1)

            def divisors(s, h):
                pe.wait_ge(q_vec, (s * 2 + h) * QV + 1)
                for t in range(HALVES[h][1]):
                    for j in range(2):
                        last = pe.matmul(c.psum[:, 2, t * HEADS1:(t + 1) * HEADS1], qT[:, h, j, t * P:(t + 1) * P],
                                         c.small1[:, j * HEADS1:(j + 1) * HEADS1], start=(j == 0), stop=(j == 1))
                last.then_inc(div_pre, 1)

            def turn_inverses(s, h):
                n = HALVES[h][1] * HEADS1
                pe.wait_ge(q_vec, (s * 2 + h) * QV + 3)
                pe.transpose(c.psum[0:n, 3, 0:P], divisor[:, h, 0:n], c.ident[:]).then_inc(div_pre, 1)

            def spread_inverses(s, h):
                nt = HALVES[h][1]
                n = nt * HEADS1
                heads = P // DH1
                pe.wait_ge(inverse_copied, s * 2 + h + 1)
                for t in range(nt):
                    for j in range(2):
                        at = t * HEADS1 + j * heads
                        last = pe.matmul(c.psum[:, 2 + j, t * P:(t + 1) * P],
                                         spread[0:n, at:at + heads, :].rearrange("p g d -> p (g d)"), inverse[0:n, :],
                                         start=True, stop=True)
                last.then_inc(div_pre, 1)

            def node_rows(bank, lhs, h, w):
                for t in range(HALVES[h][1]):
                    for k in range(2):
                        last = pe.matmul(c.psum[:, bank + t // 2, (t % 2) * D:(t % 2 + 1) * D], lhs[:, h, k, t * P:(t + 1) * P],
                                         w[:, k, :], start=(k == 0), stop=(k == 1))
                return last

            def y_products(s, h, first):
                u = s * 2 + h
                pe.wait_ge(gelu_done, u + 1)
                pe.wait_ge(y_read, u)
                if not first:
                    pe.wait_ge(copied, u - 1)
                node_rows(4, g1T, h, w2T).then_inc(y_pre, 1)

            def attention(s, h, first):
                u = s * 2 + h
                pe.wait_ge(q_vec, u * QV + QV)
                pe.wait_ge(m_read, u)
                node_rows(6, qT, h, c.m0).then_inc(m_pre, 1)

            def turn_rows(s, h, y_rows_read):
                nt, u = HALVES[h][1], s * 2 + h
                pe.wait_ge(vec, (u + 1) * PER)
                pe.wait_ge(y_read, y_rows_read)
                for k in range(2):
                    for t in range(nt):
                        last = pe.transpose(c.psum[:, 4 + k, t * P:(t + 1) * P], x2[:, h, t, k * P:(k + 1) * P], c.ident[:])
                last.then_inc(turned, 1)

            def gate_products(s, h, behind):
                u = s * 2 + h
                pe.wait_ge(copied, u + 1)
                pe.wait_ge(gelu_done, 2 * NS if behind else u + 3)
                if behind:
                    pe.wait_ge(gate_read, u)
                for t in range(HALVES[h][1]):
                    for k in range(2):
                        last = pe.matmul(c.psum[:, 0, t * GATES:(t + 1) * GATES], xn4T[:, h, k, t * P:(t + 1) * P], gw[:, k, :],
                                         start=(k == 0), stop=(k == 1))
                last.then_inc(gate_pre, 1)

            def slot(a, b, c_, first):
                if a is not None:
                    q_products(*a)
                    gelu_products(*a, first)
                if b is not None:
                    y_products(*b, first)
                if a is not None:
                    divisors(*a)
                if b is not None:
                    attention(*b, first)
                if a is not None:
                    turn_inverses(*a)
                if c_ is not None:
                    turn_rows(*c_, c_[0] * 2 + c_[1] + (2 if b is not None else 1))
                if a is not None:
                    spread_inverses(*a)
                if c_ is not None:
                    gate_products(*c_, a is None)
            pipeline(pe, slot)
    c.constants.end(144)


GATES = 4
EH1, EH2 = 128, 64
SH1, SH2 = 256, 128


class LastWeights:

    def __init__(self, part):
        self.parts = part.take([2, 6 * D * 2], F16)
        self.b3 = part.take([D])
        self.pick = part.take([GATES // 2, P])
        self.end = part.at

        def piece(first, *shape):
            size = 1
            for n in shape:
                size *= n
            view = self.parts[:, :, first:first + size]
            if len(shape) == 2:
                view = view.rearrange("p h (a b) -> p h a b", b=shape[1])
            if len(shape) == 3:
                view = view.rearrange("p h (a b c) -> p h a b c", b=shape[1], c=shape[2])
            return view, first + size
        self.s1, at = piece(0, 2, SH1)
        self.s2, at = piece(at, 2, SH2)
        self.s3, at = piece(at, D)
        self.e1, at = piece(at, GATES, 2, EH1)
        self.e2, at = piece(at, GATES, P)
        self.e3, at = piece(at, GATES // 2, D)
        assert at == 6 * D * 2


def gates(c):
    nc = c.nc
    part = Carver(c.scr, SCR)
    w = c.last = LastWeights(part)
    raw = part.take([6 * D * 2])
    raw_s1 = raw[:, 0:2 * SH1].rearrange("p (k n) -> p k n", n=SH1)
    at = 2 * SH1
    raw_s2 = raw[:, at:at + 2 * SH2].rearrange("p (k n) -> p k n", n=SH2)
    at += 2 * SH2
    raw_s3 = raw[:, at:at + D]
    at += D
    raw_e1 = raw[:, at:at + GATES * 2 * EH1].rearrange("p (e k n) -> p e k n", k=2, n=EH1)
    at += GATES * 2 * EH1
    raw_e2 = raw[:, at:at + GATES * P].rearrange("p (e n) -> p e n", n=P)
    at += GATES * P
    raw_e3 = raw[:, at:at + GATES // 2 * D].rearrange("p (q n) -> p q n", n=D)
    G4 = [NT, GATES]
    rev, p, eq, cand, rest = part.take([GATES]), part.take(G4), part.take(G4), part.take(G4), part.take(G4)
    mask = [part.take(G4), part.take(G4)]
    top, code, weight = part.take([NT]), part.take([NT]), [part.take([NT]), part.take([NT])]
    second = part.take([NT])
    gate5 = part.take([NT, GATES + 1])
    logits = c.scores[:, :, 0:GATES]
    cleared, vec, act = c.sem("last_weights_cleared"), c.sem("gates_vec"), c.sem("gates_exp")
    turned, copied, high = c.sem("gates_turned"), c.sem("gates_copied"), c.moves.sem
    groups = -(-NT // 4)
    marks = {}
    n_loads = 3 + 2 * GATES + GATES // 2 + 2
    with nc.Block() as block:

        @block.sync
        def _(sp):
            inp = {n: c.inp["L1_ffn_" + n] for n in ("sW1", "sW2", "sW3", "eW1", "eW2", "eW3", "eb3", "sb3")}
            done = c.constants.sem
            sp.dma_start(raw_s1, inp["sW1"].rearrange("(k p) n -> p k n", p=P)).then_inc(done, 16)
            sp.dma_start(raw_s2, inp["sW2"].rearrange("(k p) n -> p k n", p=P)).then_inc(done, 16)
            sp.dma_start(raw_s3, inp["sW3"]).then_inc(done, 16)
            for e in range(GATES):
                sp.dma_start(raw_e1[:, e, :, :], inp["eW1"][e, :, :].rearrange("(k p) n -> p k n", p=P)).then_inc(done, 16)
            for q in range(GATES // 2):
                sp.dma_start(raw_e3[:, q, :], inp["eW3"][2 * q:2 * q + 2, :, :].rearrange("e g o -> (e g) o")).then_inc(done, 16)
            sp.dma_start(w.b3[0:GATES, :], inp["eb3"]).then_inc(done, 16)
            sp.dma_start(w.b3[GATES:GATES + 1, :], inp["sb3"].unsqueeze(0)).then_inc(done, 16)
            sp.wait_ge(cleared, 1)
            for e in range(GATES):
                at = (e % 2) * EH2
                sp.dma_start(raw_e2[:, e, at:at + EH2], inp["eW2"][e, :, :]).then_inc(done, 16)
            sp.wait_ge(done, c.constants.at(16 * n_loads))

        @block.vector
        def _(v):
            v.memset(raw_e2, 0.0).then_inc(cleared, 1)
            for q in range(GATES // 2):
                for b in range(2):
                    e = 2 * q + b
                    v.tensor_copy(w.pick[0:GATES, q, b * EH2:(b + 1) * EH2],
                                  c.ident[0:GATES, e:e + 1].broadcast_to([GATES, EH2]))
            chain = Chain(v, vec)

            def do(ins):
                chain.done(ins)
                chain.wait()

            def over(x):
                return x.unsqueeze(2).broadcast_to([P, NT, GATES])
            rev_b = rev.unsqueeze(1).broadcast_to([P, NT, GATES])
            do(v.tensor_scalar(rev, c.iota[:, 0:GATES], -1.0, float(GATES), ALU.mult, ALU.add))
            do(v.tensor_reduce(top, logits, AX.X, ALU.max))
            do(v.tensor_tensor(p, logits, over(top), ALU.subtract))
            marks["shifted"] = chain.value()
            v.wait_ge(act, 1)
            do(v.tensor_reduce(top, p, AX.X, ALU.add))
            do(v.reciprocal(top, top))
            do(v.tensor_tensor(p, p, over(top), ALU.mult))
            for n, values in enumerate((p, rest)):
                best = (top, second)[n]
                do(v.tensor_reduce(best, values, AX.X, ALU.max))
                do(v.tensor_tensor(eq, values, over(best), ALU.is_equal))
                do(v.tensor_tensor(cand, eq, rev_b, ALU.mult))
                do(v.tensor_reduce(code, cand, AX.X, ALU.max))
                do(v.tensor_tensor(mask[n], rev_b, over(code), ALU.is_equal))
                if n == 0:
                    do(v.scalar_tensor_tensor(rest, mask[0], -2.0, p, ALU.mult, ALU.add))
            do(v.tensor_tensor(second, second, top, ALU.subtract))
            marks["second"] = chain.value()
            v.wait_ge(act, 2)
            do(v.tensor_scalar(top, second, 1.0, None, ALU.add))
            do(v.reciprocal(weight[0], top))
            do(v.tensor_tensor(weight[1], second, weight[0], ALU.mult))
            for n in range(2):
                do(v.tensor_tensor(mask[n], mask[n], over(weight[n]), ALU.mult))
            do(v.memset(gate5[:, :, GATES:GATES + 1], 1.0))
            do(v.tensor_tensor(gate5[:, :, 0:GATES], mask[0], mask[1], ALU.add))
            marks["gates"] = chain.value()
            v.wait_ge(high, c.moves.at(1))
            v.scalar_tensor_tensor(w.parts[:, 1, :], raw, WS, w.parts[:, 0, :], ALU.mult, ALU.subtract)
            v.tensor_scalar(w.b3[0:GATES + 1, :], w.b3[0:GATES + 1, :], XS * WS, None, ALU.mult)

        @block.scalar
        def _(a):
            a.wait_ge(vec, marks["shifted"])
            a.activation(p, p, ACT.Exp).then_inc(act, 1)
            a.wait_ge(vec, marks["second"])
            a.activation(second, second, ACT.Exp).then_inc(act, 1)
            a.wait_ge(c.constants.sem, c.constants.at(16 * n_loads))
            a.activation(w.parts[:, 0, :], raw, ACT.Copy, scale=WS).then_inc(high, 1)
            for q in range(groups):
                n = min(4, NT - 4 * q) * P
                a.wait_ge(turned, q + 1)
                a.activation(c.agg[0:GATES + 1, 2, q * 4 * P:q * 4 * P + n], c.psum[0:GATES + 1, q % 8, 0:n], ACT.Copy
                             ).then_inc(copied, 1)

        @block.tensor
        def _(pe):
            pe.wait_ge(vec, marks["gates"])
            for q in range(groups):
                if q >= 8:
                    pe.wait_ge(copied, q - 7)
                for t in range(min(4, NT - 4 * q)):
                    last = pe.transpose(c.psum[0:GATES + 1, q % 8, t * P:(t + 1) * P], gate5[:, 4 * q + t, :], c.ident[:])
                last.then_inc(turned, 1)
    c.constants.end(16 * n_loads)
    c.moves.end(1)


def second_mixture(c):
    nc = c.nc
    w = c.last
    part = Carver(c.scr, SCR)
    part.at = w.end
    x, s1, e1 = part.take([2, 2, 512], F16), part.take([2, 2, 512], F16), part.take([2, GATES, 512], F16)
    s2, e2w = part.take([2, 512], F16), part.take([2, 2, 512], F16)
    stage = part.take([2, 512])
    e2, e2g = part.take([2, 512]), part.take([2, 512])
    gate = part.take([2, 512])
    rows = part.take([2, 4, D])
    taken, x_low, high, low = c.sem("x_and_gates_taken"), c.sem("last_x_low"), c.sem("hidden_high"), c.sem("hidden_low")
    SCALE = 1.0 / (XS * WS)
    PARTS = ((0, 0), (0, 1), (1, 0))
    pre, relu = c.sem("mixture_products"), c.sem("mixture_relu_done")
    spread, gated = c.sem("mixture_gates_spread"), c.sem("mixture_gated")
    out_pre, out_ready = c.sem("out_products"), c.sem("out_rows_ready")
    stored = [c.sem(f"out_stored{h}") for h in range(2)]
    K = 9
    SPLIT = K - 2
    G1 = GATES + 1

    def turns(engine, body):
        body(0, True, False)
        with engine.Fori(1, NS - 1) as s:
            body(s, False, False)
        body(NS - 1, False, True)

    def columns(s, h):
        t0, nt = HALVES[h]
        return ds(s * SS + t0 * P, nt * P)

    with nc.Block() as block:

        @block.sync
        def _(sp):
            def body(s, first, last):
                for h, (t0, nt) in enumerate(HALVES):
                    sp.wait_ge(out_ready, s * 2 + h + 1)
                    if last and h == 1:
                        r0 = (NS - 1) * SS + t0 * P
                        full = nt - 1
                        sp.dma_start(c.out[r0:r0 + full * P, :].rearrange("(t p) d -> p t d", p=P), rows[:, h, 0:full, :]
                                     ).then_inc(stored[h], 16)
                        sp.dma_start(c.out[r0 + full * P:N, :], rows[0:LAST, h, full, :]).then_inc(stored[h], 16)
                    else:
                        sp.dma_start(c.out[columns(s, h), :].rearrange("(t p) d -> p t d", p=P), rows[:, h, 0:nt, :]
                                     ).then_inc(stored[h], 16)
            turns(sp, body)
            sp.wait_ge(stored[0], 16 * NS)
            sp.wait_ge(stored[1], 16 * NS + 16)

        @block.scalar
        def _(a):
            def take_x(s, h):
                n = HALVES[h][1] * P
                a.activation(x[:, 0, :, 0:n], c.xnT[:, :, columns(s, h)], ACT.Copy, scale=XS).then_inc(taken, 1)

            take_x(0, 0)

            def body(s, first, last):
                for h, (t0, nt) in enumerate(HALVES):
                    n, u = nt * P, s * 2 + h
                    if not first:
                        a.wait_ge(out_pre, u - 1)
                    a.activation(gate[0:G1, h, 0:n], c.agg[0:G1, 2, columns(s, h)], ACT.Copy).then_inc(taken, 1)
                    outs = ([(s1[:, 0, m, :], m, "L1_ffn_sb1", m) for m in range(2)] +
                            [(e1[:, 0, e, :], (2, 3, 0, 1)[e], "L1_ffn_eb1", e) for e in range(GATES)] +
                            [(s2[:, 0, :], 2, "L1_ffn_sb2", 0)])
                    for i, (to, bank, bias, j) in enumerate(outs):
                        m = u * SPLIT + i
                        if i == SPLIT - 1 and not (last and h == 1):
                            take_x(*((s + 1, 0) if h else (s, 1)))
                        a.wait_ge(pre, u * K + i + 1)
                        if not (first and h == 0 and i < 2):
                            a.wait_ge(low, m - 1)
                        a.activation(stage[:, (i + h) % 2, 0:n], c.psum[:, bank, 0:n], ACT.Relu,
                                     bias=c.column(bias, j), scale=SCALE).then_inc(relu, 1)
                        a.wait_ge(relu, u * K + i + 1)
                        a.activation(to[:, 0:n], stage[:, (i + h) % 2, 0:n], ACT.Copy, scale=XS).then_inc(high, 1)
                    for q in range(2):
                        a.wait_ge(pre, u * K + SPLIT + q + 1)
                        a.wait_ge(gated, u * 3)
                        a.activation(e2[:, q, 0:n], c.psum[:, q, 0:n], ACT.Relu, bias=c.column("L1_ffn_eb2", q), scale=SCALE
                                     ).then_inc(relu, 1)
            turns(a, body)

        @block.vector
        def _(v):
            def split_x(s, h):
                n, u = HALVES[h][1] * P, s * 2 + h
                v.wait_ge(taken, u * 2 + 1)
                v.scalar_tensor_tensor(x[:, 1, :, 0:n], c.xnT[:, :, columns(s, h)], XS, x[:, 0, :, 0:n], ALU.mult, ALU.subtract
                                       ).then_inc(x_low, 1)

            def split_hidden(s, h, parts):
                n, u = HALVES[h][1] * P, s * 2 + h
                outs = [s1[:, :, m, :] for m in range(2)] + [e1[:, :, e, :] for e in range(GATES)] + [s2]
                for i in parts:
                    v.wait_ge(high, u * SPLIT + i + 1)
                    v.scalar_tensor_tensor(outs[i][:, 1, 0:n], stage[:, (i + h) % 2, 0:n], XS, outs[i][:, 0, 0:n],
                                           ALU.mult, ALU.subtract).then_inc(low, 1)

            def gate_rows(s, h):
                n, u = HALVES[h][1] * P, s * 2 + h
                v.wait_ge(relu, (u + 1) * K)
                v.wait_ge(spread, u + 1)
                v.tensor_tensor(e2g[:, :, 0:n], e2[:, :, 0:n], c.psum[:, 4:6, 0:n], ALU.mult).then_inc(gated, 1)
                v.wait_ge(gated, u * 3 + 1)
                v.tensor_scalar(e2w[:, 0, :, 0:n], e2g[:, :, 0:n], XS, None, ALU.mult).then_inc(gated, 1)
                v.wait_ge(gated, u * 3 + 2)
                v.scalar_tensor_tensor(e2w[:, 1, :, 0:n], e2g[:, :, 0:n], XS, e2w[:, 0, :, 0:n], ALU.mult, ALU.subtract
                                       ).then_inc(gated, 1)

            def out_rows(s, h):
                t0, nt = HALVES[h]
                v.wait_ge(out_pre, s * 2 + h + 1)
                v.wait_ge(stored[h], s * 16)
                sums = c.psum[:, 6:8, :].rearrange("p a b -> p (a b)")[:, 0:nt * D].rearrange("p (t k n) -> p t k n", n=P, k=2)
                for k in range(2):
                    last = v.scalar_tensor_tensor(rows[:, h, 0:nt, k * P:(k + 1) * P], sums[:, :, k, :], SCALE,
                                                  c.agg[:, k, columns(s, h)].rearrange("p (t n) -> p t n", n=P),
                                                  ALU.mult, ALU.add)
                last.then_inc(out_ready, 1)

            def body(s, first, last):
                for h in range(2):
                    split_hidden(s, h, range(SPLIT - 1))
                    if not (last and h == 1):
                        split_x(*((s + 1, 0) if h else (s, 1)))
                    if not (first and h == 0):
                        out_rows(*((s, 0) if h else (s - 1, 1)))
                    split_hidden(s, h, [SPLIT - 1])
                    gate_rows(s, h)
            split_x(0, 0)
            turns(v, body)
            out_rows(NS - 1, 1)

        @block.tensor
        def _(pe):
            def product(out, weights, moving, k_last, first=True):
                for i, (wp, xp) in enumerate(PARTS):
                    last = pe.matmul(out, weights(wp), moving(xp), start=(first and i == 0), stop=(k_last and i == 2))
                return last

            def hidden(s, h):
                t0, nt = HALVES[h]
                n, u = nt * P, s * 2 + h
                pe.wait_ge(x_low, u + 1)
                pe.wait_ge(relu, u * K)
                for m in range(2):
                    for k in range(2):
                        last = product(c.psum[:, m, 0:n], lambda p: w.s1[:, p, k, m * P:(m + 1) * P], lambda p: x[:, p, k, 0:n],
                                       k == 1, k == 0)
                    last.then_inc(pre, 1)
                for e in range(GATES):
                    if e >= 2:
                        pe.wait_ge(relu, u * K + e - 1)
                    for k in range(2):
                        last = product(c.psum[:, (2, 3, 0, 1)[e], 0:n], lambda p: w.e1[:, p, e, k, :],
                                       lambda p: x[:, p, k, 0:n], k == 1, k == 0)
                    last.then_inc(pre, 1)

            def second(s, h):
                t0, nt = HALVES[h]
                n, u = nt * P, s * 2 + h
                pe.wait_ge(low, u * SPLIT + 3)
                for k in range(2):
                    last = product(c.psum[:, 2, 0:n], lambda p: w.s2[:, p, k, :], lambda p: s1[:, p, k, 0:n], k == 1, k == 0)
                last.then_inc(pre, 1)
                pe.wait_ge(taken, u * 2 + 2)
                pe.wait_ge(gated, u * 3)
                for q in range(2):
                    last = pe.matmul(c.psum[:, 4 + q, 0:n], w.pick[0:GATES, q, :], gate[0:GATES, h, 0:n], start=True, stop=True)
                last.then_inc(spread, 1)
                for q in range(2):
                    pe.wait_ge(low, u * SPLIT + 5 + q)
                    for b in range(2):
                        last = product(c.psum[:, q, 0:n], lambda p: w.e2[:, p, 2 * q + b, :],
                                       lambda p: e1[:, p, 2 * q + b, 0:n], b == 1, b == 0)
                    last.then_inc(pre, 1)

            def out_products(s, h):
                t0, nt = HALVES[h]
                u = s * 2 + h
                pe.wait_ge(gated, u * 3 + 3)
                pe.wait_ge(low, (u + 1) * SPLIT)
                pe.wait_ge(out_ready, u)
                for t in range(nt):
                    bank = c.psum[:, 6 + t // 2, (t % 2) * D:(t % 2 + 1) * D]
                    at = slice(t * P, (t + 1) * P)
                    product(bank, lambda p: s2[:, p, at], lambda p: w.s3[:, p, :], False)
                    for q in range(2):
                        product(bank, lambda p: e2w[:, p, q, at], lambda p: w.e3[:, p, q, :], False, False)
                    last = pe.matmul(bank, gate[0:G1, h, at], w.b3[0:G1, :], start=False, stop=True)
                last.then_inc(out_pre, 1)

            def body(s, first, last):
                hidden(s, 0)
                if not first:
                    out_products(s - 1, 1)
                second(s, 0)
                hidden(s, 1)
                out_products(s, 0)
                second(s, 1)
            turns(pe, body)
            out_products(NS - 1, 1)


PHASES = (make_constants, prepare_edges, count_degrees, scale_by_degrees, gather_first, fold_attention, first_conv,
          gather_second, first_layer_sum, route, send_to_experts, experts, second_norm, gather_third,
          fold_second_attention, second_layer_sum, gates, second_mixture)


def build(nc, inputs, out):
    with ExitStack() as ctx:
        core = Core(nc, ctx, inputs, out)
        for phase in PHASES:
            phase(core)


def kernel(**inputs):
    import numpy as _np
    import concourse.bacc as _bacc
    from concourse import mybir as _mybir
    from concourse.bass_utils import run_bass_kernel_spmd as _run

    nc = _bacc.Bacc("TRN2", target_bir_lowering=False, num_devices=1)
    arrays = {name: _np.ascontiguousarray(a) for name, a in inputs.items()}
    dram = {name: nc.dram_tensor("in_" + name, a.shape, _mybir.dt.from_np(a.dtype), kind="ExternalInput").ap()
            for name, a in arrays.items()}
    out = nc.dram_tensor("out", arrays["x"].shape, _mybir.dt.float32, kind="ExternalOutput").ap()
    build(nc, dram, out)
    got = _run(nc, [{"in_" + name: a for name, a in arrays.items()}], core_ids=[0])
    return got.results[0]["out"]
```
